# Optimizing a Trainium2 kernel written in Bass

```python
import numpy as np
import jax
import jax.numpy as jnp

def _softmax(x, axis=-1):
    return jax.nn.softmax(x, axis=axis)

def _gelu(x):
    return jax.nn.gelu(x, approximate=True)

def _silu(x):
    return jax.nn.silu(x)

def _sigmoid(x):
    return jax.nn.sigmoid(x)

def _layernorm(x, axis=-1, eps=1e-05):
    m = jnp.mean(x, axis=axis, keepdims=True)
    v = jnp.var(x, axis=axis, keepdims=True)
    return (x - m) / jnp.sqrt(v + eps)

def _scatter_add(tgt, idx, src, axis=0):
    return tgt.at[idx].add(src)

def _segment_sum(src, seg, n):
    return jax.ops.segment_sum(src, seg, n)
kernel_name = 'mk_early_fusion_embed_d4_tok_img256_r4_62a28f'

def setup_inputs(seed: int=0):
    np.random.seed(seed)
    _w = jnp.asarray

    def _rec_inputs():
        import jax
        import jax.numpy as jnp
        _rk = jax.random.key(seed)
        x = -0.000928989 + 1.00043 * jax.random.normal(jax.random.fold_in(_rk, 1), (4, 64, 64, 1), jnp.float32)
        x_txt = jax.random.randint(jax.random.fold_in(_rk, 51), (4, 512), 0, 12564, jnp.int32)
        return (x, x_txt)
    x, x_txt = _rec_inputs()

    def _L0_tok_setup():
        import jax, jax.numpy as jnp
        import numpy as np
        B, S, D_A, D_V, D_U, L, M1, M2 = (16, 64, 3, 32, 1, 4, 12, 12)
        MID = 4 * D_U

        def conv1x1(x, w, b):
            return jnp.einsum('bixy,oi->boxy', x, w) + b[None, :, None, None]

        def fourier_layer(x, fw_i):
            Bm, C, M, N = x.shape
            x_ft = jnp.fft.rfft2(x, s=(M, N), norm='ortho')
            w_lo = fw_i[0, ..., 0] + 1j * fw_i[0, ..., 1]
            w_hi = fw_i[1, ..., 0] + 1j * fw_i[1, ..., 1]
            lo = jnp.einsum('bixy,ioxy->boxy', x_ft[:, :, :M1, :M2], w_lo)
            hi = jnp.einsum('bixy,ioxy->boxy', x_ft[:, :, -M1:, :M2], w_hi)
            out_ft = jnp.zeros(x_ft.shape, dtype=x_ft.dtype)
            out_ft = out_ft.at[:, :, :M1, :M2].set(lo)
            out_ft = out_ft.at[:, :, -M1:, :M2].set(hi)
            return jnp.fft.irfft2(out_ft, s=(M, N), norm='ortho')

        def make_grid(b, sx, sy):
            gx = jnp.broadcast_to(jnp.linspace(0.0, 1.0, sx)[None, :, None], (b, sx, sy))
            gy = jnp.broadcast_to(jnp.linspace(0.0, 1.0, sy)[None, None, :], (b, sx, sy))
            return jnp.stack([gx, gy], axis=-1)
        key = jax.random.key(seed)
        ks = jax.random.split(key, 12)
        sc_v = 1.0 / np.sqrt(D_V)
        inp = {'x': jax.random.normal(ks[0], (B, S, S, D_A - 2), dtype=jnp.float32), 'p_w': jax.random.normal(ks[1], (D_V, D_A), dtype=jnp.float32) / np.sqrt(D_A), 'p_b': jnp.zeros((D_V,), dtype=jnp.float32), 'fw': jax.random.normal(ks[2], (L, 2, D_V, D_V, M1, M2, 2), dtype=jnp.float32) * sc_v, 'w1_w': jax.random.normal(ks[3], (L, D_V, D_V), dtype=jnp.float32) * sc_v, 'w1_b': jnp.zeros((L, D_V), dtype=jnp.float32), 'w2_w': jax.random.normal(ks[4], (L, D_V, D_V), dtype=jnp.float32) * sc_v, 'w2_b': jnp.zeros((L, D_V), dtype=jnp.float32), 'q1_w': jax.random.normal(ks[5], (MID, D_V), dtype=jnp.float32) * sc_v, 'q1_b': jnp.zeros((MID,), dtype=jnp.float32), 'q2_w': jax.random.normal(ks[6], (D_U, MID), dtype=jnp.float32) / np.sqrt(MID), 'q2_b': jnp.zeros((D_U,), dtype=jnp.float32)}
        return inp
    _L0_tok_all = _L0_tok_setup()
    _L0_tok_in = {k: v for k, v in _L0_tok_all.items() if k in ('p_w', 'p_b', 'fw', 'w1_w', 'w1_b', 'w2_w', 'w2_b', 'q1_w', 'q1_b', 'q2_w', 'q2_b')}
    del _L0_tok_all

    def _L0_txt_setup():
        import jax, jax.numpy as jnp
        import numpy as np
        VOCAB, N_TURNS, OUT_DIM, POLY_DEG = (50257, 4, 64, 4)
        key = jax.random.key(seed)
        k1, k2, k3 = jax.random.split(key, 3)
        token_ids = jax.random.randint(k1, (16, 1024), 0, VOCAB)
        turns = jax.random.normal(k2, (VOCAB, N_TURNS), dtype=jnp.float32) * 3.0
        poly_coeffs = jax.random.normal(k3, (N_TURNS, POLY_DEG + 1, OUT_DIM), dtype=jnp.float32) * 0.01
        return {'token_ids': token_ids, 'turns': turns, 'poly_coeffs': poly_coeffs}
    _L0_txt_all = _L0_txt_setup()
    _L0_txt_in = {k: v for k, v in _L0_txt_all.items() if k in ('turns', 'poly_coeffs')}
    del _L0_txt_all

    def _L0_attn_setup():
        import jax, jax.numpy as jnp
        import numpy as np
        SEQ_LEN = 512
        EMBED_DIM = 64
        BATCH = 8
        LN_EPS = 1e-05

        def _layernorm(x, g, b):
            mu = jnp.mean(x, axis=-1, keepdims=True)
            var = jnp.mean(jnp.square(x - mu), axis=-1, keepdims=True)
            return (x - mu) * jax.lax.rsqrt(var + LN_EPS) * g + b
        key = jax.random.key(seed)
        ks = jax.random.split(key, 8)
        C = EMBED_DIM
        x = jax.random.normal(ks[0], (BATCH, SEQ_LEN, C), dtype=jnp.float32)
        qkv_w = jax.random.normal(ks[1], (C, 3 * C), dtype=jnp.float32) * 0.02
        qkv_b = jnp.zeros((3 * C,), dtype=jnp.float32)
        proj_w = jax.random.normal(ks[2], (C, C), dtype=jnp.float32) * 0.02
        proj_b = jnp.zeros((C,), dtype=jnp.float32)
        ln1_g = jnp.ones((C,), dtype=jnp.float32)
        ln1_b = jnp.zeros((C,), dtype=jnp.float32)
        ln2_g = jnp.ones((C,), dtype=jnp.float32)
        ln2_b = jnp.zeros((C,), dtype=jnp.float32)
        bias_table = jax.random.truncated_normal(ks[3], -2.0, 2.0, (2 * SEQ_LEN - 1,), dtype=jnp.float32) * 0.02
        scale = jnp.asarray(1.0 / np.sqrt(C), dtype=jnp.float32)
        return {'x': x, 'ln1_g': ln1_g, 'ln1_b': ln1_b, 'qkv_w': qkv_w, 'qkv_b': qkv_b, 'bias_table': bias_table, 'scale': scale, 'proj_w': proj_w, 'proj_b': proj_b, 'ln2_g': ln2_g, 'ln2_b': ln2_b}
    _L0_attn_all = _L0_attn_setup()
    _L0_attn_in = {k: v for k, v in _L0_attn_all.items() if k in ('ln1_g', 'ln1_b', 'qkv_w', 'qkv_b', 'bias_table', 'scale', 'proj_w', 'proj_b', 'ln2_g', 'ln2_b')}
    del _L0_attn_all

    def _L0_ffn_setup():
        import jax, jax.numpy as jnp
        import numpy as np
        B, S, H, NH, NE = (4, 256, 64, 4, 4)
        D = H // NH
        EPS = 1e-08

        def layernorm(x, g, b):
            m = jnp.mean(x, axis=-1, keepdims=True)
            v = jnp.mean((x - m) ** 2, axis=-1, keepdims=True)
            return (x - m) / jnp.sqrt(v + EPS) * g + b
        key = jax.random.key(seed)
        ks = jax.random.split(key, 18)
        sc = 0.05
        return {'x': jax.random.normal(ks[0], (B, S, H), jnp.float32), 'hl_w': jax.random.normal(ks[1], (NH, D, H), jnp.float32) * sc, 'hl_b': jax.random.normal(ks[2], (NH, D), jnp.float32) * sc, 'wq': jax.random.normal(ks[3], (NH, NE, D, D), jnp.float32) * sc, 'wk': jax.random.normal(ks[4], (NH, D, D), jnp.float32) * sc, 'wv': jax.random.normal(ks[5], (NH, D, D), jnp.float32) * sc, 'gate_w': jax.random.normal(ks[6], (NH, NE, NE * D), jnp.float32) * sc, 'gate_b': jax.random.normal(ks[7], (NH, NE), jnp.float32) * sc, 'ln_g': jnp.ones((D,), jnp.float32), 'ln_b': jnp.zeros((D,), jnp.float32), 'fc1_w': jax.random.normal(ks[8], (D, D), jnp.float32) * sc, 'fc1_b': jax.random.normal(ks[9], (D,), jnp.float32) * sc, 'fc2_w': jax.random.normal(ks[10], (D, D), jnp.float32) * sc, 'fc2_b': jax.random.normal(ks[11], (D,), jnp.float32) * sc, 'fnorm_g': jnp.ones((D,), jnp.float32), 'fnorm_b': jnp.zeros((D,), jnp.float32), 'fgate_w': jax.random.normal(ks[12], (NH, H), jnp.float32) * sc}
    _L0_ffn_all = _L0_ffn_setup()
    _L0_ffn_in = {k: v for k, v in _L0_ffn_all.items() if k in ('hl_w', 'hl_b', 'wq', 'wk', 'wv', 'gate_w', 'gate_b', 'ln_g', 'ln_b', 'fc1_w', 'fc1_b', 'fc2_w', 'fc2_b', 'fnorm_g', 'fnorm_b', 'fgate_w')}
    del _L0_ffn_all

    def _L1_attn_setup():
        import jax, jax.numpy as jnp
        import numpy as np
        B, T, D = (2, 512, 64)

        def _layernorm(x, g, b, eps=1e-05):
            mu = jnp.mean(x, axis=-1, keepdims=True)
            var = jnp.var(x, axis=-1, keepdims=True)
            return (x - mu) * jax.lax.rsqrt(var + eps) * g + b
        key = jax.random.key(seed)
        ks = jax.random.split(key, 8)
        s = 0.02
        return {'x': jax.random.normal(ks[0], (B, T, D), jnp.float32), 'qkv_w': jax.random.normal(ks[1], (D, 3 * D), jnp.float32) * s, 'qkv_b': jnp.zeros((3 * D,), jnp.float32), 'proj_w': jax.random.normal(ks[2], (D, D), jnp.float32) * s, 'proj_b': jnp.zeros((D,), jnp.float32), 'ln1_g': jnp.ones((D,), jnp.float32), 'ln1_b': jnp.zeros((D,), jnp.float32), 'w1': jax.random.normal(ks[3], (D, 4 * D), jnp.float32) * s, 'b1': jnp.zeros((4 * D,), jnp.float32), 'w2': jax.random.normal(ks[4], (4 * D, D), jnp.float32) * s, 'b2': jnp.zeros((D,), jnp.float32), 'ln2_g': jnp.ones((D,), jnp.float32), 'ln2_b': jnp.zeros((D,), jnp.float32)}
    _L1_attn_all = _L1_attn_setup()
    _L1_attn_in = {k: v for k, v in _L1_attn_all.items() if k in ('qkv_w', 'qkv_b', 'proj_w', 'proj_b', 'ln1_g', 'ln1_b', 'w1', 'b1', 'w2', 'b2', 'ln2_g', 'ln2_b')}
    del _L1_attn_all

    def _L1_ffn_setup():
        import jax, jax.numpy as jnp
        import numpy as np
        B, T, C = (64, 96, 64)
        NH, NKV = (4, 2)
        HD = C // NH
        NREP = NH // NKV
        NE, TOPK = (8, 2)
        HID = int(8 / 3 * C)
        EPS_RMS = 1e-06

        def _rope_tables(t_len):
            inv_freq = 1.0 / 10000.0 ** (np.arange(0, HD, 2, dtype=np.float32) / HD)
            t = np.arange(t_len, dtype=np.float32)
            freqs = np.outer(t, inv_freq)
            emb = np.concatenate([freqs, freqs], axis=-1)
            return (jnp.asarray(np.cos(emb)), jnp.asarray(np.sin(emb)))

        def _rotate_half(x):
            h = x.shape[-1] // 2
            return jnp.concatenate([-x[..., h:], x[..., :h]], axis=-1)

        def _rmsnorm(v, w):
            return v * jax.lax.rsqrt(jnp.mean(v * v, axis=-1, keepdims=True) + EPS_RMS) * w
        key = jax.random.key(seed)
        ks = jax.random.split(key, 10)
        s = lambda k, shape: jax.random.normal(k, shape, jnp.float32) * 0.02
        return {'x': jax.random.normal(ks[0], (B, T, C), jnp.float32), 'ln1_w': jnp.ones((C,), jnp.float32), 'ln2_w': jnp.ones((C,), jnp.float32), 'wq': s(ks[1], (NH * HD, C)), 'wk': s(ks[2], (NKV * HD, C)), 'wv': s(ks[3], (NKV * HD, C)), 'wo': s(ks[4], (C, C)), 'router_w': s(ks[5], (NE, C)), 'w1': s(ks[6], (NE, HID, C)), 'w2': s(ks[7], (NE, C, HID)), 'w3': s(ks[8], (NE, HID, C))}
    _L1_ffn_all = _L1_ffn_setup()
    _L1_ffn_in = {k: v for k, v in _L1_ffn_all.items() if k in ('ln1_w', 'ln2_w', 'wq', 'wk', 'wv', 'wo', 'router_w', 'w1', 'w2', 'w3')}
    del _L1_ffn_all

    def _L2_attn_setup():
        import jax, jax.numpy as jnp
        import numpy as np
        H = 4
        TOP_K = 8
        CAUSAL = True
        W_STD = 0.04
        key = jax.random.key(seed)
        kx, kq, kk, kv, ko = jax.random.split(key, 5)
        B, T, d = (2, 128, 64)
        x = jax.random.normal(kx, (B, T, d), dtype=jnp.float32)
        Wq = jax.random.normal(kq, (d, d), dtype=jnp.float32) * W_STD
        Wk = jax.random.normal(kk, (d, d), dtype=jnp.float32) * W_STD
        Wv = jax.random.normal(kv, (d, d), dtype=jnp.float32) * W_STD
        Wo = jax.random.normal(ko, (d, d), dtype=jnp.float32) * W_STD
        return {'x': x, 'Wq': Wq, 'Wk': Wk, 'Wv': Wv, 'Wo': Wo}
    _L2_attn_all = _L2_attn_setup()
    _L2_attn_in = {k: v for k, v in _L2_attn_all.items() if k in ('Wq', 'Wk', 'Wv', 'Wo')}
    del _L2_attn_all

    def _L2_ffn_setup():
        import jax, jax.numpy as jnp
        import numpy as np
        B, S, D, E, H, K = (4, 1024, 64, 8, 128, 2)
        key = jax.random.key(seed)
        ks = jax.random.split(key, 6)
        x = jax.random.normal(ks[0], (B, S, D), jnp.float32)
        Wg = jax.random.normal(ks[1], (D, E), jnp.float32) * 0.02
        bg = jnp.zeros((E,), jnp.float32)
        W1 = jax.random.normal(ks[2], (E, D, H), jnp.float32) * 0.02
        b1 = jnp.zeros((E, H), jnp.float32)
        W2 = jax.random.normal(ks[3], (E, H, D), jnp.float32) * 0.02
        b2 = jnp.zeros((E, D), jnp.float32)
        return {'x': x, 'Wg': Wg, 'bg': bg, 'W1': W1, 'b1': b1, 'W2': W2, 'b2': b2}
    _L2_ffn_all = _L2_ffn_setup()
    _L2_ffn_in = {k: v for k, v in _L2_ffn_all.items() if k in ('Wg', 'bg', 'W1', 'b1', 'W2', 'b2')}
    del _L2_ffn_all

    def _L3_attn_setup():
        import jax, jax.numpy as jnp
        import numpy as np
        key = jax.random.key(seed)
        ks = jax.random.split(key, 4)
        B, S, D = (4, 1024, 64)
        x = jax.random.normal(ks[0], (B, S, D), dtype=jnp.float32)
        Wq = jax.random.normal(ks[1], (D, D), dtype=jnp.float32) * 0.02
        Wk = jax.random.normal(ks[2], (D, D), dtype=jnp.float32) * 0.02
        Wv = jax.random.normal(ks[3], (D, D), dtype=jnp.float32) * 0.02
        bq = jnp.zeros((D,), dtype=jnp.float32)
        bk = jnp.zeros((D,), dtype=jnp.float32)
        bv = jnp.zeros((D,), dtype=jnp.float32)
        return {'x': x, 'Wq': Wq, 'bq': bq, 'Wk': Wk, 'bk': bk, 'Wv': Wv, 'bv': bv}
    _L3_attn_all = _L3_attn_setup()
    _L3_attn_in = {k: v for k, v in _L3_attn_all.items() if k in ('Wq', 'bq', 'Wk', 'bk', 'Wv', 'bv')}
    del _L3_attn_all

    def _L3_ffn_setup():
        import jax, jax.numpy as jnp
        import numpy as np
        E = 8
        K = 2
        D = 64
        H = 128
        DOUT = 64
        EPS = 1e-05
        key = jax.random.key(seed)
        ks = jax.random.split(key, 9)
        s = 0.02
        return {'x': jax.random.normal(ks[0], (4, 2048, D), jnp.float32), 'gamma': 1.0 + 0.05 * jax.random.normal(ks[1], (D,), jnp.float32), 'beta': 0.05 * jax.random.normal(ks[2], (D,), jnp.float32), 'Wr': 0.01 * jax.random.normal(ks[3], (D, E), jnp.float32), 'br': jnp.zeros((E,), jnp.float32), 'W1': s * jax.random.normal(ks[4], (E, D, H), jnp.float32), 'b1': s * jax.random.normal(ks[5], (E, H), jnp.float32), 'W2': s * jax.random.normal(ks[6], (E, H, DOUT), jnp.float32), 'b2': s * jax.random.normal(ks[7], (E, DOUT), jnp.float32)}
    _L3_ffn_all = _L3_ffn_setup()
    _L3_ffn_in = {k: v for k, v in _L3_ffn_all.items() if k in ('gamma', 'beta', 'Wr', 'br', 'W1', 'b1', 'W2', 'b2')}
    del _L3_ffn_all
    return {'x': x, 'x_txt': x_txt, 'L0_tok_p_w': _L0_tok_in['p_w'], 'L0_tok_p_b': _L0_tok_in['p_b'], 'L0_tok_fw': _L0_tok_in['fw'], 'L0_tok_w1_w': _L0_tok_in['w1_w'], 'L0_tok_w1_b': _L0_tok_in['w1_b'], 'L0_tok_w2_w': _L0_tok_in['w2_w'], 'L0_tok_w2_b': _L0_tok_in['w2_b'], 'L0_tok_q1_w': _L0_tok_in['q1_w'], 'L0_tok_q1_b': _L0_tok_in['q1_b'], 'L0_tok_q2_w': _L0_tok_in['q2_w'], 'L0_tok_q2_b': _L0_tok_in['q2_b'], 'L0_txt_turns': _L0_txt_in['turns'], 'L0_txt_poly_coeffs': _L0_txt_in['poly_coeffs'], 'L0_attn_ln1_g': _L0_attn_in['ln1_g'], 'L0_attn_ln1_b': _L0_attn_in['ln1_b'], 'L0_attn_qkv_w': _L0_attn_in['qkv_w'], 'L0_attn_qkv_b': _L0_attn_in['qkv_b'], 'L0_attn_bias_table': _L0_attn_in['bias_table'], 'L0_attn_scale': _L0_attn_in['scale'], 'L0_attn_proj_w': _L0_attn_in['proj_w'], 'L0_attn_proj_b': _L0_attn_in['proj_b'], 'L0_attn_ln2_g': _L0_attn_in['ln2_g'], 'L0_attn_ln2_b': _L0_attn_in['ln2_b'], 'L0_ffn_hl_w': _L0_ffn_in['hl_w'], 'L0_ffn_hl_b': _L0_ffn_in['hl_b'], 'L0_ffn_wq': _L0_ffn_in['wq'], 'L0_ffn_wk': _L0_ffn_in['wk'], 'L0_ffn_wv': _L0_ffn_in['wv'], 'L0_ffn_gate_w': _L0_ffn_in['gate_w'], 'L0_ffn_gate_b': _L0_ffn_in['gate_b'], 'L0_ffn_ln_g': _L0_ffn_in['ln_g'], 'L0_ffn_ln_b': _L0_ffn_in['ln_b'], 'L0_ffn_fc1_w': _L0_ffn_in['fc1_w'], 'L0_ffn_fc1_b': _L0_ffn_in['fc1_b'], 'L0_ffn_fc2_w': _L0_ffn_in['fc2_w'], 'L0_ffn_fc2_b': _L0_ffn_in['fc2_b'], 'L0_ffn_fnorm_g': _L0_ffn_in['fnorm_g'], 'L0_ffn_fnorm_b': _L0_ffn_in['fnorm_b'], 'L0_ffn_fgate_w': _L0_ffn_in['fgate_w'], 'L1_attn_qkv_w': _L1_attn_in['qkv_w'], 'L1_attn_qkv_b': _L1_attn_in['qkv_b'], 'L1_attn_proj_w': _L1_attn_in['proj_w'], 'L1_attn_proj_b': _L1_attn_in['proj_b'], 'L1_attn_ln1_g': _L1_attn_in['ln1_g'], 'L1_attn_ln1_b': _L1_attn_in['ln1_b'], 'L1_attn_w1': _L1_attn_in['w1'], 'L1_attn_b1': _L1_attn_in['b1'], 'L1_attn_w2': _L1_attn_in['w2'], 'L1_attn_b2': _L1_attn_in['b2'], 'L1_attn_ln2_g': _L1_attn_in['ln2_g'], 'L1_attn_ln2_b': _L1_attn_in['ln2_b'], 'L1_ffn_ln1_w': _L1_ffn_in['ln1_w'], 'L1_ffn_ln2_w': _L1_ffn_in['ln2_w'], 'L1_ffn_wq': _L1_ffn_in['wq'], 'L1_ffn_wk': _L1_ffn_in['wk'], 'L1_ffn_wv': _L1_ffn_in['wv'], 'L1_ffn_wo': _L1_ffn_in['wo'], 'L1_ffn_router_w': _L1_ffn_in['router_w'], 'L1_ffn_w1': _L1_ffn_in['w1'], 'L1_ffn_w2': _L1_ffn_in['w2'], 'L1_ffn_w3': _L1_ffn_in['w3'], 'L2_attn_Wq': _L2_attn_in['Wq'], 'L2_attn_Wk': _L2_attn_in['Wk'], 'L2_attn_Wv': _L2_attn_in['Wv'], 'L2_attn_Wo': _L2_attn_in['Wo'], 'L2_ffn_Wg': _L2_ffn_in['Wg'], 'L2_ffn_bg': _L2_ffn_in['bg'], 'L2_ffn_W1': _L2_ffn_in['W1'], 'L2_ffn_b1': _L2_ffn_in['b1'], 'L2_ffn_W2': _L2_ffn_in['W2'], 'L2_ffn_b2': _L2_ffn_in['b2'], 'L3_attn_Wq': _L3_attn_in['Wq'], 'L3_attn_bq': _L3_attn_in['bq'], 'L3_attn_Wk': _L3_attn_in['Wk'], 'L3_attn_bk': _L3_attn_in['bk'], 'L3_attn_Wv': _L3_attn_in['Wv'], 'L3_attn_bv': _L3_attn_in['bv'], 'L3_ffn_gamma': _L3_ffn_in['gamma'], 'L3_ffn_beta': _L3_ffn_in['beta'], 'L3_ffn_Wr': _L3_ffn_in['Wr'], 'L3_ffn_br': _L3_ffn_in['br'], 'L3_ffn_W1': _L3_ffn_in['W1'], 'L3_ffn_b1': _L3_ffn_in['b1'], 'L3_ffn_W2': _L3_ffn_in['W2'], 'L3_ffn_b2': _L3_ffn_in['b2']}

def reference(x, x_txt, L0_tok_p_w, L0_tok_p_b, L0_tok_fw, L0_tok_w1_w, L0_tok_w1_b, L0_tok_w2_w, L0_tok_w2_b, L0_tok_q1_w, L0_tok_q1_b, L0_tok_q2_w, L0_tok_q2_b, L0_txt_turns, L0_txt_poly_coeffs, L0_attn_ln1_g, L0_attn_ln1_b, L0_attn_qkv_w, L0_attn_qkv_b, L0_attn_bias_table, L0_attn_scale, L0_attn_proj_w, L0_attn_proj_b, L0_attn_ln2_g, L0_attn_ln2_b, L0_ffn_hl_w, L0_ffn_hl_b, L0_ffn_wq, L0_ffn_wk, L0_ffn_wv, L0_ffn_gate_w, L0_ffn_gate_b, L0_ffn_ln_g, L0_ffn_ln_b, L0_ffn_fc1_w, L0_ffn_fc1_b, L0_ffn_fc2_w, L0_ffn_fc2_b, L0_ffn_fnorm_g, L0_ffn_fnorm_b, L0_ffn_fgate_w, L1_attn_qkv_w, L1_attn_qkv_b, L1_attn_proj_w, L1_attn_proj_b, L1_attn_ln1_g, L1_attn_ln1_b, L1_attn_w1, L1_attn_b1, L1_attn_w2, L1_attn_b2, L1_attn_ln2_g, L1_attn_ln2_b, L1_ffn_ln1_w, L1_ffn_ln2_w, L1_ffn_wq, L1_ffn_wk, L1_ffn_wv, L1_ffn_wo, L1_ffn_router_w, L1_ffn_w1, L1_ffn_w2, L1_ffn_w3, L2_attn_Wq, L2_attn_Wk, L2_attn_Wv, L2_attn_Wo, L2_ffn_Wg, L2_ffn_bg, L2_ffn_W1, L2_ffn_b1, L2_ffn_W2, L2_ffn_b2, L3_attn_Wq, L3_attn_bq, L3_attn_Wk, L3_attn_bk, L3_attn_Wv, L3_attn_bv, L3_ffn_gamma, L3_ffn_beta, L3_ffn_Wr, L3_ffn_br, L3_ffn_W1, L3_ffn_b1, L3_ffn_W2, L3_ffn_b2):
    import jax
    import jax.numpy as jnp

    def _L0_tok_ref(x, p_w, p_b, fw, w1_w, w1_b, w2_w, w2_b, q1_w, q1_b, q2_w, q2_b):
        import jax, jax.numpy as jnp
        import numpy as np
        B, S, D_A, D_V, D_U, L, M1, M2 = (16, 64, 3, 32, 1, 4, 12, 12)
        MID = 4 * D_U

        def conv1x1(x, w, b):
            return jnp.einsum('bixy,oi->boxy', x, w) + b[None, :, None, None]

        def fourier_layer(x, fw_i):
            Bm, C, M, N = x.shape
            x_ft = jnp.fft.rfft2(x, s=(M, N), norm='ortho')
            w_lo = fw_i[0, ..., 0] + 1j * fw_i[0, ..., 1]
            w_hi = fw_i[1, ..., 0] + 1j * fw_i[1, ..., 1]
            lo = jnp.einsum('bixy,ioxy->boxy', x_ft[:, :, :M1, :M2], w_lo)
            hi = jnp.einsum('bixy,ioxy->boxy', x_ft[:, :, -M1:, :M2], w_hi)
            out_ft = jnp.zeros(x_ft.shape, dtype=x_ft.dtype)
            out_ft = out_ft.at[:, :, :M1, :M2].set(lo)
            out_ft = out_ft.at[:, :, -M1:, :M2].set(hi)
            return jnp.fft.irfft2(out_ft, s=(M, N), norm='ortho')

        def make_grid(b, sx, sy):
            gx = jnp.broadcast_to(jnp.linspace(0.0, 1.0, sx)[None, :, None], (b, sx, sy))
            gy = jnp.broadcast_to(jnp.linspace(0.0, 1.0, sy)[None, None, :], (b, sx, sy))
            return jnp.stack([gx, gy], axis=-1)
        b, sx, sy = (x.shape[0], x.shape[1], x.shape[2])
        grid = make_grid(b, sx, sy)
        h = jnp.concatenate([x, grid], axis=-1)
        h = jnp.transpose(h, (0, 3, 1, 2))
        h = conv1x1(h, p_w, p_b)
        for i in range(L):
            x1 = fourier_layer(h, fw[i])
            x1 = jax.nn.relu(conv1x1(x1, w1_w[i], w1_b[i]))
            x1 = conv1x1(x1, w2_w[i], w2_b[i])
            h = h + x1
        h = conv1x1(h, q1_w, q1_b)
        h = jax.nn.relu(h)
        h = conv1x1(h, q2_w, q2_b)
        return jnp.squeeze(h)

    def _L0_txt_ref(token_ids, turns, poly_coeffs):
        import jax, jax.numpy as jnp
        import numpy as np
        VOCAB, N_TURNS, OUT_DIM, POLY_DEG = (50257, 4, 64, 4)
        base_turns = turns[token_ids]
        x = jax.lax.stop_gradient(jnp.trunc(base_turns)).astype(jnp.float32)
        degs = jnp.arange(POLY_DEG + 1, dtype=jnp.float32)
        xp = x[..., None] ** degs
        emb = jnp.einsum('bstd,tdo->bso', xp, poly_coeffs)
        return emb

    def _L0_attn_ref(x, ln1_g, ln1_b, qkv_w, qkv_b, bias_table, scale, proj_w, proj_b, ln2_g, ln2_b):
        import jax, jax.numpy as jnp
        import numpy as np
        SEQ_LEN = 512
        EMBED_DIM = 64
        BATCH = 8
        LN_EPS = 1e-05

        def _layernorm(x, g, b):
            mu = jnp.mean(x, axis=-1, keepdims=True)
            var = jnp.mean(jnp.square(x - mu), axis=-1, keepdims=True)
            return (x - mu) * jax.lax.rsqrt(var + LN_EPS) * g + b
        B, N, C = x.shape
        h = _layernorm(x, ln1_g, ln1_b)
        qkv = h @ qkv_w + qkv_b
        q, k, v = jnp.split(qkv, 3, axis=-1)
        coords = jnp.arange(N)
        rel_idx = coords[None, :] - coords[:, None] + (N - 1)
        rel_bias = bias_table[rel_idx]
        attn = jnp.einsum('bnc,bmc->bnm', q, k) + rel_bias
        attn = jax.nn.softmax(attn, axis=-1) * scale
        out = jnp.einsum('bnm,bmc->bnc', attn, v)
        out = out @ proj_w + proj_b
        out = _layernorm(out, ln2_g, ln2_b)
        return out

    def _L0_ffn_ref(x, hl_w, hl_b, wq, wk, wv, gate_w, gate_b, ln_g, ln_b, fc1_w, fc1_b, fc2_w, fc2_b, fnorm_g, fnorm_b, fgate_w):
        import jax, jax.numpy as jnp
        import numpy as np
        B, S, H, NH, NE = (4, 256, 64, 4, 4)
        D = H // NH
        EPS = 1e-08

        def layernorm(x, g, b):
            m = jnp.mean(x, axis=-1, keepdims=True)
            v = jnp.mean((x - m) ** 2, axis=-1, keepdims=True)
            return (x - m) / jnp.sqrt(v + EPS) * g + b
        b, s, h = x.shape
        nh, d, _ = wk.shape
        ne = wq.shape[1]
        sx = jnp.einsum('bsh,ndh->bnsd', x, hl_w) + hl_b[None, :, None, :]
        pad = sx == 0
        q = jnp.einsum('bnsd,neod->bneso', sx, wq)
        k = jnp.einsum('bnsd,nod->bnso', sx, wk)
        v = jnp.einsum('bnsd,nod->bnso', sx, wv)
        causal = jnp.where(jnp.tril(jnp.ones((s, s), bool)), 0.0, -jnp.inf).astype(x.dtype)
        scores = jnp.einsum('bnesd,bntd->bnest', q, k) * d ** 0.5 + causal
        att = jax.nn.softmax(scores, axis=-1)
        qkv = jnp.einsum('bnest,bntd->bnesd', att, v)
        qkv = jnp.where(pad[:, :, None], 0.0, qkv)
        out = jnp.transpose(qkv, (0, 1, 3, 2, 4)).reshape(b, nh, s, ne * d)
        gs = jax.nn.softmax(jnp.einsum('bnsf,nef->bnse', out, gate_w) + gate_b[None, :, None, :], axis=-1)
        mixed = jnp.einsum('bnsed,bnse->bnsd', out.reshape(b, nh, s, ne, d), gs)
        resid = sx[jnp.arange(nh), jnp.arange(nh)]
        hn = layernorm(mixed + resid, ln_g, ln_b)
        f_n = jnp.transpose(hn, (0, 2, 1, 3)).reshape(b, s, h)
        fx = f_n.reshape(b, s, nh, d)
        pm = fx == 0
        hx = jnp.where(pm, 0.0, fx @ fc1_w.T + fc1_b)
        hx = jax.nn.relu(hx)
        hx = jnp.where(pm, 0.0, hx @ fc2_w.T + fc2_b)
        hx = layernorm(hx + fx, fnorm_g, fnorm_b)
        fout = hx.reshape(b, s, h)
        fg = jax.nn.softmax(fout @ fgate_w.T, axis=-1)
        return (fout.reshape(b, s, nh, d) * fg[..., None]).reshape(b, s, h)

    def _L1_attn_ref(x, qkv_w, qkv_b, proj_w, proj_b, ln1_g, ln1_b, w1, b1, w2, b2, ln2_g, ln2_b):
        import jax, jax.numpy as jnp
        import numpy as np
        B, T, D = (2, 512, 64)

        def _layernorm(x, g, b, eps=1e-05):
            mu = jnp.mean(x, axis=-1, keepdims=True)
            var = jnp.var(x, axis=-1, keepdims=True)
            return (x - mu) * jax.lax.rsqrt(var + eps) * g + b
        scale = float(D) ** 0.5
        x_f32 = x.astype(jnp.float32)
        qkv = x_f32 @ qkv_w + qkv_b
        q, k, v = jnp.split(qkv, 3, axis=-1)
        q = q / scale
        k = k / scale
        q = q / jnp.maximum(jnp.linalg.norm(q, axis=-1, keepdims=True), 1e-12)
        k = k / jnp.maximum(jnp.linalg.norm(k, axis=-1, keepdims=True), 1e-12)
        q = jax.nn.softplus(q) + 1e-06
        k = jax.nn.softplus(k) + 1e-06
        kv = jnp.einsum('btd,bte->btde', k, v)
        kv_sum = jnp.cumsum(kv, axis=1)
        k_sum = jnp.cumsum(k, axis=1)
        num = jnp.einsum('btd,btde->bte', q, kv_sum)
        den = jnp.maximum(jnp.einsum('btd,btd->bt', q, k_sum)[..., None], 1e-06)
        num = jnp.clip(num, -10000.0, 10000.0)
        attn_out = num / den
        x_attn = _layernorm(x_f32 + attn_out @ proj_w + proj_b, ln1_g, ln1_b)
        h = jax.nn.gelu(x_attn @ w1 + b1, approximate=False)
        out = _layernorm(x_attn + h @ w2 + b2, ln2_g, ln2_b)
        return out.astype(x.dtype)

    def _L1_ffn_ref(x, ln1_w, ln2_w, wq, wk, wv, wo, router_w, w1, w2, w3):
        import jax, jax.numpy as jnp
        import numpy as np
        B, T, C = (64, 96, 64)
        NH, NKV = (4, 2)
        HD = C // NH
        NREP = NH // NKV
        NE, TOPK = (8, 2)
        HID = int(8 / 3 * C)
        EPS_RMS = 1e-06

        def _rope_tables(t_len):
            inv_freq = 1.0 / 10000.0 ** (np.arange(0, HD, 2, dtype=np.float32) / HD)
            t = np.arange(t_len, dtype=np.float32)
            freqs = np.outer(t, inv_freq)
            emb = np.concatenate([freqs, freqs], axis=-1)
            return (jnp.asarray(np.cos(emb)), jnp.asarray(np.sin(emb)))

        def _rotate_half(x):
            h = x.shape[-1] // 2
            return jnp.concatenate([-x[..., h:], x[..., :h]], axis=-1)

        def _rmsnorm(v, w):
            return v * jax.lax.rsqrt(jnp.mean(v * v, axis=-1, keepdims=True) + EPS_RMS) * w
        Bx, Tx, Cx = x.shape
        h = _rmsnorm(x, ln1_w)
        q = (h @ wq.T).reshape(Bx, Tx, NH, HD).transpose(0, 2, 1, 3)
        k = (h @ wk.T).reshape(Bx, Tx, NKV, HD).transpose(0, 2, 1, 3)
        v = (h @ wv.T).reshape(Bx, Tx, NKV, HD).transpose(0, 2, 1, 3)
        cos, sin = _rope_tables(Tx)
        cos, sin = (cos[None, None], sin[None, None])
        q = q * cos + _rotate_half(q) * sin
        k = k * cos + _rotate_half(k) * sin
        k = jnp.repeat(k, NREP, axis=1)
        v = jnp.repeat(v, NREP, axis=1)
        scores = jnp.einsum('bhtd,bhsd->bhts', q, k) / jnp.sqrt(jnp.float32(HD))
        causal = jnp.tril(jnp.ones((Tx, Tx), dtype=bool))
        scores = jnp.where(causal[None, None], scores, jnp.float32(-1e+30))
        att = jax.nn.softmax(scores, axis=-1)
        y = jnp.einsum('bhts,bhsd->bhtd', att, v).transpose(0, 2, 1, 3).reshape(Bx, Tx, Cx)
        x = x + y @ wo.T
        flat = _rmsnorm(x, ln2_w).reshape(-1, Cx)
        probs = jax.nn.softmax(flat @ router_w.T, axis=-1)
        tp, ti = jax.lax.top_k(probs, TOPK)
        tp = tp / (jnp.sum(tp, axis=-1, keepdims=True) + 1e-09)
        weights = jnp.sum(tp[..., None] * jax.nn.one_hot(ti, NE, dtype=flat.dtype), axis=1)
        out = jnp.zeros_like(flat)
        for e in range(NE):
            hh = jax.nn.silu(flat @ w1[e].T) * (flat @ w3[e].T)
            out = out + weights[:, e:e + 1] * (hh @ w2[e].T)
        return x + out.reshape(Bx, Tx, Cx)

    def _L2_attn_ref(x, Wq, Wk, Wv, Wo):
        import jax, jax.numpy as jnp
        import numpy as np
        H = 4
        TOP_K = 8
        CAUSAL = True
        W_STD = 0.04
        B, T, d = x.shape
        dh = d // H
        k = min(TOP_K, T)
        Q = (x @ Wq.T).reshape(B, T, H, dh).transpose(0, 2, 1, 3)
        K = (x @ Wk.T).reshape(B, T, H, dh).transpose(0, 2, 1, 3)
        V = (x @ Wv.T).reshape(B, T, H, dh).transpose(0, 2, 1, 3)
        scores = jnp.max(Q[:, :, :, None, :] + K[:, :, None, :, :], axis=-1)
        if CAUSAL:
            causal_mask = jnp.triu(jnp.ones((T, T), dtype=bool), 1)
            scores = jnp.where(causal_mask[None, None], -jnp.inf, scores)
        topk_vals, topk_idx = jax.lax.top_k(scores, k)
        attn = jax.nn.softmax(topk_vals, axis=-1)
        Vg = jnp.take_along_axis(V[:, :, None, :, :], topk_idx[..., None], axis=3)
        ctx = jnp.einsum('bhtk,bhtkd->bhtd', attn, Vg)
        ctx = ctx.transpose(0, 2, 1, 3).reshape(B, T, d)
        return ctx @ Wo.T

    def _L2_ffn_ref(x, Wg, bg, W1, b1, W2, b2):
        import jax, jax.numpy as jnp
        import numpy as np
        B, S, D, E, H, K = (4, 1024, 64, 8, 128, 2)
        Bv, Sv, Dv = x.shape
        gate_scores = x @ Wg + bg
        _, idx = jax.lax.top_k(gate_scores, K)
        mask = jax.nn.one_hot(idx, E, dtype=x.dtype).sum(axis=-2)
        xf = x.reshape(-1, Dv)
        mf = mask.reshape(-1, E)
        h = jax.nn.gelu(jnp.einsum('td,edh->teh', xf, W1) + b1[None], approximate=False)
        y = jnp.einsum('teh,ehd->ted', h, W2) + b2[None]
        out = jnp.einsum('ted,te->td', y, mf)
        return out.reshape(Bv, Sv, Dv)

    def _L3_attn_ref(x, Wq, bq, Wk, bk, Wv, bv):
        import jax, jax.numpy as jnp
        import numpy as np
        Q = jnp.einsum('bsd,de->bse', x, Wq) + bq
        K = jnp.einsum('bsd,de,->bse'.replace(',->', '->'), x, Wk) + bk
        V = jnp.einsum('bsd,de->bse', x, Wv) + bv
        scale = 1.0 / jnp.sqrt(jnp.asarray(Q.shape[-1], dtype=jnp.float32))
        scores = jnp.einsum('bqd,bkd->bqk', Q, K) * scale
        weights = jax.nn.softmax(scores, axis=-1)
        return jnp.einsum('bqk,bkd->bqd', weights, V)

    def _L3_ffn_ref(x, gamma, beta, Wr, br, W1, b1, W2, b2):
        import jax, jax.numpy as jnp
        import numpy as np
        E = 8
        K = 2
        D = 64
        H = 128
        DOUT = 64
        EPS = 1e-05
        mu = jnp.mean(x, axis=-1, keepdims=True)
        var = jnp.mean(jnp.square(x - mu), axis=-1, keepdims=True)
        xn = (x - mu) * jax.lax.rsqrt(var + EPS) * gamma + beta
        logits = jnp.einsum('bsd,de->bse', xn, Wr) + br
        top_vals, top_idx = jax.lax.top_k(logits, K)
        w = jax.nn.softmax(top_vals, axis=-1)
        w_full = jnp.einsum('bsk,bske->bse', w, jax.nn.one_hot(top_idx, E, dtype=w.dtype))
        y = jnp.zeros(x.shape[:-1] + (DOUT,), x.dtype)
        for e in range(E):
            h = jax.nn.gelu(jnp.einsum('bsd,dh->bsh', xn, W1[e]) + b1[e], approximate=False)
            y_e = jnp.einsum('bsh,hd->bsd', h, W2[e]) + b2[e]
            y = y + y_e * w_full[..., e, None]
        return y
    h = _L0_tok_ref(x, L0_tok_p_w, L0_tok_p_b, L0_tok_fw, L0_tok_w1_w, L0_tok_w1_b, L0_tok_w2_w, L0_tok_w2_b, L0_tok_q1_w, L0_tok_q1_b, L0_tok_q2_w, L0_tok_q2_b)
    h = jnp.concatenate([h, _L0_txt_ref(x_txt, L0_txt_turns, L0_txt_poly_coeffs)], axis=1)
    h = h + _L0_attn_ref(_layernorm(h, axis=-1), L0_attn_ln1_g, L0_attn_ln1_b, L0_attn_qkv_w, L0_attn_qkv_b, L0_attn_bias_table, L0_attn_scale, L0_attn_proj_w, L0_attn_proj_b, L0_attn_ln2_g, L0_attn_ln2_b)
    h = h + _L0_ffn_ref(_layernorm(h, axis=-1), L0_ffn_hl_w, L0_ffn_hl_b, L0_ffn_wq, L0_ffn_wk, L0_ffn_wv, L0_ffn_gate_w, L0_ffn_gate_b, L0_ffn_ln_g, L0_ffn_ln_b, L0_ffn_fc1_w, L0_ffn_fc1_b, L0_ffn_fc2_w, L0_ffn_fc2_b, L0_ffn_fnorm_g, L0_ffn_fnorm_b, L0_ffn_fgate_w)
    h = h + _L1_attn_ref(_layernorm(h, axis=-1), L1_attn_qkv_w, L1_attn_qkv_b, L1_attn_proj_w, L1_attn_proj_b, L1_attn_ln1_g, L1_attn_ln1_b, L1_attn_w1, L1_attn_b1, L1_attn_w2, L1_attn_b2, L1_attn_ln2_g, L1_attn_ln2_b)
    h = h + _L1_ffn_ref(_layernorm(h, axis=-1), L1_ffn_ln1_w, L1_ffn_ln2_w, L1_ffn_wq, L1_ffn_wk, L1_ffn_wv, L1_ffn_wo, L1_ffn_router_w, L1_ffn_w1, L1_ffn_w2, L1_ffn_w3)
    h = h + _L2_attn_ref(_layernorm(h, axis=-1), L2_attn_Wq, L2_attn_Wk, L2_attn_Wv, L2_attn_Wo)
    h = h + _L2_ffn_ref(_layernorm(h, axis=-1), L2_ffn_Wg, L2_ffn_bg, L2_ffn_W1, L2_ffn_b1, L2_ffn_W2, L2_ffn_b2)
    h = h + _L3_attn_ref(_layernorm(h, axis=-1), L3_attn_Wq, L3_attn_bq, L3_attn_Wk, L3_attn_bk, L3_attn_Wv, L3_attn_bv)
    h = h + _L3_ffn_ref(_layernorm(h, axis=-1), L3_ffn_gamma, L3_ffn_beta, L3_ffn_Wr, L3_ffn_br, L3_ffn_W1, L3_ffn_b1, L3_ffn_W2, L3_ffn_b2)
    return h

_drawn_inputs = setup_inputs


def setup_inputs(seed=0):
    import zlib

    import numpy as np

    out = dict(_drawn_inputs(seed))
    spreads = {'L0_tok_p_b': (0.0, 0.8),
     'L0_tok_w1_b': (0.0, 0.8),
     'L0_tok_w2_b': (0.0, 0.8),
     'L0_tok_q1_b': (0.0, 0.8),
     'L0_attn_ln1_g': (1.0, 0.6),
     'L0_attn_ln1_b': (0.0, 0.8),
     'L0_attn_qkv_b': (0.0, 0.8),
     'L0_attn_proj_b': (0.0, 0.1),
     'L0_attn_ln2_g': (1.0, 0.2),
     'L0_attn_ln2_b': (0.0, 0.515),
     'L0_ffn_ln_g': (1.0, 0.6),
     'L0_ffn_ln_b': (0.0, 0.8),
     'L0_ffn_fnorm_g': (1.0, 0.6),
     'L0_ffn_fnorm_b': (0.0, 0.8),
     'L1_attn_qkv_b': (0.0, 0.8),
     'L1_attn_proj_b': (0.0, 0.657),
     'L1_attn_ln1_g': (1.0, 0.6),
     'L1_attn_ln1_b': (0.0, 0.8),
     'L1_attn_b1': (0.0, 0.8),
     'L1_attn_b2': (0.0, 0.8),
     'L1_attn_ln2_g': (1.0, 0.6),
     'L1_attn_ln2_b': (0.0, 0.748),
     'L1_ffn_ln1_w': (1.0, 0.6),
     'L1_ffn_ln2_w': (1.0, 0.6),
     'L2_ffn_bg': (0.0, 0.784),
     'L2_ffn_b1': (0.0, 0.8),
     'L2_ffn_b2': (0.0, 0.764),
     'L3_attn_bq': (0.0, 0.8),
     'L3_attn_bk': (0.0, 2.0),
     'L3_attn_bv': (0.0, 0.8),
     'L3_ffn_br': (0.0, 0.8)}
    factors = {'L0_tok_w1_w': 2.746,
     'L0_attn_qkv_w': 8.0,
     'L0_attn_bias_table': 8.0,
     'L0_attn_proj_w': 8.0,
     'L0_ffn_hl_b': 8.0,
     'L0_ffn_wq': 8.0,
     'L0_ffn_wk': 8.0,
     'L0_ffn_wv': 7.494,
     'L0_ffn_gate_w': 8.0,
     'L0_ffn_gate_b': 8.0,
     'L0_ffn_fc1_w': 8.0,
     'L0_ffn_fc1_b': 8.0,
     'L0_ffn_fc2_w': 8.0,
     'L0_ffn_fc2_b': 8.0,
     'L0_ffn_fgate_w': 5.128,
     'L1_attn_qkv_w': 8.0,
     'L1_attn_proj_w': 8.0,
     'L1_attn_w1': 8.0,
     'L1_attn_w2': 8.0,
     'L1_ffn_wq': 8.0,
     'L1_ffn_wk': 8.0,
     'L1_ffn_wv': 8.0,
     'L1_ffn_wo': 8.0,
     'L1_ffn_router_w': 8.0,
     'L1_ffn_w1': 8.0,
     'L1_ffn_w2': 8.0,
     'L1_ffn_w3': 8.0,
     'L2_attn_Wq': 8.0,
     'L2_attn_Wk': 8.0,
     'L2_attn_Wv': 8.0,
     'L2_attn_Wo': 7.597,
     'L2_ffn_Wg': 6.975,
     'L2_ffn_W1': 8.0,
     'L2_ffn_W2': 8.0,
     'L3_attn_Wq': 8.0,
     'L3_attn_Wk': 8.0,
     'L3_attn_Wv': 8.0,
     'L3_ffn_gamma': 8.0,
     'L3_ffn_beta': 8.0,
     'L3_ffn_Wr': 8.0,
     'L3_ffn_W1': 8.0,
     'L3_ffn_b1': 44.073,
     'L3_ffn_W2': 8.0,
     'L3_ffn_b2': 64.0}
    for name, (base, spread) in spreads.items():
        noise = np.random.default_rng([zlib.crc32(name.encode()), seed]).standard_normal(out[name].shape)
        drawn = base * np.exp(spread * noise) if base else spread * noise
        out[name] = jnp.asarray(drawn.astype(out[name].dtype))
    for name, factor in factors.items():
        out[name] = (out[name] * factor).astype(out[name].dtype)
    return out
```

```python
from contextlib import ExitStack

import numpy as np

import concourse.bass as bass
from concourse import mybir

ALU = mybir.AluOpType
ACT = mybir.ActivationFunctionType
AX = mybir.AxisListType
F32 = mybir.dt.float32
BF16 = mybir.dt.bfloat16
I32 = mybir.dt.int32
U32 = mybir.dt.uint32

B, S, Q, T, D = 4, 576, 96, 6, 64
IMG, TXT = 64, 512
C, G, KX, KY, HALF = 32, 64, 24, 12, 288
NEG = -1.0e30
HID = 170
HP = HID // 2


class Chain:

    def __init__(self, eng, sem):
        self.eng, self.sem, self.n = eng, sem, 0

    def __call__(self, ins):
        self.n += 1
        ins.then_inc(self.sem, 1)
        self.eng.wait_ge(self.sem, self.n)


def wide(ap, shape):
    return ap.to_broadcast(shape)


def rsqrt(dve, link, y, v, tmp):
    link(dve.tensor_scalar(y.bitcast(I32), v.bitcast(I32), 1, None, ALU.logical_shift_right))
    link(dve.tensor_scalar(y.bitcast(I32), y.bitcast(I32), -1.0, float(0x5F3759DF), ALU.mult, ALU.add))
    for _ in range(4):
        link(dve.tensor_tensor(tmp, y, y, ALU.mult))
        link(dve.scalar_tensor_tensor(tmp, tmp, -0.5, v, ALU.mult, ALU.mult))
        link(dve.scalar_tensor_tensor(y, tmp, 1.5, y, ALU.add, ALU.mult))


def layer_norm(dve, link, out, x, sq, st, eps):
    p, g, w = x.shape
    mean, var, inv, tmp = (st[0:p, j, 0:g] for j in range(4))
    link(dve.tensor_reduce(mean, x, AX.X, ALU.add))
    link(dve.tensor_scalar(mean, mean, 1.0 / w, None, ALU.mult))
    link(dve.tensor_tensor(out, x, wide(mean.unsqueeze(2), [p, g, w]), ALU.subtract))
    link(dve.tensor_tensor(sq, out, out, ALU.mult))
    link(dve.tensor_reduce(var, sq, AX.X, ALU.add))
    link(dve.tensor_scalar(var, var, 1.0 / w, eps, ALU.mult, ALU.add))
    rsqrt(dve, link, inv, var, tmp)
    link(dve.tensor_tensor(out, out, wide(inv.unsqueeze(2), [p, g, w]), ALU.mult))


def rms_norm(dve, link, out, x, sq, st, eps, weight):
    p, g, w = x.shape
    var, inv, tmp = (st[0:p, j, 0:g] for j in range(3))
    link(dve.tensor_tensor(sq, x, x, ALU.mult))
    link(dve.tensor_reduce(var, sq, AX.X, ALU.add))
    link(dve.tensor_scalar(var, var, 1.0 / w, eps, ALU.mult, ALU.add))
    rsqrt(dve, link, inv, var, tmp)
    link(dve.tensor_tensor(out, x, wide(inv.unsqueeze(2), [p, g, w]), ALU.mult))
    link(dve.tensor_tensor(out, out, weight, ALU.mult))


def affine(dve, link, x, gamma, beta):
    link(dve.tensor_tensor(x, x, gamma, ALU.mult))
    link(dve.tensor_tensor(x, x, beta, ALU.add))


def halves(ap):
    return ap.rearrange("p (c n) -> p c n", c=2)


class Attention:

    def __init__(self, nc, st, name, ps, maps, dv, causal, q_of, k_of, v_of, out_of, mask=None, strip=None):
        self.ps, self.maps, self.dv, self.causal = ps, maps, dv, causal
        self.q_of, self.k_of, self.v_of, self.out_of, self.mask, self.strip = q_of, k_of, v_of, out_of, mask, strip
        sb = lambda n, shape: st.enter_context(nc.sbuf_tensor(f"{name}_{n}", shape, F32))
        self.probs = sb("probs", [Q, 2, S])
        self.probs_t = sb("probs_t", [Q, 2, T, Q])
        self.neg_max = sb("neg_max", [Q, 4])
        self.row_sum = sb("row_sum", [Q, 2, maps])
        self.inv_sum = sb("inv_sum", [Q, maps])
        self.biased = sb("biased", [Q, 2, S]) if strip is not None else None
        names = ("scores_ready", "max_ready", "probs_ready", "turned", "turned_copied", "product_ready", "out_ready")
        self.sems = [st.enter_context(nc.semaphore(f"{name}_{n}")) for n in names]
        (self.scores_ready, self.max_ready, self.probs_ready, self.turned, self.turned_copied,
         self.product_ready, self.out_ready) = self.sems
        self.units = [(t, m) for t in range(T) for m in range(maps)]

    def keys(self, t):
        return Q * (t + 1) if self.causal else S

    def scores_at(self, i):
        b = 2 * (i % 2)
        return self.ps[0:Q, b:b + 2, :].rearrange("p b n -> p (b n)")

    def tensor(self, pe, ident):
        n = len(self.units)
        turned = self.ps[0:Q, 4:6, :].rearrange("p b (k n) -> p (b k) n", n=128)
        for step in range(n + 2):
            if step < n:
                t, m = self.units[step]
                if step >= 2:
                    pe.wait_ge(self.probs_ready, step - 1)
                for a in range(0, self.keys(t), 512):
                    z = min(self.keys(t), a + 512)
                    mm = pe.matmul(self.scores_at(step)[:, a:z], self.q_of(m, t), self.k_of(m, a, z),
                                   start=True, stop=True)
                mm.then_inc(self.scores_ready, 1)
            if 1 <= step <= n:
                i = step - 1
                t, m = self.units[i]
                pe.wait_ge(self.probs_ready, i + 1)
                if i >= 1:
                    pe.wait_ge(self.turned_copied, i)
                for k in range(self.keys(t) // Q):
                    mm = pe.transpose(turned[:, k, 0:Q], self.probs[:, i % 2, Q * k:Q * k + Q], ident[0:Q, 0:Q])
                mm.then_inc(self.turned, 1)
            if step >= 2:
                i = step - 2
                t, m = self.units[i]
                pe.wait_ge(self.turned_copied, i + 1)
                if m == 0 and t >= 2:
                    pe.wait_ge(self.out_ready, t - 1)
                last = self.keys(t) // Q - 1
                for k in range(last + 1):
                    mm = pe.matmul(self.ps[0:Q, 6 + t % 2, m * self.dv:(m + 1) * self.dv],
                                   self.probs_t[:, i % 2, k, :], self.v_of(m, k), start=(k == 0), stop=(k == last))
                mm.then_inc(self.product_ready, 1)

    def scalar(self, act):
        for i, (t, m) in enumerate(self.units):
            act.wait_ge(self.max_ready, i + 1)
            if i >= 2:
                act.wait_ge(self.turned, i - 1)
            if m == 0 and t >= 2:
                act.wait_ge(self.out_ready, t - 1)
            src = self.scores_at(i) if self.biased is None else self.biased[:, i % 2, :]
            act.activation(self.probs[:, i % 2, 0:self.keys(t)], src[:, 0:self.keys(t)], ACT.Exp,
                           bias=self.neg_max[:, i % 4:i % 4 + 1],
                           accum_out=self.row_sum[:, t % 2, m:m + 1]).then_inc(self.probs_ready, 1)

    def vector(self, dve, link):
        n = len(self.units)
        turned = self.ps[0:Q, 4:6, :].rearrange("p b (k n) -> p (b k) n", n=128)
        for step in range(n + 2):
            if step < n:
                t, m = self.units[step]
                dve.wait_ge(self.scores_ready, step + 1)
                s = self.scores_at(step)
                if self.causal:
                    diag = s[:, Q * t:Q * t + Q]
                    link(dve.tensor_tensor(diag, diag, self.mask, ALU.add))
                if self.biased is not None:
                    if step >= 2:
                        dve.wait_ge(self.probs_ready, step - 1)
                    out = self.biased[:, step % 2, :]
                    link(dve.tensor_tensor(out, s[:, 0:S], self.strip(t), ALU.add))
                    s = out
                dve.tensor_reduce(self.neg_max[:, step % 4:step % 4 + 1], s[:, 0:self.keys(t)], AX.X, ALU.max,
                                  negate=True).then_inc(self.max_ready, 1)
            if 1 <= step <= n:
                i = step - 1
                t, m = self.units[i]
                dve.wait_ge(self.turned, i + 1)
                if i >= 2:
                    dve.wait_ge(self.product_ready, i - 1)
                k = self.keys(t) // Q
                dve.tensor_copy(self.probs_t[:, i % 2, 0:k, :], turned[:, 0:k, 0:Q]).then_inc(self.turned_copied, 1)
            if step >= 2 and self.units[step - 2][1] == self.maps - 1:
                t = self.units[step - 2][0]
                dve.wait_ge(self.product_ready, step - 1)
                if t >= 1:
                    dve.wait_ge(self.out_ready, t)
                link(dve.reciprocal(self.inv_sum[:, :], self.row_sum[:, t % 2, :]))
                prod = self.ps[0:Q, 6 + t % 2, 0:self.maps * self.dv].rearrange("p (m d) -> p m d", m=self.maps)
                dve.tensor_tensor(self.out_of(t), prod, wide(self.inv_sum[:, :].unsqueeze(2), [Q, self.maps, self.dv]),
                                  ALU.mult).then_inc(self.out_ready, 1)


def split3(dve, link, parts, value, rest):
    link(dve.tensor_copy(parts[0], value))
    link(dve.tensor_tensor(rest, value, parts[0], ALU.subtract))
    link(dve.tensor_copy(parts[1], rest))
    link(dve.tensor_tensor(parts[2], rest, parts[1], ALU.subtract))


class SplitAttention:

    def __init__(self, nc, st, name, ps, groups, members, ident, mask, mask_t, v1, out_of):
        self.ps, self.G, self.E, self.M = ps, groups, members, groups * members
        self.ident, self.mask, self.mask_t, self.v1, self.out_of = ident, mask, mask_t, v1, out_of
        sb = lambda n, shape, dt=F32: st.enter_context(nc.sbuf_tensor(f"{name}_{n}", shape, dt))
        self.q_stack = sb("q_stack", [Q, T, self.M, 96], BF16)
        self.k_stack = sb("k_stack", [Q, T, self.G, 96], BF16)
        self.rest = sb("rest", [Q, T, self.M, 16])
        self.qT = sb("qT", [99, self.M, S], BF16)
        self.kT = sb("kT", [99, self.G, S], BF16)
        self.probs_t = sb("probs_t", [Q, 2, self.E, Q])
        self.neg_max = sb("neg_max", [Q, 2, self.M])
        self.max_rest = sb("max_rest", [Q, self.M])
        self.max_parts = sb("max_parts", [Q, 2, self.M, 3], BF16)
        self.inv_sum = sb("inv_sum", [Q, self.M])
        names = ("stacks_ready", "stack_turned", "stack_copied_v", "stack_copied_s", "scores_ready", "max_ready",
                 "parts_ready", "parts_turned", "parts_copied", "turned_ready", "probs_ready", "product_ready", "out_ready")
        self.sems = [st.enter_context(nc.semaphore(f"{name}_{n}")) for n in names]
        (self.stacks_ready, self.stack_turned, self.stack_copied_v, self.stack_copied_s, self.scores_ready,
         self.max_ready, self.parts_ready, self.parts_turned, self.parts_copied, self.turned_ready,
         self.probs_ready, self.product_ready, self.out_ready) = self.sems
        self.per_bank = min(8, self.M)
        self.rounds = self.M // self.per_bank
        self.loads = [("k", t) for t in range(T)] + [("q", t, r) for t in range(T) for r in range(self.rounds)]
        self.steps = [(t, g, k) for t in range(T) for g in range(self.G) for k in range(t + 1)]

    def bank16(self, b, rows, n):
        return self.ps[rows, b, :].bitcast(BF16)[:, 0:n * Q].rearrange("p (m n) -> p m n", n=Q)

    def stack(self, dve, link, stack, value, rest, order):
        first = [order.index(j) for j in range(3)]
        parts = [stack[:, :, :, 16 * f:16 * f + 16] for f in first]
        split3(dve, link, parts, value, rest)
        for i, j in enumerate(order):
            if i not in first:
                link(dve.tensor_copy(stack[:, :, :, 16 * i:16 * i + 16], parts[j]))

    def vector_stacks(self, dve, link, q, k):
        link(dve.memset(self.kT[96:99, :, :], 1.0))
        self.stack(dve, link, self.k_stack, k, self.rest[:, :, 0:self.G, :], (0, 1, 0, 2, 1, 0))
        dve.sem_inc(self.stacks_ready, 1)
        self.stack(dve, link, self.q_stack, q, self.rest[:, :, :, :], (0, 0, 1, 0, 1, 2))
        dve.sem_inc(self.stacks_ready, 1)

    def copy_stacks(self, eng, copy, parity, done):
        for i, load in enumerate(self.loads):
            if i % 2 != parity:
                continue
            eng.wait_ge(self.stack_turned, i + 1)
            t = load[1]
            if load[0] == "k":
                dst, n = self.kT[0:96, :, Q * t:Q * t + Q], self.G
            else:
                m = load[2] * self.per_bank
                dst, n = self.qT[0:96, m:m + self.per_bank, Q * t:Q * t + Q], self.per_bank
            copy(dst, self.bank16(i % 8, slice(0, 96), n)).then_inc(done, 1)

    def tensor_stacks(self, pe):
        for i, load in enumerate(self.loads):
            if i == 0 or i == T:
                pe.wait_ge(self.stacks_ready, 1 + (i == T))
            if i >= 8:
                pe.wait_ge(self.stack_copied_s if i % 2 else self.stack_copied_v, (i - 8) // 2 + 1)
            t = load[1]
            if load[0] == "k":
                src, n = self.k_stack[:, t, :, :], self.G
            else:
                m = load[2] * self.per_bank
                src, n = self.q_stack[:, t, m:m + self.per_bank, :], self.per_bank
            dst = self.bank16(i % 8, slice(0, 96), n)
            for m in range(n):
                mm = pe.transpose(dst[:, m, :], src[:, m, :], self.ident[:, :])
            mm.then_inc(self.stack_turned, 1)
        pe.wait_ge(self.stack_copied_v, (len(self.loads) + 1) // 2)
        pe.wait_ge(self.stack_copied_s, len(self.loads) // 2)

    def tensor(self, pe):
        self.tensor_stacks(pe)
        M, E, G = self.M, self.E, self.G

        def scores(t, m):
            i = M * t + m
            if i >= 2:
                pe.wait_ge(self.max_ready, i - 1)
            if t >= 1 and m < 3:
                pe.wait_ge(self.parts_copied, self.rounds * t)
            b, n = 2 * (i % 2), Q * (t + 1)
            dst = self.ps[0:Q, b:b + 2, :].rearrange("p b n -> p (b n)")
            for a in range(0, n, 512):
                z = min(n, a + 512)
                mm = pe.matmul(dst[:, a:z], self.qT[0:96, m, Q * t:Q * t + Q], self.kT[0:96, m // E, a:z],
                               start=True, stop=False, skip_group_check=True)
            cuts = [Q * t, n] if n <= 512 else [Q * t, 512, n]
            for a, z in zip(cuts, cuts[1:]):
                mm = pe.matmul(dst[:, a:z], self.ident[:, :], self.mask[:, a - Q * t:z - Q * t],
                               start=False, stop=True, skip_group_check=True)
            mm.then_inc(self.scores_ready, 1)

        def turn_max(t):
            pe.wait_ge(self.parts_ready, t + 1)
            for r in range(self.rounds):
                dst = self.bank16(2 * r, slice(96, 99), self.per_bank)
                for m in range(self.per_bank):
                    mm = pe.transpose(dst[:, m, :], self.max_parts[:, t % 2, self.per_bank * r + m, :], self.ident[:, :])
                mm.then_inc(self.parts_turned, 1)

        def turned_scores(j):
            t, g, k = self.steps[j]
            if j >= 2:
                pe.wait_ge(self.probs_ready, j - 1)
            if g == k == 0:
                pe.wait_ge(self.parts_copied, self.rounds * (t + 1))
            dst = self.ps[0:Q, 4 + j % 2, 0:E * Q].rearrange("p (e n) -> p e n", e=E)
            mm = pe.matmul(dst, self.kT[:, g, Q * k:Q * k + Q], self.qT[:, E * g:E * g + E, Q * t:Q * t + Q],
                           start=True, stop=(k < t))
            if k == t:
                mm = pe.matmul(dst, self.ident[:, :], wide(self.mask_t[:, :].unsqueeze(1), [Q, E, Q]),
                               start=False, stop=True)
            mm.then_inc(self.turned_ready, 1)

        def product(j):
            t, g, k = self.steps[j]
            pe.wait_ge(self.probs_ready, j + 1)
            if g == k == 0 and t >= 2:
                pe.wait_ge(self.out_ready, t - 1)
            for e in range(E):
                m = E * g + e
                mm = pe.matmul(self.ps[0:Q, 6 + t % 2, 17 * m:17 * m + 17], self.probs_t[:, j % 2, e, :],
                               self.v1[:, k, g, :], start=(k == 0 and e == 0), stop=(k == t), skip_group_check=True)
            mm.then_inc(self.product_ready, 1)

        for m in range(M):
            scores(0, m)
        turn_max(0)
        j = 0
        for t in range(T):
            n = G * (t + 1)
            m = 0
            for s in range(n):
                if t + 1 < T:
                    while m < M * (s + 1) // n:
                        scores(t + 1, m)
                        m += 1
                turned_scores(j)
                if s >= 1:
                    product(j - 1)
                j += 1
            product(j - 1)
            if t + 1 < T:
                turn_max(t + 1)

    def scalar(self, act):
        self.copy_stacks(act, act.copy, 1, self.stack_copied_s)
        j = 0
        for t in range(T):
            for r in range(self.rounds):
                act.wait_ge(self.parts_turned, self.rounds * t + r + 1)
                m = self.per_bank * r
                act.copy(self.qT[96:99, m:m + self.per_bank, Q * t:Q * t + Q],
                         self.bank16(2 * r, slice(96, 99), self.per_bank)).then_inc(self.parts_copied, 1)
            for _ in range(self.G * (t + 1)):
                act.wait_ge(self.turned_ready, j + 1)
                if j >= 2:
                    act.wait_ge(self.product_ready, j - 1)
                act.activation(self.probs_t[:, j % 2, :, :],
                               self.ps[0:Q, 4 + j % 2, 0:self.E * Q].rearrange("p (e n) -> p e n", e=self.E),
                               ACT.Exp).then_inc(self.probs_ready, 1)
                j += 1

    def vector(self, dve, link):
        M = self.M
        self.copy_stacks(dve, dve.tensor_copy, 0, self.stack_copied_v)

        def finish(t):
            dve.wait_ge(self.product_ready, self.G * (t + 1) * (t + 2) // 2)
            prod = self.ps[0:Q, 6 + t % 2, 0:17 * M].rearrange("p (m d) -> p m d", m=M)
            link(dve.reciprocal(self.inv_sum[:, :], prod[:, :, 16]))
            link(dve.tensor_tensor(self.out_of(t), prod[:, :, 0:16], wide(self.inv_sum[:, :].unsqueeze(2), [Q, M, 16]),
                                   ALU.mult))
            dve.sem_inc(self.out_ready, 1)

        for t in range(T):
            for m in range(M):
                i = M * t + m
                dve.wait_ge(self.scores_ready, i + 1)
                s = self.ps[0:Q, 2 * (i % 2):2 * (i % 2) + 2, :].rearrange("p b n -> p (b n)")[:, 0:Q * (t + 1)]
                dve.tensor_reduce(self.neg_max[:, t % 2, m:m + 1], s, AX.X, ALU.max, negate=True).then_inc(self.max_ready, 1)
            dve.wait_ge(self.max_ready, M * (t + 1))
            split3(dve, link, [self.max_parts[:, t % 2, :, j] for j in range(3)], self.neg_max[:, t % 2, :],
                   self.max_rest[:, :])
            dve.sem_inc(self.parts_ready, 1)
            if t >= 1:
                finish(t - 1)
        finish(T - 1)


def build(nc, a, out, upto=99):
    ctx = ExitStack()
    with ctx:
        def sb(name, shape, dt=F32):
            return ctx.enter_context(nc.sbuf_tensor(name, shape, dt))

        ps = ctx.enter_context(nc.psum_tensor("ps", [128, 8, 512], F32))
        h_in = nc.dram_tensor("h_tokens", (B, S, D), F32, kind="Internal").ap()
        h_mid = nc.dram_tensor("h_after_attention", (B, S, D), F32, kind="Internal").ap()
        sx_all = nc.dram_tensor("head_inputs", (B, S, D), F32, kind="Internal").ap()

        ident = sb("ident", [128, 128])
        causal = sb("causal", [Q, Q])
        keep = sb("keep", [Q, Q])
        ident16 = sb("ident16", [Q, Q], BF16)
        mask16 = sb("mask16", [Q, Q], BF16)
        mask16_t = sb("mask16_t", [Q, Q], BF16)
        iota8 = sb("iota8", [Q, 8])
        cos_t = sb("cos_t", [Q, T, 8])
        sin_t = sb("sin_t", [Q, T, 8])
        ones = sb("ones", [1, Q])
        att_scale = sb("att_scale", [Q, 1])
        strip = sb("strip", [Q, S + S - Q])
        rows = {}
        for n in ("l0a_g1", "l0a_b1", "l0a_g2", "l0a_b2", "l1a_g1", "l1a_b1", "l1a_g2", "l1a_b2",
                  "l1f_w1", "l1f_w2", "l3f_g", "l3f_b"):
            rows[n] = sb("row_" + n, [Q, D])
        for n in ("l0f_g", "l0f_b", "l0f_fg", "l0f_fb", "l0f_gate"):
            rows[n] = sb("row_" + n, [Q, 16])
        rows["l2f_bg"] = sb("row_l2f_bg", [Q, 8])
        rows["l3f_br"] = sb("row_l3f_br", [Q, 8])
        w = {}
        for n, cols in (("l0a_qkv", 192), ("l0a_proj", 64), ("l0f_hl", 64), ("l0f_fc1", 64), ("l0f_fc2", 64),
                        ("l1a_qkv", 192), ("l1a_proj", 64), ("l1a_w1", 256), ("l3a_qkv", 192)):
            w[n] = sb("w_" + n, [D + 1, cols])
        for n, shape in (("l0f_qkv", [D, 384]),
                         ("l0f_gate", [128, 2, 8]), ("l0f_fgate", [D, 4]),
                         ("l1a_w2", [128, 2, 64]), ("l1a_b2", [1, 64]),
                         ("l1f_qkv", [D, 128]), ("l1f_wo", [D, 64]), ("l1f_router", [D, 8]),
                         ("l1f_w1", [D, 8, HID]), ("l1f_w3", [D, 8, HID]), ("l1f_w2", [HP, 8, 2, D]),
                         ("l2a_q", [D, 64]), ("l2a_k", [D, 64]), ("l2a_v", [D, 64]), ("l2a_o", [D, 64]),
                         ("l2f_g", [D, 8]), ("l2f_w1", [D, 8, 128]), ("l2f_w2", [128, 8, D]), ("l2f_b2", [8, D]),
                         ("l3f_r", [D, 8]), ("l3f_w1", [D, 8, 128]), ("l3f_w2", [128, 8, D]), ("l3f_b2", [8, D]),
                         ("l2f_b1", [128, 8]), ("l3f_b1", [128, 8])):
            w[n] = sb("w_" + n, shape)

        h = sb("h", [Q, T, D])
        x = sb("x", [Q, T, D])
        y = sb("y", [Q, T, D])
        sq = sb("sq", [Q, T, D])
        st = sb("st", [Q, 4, 24])
        xT = sb("xT", [D + 1, S])
        yT = sb("yT", [D + 1, S])
        resid = sb("resid", [Q, T, D])

        previous = []

        class Stage:

            def __init__(self, name):
                self.name, self.st, self.sems = name, ExitStack(), []

            def sb(self, name, shape, dt=F32):
                return self.st.enter_context(nc.sbuf_tensor(f"{self.name}_{name}", shape, dt))

            def sem(self, name):
                s = ctx.enter_context(nc.semaphore(f"{self.name}_{name}"))
                self.sems.append(s)
                return s

            def __enter__(self):
                self.st.__enter__()
                return self

            def block(self):
                return self.st.enter_context(nc.Block())

            def __exit__(self, *e):
                self.st.__exit__(*e)
                previous[:] = self.sems

        def end_of_pass(name):
            with Stage(name) as sg:
                block = sg.block()

                @block.sync
                def _(sp):
                    clear_previous(sp, sg.sems)

        def clear_previous(sp, own):
            for s in previous:
                if s not in own:
                    sp.sem_clear(s)

        def two(b, p):
            return ps[0:p, b:b + 2, 0:HALF]

        def tiles(b, width=D):
            return ps[0:Q, b, 0:T * width].rearrange("p (t n) -> p t n", t=T)

        def turn(pe, b, src, width=D):
            for t in range(T):
                mm = pe.transpose(ps[0:width, b + t // 3, Q * (t % 3):Q * (t % 3) + Q], src[:, t, :], ident[0:Q, 0:Q])
            return mm

        def by_feature(pe, b, weight, src):
            for c in range(2):
                mm = pe.matmul(ps[0:weight.shape[1], b + c, 0:HALF], weight, src[:, HALF * c:HALF * c + HALF],
                               start=True, stop=True)
            return mm

        def by_token(pe, b, src, weight):
            n = weight.shape[1]
            for t in range(T):
                mm = pe.matmul(ps[0:Q, b, n * t:n * t + n], src[:, Q * t:Q * t + Q], weight, start=True, stop=True)
            return mm

        def softmax_first(dve, link, logits, st):
            p, g, n = logits.shape
            top = st[0:p, 0, 0:g]
            link(dve.tensor_reduce(top, logits, AX.X, ALU.max))
            link(dve.tensor_tensor(logits, logits, wide(top.unsqueeze(2), [p, g, n]), ALU.subtract))

        def softmax_last(dve, link, e, st):
            p, g, n = e.shape
            total = st[0:p, 0, 0:g]
            link(dve.tensor_reduce(total, e, AX.X, ALU.add))
            link(dve.reciprocal(total, total))
            link(dve.tensor_tensor(e, e, wide(total.unsqueeze(2), [p, g, n]), ALU.mult))

        def per_tile(row):
            return wide(row[:, :].unsqueeze(1), [Q, T, row.shape[1]])

        def per_head(row):
            return wide(row[:, :].unsqueeze(1), [Q, 24, 16])

        def heads(t):
            return t[:, :, :].rearrange("p t (n d) -> p (t n) d", n=4)

        def layer0_ffn(b):
            with Stage("l0f") as sg:
                loaded, tensor_done, vector_done, scalar_done, vchain = (
                    sg.sem(n) for n in ("h_loaded", "tensor_step", "vector_step", "scalar_step", "vector_chain"))
                qk = sg.sb("qk", [Q, T, 20, 16])
                v1 = sg.sb("v1", [Q, T, 4, 17])
                live = sg.sb("live", [Q, T, D])
                ao = sg.sb("ao", [Q, T, 16, 16])
                aoT = sg.sb("aoT", [128, 12, Q])
                gate = sg.sb("gate", [Q, 24, 4])
                fgate = sg.sb("fgate", [Q, T, 4])
                att = SplitAttention(nc, sg.st, "l0f_att", ps, 4, 4, ident16, mask16, mask16_t, v1,
                                     lambda t: ao[:, t, :, :])
                sg.sems += att.sems
                block = sg.block()
                qkv_ps = ps[0:Q, 0:6, 0:384]

                @block.sync
                def _(sp):
                    clear_previous(sp, sg.sems)
                    sp.dma_start(h[:, :, :], tokens(h_mid, b)).then_inc(loaded, 16)

                @block.vector
                def _(dve):
                    link = Chain(dve, vchain)
                    dve.wait_ge(loaded, 16)
                    layer_norm(dve, link, x[:, :, :], h[:, :, :], sq[:, :, :], st, 1e-5)
                    dve.sem_inc(vector_done, 1)
                    dve.wait_ge(tensor_done, 1)
                    dve.tensor_copy(halves(xT[0:D, :]), two(0, D)).then_inc(vector_done, 1)
                    dve.wait_ge(tensor_done, 2)
                    dve.tensor_copy(halves(yT[0:D, :]), two(2, D)).then_inc(vector_done, 1)
                    link(dve.memset(v1[:, :, :, 16], 1.0))
                    dve.wait_ge(tensor_done, 4)
                    link(dve.tensor_scalar(qk[:, :, 0:16, :].rearrange("p t m d -> p t (m d)"), qkv_ps[:, :, 0:256],
                                           4.0, None, ALU.mult))
                    link(dve.tensor_copy(qk[:, :, 16:20, :].rearrange("p t m d -> p t (m d)"), qkv_ps[:, :, 256:320]))
                    link(dve.tensor_copy(v1[:, :, :, 0:16], qkv_ps[:, :, 320:384].rearrange("p t (n d) -> p t n d", n=4)))
                    dve.wait_ge(scalar_done, 1)
                    link(dve.tensor_scalar(live[:, :, :], y[:, :, :], 0.0, None, ALU.not_equal))
                    dve.sem_inc(vector_done, 4)
                    att.vector_stacks(dve, link, qk[:, :, 0:16, :], qk[:, :, 16:20, :])
                    att.vector(dve, link)
                    dve.wait_ge(att.out_ready, T)
                    four = ao[:, :, :, :].rearrange("p t (n e) d -> p (t n) e d", n=4)
                    link(dve.tensor_tensor(four, four, wide(heads(live).unsqueeze(2), [Q, 24, 4, 16]), ALU.mult))
                    dve.sem_inc(vector_done, 1)
                    dve.wait_ge(tensor_done, 5)
                    turned = ps[:, 0:3, :].rearrange("p b (k n) -> p (b k) n", n=128)[:, :, 0:Q]
                    dve.tensor_copy(aoT[:, :, :], turned).then_inc(vector_done, 1)
                    dve.wait_ge(tensor_done, 6)
                    g3 = gate[:, :, :].rearrange("p (t n) e -> p t (n e)", t=T)
                    link(dve.tensor_tensor(g3, tiles(3, 16), per_tile(rows["l0f_gate"]), ALU.add))
                    softmax_first(dve, link, gate[:, :, :], st)
                    dve.sem_inc(vector_done, 1)
                    dve.wait_ge(scalar_done, 2)
                    softmax_last(dve, link, gate[:, :, :], st)
                    link(dve.tensor_tensor(four, four, wide(gate[:, :, :].unsqueeze(3), [Q, 24, 4, 16]), ALU.mult))
                    link(dve.tensor_reduce(heads(y), four.rearrange("p g e d -> p g d e"), AX.X, ALU.add))
                    link(dve.tensor_tensor(y[:, :, :], y[:, :, :], resid[:, :, :], ALU.add))
                    layer_norm(dve, link, heads(x), heads(y), heads(sq), st, 1e-8)
                    affine(dve, link, heads(x), per_head(rows["l0f_g"]), per_head(rows["l0f_b"]))
                    dve.sem_inc(vector_done, 1)
                    link(dve.tensor_scalar(live[:, :, :], x[:, :, :], 0.0, None, ALU.not_equal))
                    dve.wait_ge(tensor_done, 7)
                    dve.tensor_copy(halves(xT[0:D, :]), two(0, D)).then_inc(vector_done, 1)
                    dve.wait_ge(tensor_done, 8)
                    dve.scalar_tensor_tensor(y[:, :, :], tiles(2), 0.0, live[:, :, :], ALU.max, ALU.mult).then_inc(vector_done, 1)
                    dve.wait_ge(tensor_done, 9)
                    dve.tensor_copy(halves(yT[0:D, :]), two(0, D)).then_inc(vector_done, 1)
                    dve.wait_ge(tensor_done, 10)
                    link(dve.tensor_tensor(y[:, :, :], tiles(3), live[:, :, :], ALU.mult))
                    link(dve.tensor_tensor(y[:, :, :], y[:, :, :], x[:, :, :], ALU.add))
                    layer_norm(dve, link, heads(x), heads(y), heads(sq), st, 1e-8)
                    affine(dve, link, heads(x), per_head(rows["l0f_fg"]), per_head(rows["l0f_fb"]))
                    dve.sem_inc(vector_done, 1)
                    dve.wait_ge(tensor_done, 11)
                    dve.tensor_copy(halves(xT[0:D, :]), two(0, D)).then_inc(vector_done, 1)
                    dve.wait_ge(tensor_done, 12)
                    link(dve.tensor_copy(fgate[:, :, :], tiles(2, 4)))
                    softmax_first(dve, link, fgate[:, :, :], st)
                    dve.sem_inc(vector_done, 1)
                    dve.wait_ge(scalar_done, 3)
                    softmax_last(dve, link, fgate[:, :, :], st)
                    fg = fgate[:, :, :].rearrange("p t n -> p (t n)")
                    link(dve.tensor_tensor(heads(x), heads(x), wide(fg.unsqueeze(2), [Q, 24, 16]), ALU.mult))
                    link(dve.tensor_tensor(h[:, :, :], h[:, :, :], x[:, :, :], ALU.add))

                @block.scalar
                def _(act):
                    act.wait_ge(tensor_done, 3)
                    act.copy(y[:, :, :], tiles(4)).then_inc(scalar_done, 1)
                    att.scalar(act)
                    act.wait_ge(vector_done, 10)
                    act.activation(gate[:, :, :], gate[:, :, :], ACT.Exp).then_inc(scalar_done, 1)
                    act.wait_ge(vector_done, 17)
                    act.activation(fgate[:, :, :], fgate[:, :, :], ACT.Exp).then_inc(scalar_done, 1)

                @block.tensor
                def _(pe):
                    pe.wait_ge(vector_done, 1)
                    turn(pe, 0, x).then_inc(tensor_done, 1)
                    pe.wait_ge(vector_done, 2)
                    by_feature(pe, 2, w["l0f_hl"][:, :], xT).then_inc(tensor_done, 1)
                    by_token(pe, 4, xT, w["l0f_hl"][:, :]).then_inc(tensor_done, 1)
                    pe.wait_ge(vector_done, 3)
                    pe.wait_ge(scalar_done, 1)
                    for t in range(T):
                        mm = pe.matmul(ps[0:Q, t, 0:384], yT[0:D, Q * t:Q * t + Q], w["l0f_qkv"][:, :], start=True, stop=True)
                    mm.then_inc(tensor_done, 1)
                    pe.wait_ge(vector_done, 7)
                    att.tensor(pe)
                    pe.wait_ge(vector_done, 8)
                    for i in range(12):
                        src = ao[:, i // 2, 8 * (i % 2):8 * (i % 2) + 8, :].rearrange("p m d -> p (m d)")
                        mm = pe.transpose(ps[:, i // 4, 128 * (i % 4):128 * (i % 4) + Q], src, ident[0:Q, 0:Q])
                    mm.then_inc(tensor_done, 1)
                    pe.wait_ge(vector_done, 9)
                    for i in range(12):
                        mm = pe.matmul(ps[0:Q, 3, 8 * i:8 * i + 8], aoT[:, i, :], w["l0f_gate"][:, i % 2, :],
                                       start=True, stop=True)
                    mm.then_inc(tensor_done, 1)
                    pe.wait_ge(vector_done, 11)
                    turn(pe, 0, x).then_inc(tensor_done, 1)
                    pe.wait_ge(vector_done, 12)
                    by_token(pe, 2, xT, w["l0f_fc1"][:, :]).then_inc(tensor_done, 1)
                    pe.wait_ge(vector_done, 13)
                    turn(pe, 0, y).then_inc(tensor_done, 1)
                    pe.wait_ge(vector_done, 14)
                    by_token(pe, 3, yT, w["l0f_fc2"][:, :]).then_inc(tensor_done, 1)
                    pe.wait_ge(vector_done, 15)
                    turn(pe, 0, x).then_inc(tensor_done, 1)
                    pe.wait_ge(vector_done, 16)
                    by_token(pe, 2, xT[0:D, :], w["l0f_fgate"][:, :]).then_inc(tensor_done, 1)

        def layer1_attention():
            with Stage("l1a") as sg:
                tensor_done, vector_done, scalar_done, vchain = (
                    sg.sem(n) for n in ("tensor_step", "vector_step", "scalar_step", "vector_chain"))
                qk = sg.sb("qk", [Q, T, 2, D])
                v1 = sg.sb("v1", [Q, T, D + 1])
                qT = sg.sb("qT", [D, S])
                kT = sg.sb("kT", [D, S])
                sT = sg.sb("sT", [Q, T, S])
                hT = sg.sb("hT", [128, 2, S])
                den = sg.sb("den", [Q, T])
                block = sg.block()
                place = [(0, 0), (2, 0), (3, 0), (4, 0), (5, 0), (5, 192)]
                flat = qk[:, :, :, :].rearrange("p t c d -> p (t c) d")

                @block.sync
                def _(sp):
                    clear_previous(sp, sg.sems)

                @block.vector
                def _(dve):
                    link = Chain(dve, vchain)
                    layer_norm(dve, link, x[:, :, :], h[:, :, :], sq[:, :, :], st, 1e-5)
                    dve.sem_inc(vector_done, 1)
                    link(dve.memset(v1[:, :, D:D + 1], 1.0))
                    dve.wait_ge(tensor_done, 1)
                    dve.tensor_copy(halves(xT[0:D, :]), two(0, D)).then_inc(vector_done, 1)
                    dve.wait_ge(tensor_done, 2)
                    qkv = ps[0:Q, 2:5, 0:384].rearrange("p b (a n) -> p b a n", a=2)
                    pairs = lambda t: t.rearrange("p (b a) n -> p b a n", a=2)
                    link(dve.tensor_scalar(pairs(qk[:, :, :, :].rearrange("p t c d -> p t (c d)")), qkv[:, :, :, 0:128],
                                           0.125, None, ALU.mult))
                    link(dve.tensor_copy(pairs(v1[:, :, 0:D]), qkv[:, :, :, 128:192]))
                    sum2, inv, tmp = (st[:, j, 0:12] for j in range(3))
                    s2 = sT[:, 0:3, 0:512].rearrange("p a (b d) -> p a b d", d=D)
                    sqr = sT[:, 0, 0:384].rearrange("p (g d) -> p g d", d=D)
                    for half in range(2):
                        part = flat[:, 6 * half:6 * half + 6, :]
                        link(dve.tensor_tensor(sqr, part, part, ALU.mult))
                        link(dve.tensor_reduce(sum2[:, 6 * half:6 * half + 6], sqr, AX.X, ALU.add))
                    link(dve.tensor_scalar(sum2, sum2, 1e-24, None, ALU.max))
                    rsqrt(dve, link, inv, sum2, tmp)
                    link(dve.tensor_tensor(flat, flat, wide(inv.unsqueeze(2), [Q, 12, D]), ALU.mult))
                    dve.sem_inc(vector_done, 1)
                    dve.wait_ge(scalar_done, 2)
                    dve.tensor_scalar(flat, flat, 1e-6, None, ALU.add).then_inc(vector_done, 1)
                    dve.wait_ge(tensor_done, 3)
                    dve.tensor_copy(halves(qT[:, :]), two(0, D)).then_inc(vector_done, 1)
                    dve.wait_ge(tensor_done, 4)
                    dve.tensor_copy(halves(kT[:, :]), two(5, D)).then_inc(vector_done, 1)
                    for k, (bank, col) in enumerate(place):
                        dve.wait_ge(tensor_done, 10)
                        n = S - Q * k
                        src = ps[0:Q, bank:bank + 2, :].rearrange("p b n -> p (b n)")[:, col:col + n]
                        dve.tensor_tensor(sT[:, k, Q * k:Q * k + Q], src[:, 0:Q], keep[:, :], ALU.mult).then_inc(vchain, 1)
                        link.n += 1
                        if n > Q:
                            link(dve.tensor_copy(sT[:, k, Q * k + Q:S], src[:, Q:n]))
                    dve.wait_ge(vchain, link.n)
                    dve.sem_inc(vector_done, 1)
                    dve.wait_ge(tensor_done, 11)
                    nd = tiles(6, D + 1)
                    link(dve.tensor_scalar(y[:, :, :], nd[:, :, 0:D], 1e4, -1e4, ALU.min, ALU.max))
                    link(dve.tensor_scalar(den[:, :], nd[:, :, D], 1e-6, None, ALU.max))
                    link(dve.reciprocal(den[:, :], den[:, :]))
                    link(dve.tensor_tensor(y[:, :, :], y[:, :, :], wide(den[:, :].unsqueeze(2), [Q, T, D]), ALU.mult))
                    dve.sem_inc(vector_done, 1)
                    dve.wait_ge(tensor_done, 12)
                    dve.tensor_copy(halves(yT[0:D, :]), two(0, D)).then_inc(vector_done, 1)
                    dve.wait_ge(tensor_done, 13)
                    link(dve.tensor_tensor(y[:, :, :], tiles(2), x[:, :, :], ALU.add))
                    layer_norm(dve, link, x[:, :, :], y[:, :, :], sq[:, :, :], st, 1e-5)
                    affine(dve, link, x[:, :, :], per_tile(rows["l1a_g1"]), per_tile(rows["l1a_b1"]))
                    dve.sem_inc(vector_done, 1)
                    dve.wait_ge(tensor_done, 14)
                    dve.tensor_copy(halves(xT[0:D, :]), two(0, D)).then_inc(vector_done, 1)
                    dve.wait_ge(tensor_done, 17)
                    link(dve.tensor_tensor(y[:, :, :], tiles(6), x[:, :, :], ALU.add))
                    layer_norm(dve, link, x[:, :, :], y[:, :, :], sq[:, :, :], st, 1e-5)
                    affine(dve, link, x[:, :, :], per_tile(rows["l1a_g2"]), per_tile(rows["l1a_b2"]))
                    link(dve.tensor_tensor(h[:, :, :], h[:, :, :], x[:, :, :], ALU.add))

                @block.scalar
                def _(act):
                    act.wait_ge(vector_done, 3)
                    act.activation(flat, flat, ACT.Exp).then_inc(scalar_done, 1)
                    act.wait_ge(scalar_done, 1)
                    act.activation(flat, flat, ACT.Ln, bias=1.0).then_inc(scalar_done, 1)
                    for c in range(2):
                        act.wait_ge(tensor_done, 15 + c)
                        act.activation(halves(hT[:, c, :]), two(2 + 2 * c, 128), ACT.Gelu).then_inc(scalar_done, 1)

                @block.tensor
                def _(pe):
                    pe.wait_ge(vector_done, 1)
                    turn(pe, 0, x).then_inc(tensor_done, 1)
                    pe.wait_ge(vector_done, 2)
                    for t in range(T):
                        mm = pe.matmul(ps[0:Q, 2 + t // 2, 192 * (t % 2):192 * (t % 2) + 192], xT[:, Q * t:Q * t + Q],
                                       w["l1a_qkv"][:, :], start=True, stop=True)
                    mm.then_inc(tensor_done, 1)
                    pe.wait_ge(vector_done, 4)
                    turn(pe, 0, qk[:, :, 0, :]).then_inc(tensor_done, 1)
                    turn(pe, 5, qk[:, :, 1, :]).then_inc(tensor_done, 1)
                    pe.wait_ge(vector_done, 6)
                    for k, (bank, col) in enumerate(place):
                        for s in range(Q * k, S, 512):
                            e = min(S, s + 512)
                            at = bank + (s - Q * k) // 512
                            mm = pe.matmul(ps[0:Q, at, col:col + e - s], kT[:, Q * k:Q * k + Q], qT[:, s:e],
                                           start=True, stop=True)
                        mm.then_inc(tensor_done, 1)
                    pe.wait_ge(vector_done, 7)
                    for t in range(T):
                        for k in range(t + 1):
                            mm = pe.matmul(ps[0:Q, 6, 65 * t:65 * t + 65], sT[:, k, Q * t:Q * t + Q], v1[:, k, :],
                                           start=(k == 0), stop=(k == t))
                    mm.then_inc(tensor_done, 1)
                    pe.wait_ge(vector_done, 8)
                    turn(pe, 0, y).then_inc(tensor_done, 1)
                    pe.wait_ge(vector_done, 9)
                    by_token(pe, 2, yT, w["l1a_proj"][:, :]).then_inc(tensor_done, 1)
                    pe.wait_ge(vector_done, 10)
                    turn(pe, 0, x).then_inc(tensor_done, 1)
                    pe.wait_ge(vector_done, 11)
                    for c in range(2):
                        by_feature(pe, 2 + 2 * c, w["l1a_w1"][:, 128 * c:128 * c + 128], xT).then_inc(tensor_done, 1)
                    pe.wait_ge(scalar_done, 4)
                    for t in range(T):
                        dst = ps[0:Q, 6, D * t:D * t + D]
                        for c in range(2):
                            pe.matmul(dst, hT[:, c, Q * t:Q * t + Q], w["l1a_w2"][:, c, :], start=(c == 0), stop=False)
                        mm = pe.matmul(dst, ones[:, :], w["l1a_b2"][:, :], start=False, stop=True)
                    mm.then_inc(tensor_done, 1)

        def top_two(dve, link, values, top, index, where, hot):
            for t in range(T):
                link(dve.max(top[:, t, :], values[:, t, :]))
                link(dve.max_index(index[:, t, :], top[:, t, :], values[:, t, :]))
            link(dve.tensor_copy(where[:, :, :], index[:, :, 0:2]))
            for j in range(2):
                link(dve.tensor_tensor(hot[:, j, :, :], per_tile(iota8), wide(where[:, :, j:j + 1], [Q, T, 8]), ALU.is_equal))

        def layer1_ffn():
            with Stage("l1f") as sg:
                tensor_done, vector_done, scalar_done, vchain = (
                    sg.sem(n) for n in ("tensor_step", "vector_step", "scalar_step", "vector_chain"))
                up_ready, silu_ready, hidden_ready, down_ready, added = (
                    sg.sem(n) for n in ("up_ready", "silu_ready", "hidden_ready", "down_ready", "added"))
                qs = sg.sb("qs", [Q, T, 128])
                ro = sg.sb("ro", [Q, T, 6, 16])
                ra = sg.sb("ra", [Q, T, 6, 8])
                rb = sg.sb("rb", [Q, T, 6, 8])
                qp = sg.sb("qp", [Q, T, 4, 32])
                kp = sg.sb("kp", [Q, T, 4, 32])
                qT = sg.sb("qT", [128, S])
                kT = sg.sb("kT", [128, S])
                ao = sg.sb("ao", [Q, T, D])
                probs = sg.sb("router_probs", [Q, T, 8])
                top = sg.sb("top", [Q, T, 8])
                index = sg.sb("index", [Q, T, 8], U32)
                where = sg.sb("where", [Q, T, 2])
                hot = sg.sb("hot", [Q, 2, T, 8])
                share = sg.sb("share", [Q, T, 8])
                silu = sg.sb("silu", [HP, 2, HALF])
                hidden = sg.sb("hidden", [HP, 2, 2, S])
                att = Attention(nc, sg.st, "l1f_att", ps, 4, 16, True,
                                lambda m, t: qT[32 * m:32 * m + 16, Q * t:Q * t + Q],
                                lambda m, s, e: kT[32 * m:32 * m + 16, s:e],
                                lambda m, k: qs[:, k, 96 + 16 * (m // 2):112 + 16 * (m // 2)],
                                lambda t: ao[:, t, :].rearrange("p (m d) -> p m d", m=4), mask=causal[:, :])
                sg.sems += att.sems
                block = sg.block()
                units = [(e, c, n) for e in range(8) for c in range(2) for n in range(2)]

                @block.sync
                def _(sp):
                    clear_previous(sp, sg.sems)

                @block.vector
                def _(dve):
                    link = Chain(dve, vchain)
                    layer_norm(dve, link, x[:, :, :], h[:, :, :], sq[:, :, :], st, 1e-5)
                    rms_norm(dve, link, y[:, :, :], x[:, :, :], sq[:, :, :], st, 1e-6, per_tile(rows["l1f_w1"]))
                    dve.sem_inc(vector_done, 1)
                    link(dve.memset(qp[:, :, :, :], 0.0))
                    link(dve.memset(kp[:, :, :, :], 0.0))
                    dve.wait_ge(tensor_done, 1)
                    dve.tensor_copy(halves(yT[0:D, :]), two(0, D)).then_inc(vector_done, 1)
                    dve.wait_ge(tensor_done, 2)
                    flat = ps[0:Q, 2:4, :].rearrange("p b n -> p (b n)")[:, 0:768]
                    link(dve.tensor_copy(qs[:, :, :].rearrange("p t n -> p (t n)"), flat))
                    v6 = qs[:, :, 0:96].rearrange("p t (n d) -> p t n d", n=6)
                    first, second = v6[:, :, :, 0:8], v6[:, :, :, 8:16]
                    c6 = wide(cos_t[:, :, :].unsqueeze(2), [Q, T, 6, 8])
                    s6 = wide(sin_t[:, :, :].unsqueeze(2), [Q, T, 6, 8])
                    link(dve.tensor_tensor(ra[:, :, :, :], first, c6, ALU.mult))
                    link(dve.tensor_tensor(rb[:, :, :, :], second, s6, ALU.mult))
                    link(dve.tensor_tensor(ro[:, :, :, 0:8], ra[:, :, :, :], rb[:, :, :, :], ALU.subtract))
                    link(dve.tensor_tensor(ra[:, :, :, :], second, c6, ALU.mult))
                    link(dve.tensor_tensor(rb[:, :, :, :], first, s6, ALU.mult))
                    link(dve.tensor_tensor(ro[:, :, :, 8:16], ra[:, :, :, :], rb[:, :, :, :], ALU.add))
                    link(dve.tensor_scalar(qp[:, :, :, 0:16], ro[:, :, 0:4, :], 0.25, None, ALU.mult))
                    for r in range(2):
                        link(dve.tensor_copy(kp[:, :, r:4:2, 0:16], ro[:, :, 4:6, :]))
                    dve.sem_inc(vector_done, 1)
                    dve.wait_ge(tensor_done, 3)
                    dve.tensor_copy(halves(qT[:, :]), two(0, 128)).then_inc(vector_done, 1)
                    dve.wait_ge(tensor_done, 4)
                    dve.tensor_copy(halves(kT[:, :]), two(4, 128)).then_inc(vector_done, 1)
                    att.vector(dve, link)
                    dve.wait_ge(tensor_done, 5)
                    dve.tensor_copy(halves(yT[0:D, :]), two(0, D)).then_inc(vector_done, 1)
                    dve.wait_ge(tensor_done, 6)
                    link(dve.tensor_tensor(x[:, :, :], tiles(2), x[:, :, :], ALU.add))
                    rms_norm(dve, link, y[:, :, :], x[:, :, :], sq[:, :, :], st, 1e-6, per_tile(rows["l1f_w2"]))
                    dve.sem_inc(vector_done, 1)
                    dve.wait_ge(tensor_done, 7)
                    dve.tensor_copy(halves(yT[0:D, :]), two(4, D)).then_inc(vector_done, 1)
                    dve.wait_ge(tensor_done, 8)
                    link(dve.tensor_copy(probs[:, :, :], tiles(6, 8)))
                    softmax_first(dve, link, probs[:, :, :], st)
                    dve.sem_inc(vector_done, 1)
                    dve.wait_ge(scalar_done, 1)
                    softmax_last(dve, link, probs[:, :, :], st)
                    top_two(dve, link, probs, top, index, where, hot)
                    total = st[:, 0, 0:T]
                    link(dve.scalar_tensor_tensor(total, top[:, :, 0], 1e-9, top[:, :, 1], ALU.add, ALU.add))
                    link(dve.reciprocal(total, total))
                    link(dve.tensor_tensor(share[:, :, :], hot[:, 0, :, :], hot[:, 1, :, :], ALU.add))
                    link(dve.tensor_tensor(share[:, :, :], share[:, :, :], probs[:, :, :], ALU.mult))
                    link(dve.tensor_tensor(share[:, :, :], share[:, :, :], wide(total.unsqueeze(2), [Q, T, 8]), ALU.mult))

                    def add_expert(e):
                        dve.wait_ge(down_ready, e + 1)
                        link(dve.tensor_tensor(sq[:, :, :], tiles(4 + e % 2), wide(share[:, :, e:e + 1], [Q, T, D]), ALU.mult))
                        dve.tensor_tensor(x[:, :, :], x[:, :, :], sq[:, :, :], ALU.add).then_inc(added, 1)
                        dve.wait_ge(added, e + 1)

                    for u, (e, c, n) in enumerate(units):
                        dve.wait_ge(silu_ready, u + 1)
                        if e >= 2 and c == n == 0:
                            dve.wait_ge(down_ready, e - 1)
                        dve.tensor_tensor(hidden[:, e % 2, c, HALF * n:HALF * n + HALF], silu[:, u % 2, :],
                                          ps[0:HP, 2 + u % 2, 0:HALF], ALU.mult).then_inc(hidden_ready, 1)
                        if c == n == 1 and e >= 1:
                            add_expert(e - 1)
                    add_expert(7)
                    link(dve.tensor_tensor(h[:, :, :], h[:, :, :], x[:, :, :], ALU.add))

                @block.scalar
                def _(act):
                    att.scalar(act)
                    act.wait_ge(vector_done, 9)
                    act.activation(probs[:, :, :], probs[:, :, :], ACT.Exp).then_inc(scalar_done, 1)
                    for u in range(len(units)):
                        act.wait_ge(up_ready, u + 1)
                        if u >= 2:
                            act.wait_ge(hidden_ready, u - 1)
                        act.activation(silu[:, u % 2, :], ps[0:HP, u % 2, 0:HALF], ACT.Silu).then_inc(silu_ready, 1)

                @block.tensor
                def _(pe):
                    pe.wait_ge(vector_done, 1)
                    turn(pe, 0, y).then_inc(tensor_done, 1)
                    pe.wait_ge(vector_done, 2)
                    for t in range(T):
                        mm = pe.matmul(ps[0:Q, 2 + t // 4, 128 * (t % 4):128 * (t % 4) + 128], yT[0:D, Q * t:Q * t + Q],
                                       w["l1f_qkv"][:, :], start=True, stop=True)
                    mm.then_inc(tensor_done, 1)
                    pe.wait_ge(vector_done, 3)
                    turn(pe, 0, qp[:, :, :, :].rearrange("p t n d -> p t (n d)"), 128).then_inc(tensor_done, 1)
                    turn(pe, 4, kp[:, :, :, :].rearrange("p t n d -> p t (n d)"), 128).then_inc(tensor_done, 1)
                    pe.wait_ge(vector_done, 5)
                    att.tensor(pe, ident)
                    pe.wait_ge(att.out_ready, T)
                    turn(pe, 0, ao).then_inc(tensor_done, 1)
                    pe.wait_ge(vector_done, 6)
                    by_token(pe, 2, yT[0:D, :], w["l1f_wo"][:, :]).then_inc(tensor_done, 1)
                    pe.wait_ge(vector_done, 7)
                    turn(pe, 4, y).then_inc(tensor_done, 1)
                    pe.wait_ge(vector_done, 8)
                    by_token(pe, 6, yT[0:D, :], w["l1f_router"][:, :]).then_inc(tensor_done, 1)

                    def down(e):
                        pe.wait_ge(hidden_ready, 4 * e + 4)
                        if e >= 2:
                            pe.wait_ge(added, e - 1)
                        for t in range(T):
                            for c in range(2):
                                mm = pe.matmul(ps[0:Q, 4 + e % 2, D * t:D * t + D], hidden[:, e % 2, c, Q * t:Q * t + Q],
                                               w["l1f_w2"][:, e, c, :], start=(c == 0), stop=(c == 1))
                        mm.then_inc(down_ready, 1)

                    for u, (e, c, n) in enumerate(units):
                        if u >= 2:
                            pe.wait_ge(hidden_ready, u - 1)
                        for bank, m in ((u % 2, "l1f_w1"), (2 + u % 2, "l1f_w3")):
                            mm = pe.matmul(ps[0:HP, bank, 0:HALF], w[m][:, e, HP * c:HP * c + HP],
                                           yT[0:D, HALF * n:HALF * n + HALF], start=True, stop=True)
                        mm.then_inc(up_ready, 1)
                        if c == n == 1 and e >= 1:
                            down(e - 1)
                    down(7)

        def layer2_attention():
            with Stage("l2a") as sg:
                tensor_done, vector_done, scalar_done, vchain = (
                    sg.sem(n) for n in ("tensor_step", "vector_step", "scalar_step", "vector_chain"))
                spread, spread_copied, best_ready, exp_ready, weights_ready, turned, turned_copied, product_ready = (
                    sg.sem(n) for n in ("spread", "spread_copied", "best_ready", "exp_ready", "weights_ready", "turned",
                                        "turned_copied", "product_ready"))
                q = sg.sb("q", [Q, T, D])
                kT = sg.sb("kT", [D, S])
                v = sg.sb("v", [Q, T, D])
                keys = sg.sb("keys", [Q, 2, 16, S])
                score = sg.sb("score", [Q, 2, S])
                taken = sg.sb("taken", [Q, 2, S])
                weight = sg.sb("weight", [Q, 2, S])
                weightT = sg.sb("weightT", [Q, 2, T, Q])
                best = sg.sb("best", [Q, 2, 8])
                neg_max = sg.sb("neg_max", [Q, 2])
                total = sg.sb("total", [Q, T, 4])
                ao = sg.sb("ao", [Q, T, D])
                block = sg.block()
                units = [(n, t) for n in range(4) for t in range(T)]
                turned_ps = ps[0:Q, 4:6, :].rearrange("p b (k n) -> p (b k) n", n=128)

                def copy_turned(act, i):
                    act.wait_ge(turned, i + 1)
                    if i >= 2:
                        act.wait_ge(product_ready, i - 1)
                    k = units[i][1] + 1
                    act.copy(weightT[:, i % 2, 0:k, :], turned_ps[:, 0:k, 0:Q]).then_inc(turned_copied, 1)

                def turn_weights(pe, i):
                    n, t = units[i]
                    pe.wait_ge(weights_ready, i + 1)
                    if i >= 1:
                        pe.wait_ge(turned_copied, i)
                    for k in range(t + 1):
                        mm = pe.transpose(turned_ps[:, k, 0:Q], weight[:, i % 2, Q * k:Q * k + Q], ident[0:Q, 0:Q])
                    mm.then_inc(turned, 1)
                    pe.wait_ge(turned_copied, i + 1)
                    col = D * t + 16 * n
                    for k in range(t + 1):
                        mm = pe.matmul(ps[0:Q, 7, col:col + 16], weightT[:, i % 2, k, :], v[:, k, 16 * n:16 * n + 16],
                                       start=(k == 0), stop=(k == t))
                    mm.then_inc(product_ready, 1)

                @block.sync
                def _(sp):
                    clear_previous(sp, sg.sems)

                @block.vector
                def _(dve):
                    link = Chain(dve, vchain)
                    layer_norm(dve, link, x[:, :, :], h[:, :, :], sq[:, :, :], st, 1e-5)
                    dve.sem_inc(vector_done, 1)
                    dve.wait_ge(tensor_done, 1)
                    dve.tensor_copy(halves(xT[0:D, :]), two(0, D)).then_inc(vector_done, 1)
                    dve.wait_ge(tensor_done, 2)
                    dve.tensor_copy(q[:, :, :], tiles(6)).then_inc(vector_done, 1)
                    dve.wait_ge(vector_done, 3)

                    def weigh(i):
                        n, t = units[i]
                        dve.wait_ge(exp_ready, i + 1)
                        e = weight[:, i % 2, 0:Q * (t + 1)]
                        dve.scalar_tensor_tensor(e, taken[:, i % 2, 0:Q * (t + 1)], 2 * NEG, e, ALU.is_le, ALU.mult,
                                                 accum_out=total[:, t, n:n + 1]).then_inc(weights_ready, 1)

                    for i, (n, t) in enumerate(units):
                        L = Q * (t + 1)
                        s = score[:, i % 2, 0:L]
                        if i >= 2:
                            dve.wait_ge(exp_ready, i - 1)
                        if t == 0:
                            dve.wait_ge(spread_copied, 16 * n + 16)
                        link(dve.tensor_scalar(s, keys[:, n % 2, 0, 0:L], q[:, t, 16 * n:16 * n + 1], None, ALU.add))
                        for d in range(1, 16):
                            link(dve.scalar_tensor_tensor(s, keys[:, n % 2, d, 0:L], q[:, t, 16 * n + d:16 * n + d + 1], s,
                                                          ALU.add, ALU.max))
                        link(dve.tensor_tensor(s[:, Q * t:L], s[:, Q * t:L], causal[:, :], ALU.add))
                        link(dve.max(best[:, i % 2, :], s))
                        link(dve.tensor_scalar(neg_max[:, i % 2:i % 2 + 1], best[:, i % 2, 0:1], -1.0, None, ALU.mult))
                        if i >= 2:
                            dve.wait_ge(weights_ready, i - 1)
                        dve.match_replace(taken[:, i % 2, 0:L], best[:, i % 2, :], s, 3 * NEG).then_inc(best_ready, 1)
                        if i >= 1:
                            weigh(i - 1)
                    weigh(len(units) - 1)
                    dve.wait_ge(weights_ready, len(units))
                    dve.wait_ge(product_ready, len(units))
                    flat = total[:, :, :].rearrange("p t n -> p (t n)")
                    link(dve.reciprocal(flat, flat))
                    prod = ps[0:Q, 7, 0:384].rearrange("p (g d) -> p g d", d=16)
                    dve.tensor_tensor(heads(ao), prod, wide(flat.unsqueeze(2), [Q, 24, 16]), ALU.mult).then_inc(vector_done, 1)
                    dve.wait_ge(tensor_done, 5)
                    dve.tensor_copy(halves(xT[0:D, :]), two(0, D)).then_inc(vector_done, 1)
                    dve.wait_ge(tensor_done, 6)
                    link(dve.tensor_tensor(h[:, :, :], h[:, :, :], tiles(2), ALU.add))

                @block.scalar
                def _(act):
                    act.wait_ge(tensor_done, 3)
                    act.copy(halves(kT[:, :]), two(4, D)).then_inc(scalar_done, 1)
                    act.wait_ge(tensor_done, 4)
                    act.copy(v[:, :, :], tiles(3)).then_inc(scalar_done, 1)

                    def spread_out(r):
                        n = r // 16
                        if r % 16 == 0 and n >= 2:
                            act.wait_ge(best_ready, T * (n - 1))
                        act.wait_ge(spread, r + 1)
                        act.copy(halves(keys[:, n % 2, r % 16, :]), two(2 * (r % 2), Q)).then_inc(spread_copied, 1)

                    for r in range(16):
                        spread_out(r)
                    r = 16
                    for i, (n, t) in enumerate(units):
                        for _ in range(3 if n < 3 else 0):
                            if r < 16 * (n + 2):
                                spread_out(r)
                                r += 1
                        L = Q * (t + 1)
                        act.wait_ge(best_ready, i + 1)
                        if i >= 2:
                            act.wait_ge(turned, i - 1)
                        act.activation(weight[:, i % 2, 0:L], score[:, i % 2, 0:L], ACT.Exp,
                                       bias=neg_max[:, i % 2:i % 2 + 1]).then_inc(exp_ready, 1)
                        if i >= 1:
                            copy_turned(act, i - 1)
                    copy_turned(act, len(units) - 1)

                @block.tensor
                def _(pe):
                    pe.wait_ge(vector_done, 1)
                    turn(pe, 0, x).then_inc(tensor_done, 1)
                    pe.wait_ge(vector_done, 2)
                    xf = xT[0:D, :]
                    by_token(pe, 6, xf, w["l2a_q"][:, :]).then_inc(tensor_done, 1)
                    by_feature(pe, 4, w["l2a_k"][:, :], xf).then_inc(tensor_done, 1)
                    by_token(pe, 3, xf, w["l2a_v"][:, :]).then_inc(tensor_done, 1)
                    pe.wait_ge(scalar_done, 2)

                    def spread_in(r):
                        if r >= 2:
                            pe.wait_ge(spread_copied, r - 1)
                        for c in range(2):
                            mm = pe.matmul(ps[0:Q, 2 * (r % 2) + c, 0:HALF], wide(ident[0:D, r:r + 1], [D, Q]),
                                           kT[:, HALF * c:HALF * c + HALF], start=True, stop=True)
                        mm.then_inc(spread, 1)

                    for r in range(16):
                        spread_in(r)
                    r = 16
                    for i, (n, t) in enumerate(units):
                        for _ in range(3 if n < 3 else 0):
                            if r < 16 * (n + 2):
                                spread_in(r)
                                r += 1
                        if i >= 1:
                            turn_weights(pe, i - 1)
                    turn_weights(pe, len(units) - 1)
                    pe.wait_ge(vector_done, 4)
                    turn(pe, 0, ao).then_inc(tensor_done, 1)
                    pe.wait_ge(vector_done, 5)
                    by_token(pe, 2, xf, w["l2a_o"][:, :]).then_inc(tensor_done, 1)

        def layer3_attention():
            with Stage("l3a") as sg:
                tensor_done, vector_done, scalar_done, vchain = (
                    sg.sem(n) for n in ("tensor_step", "vector_step", "scalar_step", "vector_chain"))
                qT = sg.sb("qT", [D, S])
                kT = sg.sb("kT", [D, S])
                v = sg.sb("v", [Q, T, D])
                o = sg.sb("o", [Q, T, D])
                att = Attention(nc, sg.st, "l3a_att", ps, 1, D, False,
                                lambda m, t: qT[:, Q * t:Q * t + Q], lambda m, s, e: kT[:, s:e],
                                lambda m, k: v[:, k, :], lambda t: o[:, t:t + 1, :])
                sg.sems += att.sems
                block = sg.block()

                @block.sync
                def _(sp):
                    clear_previous(sp, sg.sems)

                @block.vector
                def _(dve):
                    link = Chain(dve, vchain)
                    layer_norm(dve, link, x[:, :, :], h[:, :, :], sq[:, :, :], st, 1e-5)
                    dve.sem_inc(vector_done, 1)
                    dve.wait_ge(tensor_done, 1)
                    dve.tensor_copy(halves(xT[0:D, :]), two(0, D)).then_inc(vector_done, 1)
                    dve.wait_ge(tensor_done, 3)
                    dve.tensor_copy(halves(kT[:, :]), two(4, D)).then_inc(vector_done, 1)
                    att.vector(dve, link)
                    dve.wait_ge(att.out_ready, T)
                    link(dve.tensor_tensor(h[:, :, :], h[:, :, :], o[:, :, :], ALU.add))

                @block.scalar
                def _(act):
                    act.wait_ge(tensor_done, 2)
                    act.mul(halves(qT[:, :]), two(2, D), 0.125).then_inc(scalar_done, 1)
                    act.wait_ge(tensor_done, 4)
                    act.copy(v[:, :, :], tiles(6)).then_inc(scalar_done, 1)
                    att.scalar(act)

                @block.tensor
                def _(pe):
                    pe.wait_ge(vector_done, 1)
                    turn(pe, 0, x).then_inc(tensor_done, 1)
                    pe.wait_ge(vector_done, 2)
                    by_feature(pe, 2, w["l3a_qkv"][:, 0:64], xT).then_inc(tensor_done, 1)
                    by_feature(pe, 4, w["l3a_qkv"][:, 64:128], xT).then_inc(tensor_done, 1)
                    by_token(pe, 6, xT, w["l3a_qkv"][:, 128:192]).then_inc(tensor_done, 1)
                    pe.wait_ge(vector_done, 3)
                    pe.wait_ge(scalar_done, 2)
                    att.tensor(pe, ident)

        def moe_layer(name, bias_row, router, w1, b1, w2, b2, soft):
            with Stage(name) as sg:
                tensor_done, vector_done, scalar_done, vchain = (
                    sg.sem(n) for n in ("tensor_step", "vector_step", "scalar_step", "vector_chain"))
                up_ready, hidden_ready, down_ready, added = (
                    sg.sem(n) for n in ("up_ready", "hidden_ready", "down_ready", "added"))
                logits = sg.sb("logits", [Q, T, 8])
                top = sg.sb("top", [Q, T, 8])
                index = sg.sb("index", [Q, T, 8], U32)
                where = sg.sb("where", [Q, T, 2])
                hot = sg.sb("hot", [Q, 2, T, 8])
                share = sg.sb("share", [Q, T, 8])
                shareT = sg.sb("shareT", [8, S])
                second = sg.sb("second", [Q, T])
                hidden = sg.sb("hidden", [128, 2, S])
                acc = sg.sb("acc", [Q, T, D])
                block = sg.block()

                @block.sync
                def _(sp):
                    clear_previous(sp, sg.sems)

                @block.vector
                def _(dve):
                    link = Chain(dve, vchain)
                    layer_norm(dve, link, x[:, :, :], h[:, :, :], sq[:, :, :], st, 1e-5)
                    if soft:
                        layer_norm(dve, link, y[:, :, :], x[:, :, :], sq[:, :, :], st, 1e-5)
                        affine(dve, link, y[:, :, :], per_tile(rows["l3f_g"]), per_tile(rows["l3f_b"]))
                    dve.sem_inc(vector_done, 1)
                    dve.wait_ge(tensor_done, 1)
                    dve.tensor_copy(halves(xT[0:D, :]), two(0, D)).then_inc(vector_done, 1)
                    dve.wait_ge(tensor_done, 2)
                    link(dve.tensor_tensor(logits[:, :, :], tiles(6, 8), per_tile(rows[bias_row]), ALU.add))
                    top_two(dve, link, logits, top, index, where, hot)
                    if soft:
                        link(dve.tensor_tensor(second[:, :], top[:, :, 1], top[:, :, 0], ALU.subtract))
                        dve.sem_inc(vector_done, 1)
                        dve.wait_ge(scalar_done, 1)
                        first = st[:, 0, 0:T]
                        link(dve.tensor_scalar(first, second[:, :], 1.0, None, ALU.add))
                        link(dve.reciprocal(first, first))
                        link(dve.tensor_tensor(second[:, :], second[:, :], first, ALU.mult))
                        for j, part in enumerate((first, second[:, :])):
                            link(dve.tensor_tensor(hot[:, j, :, :], hot[:, j, :, :], wide(part.unsqueeze(2), [Q, T, 8]), ALU.mult))
                    else:
                        dve.sem_inc(vector_done, 1)
                    link(dve.tensor_tensor(share[:, :, :], hot[:, 0, :, :], hot[:, 1, :, :], ALU.add))
                    dve.sem_inc(vector_done, 1)
                    for e in range(8):
                        dve.wait_ge(down_ready, e + 1)
                        wide_share = wide(share[:, :, e:e + 1], [Q, T, D])
                        if e == 0:
                            dve.tensor_tensor(acc[:, :, :], tiles(4), wide_share, ALU.mult).then_inc(added, 1)
                        else:
                            link(dve.tensor_tensor(sq[:, :, :], tiles(4 + e % 2), wide_share, ALU.mult))
                            dve.tensor_tensor(acc[:, :, :], acc[:, :, :], sq[:, :, :], ALU.add).then_inc(added, 1)
                        dve.wait_ge(added, e + 1)
                    dve.wait_ge(tensor_done, 3)
                    dve.tensor_copy(halves(shareT[:, :]), two(2, 8)).then_inc(vector_done, 1)
                    link(dve.tensor_tensor(h[:, :, :], h[:, :, :], acc[:, :, :], ALU.add))
                    dve.wait_ge(tensor_done, 4)
                    link(dve.tensor_tensor(h[:, :, :], h[:, :, :], tiles(7), ALU.add))

                @block.scalar
                def _(act):
                    if soft:
                        act.wait_ge(vector_done, 3)
                        act.activation(second[:, :], second[:, :], ACT.Exp).then_inc(scalar_done, 1)
                    for u in range(16):
                        e, n = u // 2, u % 2
                        act.wait_ge(up_ready, u + 1)
                        if e >= 2:
                            act.wait_ge(down_ready, e - 1)
                        act.activation(hidden[:, e % 2, HALF * n:HALF * n + HALF], ps[:, n, 0:HALF], ACT.Gelu,
                                       bias=b1[:, e:e + 1]).then_inc(hidden_ready, 1)

                @block.tensor
                def _(pe):
                    pe.wait_ge(vector_done, 1)
                    turn(pe, 0, y if soft else x).then_inc(tensor_done, 1)
                    pe.wait_ge(vector_done, 2)
                    by_token(pe, 6, xT[0:D, :], router[:, :]).then_inc(tensor_done, 1)

                    def down(e):
                        pe.wait_ge(hidden_ready, 2 * e + 2)
                        if e >= 2:
                            pe.wait_ge(added, e - 1)
                        by_token(pe, 4 + e % 2, hidden[:, e % 2, :], w2[:, e, :]).then_inc(down_ready, 1)

                    for u in range(16):
                        e, n = u // 2, u % 2
                        if u >= 2:
                            pe.wait_ge(hidden_ready, u - 1)
                        pe.matmul(ps[:, n, 0:HALF], w1[:, e, :], xT[0:D, HALF * n:HALF * n + HALF],
                                  start=True, stop=True).then_inc(up_ready, 1)
                        if n == 1 and e >= 1:
                            down(e - 1)
                    down(7)
                    pe.wait_ge(vector_done, 4)
                    turn(pe, 2, share, 8).then_inc(tensor_done, 1)
                    pe.wait_ge(vector_done, 5)
                    by_token(pe, 7, shareT, b2[:, :]).then_inc(tensor_done, 1)

        def row1(ap, n, p=Q):
            return wide(ap.rearrange("(a n) -> a n", a=1), [p, n])

        with Stage("load") as sg:
            loaded = sg.sem("loaded")
            zeroed = sg.sem("zeroed")
            tables_loaded = sg.sem("tables_loaded")
            block = sg.block()
            count = [0]

            @block.vector
            def _(dve):
                for n in ("l0f_qkv", "l0f_gate", "l0f_fc1", "l0f_fc2"):
                    dve.memset(w[n][:], 0.0).then_inc(zeroed, 1)
                dve.memset(ones[:, :], 1.0).then_inc(zeroed, 1)
                dve.memset(xT[D:D + 1, :], 1.0).then_inc(zeroed, 1)
                dve.memset(yT[D:D + 1, :], 1.0).then_inc(zeroed, 1)
                dve.wait_ge(tables_loaded, 48)
                dve.tensor_copy(ident16[:, :], ident[0:Q, 0:Q])
                dve.tensor_copy(mask16[:, :], causal[:, :])
                dve.tensor_scalar(mask16_t[:, :], keep[:, :], -1.0, -NEG, ALU.add, ALU.mult)

            @block.sync
            def _(sp):
                def load(dst, src):
                    sp.dma_start(dst, src).then_inc(loaded, 16)
                    count[0] += 16

                for dst, src in ((ident, "c_ident"), (causal, "c_causal"), (keep, "c_keep")):
                    sp.dma_start(dst[:, :], a[src]).then_inc(tables_loaded, 16)
                load(iota8[:, :], a["c_iota8"])
                load(cos_t[:, :, :], a["c_cos"])
                load(sin_t[:, :, :], a["c_sin"])
                load(strip[:, :], a["bias_strip"])
                load(att_scale[:, :], row1(a["L0_attn_scale"], 1))
                for n, src in (("l0a_g1", "L0_attn_ln1_g"), ("l0a_b1", "L0_attn_ln1_b"), ("l0a_g2", "L0_attn_ln2_g"),
                               ("l0a_b2", "L0_attn_ln2_b"), ("l1a_g1", "L1_attn_ln1_g"), ("l1a_b1", "L1_attn_ln1_b"),
                               ("l1a_g2", "L1_attn_ln2_g"), ("l1a_b2", "L1_attn_ln2_b"), ("l1f_w1", "L1_ffn_ln1_w"),
                               ("l1f_w2", "L1_ffn_ln2_w"), ("l3f_g", "L3_ffn_gamma"), ("l3f_b", "L3_ffn_beta"),
                               ("l0f_g", "L0_ffn_ln_g"), ("l0f_b", "L0_ffn_ln_b"), ("l0f_fg", "L0_ffn_fnorm_g"),
                               ("l0f_fb", "L0_ffn_fnorm_b"), ("l2f_bg", "L2_ffn_bg"), ("l3f_br", "L3_ffn_br")):
                    load(rows[n][:, :], row1(a[src], rows[n].shape[1]))
                load(rows["l0f_gate"][:, :], row1(a["L0_ffn_gate_b"].rearrange("n e -> (n e)"), 16))

                def with_bias(n, weight, bias):
                    load(w[n][0:D, :], weight)
                    load(w[n][D:D + 1, :], bias.rearrange("(a n) -> a n", a=1))

                with_bias("l0a_qkv", a["L0_attn_qkv_w"], a["L0_attn_qkv_b"])
                with_bias("l0a_proj", a["L0_attn_proj_w"], a["L0_attn_proj_b"])
                with_bias("l0f_hl", a["hl_wT"], a["L0_ffn_hl_b"].rearrange("n d -> (n d)"))
                with_bias("l1a_qkv", a["L1_attn_qkv_w"], a["L1_attn_qkv_b"])
                with_bias("l1a_proj", a["L1_attn_proj_w"], a["L1_attn_proj_b"])
                with_bias("l1a_w1", a["L1_attn_w1"], a["L1_attn_b1"])
                for j, n in enumerate("qkv"):
                    load(w["l3a_qkv"][0:D, 64 * j:64 * j + 64], a["L3_attn_W" + n])
                    load(w["l3a_qkv"][D:D + 1, 64 * j:64 * j + 64], a["L3_attn_b" + n].rearrange("(a n) -> a n", a=1))
                load(w["l1a_w2"][:, :, :], a["L1_attn_w2"].rearrange("(c p) n -> p c n", p=128))
                load(w["l1a_b2"][:, :], a["L1_attn_b2"].rearrange("(a n) -> a n", a=1))
                load(w["l1f_qkv"][:, 0:64], a["l1_wqT"])
                load(w["l1f_qkv"][:, 64:96], a["l1_wkT"])
                load(w["l1f_qkv"][:, 96:128], a["l1_wvT"])
                load(w["l1f_wo"][:, :], a["l1_woT"])
                load(w["l1f_router"][:, :], a["l1_routerT"])
                load(w["l1f_w1"][:, :, :], a["l1_w1T"])
                load(w["l1f_w3"][:, :, :], a["l1_w3T"])
                load(w["l1f_w2"][:, :, :, :], a["l1_w2T"].rearrange("e (c p) n -> p e c n", p=HP))
                for n in "qkvo":
                    load(w["l2a_" + n][:, :], a["l2_w%sT" % n])
                load(w["l2f_g"][:, :], a["L2_ffn_Wg"])
                load(w["l3f_r"][:, :], a["L3_ffn_Wr"])
                for l in "23":
                    load(w[f"l{l}f_w1"][:, :, :], a[f"L{l}_ffn_W1"].rearrange("e d h -> d e h"))
                    load(w[f"l{l}f_w2"][:, :, :], a[f"L{l}_ffn_W2"].rearrange("e h d -> h e d"))
                    load(w[f"l{l}f_b2"][:, :], a[f"L{l}_ffn_b2"])
                    load(w[f"l{l}f_b1"][:, :], a[f"l{l}_b1T"])
                sp.wait_ge(zeroed, 7)
                for n in range(4):
                    r = slice(16 * n, 16 * n + 16)
                    load(w["l0f_qkv"][r, 64 * n:64 * n + 64], a["l0_wqT"][n].rearrange("d e o -> d (e o)"))
                    load(w["l0f_qkv"][r, 256 + 16 * n:272 + 16 * n], a["l0_wkT"][n])
                    load(w["l0f_qkv"][r, 320 + 16 * n:336 + 16 * n], a["l0_wvT"][n])
                    load(w["l0f_gate"][64 * (n % 2):64 * (n % 2) + 64, n // 2, 4 * (n % 2):4 * (n % 2) + 4],
                         a["l0_gateT"][n])
                    load(w["l0f_fc1"][r, r], a["l0_fc1T"])
                    load(w["l0f_fc2"][r, r], a["l0_fc2T"])
                    load(w["l0f_fc1"][D:D + 1, r], a["L0_ffn_fc1_b"].rearrange("(a n) -> a n", a=1))
                    load(w["l0f_fc2"][D:D + 1, r], a["L0_ffn_fc2_b"].rearrange("(a n) -> a n", a=1))
                load(w["l0f_fgate"][:, :], a["l0_fgateT"])
                sp.wait_ge(loaded, count[0])

        fourier(nc, a, ps, ident, h_in, Stage, clear_previous, end_of_pass)
        text(nc, a, ps, ident, h_in, Stage, clear_previous)
        if upto == 0:
            return dump(nc, Stage, clear_previous, h_in, out)

        with nc.Fori(0, B) as b:
            with Stage("l0a") as sg:
                loaded = sg.sem("h_loaded")
                tensor_done = sg.sem("tensor_step")
                vector_done = sg.sem("vector_step")
                scalar_done = sg.sem("scalar_step")
                vchain = sg.sem("vector_chain")
                stored = sg.sem("stored")
                qT = sg.sb("qT", [D, S])
                kT = sg.sb("kT", [D, S])
                v = sg.sb("v", [Q, T, D])
                o = sg.sb("o", [Q, T, D])
                att = Attention(nc, sg.st, "l0a_att", ps, 1, D, False,
                                lambda m, t: qT[:, Q * t:Q * t + Q], lambda m, s, e: kT[:, s:e],
                                lambda m, k: v[:, k, :], lambda t: o[:, t:t + 1, :],
                                strip=lambda t: strip[:, S - Q - Q * t:S - Q - Q * t + S])
                sg.sems += att.sems
                block = sg.block()

                @block.sync
                def _(sp):
                    clear_previous(sp, sg.sems)
                    sp.dma_start(h[:, :, :], tokens(h_in, b)).then_inc(loaded, 16)
                    sp.wait_ge(vector_done, 6)
                    sp.dma_start(tokens(h_mid, b), h[:, :, :]).then_inc(stored, 16)
                    sp.wait_ge(vector_done, 9)
                    sp.dma_start(tokens(sx_all, b), y[:, :, :]).then_inc(stored, 16)
                    sp.wait_ge(stored, 32)

                @block.vector
                def _(dve):
                    link = Chain(dve, vchain)
                    dve.wait_ge(loaded, 16)
                    layer_norm(dve, link, x[:, :, :], h[:, :, :], sq[:, :, :], st, 1e-5)
                    layer_norm(dve, link, y[:, :, :], x[:, :, :], sq[:, :, :], st, 1e-5)
                    link(dve.tensor_tensor(y[:, :, :], y[:, :, :], wide(rows["l0a_g1"][:, :].unsqueeze(1), [Q, T, D]), ALU.mult))
                    dve.tensor_tensor(y[:, :, :], y[:, :, :], wide(rows["l0a_b1"][:, :].unsqueeze(1), [Q, T, D]),
                                      ALU.add).then_inc(vector_done, 1)
                    dve.wait_ge(tensor_done, 1)
                    dve.tensor_copy(halves(xT[0:D, :]), two(0, D)).then_inc(vector_done, 1)
                    dve.wait_ge(tensor_done, 3)
                    dve.tensor_copy(halves(kT[:, :]), two(4, D)).then_inc(vector_done, 1)
                    att.vector(dve, link)
                    dve.wait_ge(att.out_ready, T)
                    dve.wait_ge(tensor_done, 5)
                    dve.tensor_copy(halves(yT[0:D, :]), two(0, D)).then_inc(vector_done, 1)
                    dve.wait_ge(tensor_done, 6)
                    link(dve.tensor_scalar(y[:, :, :], tiles(2), 1.0, None, ALU.mult))
                    layer_norm(dve, link, x[:, :, :], y[:, :, :], sq[:, :, :], st, 1e-5)
                    link(dve.tensor_tensor(x[:, :, :], x[:, :, :], wide(rows["l0a_g2"][:, :].unsqueeze(1), [Q, T, D]), ALU.mult))
                    link(dve.tensor_tensor(x[:, :, :], x[:, :, :], wide(rows["l0a_b2"][:, :].unsqueeze(1), [Q, T, D]), ALU.add))
                    link(dve.tensor_tensor(h[:, :, :], h[:, :, :], x[:, :, :], ALU.add))
                    dve.sem_inc(vector_done, 2)
                    layer_norm(dve, link, x[:, :, :], h[:, :, :], sq[:, :, :], st, 1e-5)
                    dve.sem_inc(vector_done, 1)
                    dve.wait_ge(tensor_done, 7)
                    dve.tensor_copy(halves(xT[0:D, :]), two(4, D)).then_inc(vector_done, 1)
                    dve.wait_ge(tensor_done, 8)
                    dve.tensor_copy(y[:, :, :], tiles(6)).then_inc(vector_done, 1)

                @block.scalar
                def _(act):
                    act.wait_ge(tensor_done, 2)
                    act.copy(halves(qT[:, :]), two(2, D)).then_inc(scalar_done, 1)
                    act.wait_ge(tensor_done, 4)
                    act.activation(v[:, :, :], tiles(6), ACT.Copy, scale=att_scale[:, :]).then_inc(scalar_done, 1)
                    att.scalar(act)

                @block.tensor
                def _(pe):
                    pe.wait_ge(vector_done, 1)
                    turn(pe, 0, y).then_inc(tensor_done, 1)
                    pe.wait_ge(vector_done, 2)
                    by_feature(pe, 2, w["l0a_qkv"][:, 0:64], xT).then_inc(tensor_done, 1)
                    by_feature(pe, 4, w["l0a_qkv"][:, 64:128], xT).then_inc(tensor_done, 1)
                    by_token(pe, 6, xT, w["l0a_qkv"][:, 128:192]).then_inc(tensor_done, 1)
                    pe.wait_ge(vector_done, 3)
                    pe.wait_ge(scalar_done, 2)
                    att.tensor(pe, ident)
                    pe.wait_ge(att.out_ready, T)
                    turn(pe, 0, o).then_inc(tensor_done, 1)
                    pe.wait_ge(vector_done, 4)
                    by_token(pe, 2, yT, w["l0a_proj"][:, :]).then_inc(tensor_done, 1)
                    pe.wait_ge(vector_done, 7)
                    turn(pe, 4, x).then_inc(tensor_done, 1)
                    pe.wait_ge(vector_done, 8)
                    by_token(pe, 6, xT, w["l0f_hl"][:, :]).then_inc(tensor_done, 1)

            end_of_pass("l0a_end")

        if upto == 1:
            return dump(nc, Stage, clear_previous, h_mid, out)
        if upto == 2:
            return dump(nc, Stage, clear_previous, sx_all, out)

        with Stage("resid") as sg:
            loaded = sg.sem("loaded")
            block = sg.block()

            @block.sync
            def _(sp):
                clear_previous(sp, sg.sems)
                for n in range(4):
                    sp.dma_start(resid[:, :, 16 * n:16 * n + 16],
                                 sx_all[n].rearrange("(t p) d -> p t d", p=Q)[:, :, 16 * n:16 * n + 16]).then_inc(loaded, 16)
                sp.wait_ge(loaded, 64)

        with nc.Fori(0, B) as b:
            layer0_ffn(b)
            if upto >= 4:
                layer1_attention()
            if upto >= 5:
                layer1_ffn()
            if upto >= 6:
                layer2_attention()
            if upto >= 7:
                moe_layer("l2f", "l2f_bg", w["l2f_g"], w["l2f_w1"], w["l2f_b1"], w["l2f_w2"], w["l2f_b2"], False)
            if upto >= 8:
                layer3_attention()
            if upto >= 9:
                moe_layer("l3f", "l3f_br", w["l3f_r"], w["l3f_w1"], w["l3f_b1"], w["l3f_w2"], w["l3f_b2"], True)
            with Stage("store") as sg:
                stored = sg.sem("stored")
                block = sg.block()

                @block.sync
                def _(sp):
                    clear_previous(sp, sg.sems)
                    sp.dma_start(tokens(out, b), h[:, :, :]).then_inc(stored, 16)
                    sp.wait_ge(stored, 16)

            end_of_pass("pass_end")


def tokens(dram, b):
    return dram[bass.ds(b, 1)].rearrange("a (t p) n -> p (a t) n", p=Q)


def dump(nc, Stage, clear_previous, src, out):
    with Stage("dump") as sg:
        done = sg.sem("done")
        block = sg.block()

        @block.sync
        def _(sp):
            sp.dma_start(out, src).then_inc(done, 16)
            sp.wait_ge(done, 16)


def fourier(nc, a, ps, ident, h_in, Stage, clear_previous, end_of_pass):
    NX = G // 2
    with ExitStack() as keepers:
        def sb(name, shape, dt=F32):
            return keepers.enter_context(nc.sbuf_tensor("fno_" + name, shape, dt))

        field = sb("field", [128, NX, 128])
        y_fwd = sb("y_fwd", [128, 48])
        x_fwd = sb("x_fwd", [128, 48])
        x_inv = sb("x_inv", [48, 128])
        y_inv = sb("y_inv", [96, 256])
        feats = sb("feats", [7, G * G])
        lift = sb("lift", [7, 128])
        mixw = sb("mixw", [128, C, 144])
        w1T = sb("w1T", [C, C])
        w2bd = sb("w2bd", [128, 128])
        b1 = sb("b1", [128, 1])
        b2row = sb("b2row", [128, 128])
        by_y = sb("by_y", [128, 24, G])
        by_yT = sb("by_yT", [128, KY, 128])
        modes = sb("modes", [128, B, KY, 2, 6])
        modes_i = sb("modes_i", [128, B, KY, 2, 6])
        mixed = sb("mixed", [C, B, KY, 2, KX])
        convd = sb("convd", [48, KY, 128])
        by_x = sb("by_x", [128, G, 24])
        by_xT = sb("by_xT", [96, 16, 128])
        act_g = sb("act_g", [128, G * G])
        q1 = sb("q1", [128, 16])
        q2 = sb("q2", [16, 4])
        q1b = sb("q1b", [16, 1])
        q2b = sb("q2b", [4, 1])

        with Stage("lift") as sg:
            loaded = sg.sem("loaded")
            zeroed = sg.sem("zeroed")
            lifted = sg.sem("lifted")
            block = sg.block()

            @block.vector
            def _(pool):
                pool.memset(lift[:, :], 0.0).then_inc(zeroed, 1)
                pool.memset(w2bd[:, :], 0.0).then_inc(zeroed, 1)
                pool.memset(q1[:, :], 0.0).then_inc(zeroed, 1)
                pool.memset(q2[:, :], 0.0).then_inc(zeroed, 1)

            @block.sync
            def _(sp):
                clear_previous(sp, sg.sems)
                n = 0
                for dst, src in ((y_fwd[:, :], a["c_y_fwd"]), (x_fwd[:, :], a["c_x_fwd"]), (x_inv[:, :], a["c_x_inv"]),
                                 (y_inv[:, :], a["c_y_inv"]), (feats[0:B, :], a["x"].rearrange("b x y a -> b (x y a)")),
                                 (feats[B:7, :], a["c_grid"])):
                    sp.dma_start(dst, src).then_inc(loaded, 16)
                    n += 16
                sp.wait_ge(zeroed, 4)
                for b in range(B):
                    cs = slice(C * b, C * b + C)
                    pairs = [(lift[b:b + 1, cs], a["p_wT"][0:1, :]), (lift[4:6, cs], a["p_wT"][1:3, :]),
                             (lift[6:7, cs], a["L0_tok_p_b"].rearrange("(a n) -> a n", a=1)),
                             (q1[cs, 4 * b:4 * b + 4], a["q1_T"]), (q2[4 * b:4 * b + 4, b:b + 1], a["q2_T"]),
                             (q1b[4 * b:4 * b + 4, :], a["L0_tok_q1_b"].rearrange("(n a) -> n a", a=1)),
                             (q2b[b:b + 1, :], a["L0_tok_q2_b"].rearrange("(n a) -> n a", a=1))]
                    for dst, src in pairs:
                        sp.dma_start(dst, src).then_inc(loaded, 16)
                        n += 16
                assert n == 16 * 34
                sp.wait_ge(loaded, n)

            @block.tensor
            def _(pe):
                pe.wait_ge(loaded, 16 * 34)
                for i in range(NX):
                    mm = pe.matmul(ps[:, i // 4, 128 * (i % 4):128 * (i % 4) + 128], feats[:, 128 * i:128 * i + 128],
                                   lift[:, :], start=True, stop=True)
                    if i % 4 == 3:
                        mm.then_inc(lifted, 1)

            @block.vector
            def _(dve):
                for k in range(8):
                    dve.wait_ge(lifted, k + 1)
                    dve.tensor_copy(field[:, 4 * k:4 * k + 4, :].rearrange("p a n -> p (a n)"), ps[:, k, :])

        with nc.Fori(0, 4) as layer:
            with Stage("fno") as sg:
                loaded = sg.sem("weights_loaded")
                names = ("y_step", "y_turned", "x_step", "mix", "conv", "x_back", "x_turned", "y_back", "conv2")
                did = {n: sg.sem("tensor_" + n) for n in names}
                got_v = {n: sg.sem("vector_" + n) for n in names}
                got_s = {n: sg.sem("scalar_" + n) for n in names}
                vchain = sg.sem("vector_chain")
                block = sg.block()

                @block.sync
                def _(sp):
                    clear_previous(sp, sg.sems)
                    fw = a["L0_tok_fw"][bass.ds(layer, 1)]
                    for g in range(4):
                        hh, kh = g // 2, g % 2
                        src = fw[0:1, hh].rearrange("l i o x y c -> (l i) o (x y c)")[:, :, 144 * kh:144 * kh + 144]
                        sp.dma_start(mixw[C * g:C * g + C, :, :], src).then_inc(loaded, 16)
                    w1 = a["w1_T"][bass.ds(layer, 1)].rearrange("l i o -> (l i) o")
                    w2 = a["w2_T"][bass.ds(layer, 1)].rearrange("l i o -> (l i) o")
                    sp.dma_start(w1T[:, :], w1).then_inc(loaded, 16)
                    for b in range(B):
                        cs = slice(C * b, C * b + C)
                        sp.dma_start(w2bd[cs, cs], w2).then_inc(loaded, 16)
                        sp.dma_start(b1[cs, :], a["L0_tok_w1_b"][bass.ds(layer, 1)].rearrange("l n -> n l")).then_inc(loaded, 16)
                        sp.dma_start(b2row[:, cs], wide(a["L0_tok_w2_b"][bass.ds(layer, 1)], [128, C])).then_inc(loaded, 16)
                    sp.wait_ge(loaded, 16 * 17)

                @block.tensor
                def _(pe):
                    for i in range(NX):
                        mm = pe.matmul(ps[:, i // 8, 48 * (i % 8):48 * (i % 8) + 48], field[:, i, :], y_fwd[:, :],
                                       start=True, stop=True)
                        if i % 8 == 7:
                            mm.then_inc(did["y_step"], 1)
                    pe.wait_ge(got_v["y_step"], 2)
                    pe.wait_ge(got_s["y_step"], 2)
                    for k in range(KY):
                        mm = pe.transpose(ps[:, 4 + k // 4, 128 * (k % 4):128 * (k % 4) + 128],
                                          by_y[:, 2 * k:2 * k + 2, :].rearrange("p c x -> p (c x)"), ident[:, :])
                        if k % 4 == 3:
                            mm.then_inc(did["y_turned"], 1)
                    pe.wait_ge(got_v["y_turned"], 2)
                    pe.wait_ge(got_s["y_turned"], 1)
                    for k in range(KY):
                        mm = pe.matmul(ps[:, k // 6, 48 * (k % 6):48 * (k % 6) + 48], by_yT[:, k, :], x_fwd[:, :],
                                       start=True, stop=True)
                    mm.then_inc(did["x_step"], 1)
                    pe.wait_ge(got_v["x_step"], 3)
                    pe.wait_ge(loaded, 16 * 17)
                    for m in range(72):
                        for g in range(4):
                            j, ky = m // KY, m % KY
                            p = slice(C * g, C * g + C)
                            col = 8 * ((j % 3) * KY + ky)
                            dst = ps[p, 2 * g + j // 3, col:col + 8]
                            for c, src in enumerate((modes, modes_i)):
                                mm = pe.matmul(dst, mixw[p, :, 2 * m + c], src[p, :, ky, :, j].rearrange("p b c -> p c b"),
                                               start=(c == 0), stop=(c == 1), tile_position=(C * g, C * g))
                        if m % 36 == 35:
                            mm.then_inc(did["mix"], 1)
                    pe.wait_ge(got_v["mix"], 8)
                    for ky in range(KY):
                        for b in range(B):
                            mm = pe.matmul(ps[0:48, ky // 4, 128 * (ky % 4) + C * b:128 * (ky % 4) + C * b + C],
                                           mixed[:, b, ky, :, :].rearrange("p c k -> p (c k)"), w1T[:, :],
                                           start=True, stop=True)
                    mm.then_inc(did["conv"], 1)
                    pe.wait_ge(got_v["conv"], 1)
                    pe.wait_ge(got_s["conv"], 2)
                    for ky in range(KY):
                        mm = pe.matmul(ps[:, 3 + ky // 4, 128 * (ky % 4):128 * (ky % 4) + 128], convd[:, ky, :],
                                       x_inv[:, :], start=True, stop=True)
                        if ky % 4 == 3:
                            mm.then_inc(did["x_back"], 1)
                    pe.wait_ge(got_v["x_back"], 2)
                    pe.wait_ge(got_s["x_back"], 1)
                    for i in range(16):
                        mm = pe.transpose(ps[0:96, i // 4, 128 * (i % 4):128 * (i % 4) + 128],
                                          by_x[:, 4 * i:4 * i + 4, :].rearrange("p x k -> p (x k)"), ident[:, :])
                        if i % 4 == 3:
                            mm.then_inc(did["x_turned"], 1)
                    pe.wait_ge(got_v["x_turned"], 2)
                    pe.wait_ge(got_s["x_turned"], 2)
                    for i in range(16):
                        mm = pe.matmul(ps[:, i // 2, 256 * (i % 2):256 * (i % 2) + 256], by_xT[:, i, :], y_inv[:, :],
                                       start=True, stop=True)
                        if i % 2:
                            mm.then_inc(did["y_back"], 1)
                    for i in range(NX):
                        if i % 4 == 0:
                            pe.wait_ge(got_s["y_back"], i // 4 + 1)
                        mm = pe.matmul(ps[:, i // 4, 128 * (i % 4):128 * (i % 4) + 128], act_g[:, 128 * i:128 * i + 128],
                                       w2bd[:, :], start=True, stop=True)
                        if i % 4 == 3:
                            mm.then_inc(did["conv2"], 1)

                def y_out(k):
                    return (by_y[:, :, 16 * k:16 * k + 16].rearrange("p k x -> p x k"),
                            ps[:, k, 0:384].rearrange("p (x k) -> p x k", k=24))

                def x_out(k):
                    return (by_x[:, :, 8 * k:8 * k + 8].rearrange("p x (k c) -> p k c x", c=2),
                            ps[:, 3 + k, :].rearrange("p (k c x) -> p k c x", k=4, c=2))

                @block.scalar
                def _(act):
                    for k in (1, 3):
                        act.wait_ge(did["y_step"], k + 1)
                        act.copy(*y_out(k)).then_inc(got_s["y_step"], 1)
                    act.wait_ge(did["y_turned"], 2)
                    act.copy(by_yT[:, 4:8, :].rearrange("p a n -> p (a n)"), ps[:, 5, :]).then_inc(got_s["y_turned"], 1)
                    act.wait_ge(did["conv"], 1)
                    for k in (0, 1):
                        act.copy(convd[:, 4 * k:4 * k + 4, :].rearrange("p a n -> p (a n)"), ps[0:48, k, :])\
                           .then_inc(got_s["conv"], 1)
                    act.wait_ge(did["x_back"], 2)
                    act.copy(*x_out(1)).then_inc(got_s["x_back"], 1)
                    for k in (1, 3):
                        act.wait_ge(did["x_turned"], k + 1)
                        act.copy(by_xT[:, 4 * k:4 * k + 4, :].rearrange("p a n -> p (a n)"), ps[0:96, k, :])\
                           .then_inc(got_s["x_turned"], 1)
                    for k in range(8):
                        act.wait_ge(did["y_back"], k + 1)
                        act.activation(act_g[:, 512 * k:512 * k + 512], ps[:, k, :], ACT.Relu, bias=b1[:, :])\
                           .then_inc(got_s["y_back"], 1)

                @block.vector
                def _(dve):
                    link = Chain(dve, vchain)
                    for k in (0, 2):
                        dve.wait_ge(did["y_step"], k + 1)
                        dve.tensor_copy(*y_out(k)).then_inc(got_v["y_step"], 1)
                    for k in (0, 2):
                        dve.wait_ge(did["y_turned"], k + 1)
                        dve.tensor_copy(by_yT[:, 4 * k:4 * k + 4, :].rearrange("p a n -> p (a n)"), ps[:, 4 + k, :])\
                           .then_inc(got_v["y_turned"], 1)
                    dve.wait_ge(did["x_step"], 1)
                    for g in range(4):
                        for b in range(B):
                            for k in range(2):
                                src = ps[C * b:C * b + C, k, 0:288].rearrange("p (y c k) -> p y c k", y=6, c=2)
                                ins = dve.tensor_copy(modes[C * g:C * g + C, b, 6 * k:6 * k + 6, :, :],
                                                      src[:, :, :, 6 * g:6 * g + 6])
                    link(ins)
                    dve.sem_inc(got_v["x_step"], 1)
                    flat = modes[:, :, :, :, :].rearrange("p b y c k -> p (b y) c k")
                    flat_i = modes_i[:, :, :, :, :].rearrange("p b y c k -> p (b y) c k")
                    dve.tensor_scalar(flat_i[:, :, 0, :], flat[:, :, 1, :], -1.0, None, ALU.mult).then_inc(got_v["x_step"], 1)
                    dve.tensor_copy(flat_i[:, :, 1, :], flat[:, :, 0, :]).then_inc(got_v["x_step"], 1)
                    for j3 in range(2):
                        dve.wait_ge(did["mix"], j3 + 1)
                        for g in range(4):
                            k0 = 6 * g + 3 * j3
                            for b in range(B):
                                src = ps[C * g:C * g + C, 2 * g + j3, 0:288].rearrange("p (j y c b) -> p j (y c) b", j=3, y=KY, c=2)
                                dst = mixed[:, b, :, :, k0:k0 + 3].rearrange("p y c j -> p j (y c)")
                                ins = dve.tensor_copy(dst, src[:, :, :, b])
                            ins.then_inc(got_v["mix"], 1)
                    dve.wait_ge(did["conv"], 1)
                    dve.tensor_copy(convd[:, 8:12, :].rearrange("p a n -> p (a n)"), ps[0:48, 2, :]).then_inc(got_v["conv"], 1)
                    for k in (0, 2):
                        dve.wait_ge(did["x_back"], k + 1)
                        dve.tensor_copy(*x_out(k)).then_inc(got_v["x_back"], 1)
                    for k in (0, 2):
                        dve.wait_ge(did["x_turned"], k + 1)
                        dve.tensor_copy(by_xT[:, 4 * k:4 * k + 4, :].rearrange("p a n -> p (a n)"), ps[0:96, k, :])\
                           .then_inc(got_v["x_turned"], 1)
                    for k in range(8):
                        dve.wait_ge(did["conv2"], k + 1)
                        part = field[:, 4 * k:4 * k + 4, :]
                        link(dve.tensor_tensor(part, part, ps[:, k, :].rearrange("p (a n) -> p a n", a=4), ALU.add))
                        dve.tensor_tensor(part, part, wide(b2row[:, :].unsqueeze(1), [128, 4, 128]), ALU.add)

            end_of_pass("fno_end")

        with Stage("img") as sg:
            turned, copied, read, acted, done, fin = (sg.sem(n) for n in
                                                      ("turned", "copied", "read_out", "acted", "second", "final"))
            stored = sg.sem("stored")
            res = sg.sb("res", [B, G * G])
            hidden = sg.sb("hidden", [16, G * G])
            block = sg.block()

            @block.sync
            def _(sp):
                clear_previous(sp, sg.sems)
                sp.wait_ge(fin, 8)
                sp.dma_start(h_in[:, 0:IMG, :].rearrange("b x y -> b (x y)"), res[:, :]).then_inc(stored, 16)
                sp.wait_ge(stored, 16)

            @block.tensor
            def _(pe):
                for i in range(NX):
                    mm = pe.transpose(ps[:, i // 4, 128 * (i % 4):128 * (i % 4) + 128], field[:, i, :], ident[:, :])
                    if i % 4 == 3:
                        mm.then_inc(turned, 1)
                for k in range(8):
                    pe.wait_ge(copied, k + 1)
                    pe.matmul(ps[0:16, k, :], q1[:, :], act_g[:, 512 * k:512 * k + 512], start=True, stop=True)\
                      .then_inc(read, 1)
                for k in range(8):
                    pe.wait_ge(acted, k + 1)
                    pe.matmul(ps[0:4, k, :], q2[:, :], hidden[:, 512 * k:512 * k + 512], start=True, stop=True)\
                      .then_inc(done, 1)

            @block.vector
            def _(dve):
                for k in range(8):
                    dve.wait_ge(turned, k + 1)
                    dve.tensor_copy(act_g[:, 512 * k:512 * k + 512], ps[:, k, :]).then_inc(copied, 1)
                for k in range(8):
                    dve.wait_ge(done, k + 1)
                    dve.tensor_scalar(res[:, 512 * k:512 * k + 512], ps[0:4, k, :], q2b[:, :], None, ALU.add)\
                       .then_inc(fin, 1)

            @block.scalar
            def _(act):
                for k in range(8):
                    act.wait_ge(read, k + 1)
                    act.activation(hidden[:, 512 * k:512 * k + 512], ps[0:16, k, :], ACT.Relu, bias=q1b[:, :])\
                       .then_inc(acted, 1)


def text(nc, a, ps, ident, h_in, Stage, clear_previous):
    N = 16
    with Stage("txt") as sg:
        ids = sg.sb("ids", [128, N], I32)
        base = sg.sb("base", [128, N, 4])
        mag = sg.sb("mag", [128, N, 4])
        whole_i = sg.sb("whole_i", [128, N, 4], I32)
        whole = sg.sb("whole", [128, N, 4])
        over = sg.sb("over", [128, N, 4])
        powers = sg.sb("powers", [128, N, 4, 5])
        powT = sg.sb("powT", [20, N, 128])
        coef = sg.sb("coef", [20, D])
        emb = sg.sb("emb", [128, N, D])
        loaded, gathered, ready, turned, copied, made, stored, vchain, emb_done = (sg.sem(n) for n in (
            "loaded", "gathered", "powers_ready", "turned", "copied", "made", "stored", "vector_chain", "emb_done"))
        block = sg.block()

        @block.sync
        def _(sp):
            clear_previous(sp, sg.sems)
            sp.dma_start(ids[:, :], a["x_txt"].rearrange("b (q n) -> (b q) n", n=N)).then_inc(loaded, 16)
            sp.dma_start(coef[:, :], a["L0_txt_poly_coeffs"].rearrange("t d o -> (t d) o")).then_inc(loaded, 16)
            sp.wait_ge(emb_done, 2)
            for b in range(B):
                sp.dma_start(h_in[b, IMG:S, :].rearrange("(q n) d -> q n d", n=N), emb[32 * b:32 * b + 32, :, :])\
                  .then_inc(stored, 16)
            sp.wait_ge(stored, 16 * B)

        @block.gpsimd
        def _(pool):
            pool.wait_ge(loaded, 32)
            for n in range(N):
                pool.indirect_dma_start(base[:, n, :], None, a["L0_txt_turns"],
                                        bass.IndirectOffsetOnAxis(ap=ids[:, n:n + 1], axis=0)).then_inc(gathered, 16)

        @block.vector
        def _(dve):
            link = Chain(dve, vchain)
            dve.wait_ge(gathered, 16 * N)
            flat = lambda t: t[:, :, :].rearrange("p n t -> p (n t)")
            link(dve.tensor_scalar(flat(mag), flat(base), -1.0, None, ALU.mult))
            link(dve.tensor_tensor(flat(mag), flat(mag), flat(base), ALU.max))
            link(dve.tensor_copy(flat(whole_i), flat(mag)))
            link(dve.tensor_copy(flat(whole), flat(whole_i)))
            link(dve.tensor_tensor(flat(over), flat(whole), flat(mag), ALU.is_gt))
            link(dve.tensor_tensor(flat(whole), flat(whole), flat(over), ALU.subtract))
            link(dve.tensor_scalar(flat(over), flat(base), 0.0, 2.0, ALU.is_ge, ALU.mult))
            link(dve.scalar_tensor_tensor(flat(whole), flat(over), -1.0, flat(whole), ALU.add, ALU.mult))
            pw = powers[:, :, :, :].rearrange("p n t d -> p (n t) d")
            link(dve.memset(pw[:, :, 0], 1.0))
            link(dve.tensor_copy(pw[:, :, 1], flat(whole)))
            for d in range(2, 5):
                ins = dve.tensor_tensor(pw[:, :, d], pw[:, :, d - 1], flat(whole), ALU.mult)
                link(ins)
            dve.sem_inc(ready, 1)
            for k in range(4):
                dve.wait_ge(turned, k + 1)
                dve.tensor_copy(powT[:, 4 * k:4 * k + 4, :].rearrange("p a n -> p (a n)"), ps[0:20, k, :]).then_inc(copied, 1)
            for k in range(2):
                dve.wait_ge(made, k + 1)
                dve.tensor_copy(emb[:, 8 * k:8 * k + 8, :].rearrange("p a n -> p (a n)"), ps[:, 4 + k, :]).then_inc(emb_done, 1)

        @block.tensor
        def _(pe):
            pe.wait_ge(ready, 1)
            for n in range(N):
                mm = pe.transpose(ps[0:20, n // 4, 128 * (n % 4):128 * (n % 4) + 128],
                                  powers[:, n, :, :].rearrange("p t d -> p (t d)"), ident[:, :])
                if n % 4 == 3:
                    mm.then_inc(turned, 1)
            pe.wait_ge(loaded, 32)
            for n in range(N):
                pe.wait_ge(copied, n // 4 + 1)
                mm = pe.matmul(ps[:, 4 + n // 8, D * (n % 8):D * (n % 8) + D], powT[:, n, :], coef[:, :],
                               start=True, stop=True)
                if n % 8 == 7:
                    mm.then_inc(made, 1)


def tables():
    f = np.float32
    t = {"c_ident": np.eye(128, dtype=f)}
    r = np.arange(Q)
    t["c_causal"] = np.where(r[None, :] > r[:, None], f(NEG), f(0)).astype(f)
    t["c_keep"] = (r[None, :] >= r[:, None]).astype(f)
    t["c_iota8"] = np.tile(np.arange(8, dtype=f), (Q, 1))
    inv = 1.0 / 10000.0 ** (np.arange(0, 16, 2, dtype=f) / 16)
    fr = np.outer(np.arange(S, dtype=f), inv)
    t["c_cos"] = np.ascontiguousarray(np.cos(fr).astype(f).reshape(T, Q, 8).transpose(1, 0, 2))
    t["c_sin"] = np.ascontiguousarray(np.sin(fr).astype(f).reshape(T, Q, 8).transpose(1, 0, 2))
    xs = np.arange(G)
    ky = np.arange(KY)
    kx = np.concatenate([np.arange(12), np.arange(G - 12, G)])
    ty = 2 * np.pi * ((xs[:, None] * ky[None, :]) % G) / G
    tx = 2 * np.pi * ((xs[:, None] * kx[None, :]) % G) / G
    yf = np.zeros((2, G, 2, KY, 2))
    for p in range(2):
        yf[p, :, p, :, 0], yf[p, :, p, :, 1] = np.cos(ty), -np.sin(ty)
    t["c_y_fwd"] = yf.reshape(128, 48).astype(f)
    xf = np.zeros((2, G, 2, KX))
    xf[0, :, 0], xf[0, :, 1], xf[1, :, 0], xf[1, :, 1] = np.cos(tx), -np.sin(tx), np.sin(tx), np.cos(tx)
    t["c_x_fwd"] = (xf.reshape(128, 48) / G).astype(f)
    xi = np.zeros((2, KX, 2, G))
    xi[0, :, 0], xi[0, :, 1], xi[1, :, 0], xi[1, :, 1] = np.cos(tx).T, np.sin(tx).T, -np.sin(tx).T, np.cos(tx).T
    t["c_x_inv"] = xi.reshape(48, 128).astype(f)
    c = np.where(ky == 0, 1.0, 2.0)[:, None] / G
    yi = np.zeros((4, KY, 2, 4, G))
    for p in range(4):
        yi[p, :, 0, p], yi[p, :, 1, p] = c * np.cos(ty).T, -c * np.sin(ty).T
    t["c_y_inv"] = yi.reshape(96, 256).astype(f)
    lin = np.linspace(0.0, 1.0, G).astype(f)
    t["c_grid"] = np.stack([np.repeat(lin, G), np.tile(lin, G), np.ones(G * G, f)])
    return t


def layouts(v):
    o = dict(v)
    c = np.ascontiguousarray
    idx = np.clip(np.arange(Q)[:, None] * 0 + (np.arange(S + S - Q)[None, :] - np.arange(Q)[:, None]) - (S - Q) + S - 1,
                  0, v["L0_attn_bias_table"].shape[0] - 1)
    o["bias_strip"] = c(v["L0_attn_bias_table"][idx])
    o["hl_wT"] = c(v["L0_ffn_hl_w"].reshape(64, 64).T)
    o["l0_wqT"] = c(v["L0_ffn_wq"].transpose(0, 3, 1, 2))
    o["l0_wkT"] = c(v["L0_ffn_wk"].transpose(0, 2, 1))
    o["l0_wvT"] = c(v["L0_ffn_wv"].transpose(0, 2, 1))
    o["l0_gateT"] = c(v["L0_ffn_gate_w"].transpose(0, 2, 1))
    o["l0_fc1T"] = c(v["L0_ffn_fc1_w"].T)
    o["l0_fc2T"] = c(v["L0_ffn_fc2_w"].T)
    o["l0_fgateT"] = c(v["L0_ffn_fgate_w"].T)
    for n, s in (("l1_wqT", "wq"), ("l1_wkT", "wk"), ("l1_wvT", "wv"), ("l1_woT", "wo"), ("l1_routerT", "router_w")):
        o[n] = c(v["L1_ffn_" + s].T)
    o["l1_w1T"] = c(v["L1_ffn_w1"].transpose(2, 0, 1))
    o["l1_w3T"] = c(v["L1_ffn_w3"].transpose(2, 0, 1))
    o["l1_w2T"] = c(v["L1_ffn_w2"].transpose(0, 2, 1))
    for n in "qkvo":
        o["l2_w%sT" % n] = c(v["L2_attn_W" + n].T)
    o["l2_b1T"] = c(v["L2_ffn_b1"].T)
    o["l3_b1T"] = c(v["L3_ffn_b1"].T)
    o["p_wT"] = c(v["L0_tok_p_w"].T)
    o["w1_T"] = c(v["L0_tok_w1_w"].transpose(0, 2, 1))
    o["w2_T"] = c(v["L0_tok_w2_w"].transpose(0, 2, 1))
    o["q1_T"] = c(v["L0_tok_q1_w"].T)
    o["q2_T"] = c(v["L0_tok_q2_w"].T)
    used = ("bias_table", "hl_w", "ffn_wq", "ffn_wk", "ffn_wv", "ffn_wo", "gate_w", "fc1_w", "fc2_w", "router_w",
            "L1_ffn_w1", "L1_ffn_w2", "L1_ffn_w3", "L2_attn_W", "L2_ffn_b1", "L3_ffn_b1", "p_w", "tok_w1_w",
            "tok_w2_w", "q1_w", "q2_w", "attn_scale")
    return {k: x for k, x in o.items() if not (k in v and any(u in k for u in used)) or k == "L0_attn_scale"}


def prepare(nc, inputs, upto=99):
    arrays = {}
    args = {}
    for name, x in {**layouts({k: np.asarray(x) for k, x in inputs.items()}), **tables()}.items():
        if x.ndim == 0:
            x = x.reshape(1)
        arrays["in_" + name] = np.ascontiguousarray(x)
        args[name] = nc.dram_tensor("in_" + name, x.shape, mybir.dt.from_np(x.dtype), kind="ExternalInput").ap()
    out = nc.dram_tensor("out_0", (B, S, D), F32, kind="ExternalOutput").ap()
    build(nc, args, out, upto)
    return arrays


def kernel(**inputs):
    from concourse import bacc
    from concourse.bass_utils import run_bass_kernel_spmd

    nc = bacc.Bacc("TRN2", target_bir_lowering=False, num_devices=1)
    arrays = prepare(nc, inputs)
    r = run_bass_kernel_spmd(nc, [arrays], core_ids=[0])
    return r.results[0]["out_0"]
```

```python
from contextlib import ExitStack

import numpy as np

import concourse.bass as bass
from concourse import mybir

ALU = mybir.AluOpType
ACT = mybir.ActivationFunctionType
AX = mybir.AxisListType
F32 = mybir.dt.float32
BF16 = mybir.dt.bfloat16
I32 = mybir.dt.int32
U32 = mybir.dt.uint32

B, S, Q, T, D = 4, 576, 96, 6, 64
IMG, TXT = 64, 512
C, G, KX, KY, HALF = 32, 64, 24, 12, 288
NEG = -1.0e30
HID = 170
HP = HID // 2


class Chain:

    def __init__(self, eng, sem):
        self.eng, self.sem, self.n = eng, sem, 0

    def __call__(self, ins):
        self.n += 1
        ins.then_inc(self.sem, 1)
        self.eng.wait_ge(self.sem, self.n)


def wide(ap, shape):
    return ap.to_broadcast(shape)


def rsqrt(dve, link, y, v, tmp):
    link(dve.tensor_scalar(y.bitcast(I32), v.bitcast(I32), 1, None, ALU.logical_shift_right))
    link(dve.tensor_scalar(y.bitcast(I32), y.bitcast(I32), -1.0, float(0x5F3759DF), ALU.mult, ALU.add))
    for _ in range(3):
        link(dve.tensor_tensor(tmp, y, y, ALU.mult))
        link(dve.scalar_tensor_tensor(tmp, tmp, -0.5, v, ALU.mult, ALU.mult))
        link(dve.scalar_tensor_tensor(y, tmp, 1.5, y, ALU.add, ALU.mult))


def layer_norm(dve, link, out, x, sq, st, eps):
    p, g, w = x.shape
    mean, var, inv, tmp = (st[0:p, j, 0:g] for j in range(4))
    link(dve.tensor_reduce(mean, x, AX.X, ALU.add))
    link(dve.scalar_tensor_tensor(out, wide(mean.unsqueeze(2), [p, g, w]), -1.0 / w, x, ALU.mult, ALU.add))
    link(dve.tensor_tensor(sq, out, out, ALU.mult))
    link(dve.tensor_reduce(var, sq, AX.X, ALU.add))
    link(dve.tensor_scalar(var, var, 1.0 / w, eps, ALU.mult, ALU.add))
    rsqrt(dve, link, inv, var, tmp)
    link(dve.tensor_tensor(out, out, wide(inv.unsqueeze(2), [p, g, w]), ALU.mult))


def rms_norm(dve, link, out, x, sq, st, eps, weight):
    p, g, w = x.shape
    var, inv, tmp = (st[0:p, j, 0:g] for j in range(3))
    link(dve.tensor_tensor(sq, x, x, ALU.mult))
    link(dve.tensor_reduce(var, sq, AX.X, ALU.add))
    link(dve.tensor_scalar(var, var, 1.0 / w, eps, ALU.mult, ALU.add))
    rsqrt(dve, link, inv, var, tmp)
    link(dve.tensor_tensor(out, x, wide(inv.unsqueeze(2), [p, g, w]), ALU.mult))
    link(dve.tensor_tensor(out, out, weight, ALU.mult))


def affine(dve, link, x, gamma, beta):
    link(dve.tensor_tensor(x, x, gamma, ALU.mult))
    link(dve.tensor_tensor(x, x, beta, ALU.add))


def halves(ap):
    return ap.rearrange("p (c n) -> p c n", c=2)


class Attention:

    def __init__(self, nc, st, name, ps, maps, dv, causal, q_of, k_of, v_of, out_of, mask=None, strip=None):
        self.ps, self.maps, self.dv, self.causal = ps, maps, dv, causal
        self.q_of, self.k_of, self.v_of, self.out_of, self.mask, self.strip = q_of, k_of, v_of, out_of, mask, strip
        sb = lambda n, shape: st.enter_context(nc.sbuf_tensor(f"{name}_{n}", shape, F32))
        self.probs = sb("probs", [Q, 2, S])
        self.probs_t = sb("probs_t", [Q, 2, T, Q])
        self.neg_max = sb("neg_max", [Q, 4])
        self.row_sum = sb("row_sum", [Q, 2, maps])
        self.inv_sum = sb("inv_sum", [Q, maps])
        self.biased = sb("biased", [Q, 2, S]) if strip is not None else None
        names = ("scores_ready", "max_ready", "probs_ready", "turned", "turned_copied", "product_ready", "out_ready")
        self.sems = [st.enter_context(nc.semaphore(f"{name}_{n}")) for n in names]
        (self.scores_ready, self.max_ready, self.probs_ready, self.turned, self.turned_copied,
         self.product_ready, self.out_ready) = self.sems
        self.units = [(t, m) for t in range(T) for m in range(maps)]

    def keys(self, t):
        return Q * (t + 1) if self.causal else S

    def scores_at(self, i):
        b = 2 * (i % 2)
        return self.ps[0:Q, b:b + 2, :].rearrange("p b n -> p (b n)")

    def tensor(self, pe, ident):
        n = len(self.units)
        turned = self.ps[0:Q, 4:6, :].rearrange("p b (k n) -> p (b k) n", n=128)
        for step in range(n + 2):
            if step < n:
                t, m = self.units[step]
                if step >= 2:
                    pe.wait_ge(self.probs_ready, step - 1)
                for a in range(0, self.keys(t), 512):
                    z = min(self.keys(t), a + 512)
                    mm = pe.matmul(self.scores_at(step)[:, a:z], self.q_of(m, t), self.k_of(m, a, z),
                                   start=True, stop=True)
                mm.then_inc(self.scores_ready, 1)
            if 1 <= step <= n:
                i = step - 1
                t, m = self.units[i]
                pe.wait_ge(self.probs_ready, i + 1)
                if i >= 1:
                    pe.wait_ge(self.turned_copied, i)
                for k in range(self.keys(t) // Q):
                    mm = pe.transpose(turned[:, k, 0:Q], self.probs[:, i % 2, Q * k:Q * k + Q], ident[0:Q, 0:Q])
                mm.then_inc(self.turned, 1)
            if step >= 2:
                i = step - 2
                t, m = self.units[i]
                pe.wait_ge(self.turned_copied, i + 1)
                if m == 0 and t >= 2:
                    pe.wait_ge(self.out_ready, t - 1)
                last = self.keys(t) // Q - 1
                for k in range(last + 1):
                    mm = pe.matmul(self.ps[0:Q, 6 + t % 2, m * self.dv:(m + 1) * self.dv],
                                   self.probs_t[:, i % 2, k, :], self.v_of(m, k), start=(k == 0), stop=(k == last))
                mm.then_inc(self.product_ready, 1)

    def scalar(self, act):
        for i, (t, m) in enumerate(self.units):
            act.wait_ge(self.max_ready, i + 1)
            if i >= 2:
                act.wait_ge(self.turned, i - 1)
            if m == 0 and t >= 2:
                act.wait_ge(self.out_ready, t - 1)
            src = self.scores_at(i) if self.biased is None else self.biased[:, i % 2, :]
            act.activation(self.probs[:, i % 2, 0:self.keys(t)], src[:, 0:self.keys(t)], ACT.Exp,
                           bias=self.neg_max[:, i % 4:i % 4 + 1],
                           accum_out=self.row_sum[:, t % 2, m:m + 1]).then_inc(self.probs_ready, 1)

    def vector(self, dve, link):
        n = len(self.units)
        turned = self.ps[0:Q, 4:6, :].rearrange("p b (k n) -> p (b k) n", n=128)
        for step in range(n + 2):
            if step < n:
                t, m = self.units[step]
                dve.wait_ge(self.scores_ready, step + 1)
                s = self.scores_at(step)
                if self.causal:
                    diag = s[:, Q * t:Q * t + Q]
                    link(dve.tensor_tensor(diag, diag, self.mask, ALU.add))
                if self.biased is not None:
                    if step >= 2:
                        dve.wait_ge(self.probs_ready, step - 1)
                    out = self.biased[:, step % 2, :]
                    link(dve.tensor_tensor(out, s[:, 0:S], self.strip(t), ALU.add))
                    s = out
                dve.tensor_reduce(self.neg_max[:, step % 4:step % 4 + 1], s[:, 0:self.keys(t)], AX.X, ALU.max,
                                  negate=True).then_inc(self.max_ready, 1)
            if 1 <= step <= n:
                i = step - 1
                t, m = self.units[i]
                dve.wait_ge(self.turned, i + 1)
                if i >= 2:
                    dve.wait_ge(self.product_ready, i - 1)
                k = self.keys(t) // Q
                dve.tensor_copy(self.probs_t[:, i % 2, 0:k, :], turned[:, 0:k, 0:Q]).then_inc(self.turned_copied, 1)
            if step >= 2 and self.units[step - 2][1] == self.maps - 1:
                t = self.units[step - 2][0]
                dve.wait_ge(self.product_ready, step - 1)
                if t >= 1:
                    dve.wait_ge(self.out_ready, t)
                link(dve.reciprocal(self.inv_sum[:, :], self.row_sum[:, t % 2, :]))
                prod = self.ps[0:Q, 6 + t % 2, 0:self.maps * self.dv].rearrange("p (m d) -> p m d", m=self.maps)
                dve.tensor_tensor(self.out_of(t), prod, wide(self.inv_sum[:, :].unsqueeze(2), [Q, self.maps, self.dv]),
                                  ALU.mult).then_inc(self.out_ready, 1)


def split3(dve, link, parts, value, rest):
    link(dve.tensor_copy(parts[0], value))
    link(dve.tensor_tensor(rest, value, parts[0], ALU.subtract))
    link(dve.tensor_copy(parts[1], rest))
    link(dve.tensor_tensor(parts[2], rest, parts[1], ALU.subtract))


class SplitAttention:

    LAG = 2

    def __init__(self, nc, st, name, ps, groups, members, ident, ident32, mask, mask_t, v1, out_of):
        self.ps, self.G, self.E, self.M = ps, groups, members, groups * members
        self.ident32 = ident32
        self.ident, self.mask, self.mask_t, self.v1, self.out_of = ident, mask, mask_t, v1, out_of
        sb = lambda n, shape, dt=F32: st.enter_context(nc.sbuf_tensor(f"{name}_{n}", shape, dt))
        self.q_stack = sb("q_stack", [Q, T, self.M, 96], BF16)
        self.k_stack = sb("k_stack", [Q, T, self.G, 96], BF16)
        self.rest = sb("rest", [Q, T, self.M, 16])
        self.qT = sb("qT", [99, self.M, S], BF16)
        self.kT = sb("kT", [99, self.G, S], BF16)
        self.probs_t = sb("probs_t", [Q, 3, self.E, Q])
        self.out_f = sb("out_f", [32 * groups, 2, self.E, Q])
        self.neg_max = sb("neg_max", [Q, 2, self.M])
        self.max_rest = sb("max_rest", [Q, self.M])
        self.max_parts = sb("max_parts", [Q, 2, self.M, 3], BF16)
        self.inv_sum = sb("inv_sum", [Q, self.G, self.E])
        names = ("stacks_ready", "stack_turned", "stack_copied_v", "stack_copied_s", "scores_ready", "max_ready",
                 "parts_ready", "parts_turned", "parts_copied", "turned_ready", "probs_ready", "product_ready",
                 "out_copied", "out_turned", "out_ready")
        self.sems = [st.enter_context(nc.semaphore(f"{name}_{n}")) for n in names]
        (self.stacks_ready, self.stack_turned, self.stack_copied_v, self.stack_copied_s, self.scores_ready,
         self.max_ready, self.parts_ready, self.parts_turned, self.parts_copied, self.turned_ready,
         self.probs_ready, self.product_ready, self.out_copied, self.out_turned, self.out_ready) = self.sems
        self.per_bank = min(8, self.M)
        self.rounds = self.M // self.per_bank
        self.loads = [("k", t) for t in range(T)] + [("q", t, r) for t in range(T) for r in range(self.rounds)]
        self.steps = [(t, g, k) for t in range(T) for g in range(self.G) for k in range(t + 1)]

    def bank16(self, b, rows, n):
        return self.ps[rows, b, :].bitcast(BF16)[:, 0:n * Q].rearrange("p (m n) -> p m n", n=Q)

    def stack(self, dve, link, stack, value, rest, order):
        first = [order.index(j) for j in range(3)]
        parts = [stack[:, :, :, 16 * f:16 * f + 16] for f in first]
        split3(dve, link, parts, value, rest)
        for i, j in enumerate(order):
            if i not in first:
                link(dve.tensor_copy(stack[:, :, :, 16 * i:16 * i + 16], parts[j]))

    def vector_stacks(self, dve, link, q, k):
        link(dve.memset(self.kT[96:99, :, :], 1.0))
        self.stack(dve, link, self.k_stack, k, self.rest[:, :, 0:self.G, :], (0, 1, 0, 2, 1, 0))
        dve.sem_inc(self.stacks_ready, 1)
        self.stack(dve, link, self.q_stack, q, self.rest[:, :, :, :], (0, 0, 1, 0, 1, 2))
        dve.sem_inc(self.stacks_ready, 1)

    def copy_stacks(self, eng, copy, parity, done):
        for i, load in enumerate(self.loads):
            if i % 2 != parity:
                continue
            eng.wait_ge(self.stack_turned, i + 1)
            t = load[1]
            if load[0] == "k":
                dst, n = self.kT[0:96, :, Q * t:Q * t + Q], self.G
            else:
                m = load[2] * self.per_bank
                dst, n = self.qT[0:96, m:m + self.per_bank, Q * t:Q * t + Q], self.per_bank
            copy(dst, self.bank16(i % 8, slice(0, 96), n)).then_inc(done, 1)

    def tensor_stacks(self, pe):
        for i, load in enumerate(self.loads):
            if i == 0 or i == T:
                pe.wait_ge(self.stacks_ready, 1 + (i == T))
            if i >= 8:
                pe.wait_ge(self.stack_copied_s if i % 2 else self.stack_copied_v, (i - 8) // 2 + 1)
            t = load[1]
            if load[0] == "k":
                src, n = self.k_stack[:, t, :, :], self.G
            else:
                m = load[2] * self.per_bank
                src, n = self.q_stack[:, t, m:m + self.per_bank, :], self.per_bank
            dst = self.bank16(i % 8, slice(0, 96), n)
            for m in range(n):
                mm = pe.transpose(dst[:, m, :], src[:, m, :], self.ident[:, :])
            mm.then_inc(self.stack_turned, 1)
        pe.wait_ge(self.stack_copied_v, (len(self.loads) + 1) // 2)
        pe.wait_ge(self.stack_copied_s, len(self.loads) // 2)

    def tensor(self, pe):
        self.tensor_stacks(pe)
        M, E, G = self.M, self.E, self.G

        def scores(t, m):
            i = M * t + m
            if i >= 2:
                pe.wait_ge(self.max_ready, i - 1)
            if t >= 1 and m < 3:
                pe.wait_ge(self.parts_copied, self.rounds * t)
            b, n = 2 * (i % 2), Q * (t + 1)
            dst = self.ps[0:Q, b:b + 2, :].rearrange("p b n -> p (b n)")
            for a in range(0, n, 512):
                z = min(n, a + 512)
                mm = pe.matmul(dst[:, a:z], self.qT[0:96, m, Q * t:Q * t + Q], self.kT[0:96, m // E, a:z],
                               start=True, stop=False, skip_group_check=True)
            cuts = [Q * t, n] if n <= 512 else [Q * t, 512, n]
            for a, z in zip(cuts, cuts[1:]):
                mm = pe.matmul(dst[:, a:z], self.ident[:, :], self.mask[:, a - Q * t:z - Q * t],
                               start=False, stop=True, skip_group_check=True)
            mm.then_inc(self.scores_ready, 1)

        def turn_max(t):
            pe.wait_ge(self.parts_ready, t + 1)
            for r in range(self.rounds):
                dst = self.bank16(2 * r, slice(96, 99), self.per_bank)
                for m in range(self.per_bank):
                    mm = pe.transpose(dst[:, m, :], self.max_parts[:, t % 2, self.per_bank * r + m, :], self.ident[:, :])
                mm.then_inc(self.parts_turned, 1)

        def turned_scores(j):
            t, g, k = self.steps[j]
            if j >= 2:
                pe.wait_ge(self.probs_ready, j - 1)
            if g == k == 0:
                pe.wait_ge(self.parts_copied, self.rounds * (t + 1))
            dst = self.ps[0:Q, 4 + j % 2, 0:E * Q].rearrange("p (e n) -> p e n", e=E)
            mm = pe.matmul(dst, self.kT[:, g, Q * k:Q * k + Q], self.qT[:, E * g:E * g + E, Q * t:Q * t + Q],
                           start=True, stop=(k < t))
            if k == t:
                mm = pe.matmul(dst, self.ident[:, :], wide(self.mask_t[:, :].unsqueeze(1), [Q, E, Q]),
                               start=False, stop=True)
            mm.then_inc(self.turned_ready, 1)

        def product(j):
            t, g, k = self.steps[j]
            pe.wait_ge(self.probs_ready, j + 1)
            if g == k == 0 and t >= 2:
                pe.wait_ge(self.out_ready, t - 1)
            pe.matmul(self.ps[32 * g:32 * g + 32, 6 + t % 2, 0:E * Q], self.v1[:, k, g, :],
                      self.probs_t[:, j % 3, :, :], start=(k == 0), stop=(k == t)).then_inc(self.product_ready, 1)

        def turn_out(t):
            pe.wait_ge(self.out_copied, t + 1)
            for e in range(E):
                mm = pe.transpose(self.ps[0:Q, 6 + t % 2, 128 * e:128 * e + 32 * G], self.out_f[:, t % 2, e, :],
                                  self.ident32[0:32 * G, 0:32 * G])
            mm.then_inc(self.out_turned, 1)

        for m in range(M):
            scores(0, m)
        turn_max(0)
        j = 0
        for t in range(T):
            n = G * (t + 1)
            m = 0
            for s in range(n):
                if t + 1 < T:
                    while m < min(M, -(-M * (s + 1) // (n - 1))):
                        scores(t + 1, m)
                        m += 1
                turned_scores(j)
                if j >= self.LAG:
                    product(j - self.LAG)
                if t >= 1 and s == min(4, n - 1):
                    turn_out(t - 1)
                j += 1
            if t + 1 < T:
                turn_max(t + 1)
        for i in range(j - self.LAG, j):
            product(i)
        turn_out(T - 1)

    def scalar(self, act):
        self.copy_stacks(act, act.copy, 1, self.stack_copied_s)

        def copy_out(t):
            act.wait_ge(self.product_ready, self.G * (t + 1) * (t + 2) // 2)
            act.copy(self.out_f[:, t % 2, :, :],
                     self.ps[0:32 * self.G, 6 + t % 2, 0:self.E * Q].rearrange("p (e n) -> p e n", e=self.E))\
               .then_inc(self.out_copied, 1)

        j = 0
        for t in range(T):
            for r in range(self.rounds):
                act.wait_ge(self.parts_turned, self.rounds * t + r + 1)
                m = self.per_bank * r
                act.copy(self.qT[96:99, m:m + self.per_bank, Q * t:Q * t + Q],
                         self.bank16(2 * r, slice(96, 99), self.per_bank)).then_inc(self.parts_copied, 1)
            for s in range(self.G * (t + 1)):
                act.wait_ge(self.turned_ready, j + 1)
                if j >= 3:
                    act.wait_ge(self.product_ready, j - 2)
                act.activation(self.probs_t[:, j % 3, :, :],
                               self.ps[0:Q, 4 + j % 2, 0:self.E * Q].rearrange("p (e n) -> p e n", e=self.E),
                               ACT.Exp).then_inc(self.probs_ready, 1)
                j += 1
                if t >= 1 and s == self.LAG:
                    copy_out(t - 1)
        copy_out(T - 1)

    def vector(self, dve, link):
        M = self.M
        self.copy_stacks(dve, dve.tensor_copy, 0, self.stack_copied_v)

        def finish(t):
            dve.wait_ge(self.out_turned, t + 1)
            prod = self.ps[0:Q, 6 + t % 2, 0:128 * self.E].rearrange("p (e n) -> p e n", e=self.E)[:, :, 0:32 * self.G]
            prod = prod.rearrange("p e (g n) -> p g e n", n=32)
            link(dve.reciprocal(self.inv_sum[:, :, :], prod[:, :, :, 16]))
            out = self.out_of(t).rearrange("p (g e) d -> p g e d", g=self.G)
            link(dve.tensor_tensor(out, prod[:, :, :, 0:16], wide(self.inv_sum[:, :, :].unsqueeze(3), [Q, self.G, self.E, 16]),
                                   ALU.mult))
            dve.sem_inc(self.out_ready, 1)

        for t in range(T):
            for m in range(M):
                i = M * t + m
                dve.wait_ge(self.scores_ready, i + 1)
                s = self.ps[0:Q, 2 * (i % 2):2 * (i % 2) + 2, :].rearrange("p b n -> p (b n)")[:, 0:Q * (t + 1)]
                dve.tensor_reduce(self.neg_max[:, t % 2, m:m + 1], s, AX.X, ALU.max, negate=True).then_inc(self.max_ready, 1)
            dve.wait_ge(self.max_ready, M * (t + 1))
            split3(dve, link, [self.max_parts[:, t % 2, :, j] for j in range(3)], self.neg_max[:, t % 2, :],
                   self.max_rest[:, :])
            dve.sem_inc(self.parts_ready, 1)
            if t >= 2:
                finish(t - 2)
        finish(T - 2)
        finish(T - 1)


def build(nc, a, out, upto=99):
    ctx = ExitStack()
    with ctx:
        def sb(name, shape, dt=F32):
            return ctx.enter_context(nc.sbuf_tensor(name, shape, dt))

        ps = ctx.enter_context(nc.psum_tensor("ps", [128, 8, 512], F32))
        h_in = nc.dram_tensor("h_tokens", (B, S, D), F32, kind="Internal").ap()
        h_mid = nc.dram_tensor("h_after_attention", (B, S, D), F32, kind="Internal").ap()
        sx_all = nc.dram_tensor("head_inputs", (B, S, D), F32, kind="Internal").ap()

        ident = sb("ident", [128, 128])
        causal = sb("causal", [Q, Q])
        keep = sb("keep", [Q, Q])
        ident16 = sb("ident16", [Q, Q], BF16)
        mask16 = sb("mask16", [Q, Q], BF16)
        mask16_t = sb("mask16_t", [Q, Q], BF16)
        causal32 = sb("causal32", [128, 32])
        iota8 = sb("iota8", [Q, 8])
        cos_t = sb("cos_t", [Q, T, 8])
        sin_t = sb("sin_t", [Q, T, 8])
        ones = sb("ones", [1, Q])
        att_scale = sb("att_scale", [Q, 1])
        strip = sb("strip", [Q, S + S - Q])
        rows = {}
        for n in ("l0a_g1", "l0a_b1", "l0a_g2", "l0a_b2", "l1a_g1", "l1a_b1", "l1a_g2", "l1a_b2",
                  "l1f_w1", "l1f_w2", "l3f_g", "l3f_b"):
            rows[n] = sb("row_" + n, [Q, D])
        for n in ("l0f_g", "l0f_b", "l0f_fg", "l0f_fb", "l0f_gate"):
            rows[n] = sb("row_" + n, [Q, 16])
        rows["l2f_bg"] = sb("row_l2f_bg", [Q, 8])
        rows["l3f_br"] = sb("row_l3f_br", [Q, 8])
        w = {}
        for n, cols in (("l0a_qkv", 192), ("l0a_proj", 64), ("l0f_hl", 64), ("l0f_fc1", 64), ("l0f_fc2", 64),
                        ("l1a_qkv", 192), ("l1a_proj", 64), ("l1a_w1", 256), ("l3a_qkv", 192)):
            w[n] = sb("w_" + n, [D + 1, cols])
        for n, shape in (("l0f_qkv", [D, 384]),
                         ("l0f_gate", [128, 2, 8]), ("l0f_fgate", [D, 4]),
                         ("l1a_w2", [128, 2, 64]), ("l1a_b2", [1, 64]),
                         ("l1f_qkv", [D, 128]), ("l1f_wo", [D, 64]), ("l1f_router", [D, 8]),
                         ("l1f_w1", [D, 8, HID]), ("l1f_w3", [D, 8, HID]), ("l1f_w2", [HP, 8, 2, D]),
                         ("l2a_q", [D, 64]), ("l2a_k", [D, 64]), ("l2a_v", [16, 4, D]), ("l2a_o", [16, 4, D]),
                         ("l2f_g", [D, 8]), ("l2f_w1", [D, 8, 128]), ("l2f_w2", [128, 8, D]), ("l2f_b2", [8, D]),
                         ("l3f_r", [D, 8]), ("l3f_w1", [D, 8, 128]), ("l3f_w2", [128, 8, D]), ("l3f_b2", [8, D]),
                         ("l2f_b1", [128, 8]), ("l3f_b1", [128, 8])):
            w[n] = sb("w_" + n, shape)

        h = sb("h", [Q, T, D])
        x = sb("x", [Q, T, D])
        y = sb("y", [Q, T, D])
        sq = sb("sq", [Q, T, D])
        st = sb("st", [Q, 4, 24])
        xT = sb("xT", [D + 1, S])
        yT = sb("yT", [D + 1, S])
        resid = sb("resid", [Q, T, D])

        previous = []

        class Stage:

            def __init__(self, name):
                self.name, self.st, self.sems = name, ExitStack(), []

            def sb(self, name, shape, dt=F32):
                return self.st.enter_context(nc.sbuf_tensor(f"{self.name}_{name}", shape, dt))

            def sem(self, name):
                s = ctx.enter_context(nc.semaphore(f"{self.name}_{name}"))
                self.sems.append(s)
                return s

            def __enter__(self):
                self.st.__enter__()
                return self

            def block(self):
                return self.st.enter_context(nc.Block())

            def __exit__(self, *e):
                self.st.__exit__(*e)
                previous[:] = self.sems

        def end_of_pass(name):
            with Stage(name) as sg:
                block = sg.block()

                @block.sync
                def _(sp):
                    clear_previous(sp, sg.sems)

        def clear_previous(sp, own):
            for s in previous:
                if s not in own:
                    sp.sem_clear(s)

        def two(b, p):
            return ps[0:p, b:b + 2, 0:HALF]

        def tiles(b, width=D):
            return ps[0:Q, b, 0:T * width].rearrange("p (t n) -> p t n", t=T)

        def turn(pe, b, src, width=D):
            for t in range(T):
                mm = pe.transpose(ps[0:width, b + t // 3, Q * (t % 3):Q * (t % 3) + Q], src[:, t, :], ident[0:Q, 0:Q])
            return mm

        def by_feature(pe, b, weight, src):
            for c in range(2):
                mm = pe.matmul(ps[0:weight.shape[1], b + c, 0:HALF], weight, src[:, HALF * c:HALF * c + HALF],
                               start=True, stop=True)
            return mm

        def by_token(pe, b, src, weight):
            n = weight.shape[1]
            for t in range(T):
                mm = pe.matmul(ps[0:Q, b, n * t:n * t + n], src[:, Q * t:Q * t + Q], weight, start=True, stop=True)
            return mm

        def softmax_first(dve, link, logits, st):
            p, g, n = logits.shape
            top = st[0:p, 0, 0:g]
            link(dve.tensor_reduce(top, logits, AX.X, ALU.max))
            link(dve.tensor_tensor(logits, logits, wide(top.unsqueeze(2), [p, g, n]), ALU.subtract))

        def softmax_last(dve, link, e, st):
            p, g, n = e.shape
            total = st[0:p, 0, 0:g]
            link(dve.tensor_reduce(total, e, AX.X, ALU.add))
            link(dve.reciprocal(total, total))
            link(dve.tensor_tensor(e, e, wide(total.unsqueeze(2), [p, g, n]), ALU.mult))

        def per_tile(row):
            return wide(row[:, :].unsqueeze(1), [Q, T, row.shape[1]])

        def per_head(row):
            return wide(row[:, :].unsqueeze(1), [Q, 24, 16])

        def heads(t):
            return t[:, :, :].rearrange("p t (n d) -> p (t n) d", n=4)

        def layer0_ffn(b):
            with Stage("l0f") as sg:
                loaded, tensor_done, vector_done, scalar_done, vchain = (
                    sg.sem(n) for n in ("h_loaded", "tensor_step", "vector_step", "scalar_step", "vector_chain"))
                qk = sg.sb("qk", [Q, T, 20, 16])
                v1 = sg.sb("v1", [Q, T, 4, 32])
                live = sg.sb("live", [Q, T, D])
                ao = sg.sb("ao", [Q, T, 16, 16])
                aoT = sg.sb("aoT", [128, 12, Q])
                gate = sg.sb("gate", [Q, 24, 4])
                fgate = sg.sb("fgate", [Q, T, 4])
                att = SplitAttention(nc, sg.st, "l0f_att", ps, 4, 4, ident16, ident, mask16, mask16_t, v1,
                                     lambda t: ao[:, t, :, :])
                sg.sems += att.sems
                block = sg.block()
                qkv_ps = ps[0:Q, 0:6, 0:384]

                @block.sync
                def _(sp):
                    clear_previous(sp, sg.sems)
                    sp.dma_start(h[:, :, :], tokens(h_mid, b)).then_inc(loaded, 16)

                @block.vector
                def _(dve):
                    link = Chain(dve, vchain)
                    dve.wait_ge(loaded, 16)
                    layer_norm(dve, link, x[:, :, :], h[:, :, :], sq[:, :, :], st, 1e-5)
                    dve.sem_inc(vector_done, 1)
                    dve.wait_ge(tensor_done, 1)
                    dve.tensor_copy(halves(xT[0:D, :]), two(0, D)).then_inc(vector_done, 1)
                    dve.wait_ge(tensor_done, 2)
                    dve.tensor_copy(halves(yT[0:D, :]), two(2, D)).then_inc(vector_done, 1)
                    link(dve.memset(v1[:, :, :, :], 0.0))
                    link(dve.memset(v1[:, :, :, 16], 1.0))
                    dve.wait_ge(tensor_done, 4)
                    link(dve.tensor_scalar(qk[:, :, 0:16, :].rearrange("p t m d -> p t (m d)"), qkv_ps[:, :, 0:256],
                                           4.0, None, ALU.mult))
                    link(dve.tensor_copy(qk[:, :, 16:20, :].rearrange("p t m d -> p t (m d)"), qkv_ps[:, :, 256:320]))
                    link(dve.tensor_copy(v1[:, :, :, 0:16], qkv_ps[:, :, 320:384].rearrange("p t (n d) -> p t n d", n=4)))
                    dve.wait_ge(scalar_done, 1)
                    link(dve.tensor_scalar(live[:, :, :], y[:, :, :], 0.0, None, ALU.not_equal))
                    dve.sem_inc(vector_done, 4)
                    att.vector_stacks(dve, link, qk[:, :, 0:16, :], qk[:, :, 16:20, :])
                    att.vector(dve, link)
                    dve.wait_ge(att.out_ready, T)
                    four = ao[:, :, :, :].rearrange("p t (n e) d -> p (t n) e d", n=4)
                    link(dve.tensor_tensor(four, four, wide(heads(live).unsqueeze(2), [Q, 24, 4, 16]), ALU.mult))
                    dve.sem_inc(vector_done, 1)
                    dve.wait_ge(tensor_done, 5)
                    turned = ps[:, 0:3, :].rearrange("p b (k n) -> p (b k) n", n=128)[:, :, 0:Q]
                    dve.tensor_copy(aoT[:, :, :], turned).then_inc(vector_done, 1)
                    dve.wait_ge(tensor_done, 6)
                    g3 = gate[:, :, :].rearrange("p (t n) e -> p t (n e)", t=T)
                    link(dve.tensor_tensor(g3, tiles(3, 16), per_tile(rows["l0f_gate"]), ALU.add))
                    softmax_first(dve, link, gate[:, :, :], st)
                    dve.sem_inc(vector_done, 1)
                    dve.wait_ge(scalar_done, 2)
                    softmax_last(dve, link, gate[:, :, :], st)
                    link(dve.tensor_tensor(four, four, wide(gate[:, :, :].unsqueeze(3), [Q, 24, 4, 16]), ALU.mult))
                    link(dve.tensor_reduce(heads(y), four.rearrange("p g e d -> p g d e"), AX.X, ALU.add))
                    link(dve.tensor_tensor(y[:, :, :], y[:, :, :], resid[:, :, :], ALU.add))
                    layer_norm(dve, link, heads(x), heads(y), heads(sq), st, 1e-8)
                    affine(dve, link, heads(x), per_head(rows["l0f_g"]), per_head(rows["l0f_b"]))
                    dve.sem_inc(vector_done, 1)
                    link(dve.tensor_scalar(live[:, :, :], x[:, :, :], 0.0, None, ALU.not_equal))
                    dve.wait_ge(tensor_done, 7)
                    dve.tensor_copy(halves(xT[0:D, :]), two(0, D)).then_inc(vector_done, 1)
                    dve.wait_ge(tensor_done, 8)
                    dve.scalar_tensor_tensor(y[:, :, :], tiles(2), 0.0, live[:, :, :], ALU.max, ALU.mult).then_inc(vector_done, 1)
                    dve.wait_ge(tensor_done, 9)
                    dve.tensor_copy(halves(yT[0:D, :]), two(0, D)).then_inc(vector_done, 1)
                    dve.wait_ge(tensor_done, 10)
                    link(dve.tensor_tensor(y[:, :, :], tiles(3), live[:, :, :], ALU.mult))
                    link(dve.tensor_tensor(y[:, :, :], y[:, :, :], x[:, :, :], ALU.add))
                    layer_norm(dve, link, heads(x), heads(y), heads(sq), st, 1e-8)
                    affine(dve, link, heads(x), per_head(rows["l0f_fg"]), per_head(rows["l0f_fb"]))
                    dve.sem_inc(vector_done, 1)
                    dve.wait_ge(tensor_done, 11)
                    dve.tensor_copy(halves(xT[0:D, :]), two(0, D)).then_inc(vector_done, 1)
                    dve.wait_ge(tensor_done, 12)
                    link(dve.tensor_copy(fgate[:, :, :], tiles(2, 4)))
                    softmax_first(dve, link, fgate[:, :, :], st)
                    dve.sem_inc(vector_done, 1)
                    dve.wait_ge(scalar_done, 3)
                    softmax_last(dve, link, fgate[:, :, :], st)
                    fg = fgate[:, :, :].rearrange("p t n -> p (t n)")
                    link(dve.tensor_tensor(heads(x), heads(x), wide(fg.unsqueeze(2), [Q, 24, 16]), ALU.mult))
                    link(dve.tensor_tensor(h[:, :, :], h[:, :, :], x[:, :, :], ALU.add))

                @block.scalar
                def _(act):
                    act.wait_ge(tensor_done, 3)
                    act.copy(y[:, :, :], tiles(4)).then_inc(scalar_done, 1)
                    att.scalar(act)
                    act.wait_ge(vector_done, 10)
                    act.activation(gate[:, :, :], gate[:, :, :], ACT.Exp).then_inc(scalar_done, 1)
                    act.wait_ge(vector_done, 17)
                    act.activation(fgate[:, :, :], fgate[:, :, :], ACT.Exp).then_inc(scalar_done, 1)

                @block.tensor
                def _(pe):
                    pe.wait_ge(vector_done, 1)
                    turn(pe, 0, x).then_inc(tensor_done, 1)
                    pe.wait_ge(vector_done, 2)
                    by_feature(pe, 2, w["l0f_hl"][:, :], xT).then_inc(tensor_done, 1)
                    by_token(pe, 4, xT, w["l0f_hl"][:, :]).then_inc(tensor_done, 1)
                    pe.wait_ge(vector_done, 3)
                    pe.wait_ge(scalar_done, 1)
                    for t in range(T):
                        mm = pe.matmul(ps[0:Q, t, 0:384], yT[0:D, Q * t:Q * t + Q], w["l0f_qkv"][:, :], start=True, stop=True)
                    mm.then_inc(tensor_done, 1)
                    pe.wait_ge(vector_done, 7)
                    att.tensor(pe)
                    pe.wait_ge(vector_done, 8)
                    for i in range(12):
                        src = ao[:, i // 2, 8 * (i % 2):8 * (i % 2) + 8, :].rearrange("p m d -> p (m d)")
                        mm = pe.transpose(ps[:, i // 4, 128 * (i % 4):128 * (i % 4) + Q], src, ident[0:Q, 0:Q])
                    mm.then_inc(tensor_done, 1)
                    pe.wait_ge(vector_done, 9)
                    for i in range(12):
                        mm = pe.matmul(ps[0:Q, 3, 8 * i:8 * i + 8], aoT[:, i, :], w["l0f_gate"][:, i % 2, :],
                                       start=True, stop=True)
                    mm.then_inc(tensor_done, 1)
                    pe.wait_ge(vector_done, 11)
                    turn(pe, 0, x).then_inc(tensor_done, 1)
                    pe.wait_ge(vector_done, 12)
                    by_token(pe, 2, xT, w["l0f_fc1"][:, :]).then_inc(tensor_done, 1)
                    pe.wait_ge(vector_done, 13)
                    turn(pe, 0, y).then_inc(tensor_done, 1)
                    pe.wait_ge(vector_done, 14)
                    by_token(pe, 3, yT, w["l0f_fc2"][:, :]).then_inc(tensor_done, 1)
                    pe.wait_ge(vector_done, 15)
                    turn(pe, 0, x).then_inc(tensor_done, 1)
                    pe.wait_ge(vector_done, 16)
                    by_token(pe, 2, xT[0:D, :], w["l0f_fgate"][:, :]).then_inc(tensor_done, 1)

        def layer1_attention():
            with Stage("l1a") as sg:
                tensor_done, vector_done, scalar_done, vchain = (
                    sg.sem(n) for n in ("tensor_step", "vector_step", "scalar_step", "vector_chain"))
                qk = sg.sb("qk", [Q, T, 2, D])
                v1 = sg.sb("v1", [Q, T, D + 1])
                qT = sg.sb("qT", [D, S])
                kT = sg.sb("kT", [D, S])
                sT = sg.sb("sT", [Q, T, S])
                hT = sg.sb("hT", [128, 2, S])
                den = sg.sb("den", [Q, T])
                block = sg.block()
                place = [(0, 0), (2, 0), (3, 0), (4, 0), (5, 0), (5, 192)]
                flat = qk[:, :, :, :].rearrange("p t c d -> p (t c) d")

                @block.sync
                def _(sp):
                    clear_previous(sp, sg.sems)

                @block.vector
                def _(dve):
                    link = Chain(dve, vchain)
                    layer_norm(dve, link, x[:, :, :], h[:, :, :], sq[:, :, :], st, 1e-5)
                    dve.sem_inc(vector_done, 1)
                    link(dve.memset(v1[:, :, D:D + 1], 1.0))
                    dve.wait_ge(tensor_done, 1)
                    dve.tensor_copy(halves(xT[0:D, :]), two(0, D)).then_inc(vector_done, 1)
                    dve.wait_ge(tensor_done, 2)
                    qkv = ps[0:Q, 2:5, 0:384].rearrange("p b (a n) -> p b a n", a=2)
                    pairs = lambda t: t.rearrange("p (b a) n -> p b a n", a=2)
                    link(dve.tensor_scalar(pairs(qk[:, :, :, :].rearrange("p t c d -> p t (c d)")), qkv[:, :, :, 0:128],
                                           0.125, None, ALU.mult))
                    link(dve.tensor_copy(pairs(v1[:, :, 0:D]), qkv[:, :, :, 128:192]))
                    sum2, inv, tmp = (st[:, j, 0:12] for j in range(3))
                    s2 = sT[:, 0:3, 0:512].rearrange("p a (b d) -> p a b d", d=D)
                    sqr = sT[:, 0, 0:384].rearrange("p (g d) -> p g d", d=D)
                    for half in range(2):
                        part = flat[:, 6 * half:6 * half + 6, :]
                        link(dve.tensor_tensor(sqr, part, part, ALU.mult))
                        link(dve.tensor_reduce(sum2[:, 6 * half:6 * half + 6], sqr, AX.X, ALU.add))
                    link(dve.tensor_scalar(sum2, sum2, 1e-24, None, ALU.max))
                    rsqrt(dve, link, inv, sum2, tmp)
                    link(dve.tensor_tensor(flat, flat, wide(inv.unsqueeze(2), [Q, 12, D]), ALU.mult))
                    dve.sem_inc(vector_done, 1)
                    dve.wait_ge(scalar_done, 2)
                    dve.tensor_scalar(flat, flat, 1e-6, None, ALU.add).then_inc(vector_done, 1)
                    dve.wait_ge(tensor_done, 3)
                    dve.tensor_copy(halves(qT[:, :]), two(0, D)).then_inc(vector_done, 1)
                    dve.wait_ge(tensor_done, 4)
                    dve.tensor_copy(halves(kT[:, :]), two(5, D)).then_inc(vector_done, 1)
                    for k, (bank, col) in enumerate(place):
                        dve.wait_ge(tensor_done, 10)
                        n = S - Q * k
                        src = ps[0:Q, bank:bank + 2, :].rearrange("p b n -> p (b n)")[:, col:col + n]
                        dve.tensor_tensor(sT[:, k, Q * k:Q * k + Q], src[:, 0:Q], keep[:, :], ALU.mult).then_inc(vchain, 1)
                        link.n += 1
                        if n > Q:
                            link(dve.tensor_copy(sT[:, k, Q * k + Q:S], src[:, Q:n]))
                    dve.wait_ge(vchain, link.n)
                    dve.sem_inc(vector_done, 1)
                    dve.wait_ge(tensor_done, 11)
                    nd = tiles(6, D + 1)
                    link(dve.tensor_scalar(y[:, :, :], nd[:, :, 0:D], 1e4, -1e4, ALU.min, ALU.max))
                    link(dve.tensor_scalar(den[:, :], nd[:, :, D], 1e-6, None, ALU.max))
                    link(dve.reciprocal(den[:, :], den[:, :]))
                    link(dve.tensor_tensor(y[:, :, :], y[:, :, :], wide(den[:, :].unsqueeze(2), [Q, T, D]), ALU.mult))
                    dve.sem_inc(vector_done, 1)
                    dve.wait_ge(tensor_done, 12)
                    dve.tensor_copy(halves(yT[0:D, :]), two(0, D)).then_inc(vector_done, 1)
                    dve.wait_ge(tensor_done, 13)
                    link(dve.tensor_tensor(y[:, :, :], tiles(2), x[:, :, :], ALU.add))
                    layer_norm(dve, link, x[:, :, :], y[:, :, :], sq[:, :, :], st, 1e-5)
                    affine(dve, link, x[:, :, :], per_tile(rows["l1a_g1"]), per_tile(rows["l1a_b1"]))
                    dve.sem_inc(vector_done, 1)
                    dve.wait_ge(tensor_done, 14)
                    dve.tensor_copy(halves(xT[0:D, :]), two(0, D)).then_inc(vector_done, 1)
                    dve.wait_ge(tensor_done, 17)
                    link(dve.tensor_tensor(y[:, :, :], tiles(6), x[:, :, :], ALU.add))
                    layer_norm(dve, link, x[:, :, :], y[:, :, :], sq[:, :, :], st, 1e-5)
                    affine(dve, link, x[:, :, :], per_tile(rows["l1a_g2"]), per_tile(rows["l1a_b2"]))
                    link(dve.tensor_tensor(h[:, :, :], h[:, :, :], x[:, :, :], ALU.add))

                @block.scalar
                def _(act):
                    act.wait_ge(vector_done, 3)
                    act.activation(flat, flat, ACT.Exp).then_inc(scalar_done, 1)
                    act.wait_ge(scalar_done, 1)
                    act.activation(flat, flat, ACT.Ln, bias=1.0).then_inc(scalar_done, 1)
                    for c in range(2):
                        act.wait_ge(tensor_done, 15 + c)
                        act.activation(halves(hT[:, c, :]), two(2 + 2 * c, 128), ACT.Gelu).then_inc(scalar_done, 1)

                @block.tensor
                def _(pe):
                    pe.wait_ge(vector_done, 1)
                    turn(pe, 0, x).then_inc(tensor_done, 1)
                    pe.wait_ge(vector_done, 2)
                    for t in range(T):
                        mm = pe.matmul(ps[0:Q, 2 + t // 2, 192 * (t % 2):192 * (t % 2) + 192], xT[:, Q * t:Q * t + Q],
                                       w["l1a_qkv"][:, :], start=True, stop=True)
                    mm.then_inc(tensor_done, 1)
                    pe.wait_ge(vector_done, 4)
                    turn(pe, 0, qk[:, :, 0, :]).then_inc(tensor_done, 1)
                    turn(pe, 5, qk[:, :, 1, :]).then_inc(tensor_done, 1)
                    pe.wait_ge(vector_done, 6)
                    for k, (bank, col) in enumerate(place):
                        for s in range(Q * k, S, 512):
                            e = min(S, s + 512)
                            at = bank + (s - Q * k) // 512
                            mm = pe.matmul(ps[0:Q, at, col:col + e - s], kT[:, Q * k:Q * k + Q], qT[:, s:e],
                                           start=True, stop=True)
                        mm.then_inc(tensor_done, 1)
                    pe.wait_ge(vector_done, 7)
                    for t in range(T):
                        for k in range(t + 1):
                            mm = pe.matmul(ps[0:Q, 6, 65 * t:65 * t + 65], sT[:, k, Q * t:Q * t + Q], v1[:, k, :],
                                           start=(k == 0), stop=(k == t))
                    mm.then_inc(tensor_done, 1)
                    pe.wait_ge(vector_done, 8)
                    turn(pe, 0, y).then_inc(tensor_done, 1)
                    pe.wait_ge(vector_done, 9)
                    by_token(pe, 2, yT, w["l1a_proj"][:, :]).then_inc(tensor_done, 1)
                    pe.wait_ge(vector_done, 10)
                    turn(pe, 0, x).then_inc(tensor_done, 1)
                    pe.wait_ge(vector_done, 11)
                    for c in range(2):
                        by_feature(pe, 2 + 2 * c, w["l1a_w1"][:, 128 * c:128 * c + 128], xT).then_inc(tensor_done, 1)
                    pe.wait_ge(scalar_done, 4)
                    for t in range(T):
                        dst = ps[0:Q, 6, D * t:D * t + D]
                        for c in range(2):
                            pe.matmul(dst, hT[:, c, Q * t:Q * t + Q], w["l1a_w2"][:, c, :], start=(c == 0), stop=False)
                        mm = pe.matmul(dst, ones[:, :], w["l1a_b2"][:, :], start=False, stop=True)
                    mm.then_inc(tensor_done, 1)

        def top_two(dve, link, values, top, index, where, hot):
            for t in range(T):
                link(dve.max(top[:, t, :], values[:, t, :]))
                link(dve.max_index(index[:, t, :], top[:, t, :], values[:, t, :]))
            link(dve.tensor_copy(where[:, :, :], index[:, :, 0:2]))
            for j in range(2):
                link(dve.tensor_tensor(hot[:, j, :, :], per_tile(iota8), wide(where[:, :, j:j + 1], [Q, T, 8]), ALU.is_equal))

        def layer1_ffn():
            with Stage("l1f") as sg:
                tensor_done, vector_done, scalar_done, vchain = (
                    sg.sem(n) for n in ("tensor_step", "vector_step", "scalar_step", "vector_chain"))
                up_ready, silu_ready, hidden_ready, down_ready, added = (
                    sg.sem(n) for n in ("up_ready", "silu_ready", "hidden_ready", "down_ready", "added"))
                qs = sg.sb("qs", [Q, T, 128])
                ro = sg.sb("ro", [Q, T, 6, 16])
                ra = sg.sb("ra", [Q, T, 6, 8])
                rb = sg.sb("rb", [Q, T, 6, 8])
                v1 = sg.sb("v1", [Q, T, 2, 32])
                ao = sg.sb("ao", [Q, T, D])
                probs = sg.sb("router_probs", [Q, T, 8])
                top = sg.sb("top", [Q, T, 8])
                index = sg.sb("index", [Q, T, 8], U32)
                where = sg.sb("where", [Q, T, 2])
                hot = sg.sb("hot", [Q, 2, T, 8])
                share = sg.sb("share", [Q, T, 8])
                silu = sg.sb("silu", [HP, 2, HALF])
                hidden = sg.sb("hidden", [HP, 2, 2, S])
                att = SplitAttention(nc, sg.st, "l1f_att", ps, 2, 2, ident16, ident, mask16, mask16_t, v1,
                                     lambda t: ao[:, t, :].rearrange("p (m d) -> p m d", m=4))
                sg.sems += att.sems
                block = sg.block()
                units = [(e, c, n) for e in range(8) for c in range(2) for n in range(2)]

                @block.sync
                def _(sp):
                    clear_previous(sp, sg.sems)

                @block.vector
                def _(dve):
                    link = Chain(dve, vchain)
                    layer_norm(dve, link, x[:, :, :], h[:, :, :], sq[:, :, :], st, 1e-5)
                    rms_norm(dve, link, y[:, :, :], x[:, :, :], sq[:, :, :], st, 1e-6, per_tile(rows["l1f_w1"]))
                    dve.sem_inc(vector_done, 1)
                    link(dve.memset(v1[:, :, :, :], 0.0))
                    link(dve.memset(v1[:, :, :, 16], 1.0))
                    dve.wait_ge(tensor_done, 1)
                    dve.tensor_copy(halves(yT[0:D, :]), two(0, D)).then_inc(vector_done, 1)
                    dve.wait_ge(tensor_done, 2)
                    flat = ps[0:Q, 2:4, :].rearrange("p b n -> p (b n)")[:, 0:768]
                    link(dve.tensor_copy(qs[:, :, :].rearrange("p t n -> p (t n)"), flat))
                    v6 = qs[:, :, 0:96].rearrange("p t (n d) -> p t n d", n=6)
                    first, second = v6[:, :, :, 0:8], v6[:, :, :, 8:16]
                    c6 = wide(cos_t[:, :, :].unsqueeze(2), [Q, T, 6, 8])
                    s6 = wide(sin_t[:, :, :].unsqueeze(2), [Q, T, 6, 8])
                    link(dve.tensor_tensor(ra[:, :, :, :], first, c6, ALU.mult))
                    link(dve.tensor_tensor(rb[:, :, :, :], second, s6, ALU.mult))
                    link(dve.tensor_tensor(ro[:, :, :, 0:8], ra[:, :, :, :], rb[:, :, :, :], ALU.subtract))
                    link(dve.tensor_tensor(ra[:, :, :, :], second, c6, ALU.mult))
                    link(dve.tensor_tensor(rb[:, :, :, :], first, s6, ALU.mult))
                    link(dve.tensor_tensor(ro[:, :, :, 8:16], ra[:, :, :, :], rb[:, :, :, :], ALU.add))
                    link(dve.tensor_scalar(ro[:, :, 0:4, :], ro[:, :, 0:4, :], 0.25, None, ALU.mult))
                    link(dve.tensor_copy(v1[:, :, :, 0:16], qs[:, :, 96:128].rearrange("p t (g d) -> p t g d", g=2)))
                    att.vector_stacks(dve, link, ro[:, :, 0:4, :], ro[:, :, 4:6, :])
                    att.vector(dve, link)
                    dve.wait_ge(tensor_done, 3)
                    dve.tensor_copy(halves(yT[0:D, :]), two(0, D)).then_inc(vector_done, 1)
                    dve.wait_ge(tensor_done, 4)
                    link(dve.tensor_tensor(x[:, :, :], tiles(2), x[:, :, :], ALU.add))
                    rms_norm(dve, link, y[:, :, :], x[:, :, :], sq[:, :, :], st, 1e-6, per_tile(rows["l1f_w2"]))
                    dve.sem_inc(vector_done, 1)
                    dve.wait_ge(tensor_done, 5)
                    dve.tensor_copy(halves(yT[0:D, :]), two(4, D)).then_inc(vector_done, 1)
                    dve.wait_ge(tensor_done, 6)
                    link(dve.tensor_copy(probs[:, :, :], tiles(6, 8)))
                    softmax_first(dve, link, probs[:, :, :], st)
                    dve.sem_inc(vector_done, 1)
                    dve.wait_ge(scalar_done, 1)
                    softmax_last(dve, link, probs[:, :, :], st)
                    top_two(dve, link, probs, top, index, where, hot)
                    total = st[:, 0, 0:T]
                    link(dve.scalar_tensor_tensor(total, top[:, :, 0], 1e-9, top[:, :, 1], ALU.add, ALU.add))
                    link(dve.reciprocal(total, total))
                    link(dve.tensor_tensor(share[:, :, :], hot[:, 0, :, :], hot[:, 1, :, :], ALU.add))
                    link(dve.tensor_tensor(share[:, :, :], share[:, :, :], probs[:, :, :], ALU.mult))
                    link(dve.tensor_tensor(share[:, :, :], share[:, :, :], wide(total.unsqueeze(2), [Q, T, 8]), ALU.mult))

                    def add_expert(e):
                        dve.wait_ge(down_ready, e + 1)
                        link(dve.tensor_tensor(sq[:, :, :], tiles(4 + e % 2), wide(share[:, :, e:e + 1], [Q, T, D]), ALU.mult))
                        dve.tensor_tensor(x[:, :, :], x[:, :, :], sq[:, :, :], ALU.add).then_inc(added, 1)
                        dve.wait_ge(added, e + 1)

                    for u, (e, c, n) in enumerate(units):
                        dve.wait_ge(silu_ready, u + 1)
                        if e >= 2 and c == n == 0:
                            dve.wait_ge(down_ready, e - 1)
                        dve.tensor_tensor(hidden[:, e % 2, c, HALF * n:HALF * n + HALF], silu[:, u % 2, :],
                                          ps[0:HP, 2 + u % 2, 0:HALF], ALU.mult).then_inc(hidden_ready, 1)
                        if c == n == 1 and e >= 1:
                            add_expert(e - 1)
                    add_expert(7)
                    link(dve.tensor_tensor(h[:, :, :], h[:, :, :], x[:, :, :], ALU.add))

                @block.scalar
                def _(act):
                    att.scalar(act)
                    act.wait_ge(vector_done, 6)
                    act.activation(probs[:, :, :], probs[:, :, :], ACT.Exp).then_inc(scalar_done, 1)
                    for u in range(len(units)):
                        act.wait_ge(up_ready, u + 1)
                        if u >= 2:
                            act.wait_ge(hidden_ready, u - 1)
                        act.activation(silu[:, u % 2, :], ps[0:HP, u % 2, 0:HALF], ACT.Silu).then_inc(silu_ready, 1)

                @block.tensor
                def _(pe):
                    pe.wait_ge(vector_done, 1)
                    turn(pe, 0, y).then_inc(tensor_done, 1)
                    pe.wait_ge(vector_done, 2)
                    for t in range(T):
                        mm = pe.matmul(ps[0:Q, 2 + t // 4, 128 * (t % 4):128 * (t % 4) + 128], yT[0:D, Q * t:Q * t + Q],
                                       w["l1f_qkv"][:, :], start=True, stop=True)
                    mm.then_inc(tensor_done, 1)
                    att.tensor(pe)
                    pe.wait_ge(att.out_ready, T)
                    turn(pe, 0, ao).then_inc(tensor_done, 1)
                    pe.wait_ge(vector_done, 3)
                    by_token(pe, 2, yT[0:D, :], w["l1f_wo"][:, :]).then_inc(tensor_done, 1)
                    pe.wait_ge(vector_done, 4)
                    turn(pe, 4, y).then_inc(tensor_done, 1)
                    pe.wait_ge(vector_done, 5)
                    by_token(pe, 6, yT[0:D, :], w["l1f_router"][:, :]).then_inc(tensor_done, 1)

                    def down(e):
                        pe.wait_ge(hidden_ready, 4 * e + 4)
                        if e >= 2:
                            pe.wait_ge(added, e - 1)
                        for t in range(T):
                            for c in range(2):
                                mm = pe.matmul(ps[0:Q, 4 + e % 2, D * t:D * t + D], hidden[:, e % 2, c, Q * t:Q * t + Q],
                                               w["l1f_w2"][:, e, c, :], start=(c == 0), stop=(c == 1))
                        mm.then_inc(down_ready, 1)

                    for u, (e, c, n) in enumerate(units):
                        if u >= 2:
                            pe.wait_ge(hidden_ready, u - 1)
                        for bank, m in ((u % 2, "l1f_w1"), (2 + u % 2, "l1f_w3")):
                            mm = pe.matmul(ps[0:HP, bank, 0:HALF], w[m][:, e, HP * c:HP * c + HP],
                                           yT[0:D, HALF * n:HALF * n + HALF], start=True, stop=True)
                        mm.then_inc(up_ready, 1)
                        if c == n == 1 and e >= 1:
                            down(e - 1)
                    down(7)

        def layer2_attention():
            H, R = 4, D // 2
            NT = S // R
            KC = (S + 127) // 128
            COLS = 6 * R
            SPREADS = 8
            with Stage("l2a") as sg:
                tensor_done, vector_done, scalar_done, vchain = (
                    sg.sem(n) for n in ("tensor_step", "vector_step", "scalar_step", "vector_chain"))
                pick_ready, folded, spread, spread_copied, paired, best_ready, exp_ready, total_ready, diagonal_ready, turned, \
                    turned_copied, product_ready = (sg.sem(n) for n in (
                        "pick_ready", "folded", "spread", "spread_copied", "paired_passes", "best_ready", "exp_ready", "total_ready",
                        "diagonal_ready", "turned", "turned_copied", "product_ready"))
                q = sg.sb("q", [128, NT, 16])
                kT = sg.sb("kT", [D, S])
                wvo = sg.sb("wvo", [D, H, D])
                vo = sg.sb("vo", [128, KC, H, D])
                pick = sg.sb("pick", [D, 16, H, R])
                keys = sg.sb("keys", [128, 16, S])
                score = sg.sb("score", [128, 4, S])
                taken = sg.sb("taken", [128, 2, S])
                weight = sg.sb("weight", [128, 4, S])
                diagonal = sg.sb("diagonal", [128, 2, 128])
                weightT = sg.sb("weightT", [128, 2, KC, 128])
                best = sg.sb("best", [128, 4, 8])
                neg_max = sg.sb("neg_max", [128, 4])
                total = sg.sb("total", [128, 4])
                block = sg.block()
                order = [t for p in (2, 3, 4, 5, 6, 7, 8, 1, 0) for t in (2 * p, 2 * p + 1)]
                pairs = [((i, order[i]), (i + 1, order[i + 1])) for i in range(0, NT, 2)]
                rows_of = lambda k, t: min(128, R * (t + 1) - 128 * k)

                @block.sync
                def _(sp):
                    clear_previous(sp, sg.sems)

                @block.vector
                def _(dve):
                    link = Chain(dve, vchain)
                    layer_norm(dve, link, x[:, :, :], h[:, :, :], sq[:, :, :], st, 1e-5)
                    dve.sem_inc(vector_done, 1)
                    dve.wait_ge(tensor_done, 1)
                    dve.tensor_copy(halves(xT[0:D, :]), two(0, D)).then_inc(vector_done, 1)
                    dve.wait_ge(tensor_done, 3)
                    dve.tensor_copy(q[:, :, :].rearrange("p t d -> p (t d)"), ps[:, 6, 0:16 * NT]).then_inc(vector_done, 1)
                    dve.wait_ge(vector_done, 3)

                    issued = [0]

                    def alternate(ins):
                        ins.then_inc(paired, 1)
                        issued[0] += 1
                        if issued[0] >= 2:
                            dve.wait_ge(paired, issued[0] - 1)

                    def weigh(i, t):
                        dve.wait_ge(exp_ready, i + 1)
                        e = weight[:, i % 4, 0:R * (t + 1)]
                        link(dve.scalar_tensor_tensor(e, taken[:, i % 2, 0:R * (t + 1)], 2 * NEG, e, ALU.is_le, ALU.mult,
                                                      accum_out=total[:, i % 4:i % 4 + 1]))
                        dve.reciprocal(total[:, i % 4:i % 4 + 1], total[:, i % 4:i % 4 + 1]).then_inc(total_ready, 1)

                    for p, pair in enumerate(pairs):
                        part = lambda buf, i, t: buf[:, i % 4, 0:R * (t + 1)]
                        dve.wait_ge(spread_copied, SPREADS * -(-R * (pair[1][1] + 1) // COLS))
                        if p >= 2:
                            dve.wait_ge(exp_ready, 2 * p - 2)
                        for i, t in pair:
                            alternate(dve.tensor_scalar(part(score, i, t), keys[:, 0, 0:R * (t + 1)], q[:, t, 0:1], None, ALU.add))
                        for d in range(1, 16):
                            for i, t in pair:
                                alternate(dve.scalar_tensor_tensor(part(score, i, t), keys[:, d, 0:R * (t + 1)],
                                                                   q[:, t, d:d + 1], part(score, i, t), ALU.add, ALU.max))
                        for i, t in pair:
                            diag = score[:, i % 4, R * t:R * t + R]
                            alternate(dve.tensor_tensor(diag, diag, causal32[:, :], ALU.add))
                        for i, t in pair:
                            alternate(dve.max(best[:, i % 4, :], part(score, i, t)))
                        for i, t in pair:
                            alternate(dve.tensor_scalar(neg_max[:, i % 4:i % 4 + 1], best[:, i % 4, 0:1], -1.0, None, ALU.mult))
                        dve.wait_ge(paired, issued[0])
                        dve.sem_inc(best_ready, 2)
                        if p >= 1:
                            for i, t in pairs[p - 1]:
                                weigh(i, t)
                            dve.wait_ge(total_ready, 2 * p)
                        for i, t in pair:
                            alternate(dve.match_replace(taken[:, i % 2, 0:R * (t + 1)], best[:, i % 4, :], part(score, i, t),
                                                        3 * NEG))
                    dve.wait_ge(paired, issued[0])
                    for i, t in pairs[-1]:
                        weigh(i, t)
                    dve.wait_ge(product_ready, NT)
                    link(dve.tensor_tensor(h[:, :, :], h[:, :, :], tiles(7), ALU.add))

                @block.scalar
                def _(act):
                    act.copy(pick[:, :, :, :], wide(ident[0:D, 0:D].rearrange("p (n d) -> p d n", n=H).unsqueeze(3),
                                                    [D, 16, H, R])).then_inc(pick_ready, 1)
                    act.wait_ge(folded, 1)
                    act.copy(wvo[:, :, :].rearrange("p n o -> p (n o)"), ps[0:D, 4, 0:H * D]).then_inc(scalar_done, 1)
                    act.wait_ge(tensor_done, 2)
                    act.copy(halves(kT[:, :]), two(2, D)).then_inc(scalar_done, 1)
                    act.wait_ge(tensor_done, 4)
                    flat = vo[:, :, :, :].rearrange("p k n o -> p (k n o)")
                    act.copy(flat[:, 0:1024], ps[:, 4:6, :].rearrange("p b n -> p (b n)")).then_inc(scalar_done, 1)
                    act.copy(flat[0:S - 512, 1024:1280], ps[0:S - 512, 7, 0:256]).then_inc(scalar_done, 1)

                    def spread_out(s):
                        act.wait_ge(spread, s + 1)
                        c, d = s // SPREADS, 2 * (s % SPREADS)
                        act.copy(keys[:, d:d + 2, COLS * c:COLS * c + COLS],
                                 ps[:, s % 2, 0:2 * COLS].rearrange("p (d n) -> p d n", d=2)).then_inc(spread_copied, 1)

                    def diagonal_out(i):
                        act.wait_ge(total_ready, i + 1)
                        if i >= 2:
                            act.wait_ge(turned, i - 1)
                        act.activation(diagonal[:, i % 2, :], ident[:, :], ACT.Copy,
                                       scale=total[:, i % 4:i % 4 + 1]).then_inc(diagonal_ready, 1)

                    def turned_out(i, t):
                        act.wait_ge(turned, i + 1)
                        if i >= 2:
                            act.wait_ge(product_ready, i - 1)
                        full, b = R * (t + 1) // 128, 2 + 2 * (i % 2)
                        src = ps[:, b:b + 2, :].rearrange("p b (k n) -> p (b k) n", n=128)
                        if full:
                            act.copy(weightT[:, i % 2, 0:full, :], src[:, 0:full, :]).then_inc(turned_copied, 1)
                        else:
                            act.sem_inc(turned_copied, 1)
                        if R * (t + 1) % 128:
                            r = rows_of(full, t)
                            act.copy(weightT[0:r, i % 2, full, :], src[0:r, full, :]).then_inc(turned_copied, 1)
                        else:
                            act.sem_inc(turned_copied, 1)

                    for s in range(SPREADS):
                        spread_out(s)
                    for p, pair in enumerate(pairs):
                        if p < 2:
                            for s in range(SPREADS * (p + 1), SPREADS * (p + 2)):
                                spread_out(s)
                        for i, t in pair:
                            act.wait_ge(best_ready, 2 * p + 2)
                            if i >= 4:
                                act.wait_ge(turned, i - 3)
                            act.activation(weight[:, i % 4, 0:R * (t + 1)], score[:, i % 4, 0:R * (t + 1)], ACT.Exp,
                                           bias=neg_max[:, i % 4:i % 4 + 1]).then_inc(exp_ready, 1)
                        if p >= 1:
                            for i, t in pairs[p - 1]:
                                diagonal_out(i)
                                turned_out(i, t)
                    for i, t in pairs[-1]:
                        diagonal_out(i)
                        turned_out(i, t)

                @block.tensor
                def _(pe):
                    for n in range(H):
                        mm = pe.matmul(ps[0:D, 4, D * n:D * n + D], w["l2a_v"][:, n, :], w["l2a_o"][:, n, :], start=True, stop=True)
                    mm.then_inc(folded, 1)
                    pe.wait_ge(vector_done, 1)
                    turn(pe, 0, x).then_inc(tensor_done, 1)
                    pe.wait_ge(vector_done, 2)
                    xf = xT[0:D, :]
                    by_feature(pe, 2, w["l2a_k"][:, :], xf).then_inc(tensor_done, 1)
                    for t in range(NT):
                        for n in range(H):
                            mm = pe.matmul(ps[R * n:R * n + R, 6, 16 * t:16 * t + 16], xf[:, R * t:R * t + R],
                                           w["l2a_q"][:, 16 * n:16 * n + 16], start=True, stop=True)
                    mm.then_inc(tensor_done, 1)
                    pe.wait_ge(scalar_done, 1)
                    for k in range(KC):
                        n = min(128, S - 128 * k)
                        dst = ps[0:n, 4 + k // 2, 256 * (k % 2):256 * (k % 2) + 256] if k < 4 else ps[0:n, 7, 0:256]
                        mm = pe.matmul(dst, xf[:, 128 * k:128 * k + n], wvo[:, :, :], start=True, stop=True)
                    mm.then_inc(tensor_done, 1)
                    pe.wait_ge(scalar_done, 2)
                    pe.wait_ge(pick_ready, 1)

                    def spread_in(s):
                        if s >= 2:
                            pe.wait_ge(spread_copied, s - 1)
                        c = s // SPREADS
                        for j in range(2):
                            d = 2 * (s % SPREADS) + j
                            mm = pe.matmul(ps[:, s % 2, COLS * j:COLS * j + COLS],
                                           pick[:, d, :, :].rearrange("p n i -> p (n i)"),
                                           kT[:, COLS * c:COLS * c + COLS], start=True, stop=True)
                        mm.then_inc(spread, 1)

                    def turn_weights(i, t):
                        pe.wait_ge(diagonal_ready, i + 1)
                        if i == 0:
                            pe.wait_ge(scalar_done, 4)
                        if i >= 2:
                            pe.wait_ge(turned_copied, 2 * i - 2)
                        b = 2 + 2 * (i % 2)
                        dst = ps[:, b:b + 2, :].rearrange("p b (k n) -> p (b k) n", n=128)
                        for k in range(-(-R * (t + 1) // 128)):
                            r = rows_of(k, t)
                            mm = pe.matmul(dst[0:r, k, :], weight[:, i % 4, 128 * k:128 * k + r], diagonal[:, i % 2, :],
                                           start=True, stop=True)
                        mm.then_inc(turned, 1)

                    def products(i, t):
                        pe.wait_ge(turned_copied, 2 * i + 2)
                        chunks = range(-(-R * (t + 1) // 128))
                        out = ps[R * (t % 3):R * (t % 3) + R, 7, D * (t // 3):D * (t // 3) + D]
                        for k in chunks:
                            for n in range(H):
                                r = rows_of(k, t)
                                mm = pe.matmul(out, weightT[0:r, i % 2, k, R * n:R * n + R], vo[0:r, k, n, :],
                                               start=(k == n == 0), stop=(k == chunks[-1] and n == H - 1))
                        mm.then_inc(product_ready, 1)

                    for s in range(SPREADS):
                        spread_in(s)
                    for p, pair in enumerate(pairs):
                        if p < 2:
                            for s in range(SPREADS * (p + 1), SPREADS * (p + 2)):
                                spread_in(s)
                        if p >= 1:
                            for i, t in pairs[p - 1]:
                                turn_weights(i, t)
                            for i, t in pairs[p - 1]:
                                products(i, t)
                    for i, t in pairs[-1]:
                        turn_weights(i, t)
                    for i, t in pairs[-1]:
                        products(i, t)

        def layer3_attention():
            with Stage("l3a") as sg:
                tensor_done, vector_done, scalar_done, vchain = (
                    sg.sem(n) for n in ("tensor_step", "vector_step", "scalar_step", "vector_chain"))
                qT = sg.sb("qT", [D, S])
                kT = sg.sb("kT", [D, S])
                v = sg.sb("v", [Q, T, D])
                o = sg.sb("o", [Q, T, D])
                att = Attention(nc, sg.st, "l3a_att", ps, 1, D, False,
                                lambda m, t: qT[:, Q * t:Q * t + Q], lambda m, s, e: kT[:, s:e],
                                lambda m, k: v[:, k, :], lambda t: o[:, t:t + 1, :])
                sg.sems += att.sems
                block = sg.block()

                @block.sync
                def _(sp):
                    clear_previous(sp, sg.sems)

                @block.vector
                def _(dve):
                    link = Chain(dve, vchain)
                    layer_norm(dve, link, x[:, :, :], h[:, :, :], sq[:, :, :], st, 1e-5)
                    dve.sem_inc(vector_done, 1)
                    dve.wait_ge(tensor_done, 1)
                    dve.tensor_copy(halves(xT[0:D, :]), two(0, D)).then_inc(vector_done, 1)
                    dve.wait_ge(tensor_done, 3)
                    dve.tensor_copy(halves(kT[:, :]), two(4, D)).then_inc(vector_done, 1)
                    att.vector(dve, link)
                    dve.wait_ge(att.out_ready, T)
                    link(dve.tensor_tensor(h[:, :, :], h[:, :, :], o[:, :, :], ALU.add))

                @block.scalar
                def _(act):
                    act.wait_ge(tensor_done, 2)
                    act.mul(halves(qT[:, :]), two(2, D), 0.125).then_inc(scalar_done, 1)
                    act.wait_ge(tensor_done, 4)
                    act.copy(v[:, :, :], tiles(6)).then_inc(scalar_done, 1)
                    att.scalar(act)

                @block.tensor
                def _(pe):
                    pe.wait_ge(vector_done, 1)
                    turn(pe, 0, x).then_inc(tensor_done, 1)
                    pe.wait_ge(vector_done, 2)
                    by_feature(pe, 2, w["l3a_qkv"][:, 0:64], xT).then_inc(tensor_done, 1)
                    by_feature(pe, 4, w["l3a_qkv"][:, 64:128], xT).then_inc(tensor_done, 1)
                    by_token(pe, 6, xT, w["l3a_qkv"][:, 128:192]).then_inc(tensor_done, 1)
                    pe.wait_ge(vector_done, 3)
                    pe.wait_ge(scalar_done, 2)
                    att.tensor(pe, ident)

        def moe_layer(name, bias_row, router, w1, b1, w2, b2, soft):
            with Stage(name) as sg:
                tensor_done, vector_done, scalar_done, vchain = (
                    sg.sem(n) for n in ("tensor_step", "vector_step", "scalar_step", "vector_chain"))
                up_ready, hidden_ready, down_ready, added = (
                    sg.sem(n) for n in ("up_ready", "hidden_ready", "down_ready", "added"))
                logits = sg.sb("logits", [Q, T, 8])
                top = sg.sb("top", [Q, T, 8])
                index = sg.sb("index", [Q, T, 8], U32)
                where = sg.sb("where", [Q, T, 2])
                hot = sg.sb("hot", [Q, 2, T, 8])
                share = sg.sb("share", [Q, T, 8])
                shareT = sg.sb("shareT", [8, S])
                second = sg.sb("second", [Q, T])
                hidden = sg.sb("hidden", [128, 2, S])
                acc = sg.sb("acc", [Q, T, D])
                block = sg.block()

                @block.sync
                def _(sp):
                    clear_previous(sp, sg.sems)

                @block.vector
                def _(dve):
                    link = Chain(dve, vchain)
                    layer_norm(dve, link, x[:, :, :], h[:, :, :], sq[:, :, :], st, 1e-5)
                    if soft:
                        layer_norm(dve, link, y[:, :, :], x[:, :, :], sq[:, :, :], st, 1e-5)
                        affine(dve, link, y[:, :, :], per_tile(rows["l3f_g"]), per_tile(rows["l3f_b"]))
                    dve.sem_inc(vector_done, 1)
                    dve.wait_ge(tensor_done, 1)
                    dve.tensor_copy(halves(xT[0:D, :]), two(0, D)).then_inc(vector_done, 1)
                    dve.wait_ge(tensor_done, 2)
                    link(dve.tensor_tensor(logits[:, :, :], tiles(6, 8), per_tile(rows[bias_row]), ALU.add))
                    top_two(dve, link, logits, top, index, where, hot)
                    if soft:
                        link(dve.tensor_tensor(second[:, :], top[:, :, 1], top[:, :, 0], ALU.subtract))
                        dve.sem_inc(vector_done, 1)
                        dve.wait_ge(scalar_done, 1)
                        first = st[:, 0, 0:T]
                        link(dve.tensor_scalar(first, second[:, :], 1.0, None, ALU.add))
                        link(dve.reciprocal(first, first))
                        link(dve.tensor_tensor(second[:, :], second[:, :], first, ALU.mult))
                        for j, part in enumerate((first, second[:, :])):
                            link(dve.tensor_tensor(hot[:, j, :, :], hot[:, j, :, :], wide(part.unsqueeze(2), [Q, T, 8]), ALU.mult))
                    else:
                        dve.sem_inc(vector_done, 1)
                    link(dve.tensor_tensor(share[:, :, :], hot[:, 0, :, :], hot[:, 1, :, :], ALU.add))
                    dve.sem_inc(vector_done, 1)
                    for e in range(8):
                        dve.wait_ge(down_ready, e + 1)
                        wide_share = wide(share[:, :, e:e + 1], [Q, T, D])
                        if e == 0:
                            dve.tensor_tensor(acc[:, :, :], tiles(4), wide_share, ALU.mult).then_inc(added, 1)
                        else:
                            link(dve.tensor_tensor(sq[:, :, :], tiles(4 + e % 2), wide_share, ALU.mult))
                            dve.tensor_tensor(acc[:, :, :], acc[:, :, :], sq[:, :, :], ALU.add).then_inc(added, 1)
                        dve.wait_ge(added, e + 1)
                    dve.wait_ge(tensor_done, 3)
                    dve.tensor_copy(halves(shareT[:, :]), two(2, 8)).then_inc(vector_done, 1)
                    link(dve.tensor_tensor(h[:, :, :], h[:, :, :], acc[:, :, :], ALU.add))
                    dve.wait_ge(tensor_done, 4)
                    link(dve.tensor_tensor(h[:, :, :], h[:, :, :], tiles(7), ALU.add))

                @block.scalar
                def _(act):
                    if soft:
                        act.wait_ge(vector_done, 3)
                        act.activation(second[:, :], second[:, :], ACT.Exp).then_inc(scalar_done, 1)
                    for u in range(16):
                        e, n = u // 2, u % 2
                        act.wait_ge(up_ready, u + 1)
                        if e >= 2:
                            act.wait_ge(down_ready, e - 1)
                        act.activation(hidden[:, e % 2, HALF * n:HALF * n + HALF], ps[:, n, 0:HALF], ACT.Gelu,
                                       bias=b1[:, e:e + 1]).then_inc(hidden_ready, 1)

                @block.tensor
                def _(pe):
                    pe.wait_ge(vector_done, 1)
                    turn(pe, 0, y if soft else x).then_inc(tensor_done, 1)
                    pe.wait_ge(vector_done, 2)
                    by_token(pe, 6, xT[0:D, :], router[:, :]).then_inc(tensor_done, 1)

                    def down(e):
                        pe.wait_ge(hidden_ready, 2 * e + 2)
                        if e >= 2:
                            pe.wait_ge(added, e - 1)
                        by_token(pe, 4 + e % 2, hidden[:, e % 2, :], w2[:, e, :]).then_inc(down_ready, 1)

                    for u in range(16):
                        e, n = u // 2, u % 2
                        if u >= 2:
                            pe.wait_ge(hidden_ready, u - 1)
                        pe.matmul(ps[:, n, 0:HALF], w1[:, e, :], xT[0:D, HALF * n:HALF * n + HALF],
                                  start=True, stop=True).then_inc(up_ready, 1)
                        if n == 1 and e >= 1:
                            down(e - 1)
                    down(7)
                    pe.wait_ge(vector_done, 4)
                    turn(pe, 2, share, 8).then_inc(tensor_done, 1)
                    pe.wait_ge(vector_done, 5)
                    by_token(pe, 7, shareT, b2[:, :]).then_inc(tensor_done, 1)

        def row1(ap, n, p=Q):
            return wide(ap.rearrange("(a n) -> a n", a=1), [p, n])

        with Stage("load") as sg:
            loaded = sg.sem("loaded")
            zeroed = sg.sem("zeroed")
            tables_loaded = sg.sem("tables_loaded")
            block = sg.block()
            count = [0]

            @block.vector
            def _(dve):
                for n in ("l0f_qkv", "l0f_gate", "l0f_fc1", "l0f_fc2"):
                    dve.memset(w[n][:], 0.0).then_inc(zeroed, 1)
                dve.memset(ones[:, :], 1.0).then_inc(zeroed, 1)
                dve.memset(xT[D:D + 1, :], 1.0).then_inc(zeroed, 1)
                dve.memset(yT[D:D + 1, :], 1.0).then_inc(zeroed, 1)
                dve.wait_ge(tables_loaded, 48)
                dve.tensor_copy(ident16[:, :], ident[0:Q, 0:Q])
                dve.tensor_copy(mask16[:, :], causal[:, :])
                dve.tensor_scalar(mask16_t[:, :], keep[:, :], -1.0, -NEG, ALU.add, ALU.mult)

            @block.sync
            def _(sp):
                def load(dst, src):
                    sp.dma_start(dst, src).then_inc(loaded, 16)
                    count[0] += 16

                for dst, src in ((ident, "c_ident"), (causal, "c_causal"), (keep, "c_keep")):
                    sp.dma_start(dst[:, :], a[src]).then_inc(tables_loaded, 16)
                load(iota8[:, :], a["c_iota8"])
                load(cos_t[:, :, :], a["c_cos"])
                load(sin_t[:, :, :], a["c_sin"])
                load(strip[:, :], a["bias_strip"])
                load(att_scale[:, :], row1(a["L0_attn_scale"], 1))
                for n, src in (("l0a_g1", "L0_attn_ln1_g"), ("l0a_b1", "L0_attn_ln1_b"), ("l0a_g2", "L0_attn_ln2_g"),
                               ("l0a_b2", "L0_attn_ln2_b"), ("l1a_g1", "L1_attn_ln1_g"), ("l1a_b1", "L1_attn_ln1_b"),
                               ("l1a_g2", "L1_attn_ln2_g"), ("l1a_b2", "L1_attn_ln2_b"), ("l1f_w1", "L1_ffn_ln1_w"),
                               ("l1f_w2", "L1_ffn_ln2_w"), ("l3f_g", "L3_ffn_gamma"), ("l3f_b", "L3_ffn_beta"),
                               ("l0f_g", "L0_ffn_ln_g"), ("l0f_b", "L0_ffn_ln_b"), ("l0f_fg", "L0_ffn_fnorm_g"),
                               ("l0f_fb", "L0_ffn_fnorm_b"), ("l2f_bg", "L2_ffn_bg"), ("l3f_br", "L3_ffn_br")):
                    load(rows[n][:, :], row1(a[src], rows[n].shape[1]))
                load(rows["l0f_gate"][:, :], row1(a["L0_ffn_gate_b"].rearrange("n e -> (n e)"), 16))

                def with_bias(n, weight, bias):
                    load(w[n][0:D, :], weight)
                    load(w[n][D:D + 1, :], bias.rearrange("(a n) -> a n", a=1))

                with_bias("l0a_qkv", a["L0_attn_qkv_w"], a["L0_attn_qkv_b"])
                with_bias("l0a_proj", a["L0_attn_proj_w"], a["L0_attn_proj_b"])
                with_bias("l0f_hl", a["hl_wT"], a["L0_ffn_hl_b"].rearrange("n d -> (n d)"))
                with_bias("l1a_qkv", a["L1_attn_qkv_w"], a["L1_attn_qkv_b"])
                with_bias("l1a_proj", a["L1_attn_proj_w"], a["L1_attn_proj_b"])
                with_bias("l1a_w1", a["L1_attn_w1"], a["L1_attn_b1"])
                for j, n in enumerate("qkv"):
                    load(w["l3a_qkv"][0:D, 64 * j:64 * j + 64], a["L3_attn_W" + n])
                    load(w["l3a_qkv"][D:D + 1, 64 * j:64 * j + 64], a["L3_attn_b" + n].rearrange("(a n) -> a n", a=1))
                load(w["l1a_w2"][:, :, :], a["L1_attn_w2"].rearrange("(c p) n -> p c n", p=128))
                load(w["l1a_b2"][:, :], a["L1_attn_b2"].rearrange("(a n) -> a n", a=1))
                load(w["l1f_qkv"][:, 0:64], a["l1_wqT"])
                load(w["l1f_qkv"][:, 64:96], a["l1_wkT"])
                load(w["l1f_qkv"][:, 96:128], a["l1_wvT"])
                load(w["l1f_wo"][:, :], a["l1_woT"])
                load(w["l1f_router"][:, :], a["l1_routerT"])
                load(w["l1f_w1"][:, :, :], a["l1_w1T"])
                load(w["l1f_w3"][:, :, :], a["l1_w3T"])
                load(w["l1f_w2"][:, :, :, :], a["l1_w2T"].rearrange("e (c p) n -> p e c n", p=HP))
                for n in "qk":
                    load(w["l2a_" + n][:, :], a["l2_w%sT" % n])
                for n in "vo":
                    load(w["l2a_" + n][:, :, :], a["l2_w%s_heads" % n])
                load(causal32[:, :], a["c_causal32"])
                load(w["l2f_g"][:, :], a["L2_ffn_Wg"])
                load(w["l3f_r"][:, :], a["L3_ffn_Wr"])
                for l in "23":
                    load(w[f"l{l}f_w1"][:, :, :], a[f"L{l}_ffn_W1"].rearrange("e d h -> d e h"))
                    load(w[f"l{l}f_w2"][:, :, :], a[f"L{l}_ffn_W2"].rearrange("e h d -> h e d"))
                    load(w[f"l{l}f_b2"][:, :], a[f"L{l}_ffn_b2"])
                    load(w[f"l{l}f_b1"][:, :], a[f"l{l}_b1T"])
                sp.wait_ge(zeroed, 7)
                for n in range(4):
                    r = slice(16 * n, 16 * n + 16)
                    load(w["l0f_qkv"][r, 64 * n:64 * n + 64], a["l0_wqT"][n].rearrange("d e o -> d (e o)"))
                    load(w["l0f_qkv"][r, 256 + 16 * n:272 + 16 * n], a["l0_wkT"][n])
                    load(w["l0f_qkv"][r, 320 + 16 * n:336 + 16 * n], a["l0_wvT"][n])
                    load(w["l0f_gate"][64 * (n % 2):64 * (n % 2) + 64, n // 2, 4 * (n % 2):4 * (n % 2) + 4],
                         a["l0_gateT"][n])
                    load(w["l0f_fc1"][r, r], a["l0_fc1T"])
                    load(w["l0f_fc2"][r, r], a["l0_fc2T"])
                    load(w["l0f_fc1"][D:D + 1, r], a["L0_ffn_fc1_b"].rearrange("(a n) -> a n", a=1))
                    load(w["l0f_fc2"][D:D + 1, r], a["L0_ffn_fc2_b"].rearrange("(a n) -> a n", a=1))
                load(w["l0f_fgate"][:, :], a["l0_fgateT"])
                sp.wait_ge(loaded, count[0])

        fourier(nc, a, ps, ident, h_in, Stage, clear_previous, end_of_pass)
        text(nc, a, ps, ident, h_in, Stage, clear_previous)
        if upto == 0:
            return dump(nc, Stage, clear_previous, h_in, out)

        with nc.Fori(0, B) as b:
            with Stage("l0a") as sg:
                loaded = sg.sem("h_loaded")
                tensor_done = sg.sem("tensor_step")
                vector_done = sg.sem("vector_step")
                scalar_done = sg.sem("scalar_step")
                vchain = sg.sem("vector_chain")
                stored = sg.sem("stored")
                qT = sg.sb("qT", [D, S])
                kT = sg.sb("kT", [D, S])
                v = sg.sb("v", [Q, T, D])
                o = sg.sb("o", [Q, T, D])
                att = Attention(nc, sg.st, "l0a_att", ps, 1, D, False,
                                lambda m, t: qT[:, Q * t:Q * t + Q], lambda m, s, e: kT[:, s:e],
                                lambda m, k: v[:, k, :], lambda t: o[:, t:t + 1, :],
                                strip=lambda t: strip[:, S - Q - Q * t:S - Q - Q * t + S])
                sg.sems += att.sems
                block = sg.block()

                @block.sync
                def _(sp):
                    clear_previous(sp, sg.sems)
                    sp.dma_start(h[:, :, :], tokens(h_in, b)).then_inc(loaded, 16)
                    sp.wait_ge(vector_done, 6)
                    sp.dma_start(tokens(h_mid, b), h[:, :, :]).then_inc(stored, 16)
                    sp.wait_ge(vector_done, 9)
                    sp.dma_start(tokens(sx_all, b), y[:, :, :]).then_inc(stored, 16)
                    sp.wait_ge(stored, 32)

                @block.vector
                def _(dve):
                    link = Chain(dve, vchain)
                    dve.wait_ge(loaded, 16)
                    layer_norm(dve, link, x[:, :, :], h[:, :, :], sq[:, :, :], st, 1e-5)
                    layer_norm(dve, link, y[:, :, :], x[:, :, :], sq[:, :, :], st, 1e-5)
                    link(dve.tensor_tensor(y[:, :, :], y[:, :, :], wide(rows["l0a_g1"][:, :].unsqueeze(1), [Q, T, D]), ALU.mult))
                    dve.tensor_tensor(y[:, :, :], y[:, :, :], wide(rows["l0a_b1"][:, :].unsqueeze(1), [Q, T, D]),
                                      ALU.add).then_inc(vector_done, 1)
                    dve.wait_ge(tensor_done, 1)
                    dve.tensor_copy(halves(xT[0:D, :]), two(0, D)).then_inc(vector_done, 1)
                    dve.wait_ge(tensor_done, 3)
                    dve.tensor_copy(halves(kT[:, :]), two(4, D)).then_inc(vector_done, 1)
                    att.vector(dve, link)
                    dve.wait_ge(att.out_ready, T)
                    dve.wait_ge(tensor_done, 5)
                    dve.tensor_copy(halves(yT[0:D, :]), two(0, D)).then_inc(vector_done, 1)
                    dve.wait_ge(tensor_done, 6)
                    link(dve.tensor_scalar(y[:, :, :], tiles(2), 1.0, None, ALU.mult))
                    layer_norm(dve, link, x[:, :, :], y[:, :, :], sq[:, :, :], st, 1e-5)
                    link(dve.tensor_tensor(x[:, :, :], x[:, :, :], wide(rows["l0a_g2"][:, :].unsqueeze(1), [Q, T, D]), ALU.mult))
                    link(dve.tensor_tensor(x[:, :, :], x[:, :, :], wide(rows["l0a_b2"][:, :].unsqueeze(1), [Q, T, D]), ALU.add))
                    link(dve.tensor_tensor(h[:, :, :], h[:, :, :], x[:, :, :], ALU.add))
                    dve.sem_inc(vector_done, 2)
                    layer_norm(dve, link, x[:, :, :], h[:, :, :], sq[:, :, :], st, 1e-5)
                    dve.sem_inc(vector_done, 1)
                    dve.wait_ge(tensor_done, 7)
                    dve.tensor_copy(halves(xT[0:D, :]), two(4, D)).then_inc(vector_done, 1)
                    dve.wait_ge(tensor_done, 8)
                    dve.tensor_copy(y[:, :, :], tiles(6)).then_inc(vector_done, 1)

                @block.scalar
                def _(act):
                    act.wait_ge(tensor_done, 2)
                    act.copy(halves(qT[:, :]), two(2, D)).then_inc(scalar_done, 1)
                    act.wait_ge(tensor_done, 4)
                    act.activation(v[:, :, :], tiles(6), ACT.Copy, scale=att_scale[:, :]).then_inc(scalar_done, 1)
                    att.scalar(act)

                @block.tensor
                def _(pe):
                    pe.wait_ge(vector_done, 1)
                    turn(pe, 0, y).then_inc(tensor_done, 1)
                    pe.wait_ge(vector_done, 2)
                    by_feature(pe, 2, w["l0a_qkv"][:, 0:64], xT).then_inc(tensor_done, 1)
                    by_feature(pe, 4, w["l0a_qkv"][:, 64:128], xT).then_inc(tensor_done, 1)
                    by_token(pe, 6, xT, w["l0a_qkv"][:, 128:192]).then_inc(tensor_done, 1)
                    pe.wait_ge(vector_done, 3)
                    pe.wait_ge(scalar_done, 2)
                    att.tensor(pe, ident)
                    pe.wait_ge(att.out_ready, T)
                    turn(pe, 0, o).then_inc(tensor_done, 1)
                    pe.wait_ge(vector_done, 4)
                    by_token(pe, 2, yT, w["l0a_proj"][:, :]).then_inc(tensor_done, 1)
                    pe.wait_ge(vector_done, 7)
                    turn(pe, 4, x).then_inc(tensor_done, 1)
                    pe.wait_ge(vector_done, 8)
                    by_token(pe, 6, xT, w["l0f_hl"][:, :]).then_inc(tensor_done, 1)

            end_of_pass("l0a_end")

        if upto == 1:
            return dump(nc, Stage, clear_previous, h_mid, out)
        if upto == 2:
            return dump(nc, Stage, clear_previous, sx_all, out)

        with Stage("resid") as sg:
            loaded = sg.sem("loaded")
            block = sg.block()

            @block.sync
            def _(sp):
                clear_previous(sp, sg.sems)
                for n in range(4):
                    sp.dma_start(resid[:, :, 16 * n:16 * n + 16],
                                 sx_all[n].rearrange("(t p) d -> p t d", p=Q)[:, :, 16 * n:16 * n + 16]).then_inc(loaded, 16)
                sp.wait_ge(loaded, 64)

        with nc.Fori(0, B) as b:
            layer0_ffn(b)
            if upto >= 4:
                layer1_attention()
            if upto >= 5:
                layer1_ffn()
            if upto >= 6:
                layer2_attention()
            if upto >= 7:
                moe_layer("l2f", "l2f_bg", w["l2f_g"], w["l2f_w1"], w["l2f_b1"], w["l2f_w2"], w["l2f_b2"], False)
            if upto >= 8:
                layer3_attention()
            if upto >= 9:
                moe_layer("l3f", "l3f_br", w["l3f_r"], w["l3f_w1"], w["l3f_b1"], w["l3f_w2"], w["l3f_b2"], True)
            with Stage("store") as sg:
                stored = sg.sem("stored")
                block = sg.block()

                @block.sync
                def _(sp):
                    clear_previous(sp, sg.sems)
                    sp.dma_start(tokens(out, b), h[:, :, :]).then_inc(stored, 16)
                    sp.wait_ge(stored, 16)

            end_of_pass("pass_end")


def tokens(dram, b):
    return dram[bass.ds(b, 1)].rearrange("a (t p) n -> p (a t) n", p=Q)


def dump(nc, Stage, clear_previous, src, out):
    with Stage("dump") as sg:
        done = sg.sem("done")
        block = sg.block()

        @block.sync
        def _(sp):
            sp.dma_start(out, src).then_inc(done, 16)
            sp.wait_ge(done, 16)


def fourier(nc, a, ps, ident, h_in, Stage, clear_previous, end_of_pass):
    NX = G // 2
    with ExitStack() as keepers:
        def sb(name, shape, dt=F32):
            return keepers.enter_context(nc.sbuf_tensor("fno_" + name, shape, dt))

        field = sb("field", [128, NX, 128])
        y_fwd = sb("y_fwd", [128, 48])
        x_fwd = sb("x_fwd", [128, 48])
        x_inv = sb("x_inv", [48, 128])
        y_inv = sb("y_inv", [96, 256])
        feats = sb("feats", [7, G * G])
        lift = sb("lift", [7, 128])
        mixw = sb("mixw", [128, C, 144])
        w1T = sb("w1T", [C, C])
        w2bd = sb("w2bd", [128, 128])
        b1 = sb("b1", [128, 1])
        b2row = sb("b2row", [128, 128])
        by_y = sb("by_y", [128, 24, G])
        by_yT = sb("by_yT", [128, KY, 128])
        modes = sb("modes", [128, B, KY, 2, 6])
        modes_i = sb("modes_i", [128, B, KY, 2, 6])
        mixed = sb("mixed", [C, B, KY, 2, KX])
        convd = sb("convd", [48, KY, 128])
        by_x = sb("by_x", [128, G, 24])
        by_xT = sb("by_xT", [96, 16, 128])
        act_g = sb("act_g", [128, G * G])
        q1 = sb("q1", [128, 16])
        q2 = sb("q2", [16, 4])
        q1b = sb("q1b", [16, 1])
        q2b = sb("q2b", [4, 1])

        with Stage("lift") as sg:
            loaded = sg.sem("loaded")
            zeroed = sg.sem("zeroed")
            lifted = sg.sem("lifted")
            block = sg.block()

            @block.vector
            def _(pool):
                pool.memset(lift[:, :], 0.0).then_inc(zeroed, 1)
                pool.memset(w2bd[:, :], 0.0).then_inc(zeroed, 1)
                pool.memset(q1[:, :], 0.0).then_inc(zeroed, 1)
                pool.memset(q2[:, :], 0.0).then_inc(zeroed, 1)

            @block.sync
            def _(sp):
                clear_previous(sp, sg.sems)
                n = 0
                for dst, src in ((y_fwd[:, :], a["c_y_fwd"]), (x_fwd[:, :], a["c_x_fwd"]), (x_inv[:, :], a["c_x_inv"]),
                                 (y_inv[:, :], a["c_y_inv"]), (feats[0:B, :], a["x"].rearrange("b x y a -> b (x y a)")),
                                 (feats[B:7, :], a["c_grid"])):
                    sp.dma_start(dst, src).then_inc(loaded, 16)
                    n += 16
                sp.wait_ge(zeroed, 4)
                for b in range(B):
                    cs = slice(C * b, C * b + C)
                    pairs = [(lift[b:b + 1, cs], a["p_wT"][0:1, :]), (lift[4:6, cs], a["p_wT"][1:3, :]),
                             (lift[6:7, cs], a["L0_tok_p_b"].rearrange("(a n) -> a n", a=1)),
                             (q1[cs, 4 * b:4 * b + 4], a["q1_T"]), (q2[4 * b:4 * b + 4, b:b + 1], a["q2_T"]),
                             (q1b[4 * b:4 * b + 4, :], a["L0_tok_q1_b"].rearrange("(n a) -> n a", a=1)),
                             (q2b[b:b + 1, :], a["L0_tok_q2_b"].rearrange("(n a) -> n a", a=1))]
                    for dst, src in pairs:
                        sp.dma_start(dst, src).then_inc(loaded, 16)
                        n += 16
                assert n == 16 * 34
                sp.wait_ge(loaded, n)

            @block.tensor
            def _(pe):
                pe.wait_ge(loaded, 16 * 34)
                for i in range(NX):
                    mm = pe.matmul(ps[:, i // 4, 128 * (i % 4):128 * (i % 4) + 128], feats[:, 128 * i:128 * i + 128],
                                   lift[:, :], start=True, stop=True)
                    if i % 4 == 3:
                        mm.then_inc(lifted, 1)

            @block.vector
            def _(dve):
                for k in range(8):
                    dve.wait_ge(lifted, k + 1)
                    dve.tensor_copy(field[:, 4 * k:4 * k + 4, :].rearrange("p a n -> p (a n)"), ps[:, k, :])

        with nc.Fori(0, 4) as layer:
            with Stage("fno") as sg:
                loaded = sg.sem("weights_loaded")
                names = ("y_step", "y_turned", "x_step", "mix", "conv", "x_back", "x_turned", "y_back", "conv2")
                did = {n: sg.sem("tensor_" + n) for n in names}
                got_v = {n: sg.sem("vector_" + n) for n in names}
                got_s = {n: sg.sem("scalar_" + n) for n in names}
                vchain = sg.sem("vector_chain")
                block = sg.block()

                @block.sync
                def _(sp):
                    clear_previous(sp, sg.sems)
                    fw = a["L0_tok_fw"][bass.ds(layer, 1)]
                    for g in range(4):
                        hh, kh = g // 2, g % 2
                        src = fw[0:1, hh].rearrange("l i o x y c -> (l i) o (x y c)")[:, :, 144 * kh:144 * kh + 144]
                        sp.dma_start(mixw[C * g:C * g + C, :, :], src).then_inc(loaded, 16)
                    w1 = a["w1_T"][bass.ds(layer, 1)].rearrange("l i o -> (l i) o")
                    w2 = a["w2_T"][bass.ds(layer, 1)].rearrange("l i o -> (l i) o")
                    sp.dma_start(w1T[:, :], w1).then_inc(loaded, 16)
                    for b in range(B):
                        cs = slice(C * b, C * b + C)
                        sp.dma_start(w2bd[cs, cs], w2).then_inc(loaded, 16)
                        sp.dma_start(b1[cs, :], a["L0_tok_w1_b"][bass.ds(layer, 1)].rearrange("l n -> n l")).then_inc(loaded, 16)
                        sp.dma_start(b2row[:, cs], wide(a["L0_tok_w2_b"][bass.ds(layer, 1)], [128, C])).then_inc(loaded, 16)
                    sp.wait_ge(loaded, 16 * 17)

                @block.tensor
                def _(pe):
                    for i in range(NX):
                        mm = pe.matmul(ps[:, i // 8, 48 * (i % 8):48 * (i % 8) + 48], field[:, i, :], y_fwd[:, :],
                                       start=True, stop=True)
                        if i % 8 == 7:
                            mm.then_inc(did["y_step"], 1)
                    pe.wait_ge(got_v["y_step"], 2)
                    pe.wait_ge(got_s["y_step"], 2)
                    for k in range(KY):
                        mm = pe.transpose(ps[:, 4 + k // 4, 128 * (k % 4):128 * (k % 4) + 128],
                                          by_y[:, 2 * k:2 * k + 2, :].rearrange("p c x -> p (c x)"), ident[:, :])
                        if k % 4 == 3:
                            mm.then_inc(did["y_turned"], 1)
                    pe.wait_ge(got_v["y_turned"], 2)
                    pe.wait_ge(got_s["y_turned"], 1)
                    for k in range(KY):
                        mm = pe.matmul(ps[:, k // 6, 48 * (k % 6):48 * (k % 6) + 48], by_yT[:, k, :], x_fwd[:, :],
                                       start=True, stop=True)
                    mm.then_inc(did["x_step"], 1)
                    pe.wait_ge(got_v["x_step"], 3)
                    pe.wait_ge(loaded, 16 * 17)
                    for m in range(72):
                        for g in range(4):
                            j, ky = m // KY, m % KY
                            p = slice(C * g, C * g + C)
                            col = 8 * ((j % 3) * KY + ky)
                            dst = ps[p, 2 * g + j // 3, col:col + 8]
                            for c, src in enumerate((modes, modes_i)):
                                mm = pe.matmul(dst, mixw[p, :, 2 * m + c], src[p, :, ky, :, j].rearrange("p b c -> p c b"),
                                               start=(c == 0), stop=(c == 1), tile_position=(C * g, C * g))
                        if m % 36 == 35:
                            mm.then_inc(did["mix"], 1)
                    pe.wait_ge(got_v["mix"], 8)
                    for ky in range(KY):
                        for b in range(B):
                            mm = pe.matmul(ps[0:48, ky // 4, 128 * (ky % 4) + C * b:128 * (ky % 4) + C * b + C],
                                           mixed[:, b, ky, :, :].rearrange("p c k -> p (c k)"), w1T[:, :],
                                           start=True, stop=True)
                    mm.then_inc(did["conv"], 1)
                    pe.wait_ge(got_v["conv"], 1)
                    pe.wait_ge(got_s["conv"], 2)
                    for ky in range(KY):
                        mm = pe.matmul(ps[:, 3 + ky // 4, 128 * (ky % 4):128 * (ky % 4) + 128], convd[:, ky, :],
                                       x_inv[:, :], start=True, stop=True)
                        if ky % 4 == 3:
                            mm.then_inc(did["x_back"], 1)
                    pe.wait_ge(got_v["x_back"], 2)
                    pe.wait_ge(got_s["x_back"], 1)
                    for i in range(16):
                        mm = pe.transpose(ps[0:96, i // 4, 128 * (i % 4):128 * (i % 4) + 128],
                                          by_x[:, 4 * i:4 * i + 4, :].rearrange("p x k -> p (x k)"), ident[:, :])
                        if i % 4 == 3:
                            mm.then_inc(did["x_turned"], 1)
                    pe.wait_ge(got_v["x_turned"], 2)
                    pe.wait_ge(got_s["x_turned"], 2)
                    for i in range(16):
                        mm = pe.matmul(ps[:, i // 2, 256 * (i % 2):256 * (i % 2) + 256], by_xT[:, i, :], y_inv[:, :],
                                       start=True, stop=True)
                        if i % 2:
                            mm.then_inc(did["y_back"], 1)
                    for i in range(NX):
                        if i % 4 == 0:
                            pe.wait_ge(got_s["y_back"], i // 4 + 1)
                        mm = pe.matmul(ps[:, i // 4, 128 * (i % 4):128 * (i % 4) + 128], act_g[:, 128 * i:128 * i + 128],
                                       w2bd[:, :], start=True, stop=True)
                        if i % 4 == 3:
                            mm.then_inc(did["conv2"], 1)

                def y_out(k):
                    return (by_y[:, :, 16 * k:16 * k + 16].rearrange("p k x -> p x k"),
                            ps[:, k, 0:384].rearrange("p (x k) -> p x k", k=24))

                def x_out(k):
                    return (by_x[:, :, 8 * k:8 * k + 8].rearrange("p x (k c) -> p k c x", c=2),
                            ps[:, 3 + k, :].rearrange("p (k c x) -> p k c x", k=4, c=2))

                @block.scalar
                def _(act):
                    for k in (1, 3):
                        act.wait_ge(did["y_step"], k + 1)
                        act.copy(*y_out(k)).then_inc(got_s["y_step"], 1)
                    act.wait_ge(did["y_turned"], 2)
                    act.copy(by_yT[:, 4:8, :].rearrange("p a n -> p (a n)"), ps[:, 5, :]).then_inc(got_s["y_turned"], 1)
                    act.wait_ge(did["conv"], 1)
                    for k in (0, 1):
                        act.copy(convd[:, 4 * k:4 * k + 4, :].rearrange("p a n -> p (a n)"), ps[0:48, k, :])\
                           .then_inc(got_s["conv"], 1)
                    act.wait_ge(did["x_back"], 2)
                    act.copy(*x_out(1)).then_inc(got_s["x_back"], 1)
                    for k in (1, 3):
                        act.wait_ge(did["x_turned"], k + 1)
                        act.copy(by_xT[:, 4 * k:4 * k + 4, :].rearrange("p a n -> p (a n)"), ps[0:96, k, :])\
                           .then_inc(got_s["x_turned"], 1)
                    for k in range(8):
                        act.wait_ge(did["y_back"], k + 1)
                        act.activation(act_g[:, 512 * k:512 * k + 512], ps[:, k, :], ACT.Relu, bias=b1[:, :])\
                           .then_inc(got_s["y_back"], 1)

                @block.vector
                def _(dve):
                    link = Chain(dve, vchain)
                    for k in (0, 2):
                        dve.wait_ge(did["y_step"], k + 1)
                        dve.tensor_copy(*y_out(k)).then_inc(got_v["y_step"], 1)
                    for k in (0, 2):
                        dve.wait_ge(did["y_turned"], k + 1)
                        dve.tensor_copy(by_yT[:, 4 * k:4 * k + 4, :].rearrange("p a n -> p (a n)"), ps[:, 4 + k, :])\
                           .then_inc(got_v["y_turned"], 1)
                    dve.wait_ge(did["x_step"], 1)
                    for g in range(4):
                        for b in range(B):
                            for k in range(2):
                                src = ps[C * b:C * b + C, k, 0:288].rearrange("p (y c k) -> p y c k", y=6, c=2)
                                ins = dve.tensor_copy(modes[C * g:C * g + C, b, 6 * k:6 * k + 6, :, :],
                                                      src[:, :, :, 6 * g:6 * g + 6])
                    link(ins)
                    dve.sem_inc(got_v["x_step"], 1)
                    flat = modes[:, :, :, :, :].rearrange("p b y c k -> p (b y) c k")
                    flat_i = modes_i[:, :, :, :, :].rearrange("p b y c k -> p (b y) c k")
                    dve.tensor_scalar(flat_i[:, :, 0, :], flat[:, :, 1, :], -1.0, None, ALU.mult).then_inc(got_v["x_step"], 1)
                    dve.tensor_copy(flat_i[:, :, 1, :], flat[:, :, 0, :]).then_inc(got_v["x_step"], 1)
                    for j3 in range(2):
                        dve.wait_ge(did["mix"], j3 + 1)
                        for g in range(4):
                            k0 = 6 * g + 3 * j3
                            for b in range(B):
                                src = ps[C * g:C * g + C, 2 * g + j3, 0:288].rearrange("p (j y c b) -> p j (y c) b", j=3, y=KY, c=2)
                                dst = mixed[:, b, :, :, k0:k0 + 3].rearrange("p y c j -> p j (y c)")
                                ins = dve.tensor_copy(dst, src[:, :, :, b])
                            ins.then_inc(got_v["mix"], 1)
                    dve.wait_ge(did["conv"], 1)
                    dve.tensor_copy(convd[:, 8:12, :].rearrange("p a n -> p (a n)"), ps[0:48, 2, :]).then_inc(got_v["conv"], 1)
                    for k in (0, 2):
                        dve.wait_ge(did["x_back"], k + 1)
                        dve.tensor_copy(*x_out(k)).then_inc(got_v["x_back"], 1)
                    for k in (0, 2):
                        dve.wait_ge(did["x_turned"], k + 1)
                        dve.tensor_copy(by_xT[:, 4 * k:4 * k + 4, :].rearrange("p a n -> p (a n)"), ps[0:96, k, :])\
                           .then_inc(got_v["x_turned"], 1)
                    for k in range(8):
                        dve.wait_ge(did["conv2"], k + 1)
                        part = field[:, 4 * k:4 * k + 4, :]
                        link(dve.tensor_tensor(part, part, ps[:, k, :].rearrange("p (a n) -> p a n", a=4), ALU.add))
                        dve.tensor_tensor(part, part, wide(b2row[:, :].unsqueeze(1), [128, 4, 128]), ALU.add)

            end_of_pass("fno_end")

        with Stage("img") as sg:
            turned, copied, read, acted, done, fin = (sg.sem(n) for n in
                                                      ("turned", "copied", "read_out", "acted", "second", "final"))
            stored = sg.sem("stored")
            res = sg.sb("res", [B, G * G])
            hidden = sg.sb("hidden", [16, G * G])
            block = sg.block()

            @block.sync
            def _(sp):
                clear_previous(sp, sg.sems)
                sp.wait_ge(fin, 8)
                sp.dma_start(h_in[:, 0:IMG, :].rearrange("b x y -> b (x y)"), res[:, :]).then_inc(stored, 16)
                sp.wait_ge(stored, 16)

            @block.tensor
            def _(pe):
                for i in range(NX):
                    mm = pe.transpose(ps[:, i // 4, 128 * (i % 4):128 * (i % 4) + 128], field[:, i, :], ident[:, :])
                    if i % 4 == 3:
                        mm.then_inc(turned, 1)
                for k in range(8):
                    pe.wait_ge(copied, k + 1)
                    pe.matmul(ps[0:16, k, :], q1[:, :], act_g[:, 512 * k:512 * k + 512], start=True, stop=True)\
                      .then_inc(read, 1)
                for k in range(8):
                    pe.wait_ge(acted, k + 1)
                    pe.matmul(ps[0:4, k, :], q2[:, :], hidden[:, 512 * k:512 * k + 512], start=True, stop=True)\
                      .then_inc(done, 1)

            @block.vector
            def _(dve):
                for k in range(8):
                    dve.wait_ge(turned, k + 1)
                    dve.tensor_copy(act_g[:, 512 * k:512 * k + 512], ps[:, k, :]).then_inc(copied, 1)
                for k in range(8):
                    dve.wait_ge(done, k + 1)
                    dve.tensor_scalar(res[:, 512 * k:512 * k + 512], ps[0:4, k, :], q2b[:, :], None, ALU.add)\
                       .then_inc(fin, 1)

            @block.scalar
            def _(act):
                for k in range(8):
                    act.wait_ge(read, k + 1)
                    act.activation(hidden[:, 512 * k:512 * k + 512], ps[0:16, k, :], ACT.Relu, bias=q1b[:, :])\
                       .then_inc(acted, 1)


def text(nc, a, ps, ident, h_in, Stage, clear_previous):
    N = 16
    with Stage("txt") as sg:
        ids = sg.sb("ids", [128, N], I32)
        base = sg.sb("base", [128, N, 4])
        mag = sg.sb("mag", [128, N, 4])
        whole_i = sg.sb("whole_i", [128, N, 4], I32)
        whole = sg.sb("whole", [128, N, 4])
        over = sg.sb("over", [128, N, 4])
        powers = sg.sb("powers", [128, N, 4, 5])
        powT = sg.sb("powT", [20, N, 128])
        coef = sg.sb("coef", [20, D])
        emb = sg.sb("emb", [128, N, D])
        loaded, gathered, ready, turned, copied, made, stored, vchain, emb_done = (sg.sem(n) for n in (
            "loaded", "gathered", "powers_ready", "turned", "copied", "made", "stored", "vector_chain", "emb_done"))
        block = sg.block()

        @block.sync
        def _(sp):
            clear_previous(sp, sg.sems)
            sp.dma_start(ids[:, :], a["x_txt"].rearrange("b (q n) -> (b q) n", n=N)).then_inc(loaded, 16)
            sp.dma_start(coef[:, :], a["L0_txt_poly_coeffs"].rearrange("t d o -> (t d) o")).then_inc(loaded, 16)
            sp.wait_ge(emb_done, 2)
            for b in range(B):
                sp.dma_start(h_in[b, IMG:S, :].rearrange("(q n) d -> q n d", n=N), emb[32 * b:32 * b + 32, :, :])\
                  .then_inc(stored, 16)
            sp.wait_ge(stored, 16 * B)

        @block.gpsimd
        def _(pool):
            pool.wait_ge(loaded, 32)
            for n in range(N):
                pool.indirect_dma_start(base[:, n, :], None, a["L0_txt_turns"],
                                        bass.IndirectOffsetOnAxis(ap=ids[:, n:n + 1], axis=0)).then_inc(gathered, 16)

        @block.vector
        def _(dve):
            link = Chain(dve, vchain)
            dve.wait_ge(gathered, 16 * N)
            flat = lambda t: t[:, :, :].rearrange("p n t -> p (n t)")
            link(dve.tensor_scalar(flat(mag), flat(base), -1.0, None, ALU.mult))
            link(dve.tensor_tensor(flat(mag), flat(mag), flat(base), ALU.max))
            link(dve.tensor_copy(flat(whole_i), flat(mag)))
            link(dve.tensor_copy(flat(whole), flat(whole_i)))
            link(dve.tensor_tensor(flat(over), flat(whole), flat(mag), ALU.is_gt))
            link(dve.tensor_tensor(flat(whole), flat(whole), flat(over), ALU.subtract))
            link(dve.tensor_scalar(flat(over), flat(base), 0.0, 2.0, ALU.is_ge, ALU.mult))
            link(dve.scalar_tensor_tensor(flat(whole), flat(over), -1.0, flat(whole), ALU.add, ALU.mult))
            pw = powers[:, :, :, :].rearrange("p n t d -> p (n t) d")
            link(dve.memset(pw[:, :, 0], 1.0))
            link(dve.tensor_copy(pw[:, :, 1], flat(whole)))
            for d in range(2, 5):
                ins = dve.tensor_tensor(pw[:, :, d], pw[:, :, d - 1], flat(whole), ALU.mult)
                link(ins)
            dve.sem_inc(ready, 1)
            for k in range(4):
                dve.wait_ge(turned, k + 1)
                dve.tensor_copy(powT[:, 4 * k:4 * k + 4, :].rearrange("p a n -> p (a n)"), ps[0:20, k, :]).then_inc(copied, 1)
            for k in range(2):
                dve.wait_ge(made, k + 1)
                dve.tensor_copy(emb[:, 8 * k:8 * k + 8, :].rearrange("p a n -> p (a n)"), ps[:, 4 + k, :]).then_inc(emb_done, 1)

        @block.tensor
        def _(pe):
            pe.wait_ge(ready, 1)
            for n in range(N):
                mm = pe.transpose(ps[0:20, n // 4, 128 * (n % 4):128 * (n % 4) + 128],
                                  powers[:, n, :, :].rearrange("p t d -> p (t d)"), ident[:, :])
                if n % 4 == 3:
                    mm.then_inc(turned, 1)
            pe.wait_ge(loaded, 32)
            for n in range(N):
                pe.wait_ge(copied, n // 4 + 1)
                mm = pe.matmul(ps[:, 4 + n // 8, D * (n % 8):D * (n % 8) + D], powT[:, n, :], coef[:, :],
                               start=True, stop=True)
                if n % 8 == 7:
                    mm.then_inc(made, 1)


def tables():
    f = np.float32
    t = {"c_ident": np.eye(128, dtype=f)}
    r = np.arange(Q)
    t["c_causal"] = np.where(r[None, :] > r[:, None], f(NEG), f(0)).astype(f)
    t["c_causal32"] = np.tile(t["c_causal"][0:32, 0:32], (4, 1))
    t["c_keep"] = (r[None, :] >= r[:, None]).astype(f)
    t["c_iota8"] = np.tile(np.arange(8, dtype=f), (Q, 1))
    inv = 1.0 / 10000.0 ** (np.arange(0, 16, 2, dtype=f) / 16)
    fr = np.outer(np.arange(S, dtype=f), inv)
    t["c_cos"] = np.ascontiguousarray(np.cos(fr).astype(f).reshape(T, Q, 8).transpose(1, 0, 2))
    t["c_sin"] = np.ascontiguousarray(np.sin(fr).astype(f).reshape(T, Q, 8).transpose(1, 0, 2))
    xs = np.arange(G)
    ky = np.arange(KY)
    kx = np.concatenate([np.arange(12), np.arange(G - 12, G)])
    ty = 2 * np.pi * ((xs[:, None] * ky[None, :]) % G) / G
    tx = 2 * np.pi * ((xs[:, None] * kx[None, :]) % G) / G
    yf = np.zeros((2, G, 2, KY, 2))
    for p in range(2):
        yf[p, :, p, :, 0], yf[p, :, p, :, 1] = np.cos(ty), -np.sin(ty)
    t["c_y_fwd"] = yf.reshape(128, 48).astype(f)
    xf = np.zeros((2, G, 2, KX))
    xf[0, :, 0], xf[0, :, 1], xf[1, :, 0], xf[1, :, 1] = np.cos(tx), -np.sin(tx), np.sin(tx), np.cos(tx)
    t["c_x_fwd"] = (xf.reshape(128, 48) / G).astype(f)
    xi = np.zeros((2, KX, 2, G))
    xi[0, :, 0], xi[0, :, 1], xi[1, :, 0], xi[1, :, 1] = np.cos(tx).T, np.sin(tx).T, -np.sin(tx).T, np.cos(tx).T
    t["c_x_inv"] = xi.reshape(48, 128).astype(f)
    c = np.where(ky == 0, 1.0, 2.0)[:, None] / G
    yi = np.zeros((4, KY, 2, 4, G))
    for p in range(4):
        yi[p, :, 0, p], yi[p, :, 1, p] = c * np.cos(ty).T, -c * np.sin(ty).T
    t["c_y_inv"] = yi.reshape(96, 256).astype(f)
    lin = np.linspace(0.0, 1.0, G).astype(f)
    t["c_grid"] = np.stack([np.repeat(lin, G), np.tile(lin, G), np.ones(G * G, f)])
    return t


def layouts(v):
    o = dict(v)
    c = np.ascontiguousarray
    idx = np.clip(np.arange(Q)[:, None] * 0 + (np.arange(S + S - Q)[None, :] - np.arange(Q)[:, None]) - (S - Q) + S - 1,
                  0, v["L0_attn_bias_table"].shape[0] - 1)
    o["bias_strip"] = c(v["L0_attn_bias_table"][idx])
    o["hl_wT"] = c(v["L0_ffn_hl_w"].reshape(64, 64).T)
    o["l0_wqT"] = c(v["L0_ffn_wq"].transpose(0, 3, 1, 2))
    o["l0_wkT"] = c(v["L0_ffn_wk"].transpose(0, 2, 1))
    o["l0_wvT"] = c(v["L0_ffn_wv"].transpose(0, 2, 1))
    o["l0_gateT"] = c(v["L0_ffn_gate_w"].transpose(0, 2, 1))
    o["l0_fc1T"] = c(v["L0_ffn_fc1_w"].T)
    o["l0_fc2T"] = c(v["L0_ffn_fc2_w"].T)
    o["l0_fgateT"] = c(v["L0_ffn_fgate_w"].T)
    for n, s in (("l1_wqT", "wq"), ("l1_wkT", "wk"), ("l1_wvT", "wv"), ("l1_woT", "wo"), ("l1_routerT", "router_w")):
        o[n] = c(v["L1_ffn_" + s].T)
    o["l1_w1T"] = c(v["L1_ffn_w1"].transpose(2, 0, 1))
    o["l1_w3T"] = c(v["L1_ffn_w3"].transpose(2, 0, 1))
    o["l1_w2T"] = c(v["L1_ffn_w2"].transpose(0, 2, 1))
    for n in "qk":
        o["l2_w%sT" % n] = c(v["L2_attn_W" + n].T)
    o["l2_wv_heads"] = c(v["L2_attn_Wv"].reshape(4, 16, D).transpose(1, 0, 2))
    o["l2_wo_heads"] = c(v["L2_attn_Wo"].T.reshape(4, 16, D).transpose(1, 0, 2))
    o["l2_b1T"] = c(v["L2_ffn_b1"].T)
    o["l3_b1T"] = c(v["L3_ffn_b1"].T)
    o["p_wT"] = c(v["L0_tok_p_w"].T)
    o["w1_T"] = c(v["L0_tok_w1_w"].transpose(0, 2, 1))
    o["w2_T"] = c(v["L0_tok_w2_w"].transpose(0, 2, 1))
    o["q1_T"] = c(v["L0_tok_q1_w"].T)
    o["q2_T"] = c(v["L0_tok_q2_w"].T)
    used = ("bias_table", "hl_w", "ffn_wq", "ffn_wk", "ffn_wv", "ffn_wo", "gate_w", "fc1_w", "fc2_w", "router_w",
            "L1_ffn_w1", "L1_ffn_w2", "L1_ffn_w3", "L2_attn_W", "L2_ffn_b1", "L3_ffn_b1", "p_w", "tok_w1_w",
            "tok_w2_w", "q1_w", "q2_w", "attn_scale")
    return {k: x for k, x in o.items() if not (k in v and any(u in k for u in used)) or k == "L0_attn_scale"}


def prepare(nc, inputs, upto=99):
    arrays = {}
    args = {}
    for name, x in {**layouts({k: np.asarray(x) for k, x in inputs.items()}), **tables()}.items():
        if x.ndim == 0:
            x = x.reshape(1)
        arrays["in_" + name] = np.ascontiguousarray(x)
        args[name] = nc.dram_tensor("in_" + name, x.shape, mybir.dt.from_np(x.dtype), kind="ExternalInput").ap()
    out = nc.dram_tensor("out_0", (B, S, D), F32, kind="ExternalOutput").ap()
    build(nc, args, out, upto)
    return arrays


def kernel(**inputs):
    from concourse import bacc
    from concourse.bass_utils import run_bass_kernel_spmd

    nc = bacc.Bacc("TRN2", target_bir_lowering=False, num_devices=1)
    arrays = prepare(nc, inputs)
    r = run_bass_kernel_spmd(nc, [arrays], core_ids=[0])
    return r.results[0]["out_0"]
```

```python
from contextlib import ExitStack

import numpy as np

import concourse.bass as bass
from concourse import mybir

ALU = mybir.AluOpType
ACT = mybir.ActivationFunctionType
AX = mybir.AxisListType
F32 = mybir.dt.float32
BF16 = mybir.dt.bfloat16
I32 = mybir.dt.int32
U32 = mybir.dt.uint32

B, S, Q, T, D = 4, 576, 96, 6, 64
IMG, TXT = 64, 512
C, G, KX, KY, HALF = 32, 64, 24, 12, 288
NEG = -1.0e30
HID = 170
HP = HID // 2


PACKS = {
    "w128": (128, [("ident", (128,)), ("causal32", (32,)), ("l0f_gate", (2, 8)), ("l1a_w2", (2, D)),
                   ("l2f_w2", (8, D)), ("l3f_w2", (8, D)), ("l2f_b1", (8,)), ("l3f_b1", (8,))]),
    "w96": (Q, [("causal", (Q,)), ("keep", (Q,)), ("iota8", (8,)), ("cos", (T, 8)), ("sin", (T, 8)),
                ("strip", (S + S - Q,))]),
    "w65": (D + 1, [("l0a_qkv", (192,)), ("l0a_proj", (64,)), ("l0f_hl", (64,)), ("l0f_fc1", (64,)), ("l0f_fc2", (64,)),
                    ("l1a_qkv", (192,)), ("l1a_proj", (64,)), ("l1a_w1", (256,)), ("l3a_qkv", (192,))]),
    "w64": (D, [("l0f_fgate", (4,)), ("l1f_qkv", (128,)), ("l1f_wo", (D,)),
                ("l2a_q", (D,)), ("l2a_k", (D,))]),
    "w85": (HP, [("l1f_w2", (8, 2, D))]),
    "w16": (16, [("l2a_v", (4, D)), ("l2a_o", (4, D))]),
    "w96b": (Q, [("l2f_b2", (12 * D,)), ("l3f_b2", (12 * D,))]),
    "rows": (1, [(n, (D,)) for n in ("l0a_g1", "l0a_b1", "l0a_g2", "l0a_b2", "l1a_g1", "l1a_b1", "l1a_g2", "l1a_nb2",
                                     "l1f_w1", "l1f_w2", "l3f_g", "l3f_b", "l1a_b2")]
             + [(n, (16,)) for n in ("l0f_g", "l0f_b", "l0f_fg", "l0f_fb", "l0f_gate")]
             + [("l2f_bg", (8,)), ("l3f_br", (8,)), ("att_scale", (1,))]),
    "up": (D, [("l0f_qkv", (384,)), ("l1f_w1", (8, HID)), ("l1f_w3", (8, HID)), ("l2f_w1", (8, 128)), ("l3f_w1", (8, 128)),
               ("l1f_router", (8,)), ("l2f_g", (8,)), ("l3f_r", (8,))]),
}


def size(shape):
    return int(np.prod(shape))


class Parts:

    def __init__(self, sb, rows, pieces):
        self.n = sum(size(s) for _, s in pieces)
        self.pp, self.qq, self.rp = (sb("up_" + n, [2 * rows, self.n], BF16) for n in ("pp", "qq", "rp"))
        starts = np.cumsum([0] + [size(s) for _, s in pieces])
        self.start = {n: int(at) for (n, _), at in zip(pieces, starts)}

    def by_feature(self, pe, dst, name, at, width, ab, ac):
        c = self.start[name] + at
        pe.matmul(dst, self.pp[:, c:c + width], ab, start=True, stop=False)
        pe.matmul(dst, self.qq[:, c:c + width], ab, start=False, stop=False)
        return pe.matmul(dst, self.rp[:, c:c + width], ac, start=False, stop=True)

    def by_token(self, pe, dst, name, width, ab, ac):
        c = self.start[name]
        pe.matmul(dst, ab, self.pp[:, c:c + width], start=True, stop=False)
        pe.matmul(dst, ab, self.qq[:, c:c + width], start=False, stop=False)
        return pe.matmul(dst, ac, self.rp[:, c:c + width], start=False, stop=True)


def split_tokens(dve, link, stacks, x, rest):
    link(dve.tensor_copy(stacks[:, :, 0, 0:D], x))
    link(dve.tensor_tensor(rest, x, stacks[:, :, 0, 0:D], ALU.subtract))
    link(dve.tensor_copy(stacks[:, :, 0, D:2 * D], rest))
    link(dve.tensor_tensor(stacks[:, :, 1, D:2 * D], rest, stacks[:, :, 0, D:2 * D], ALU.subtract))
    link(dve.tensor_copy(stacks[:, :, 1, 0:D], stacks[:, :, 0, 0:D]))


class Chain:

    def __init__(self, eng, sem):
        self.eng, self.sem, self.n = eng, sem, 0

    def __call__(self, ins):
        self.n += 1
        ins.then_inc(self.sem, 1)
        self.eng.wait_ge(self.sem, self.n)


def wide(ap, shape):
    return ap.to_broadcast(shape)


def rsqrt(dve, link, y, v, tmp):
    link(dve.tensor_scalar(y.bitcast(I32), v.bitcast(I32), 1, None, ALU.logical_shift_right))
    link(dve.tensor_scalar(y.bitcast(I32), y.bitcast(I32), -1.0, float(0x5F3759DF), ALU.mult, ALU.add))
    for _ in range(3):
        link(dve.tensor_tensor(tmp, y, y, ALU.mult))
        link(dve.scalar_tensor_tensor(tmp, tmp, -0.5, v, ALU.mult, ALU.mult))
        link(dve.scalar_tensor_tensor(y, tmp, 1.5, y, ALU.add, ALU.mult))


def layer_norm(dve, link, out, x, sq, st, eps):
    p, g, w = x.shape
    mean, var, inv, tmp = (st[0:p, j, 0:g] for j in range(4))
    link(dve.tensor_reduce(mean, x, AX.X, ALU.add))
    link(dve.scalar_tensor_tensor(out, wide(mean.unsqueeze(2), [p, g, w]), -1.0 / w, x, ALU.mult, ALU.add))
    link(dve.tensor_tensor(sq, out, out, ALU.mult))
    link(dve.tensor_reduce(var, sq, AX.X, ALU.add))
    link(dve.tensor_scalar(var, var, 1.0 / w, eps, ALU.mult, ALU.add))
    rsqrt(dve, link, inv, var, tmp)
    link(dve.tensor_tensor(out, out, wide(inv.unsqueeze(2), [p, g, w]), ALU.mult))


def rms_norm(dve, link, out, x, sq, st, eps, weight):
    p, g, w = x.shape
    var, inv, tmp = (st[0:p, j, 0:g] for j in range(3))
    link(dve.tensor_tensor(sq, x, x, ALU.mult))
    link(dve.tensor_reduce(var, sq, AX.X, ALU.add))
    link(dve.tensor_scalar(var, var, 1.0 / w, eps, ALU.mult, ALU.add))
    rsqrt(dve, link, inv, var, tmp)
    link(dve.tensor_tensor(out, x, wide(inv.unsqueeze(2), [p, g, w]), ALU.mult))
    link(dve.tensor_tensor(out, out, weight, ALU.mult))


def affine(dve, link, x, gamma, beta):
    link(dve.tensor_tensor(x, x, gamma, ALU.mult))
    link(dve.tensor_tensor(x, x, beta, ALU.add))


def halves(ap):
    return ap.rearrange("p (c n) -> p c n", c=2)


class Attention:

    def __init__(self, nc, sg, name, ps, maps, dv, causal, q_of, k_of, v_of, out_of, mask=None, strip=None):
        self.ps, self.maps, self.dv, self.causal = ps, maps, dv, causal
        self.q_of, self.k_of, self.v_of, self.out_of, self.mask, self.strip = q_of, k_of, v_of, out_of, mask, strip
        sb = lambda n, shape: sg.st.enter_context(nc.sbuf_tensor(f"{name}_{n}", shape, F32))
        self.probs = sb("probs", [Q, 2, S])
        self.probs_t = sb("probs_t", [Q, 2, T, Q])
        self.neg_max = sb("neg_max", [Q, 4])
        self.row_sum = sb("row_sum", [Q, 2, maps])
        self.inv_sum = sb("inv_sum", [Q, maps])
        self.biased = sb("biased", [Q, 2, S]) if strip is not None else None
        names = ("scores_ready", "max_ready", "probs_ready", "turned", "turned_copied", "product_ready", "out_ready")
        self.sems = [sg.sem("att_" + n) for n in names]
        (self.scores_ready, self.max_ready, self.probs_ready, self.turned, self.turned_copied,
         self.product_ready, self.out_ready) = self.sems
        self.units = [(t, m) for t in range(T) for m in range(maps)]

    def keys(self, t):
        return Q * (t + 1) if self.causal else S

    def scores_at(self, i):
        b = 2 * (i % 2)
        return self.ps[0:Q, b:b + 2, :].rearrange("p b n -> p (b n)")

    def tensor(self, pe, ident):
        n = len(self.units)
        turned = self.ps[0:Q, 4:6, :].rearrange("p b (k n) -> p (b k) n", n=128)
        for step in range(n + 2):
            if step < n:
                t, m = self.units[step]
                if step >= 2:
                    pe.wait_ge(self.probs_ready, step - 1)
                for a in range(0, self.keys(t), 512):
                    z = min(self.keys(t), a + 512)
                    mm = pe.matmul(self.scores_at(step)[:, a:z], self.q_of(m, t), self.k_of(m, a, z),
                                   start=True, stop=True)
                mm.then_inc(self.scores_ready, 1)
            if 1 <= step <= n:
                i = step - 1
                t, m = self.units[i]
                pe.wait_ge(self.probs_ready, i + 1)
                if i >= 1:
                    pe.wait_ge(self.turned_copied, i)
                for k in range(self.keys(t) // Q):
                    mm = pe.transpose(turned[:, k, 0:Q], self.probs[:, i % 2, Q * k:Q * k + Q], ident[0:Q, 0:Q])
                mm.then_inc(self.turned, 1)
            if step >= 2:
                i = step - 2
                t, m = self.units[i]
                pe.wait_ge(self.turned_copied, i + 1)
                if m == 0 and t >= 2:
                    pe.wait_ge(self.out_ready, t - 1)
                last = self.keys(t) // Q - 1
                for k in range(last + 1):
                    mm = pe.matmul(self.ps[0:Q, 6 + t % 2, m * self.dv:(m + 1) * self.dv],
                                   self.probs_t[:, i % 2, k, :], self.v_of(m, k), start=(k == 0), stop=(k == last))
                mm.then_inc(self.product_ready, 1)

    def scalar(self, act):
        for i, (t, m) in enumerate(self.units):
            act.wait_ge(self.max_ready, i + 1)
            if i >= 2:
                act.wait_ge(self.turned, i - 1)
            if m == 0 and t >= 2:
                act.wait_ge(self.out_ready, t - 1)
            src = self.scores_at(i) if self.biased is None else self.biased[:, i % 2, :]
            act.activation(self.probs[:, i % 2, 0:self.keys(t)], src[:, 0:self.keys(t)], ACT.Exp,
                           bias=self.neg_max[:, i % 4:i % 4 + 1],
                           accum_out=self.row_sum[:, t % 2, m:m + 1]).then_inc(self.probs_ready, 1)

    def vector(self, dve, link):
        n = len(self.units)
        turned = self.ps[0:Q, 4:6, :].rearrange("p b (k n) -> p (b k) n", n=128)
        for step in range(n + 2):
            if step < n:
                t, m = self.units[step]
                dve.wait_ge(self.scores_ready, step + 1)
                s = self.scores_at(step)
                if self.causal:
                    diag = s[:, Q * t:Q * t + Q]
                    link(dve.tensor_tensor(diag, diag, self.mask, ALU.add))
                if self.biased is not None:
                    if step >= 2:
                        dve.wait_ge(self.probs_ready, step - 1)
                    out = self.biased[:, step % 2, :]
                    link(dve.tensor_tensor(out, s[:, 0:S], self.strip(t), ALU.add))
                    s = out
                dve.tensor_reduce(self.neg_max[:, step % 4:step % 4 + 1], s[:, 0:self.keys(t)], AX.X, ALU.max,
                                  negate=True).then_inc(self.max_ready, 1)
            if 1 <= step <= n:
                i = step - 1
                t, m = self.units[i]
                dve.wait_ge(self.turned, i + 1)
                if i >= 2:
                    dve.wait_ge(self.product_ready, i - 1)
                k = self.keys(t) // Q
                dve.tensor_copy(self.probs_t[:, i % 2, 0:k, :], turned[:, 0:k, 0:Q]).then_inc(self.turned_copied, 1)
            if step >= 2 and self.units[step - 2][1] == self.maps - 1:
                t = self.units[step - 2][0]
                dve.wait_ge(self.product_ready, step - 1)
                if t >= 1:
                    dve.wait_ge(self.out_ready, t)
                link(dve.reciprocal(self.inv_sum[:, :], self.row_sum[:, t % 2, :]))
                prod = self.ps[0:Q, 6 + t % 2, 0:self.maps * self.dv].rearrange("p (m d) -> p m d", m=self.maps)
                dve.tensor_tensor(self.out_of(t), prod, wide(self.inv_sum[:, :].unsqueeze(2), [Q, self.maps, self.dv]),
                                  ALU.mult).then_inc(self.out_ready, 1)


def split3(dve, link, parts, value, rest):
    link(dve.tensor_copy(parts[0], value))
    link(dve.tensor_tensor(rest, value, parts[0], ALU.subtract))
    link(dve.tensor_copy(parts[1], rest))
    link(dve.tensor_tensor(parts[2], rest, parts[1], ALU.subtract))


class SplitAttention:

    LAG = 2
    EARLY = 2

    def __init__(self, nc, sg, name, ps, groups, members, ident, ident32, mask, mask_t, v1, out_of):
        self.ps, self.G, self.E, self.M = ps, groups, members, groups * members
        self.ident32 = ident32
        self.ident, self.mask, self.mask_t, self.v1, self.out_of = ident, mask, mask_t, v1, out_of
        sb = lambda n, shape, dt=F32: sg.st.enter_context(nc.sbuf_tensor(f"{name}_{n}", shape, dt))
        self.q_stack = sb("q_stack", [Q, T, self.M, 96], BF16)
        self.k_stack = sb("k_stack", [Q, T, self.G, 96], BF16)
        self.rest = sb("rest", [Q, T, self.M, 16])
        self.qT = sb("qT", [99, self.M, S], BF16)
        self.kT = sb("kT", [99, self.G, S], BF16)
        self.probs_t = sb("probs_t", [Q, 3, self.E, Q])
        self.out_f = sb("out_f", [32 * groups, 2, self.E, Q])
        self.neg_max = sb("neg_max", [Q, 2, self.M])
        self.max_rest = sb("max_rest", [Q, self.M])
        self.max_parts = sb("max_parts", [Q, 2, self.M, 3], BF16)
        self.inv_sum = sb("inv_sum", [Q, self.G, self.E])
        names = ("first_ready", "repeats_ready", "stacks_ready", "stack_turned", "stack_copied_v", "stack_copied_s", "scores_ready", "max_ready",
                 "parts_ready", "parts_turned", "parts_copied", "turned_ready", "probs_ready", "product_ready",
                 "out_copied", "out_turned", "out_ready")
        self.sems = [sg.sem("att_" + n) for n in names]
        (self.first_ready, self.repeats_ready, self.stacks_ready, self.stack_turned, self.stack_copied_v, self.stack_copied_s, self.scores_ready,
         self.max_ready, self.parts_ready, self.parts_turned, self.parts_copied, self.turned_ready,
         self.probs_ready, self.product_ready, self.out_copied, self.out_turned, self.out_ready) = self.sems
        self.per_bank = min(8, self.M)
        self.rounds = self.M // self.per_bank
        self.loads = [("k", t) for t in range(T)] + [("q", t, r) for t in range(T) for r in range(self.rounds)]
        self.steps = [(t, g, k) for t in range(T) for g in range(self.G) for k in range(t + 1)]

    def bank16(self, b, rows, n):
        return self.ps[rows, b, :].bitcast(BF16)[:, 0:n * Q].rearrange("p (m n) -> p m n", n=Q)

    def vector_stacks(self, dve, link, q, k):
        group = lambda stack, i: stack[:, :, :, 16 * i:16 * i + 16]
        split3(dve, link, [group(self.k_stack, i) for i in (0, 1, 3)], k, self.rest[:, :, 0:self.G, :])
        for i, j in ((2, 0), (4, 1), (5, 0)):
            ins = dve.tensor_copy(group(self.k_stack, i), group(self.k_stack, j))
        ins.then_inc(self.stacks_ready, 1)
        dve.tensor_copy(group(self.q_stack, 0), q).then_inc(self.first_ready, 1)
        dve.wait_ge(self.first_ready, 1)
        link(dve.tensor_tensor(self.rest[:, :, :, :], q, group(self.q_stack, 0), ALU.subtract))
        link(dve.tensor_copy(group(self.q_stack, 2), self.rest[:, :, :, :]))
        dve.tensor_tensor(group(self.q_stack, 5), self.rest[:, :, :, :], group(self.q_stack, 2), ALU.subtract)
        dve.tensor_copy(group(self.q_stack, 4), group(self.q_stack, 2)).then_inc(self.stacks_ready, 1)

    def scalar_stacks(self, act):
        act.wait_ge(self.first_ready, 1)
        for i in (1, 3):
            act.copy(self.q_stack[:, :, :, 16 * i:16 * i + 16], self.q_stack[:, :, :, 0:16]).then_inc(self.repeats_ready, 1)

    def copy_stacks(self, eng, copy, parity, done, between=None):
        for i, load in enumerate(self.loads):
            if i == T and between is not None:
                between(eng)
            if i % 2 != parity:
                continue
            eng.wait_ge(self.stack_turned, i + 1)
            t = load[1]
            if load[0] == "k":
                dst, n = self.kT[0:96, :, Q * t:Q * t + Q], self.G
            else:
                m = load[2] * self.per_bank
                dst, n = self.qT[0:96, m:m + self.per_bank, Q * t:Q * t + Q], self.per_bank
            copy(dst, self.bank16(i % 8, slice(0, 96), n)).then_inc(done, 1)

    def tensor_stacks(self, pe):
        for i, load in enumerate(self.loads):
            if i == 0 or i == T:
                pe.wait_ge(self.stacks_ready, 1 + (i == T))
            if i == T:
                pe.wait_ge(self.repeats_ready, 2)
            if i >= 8:
                pe.wait_ge(self.stack_copied_s if i % 2 else self.stack_copied_v, (i - 8) // 2 + 1)
            t = load[1]
            if load[0] == "k":
                src, n = self.k_stack[:, t, :, :], self.G
            else:
                m = load[2] * self.per_bank
                src, n = self.q_stack[:, t, m:m + self.per_bank, :], self.per_bank
            dst = self.bank16(i % 8, slice(0, 96), n)
            for m in range(n):
                mm = pe.transpose(dst[:, m, :], src[:, m, :], self.ident[:, :])
            mm.then_inc(self.stack_turned, 1)
        pe.wait_ge(self.stack_copied_v, (len(self.loads) + 1) // 2)
        pe.wait_ge(self.stack_copied_s, len(self.loads) // 2)

    def turn_step(self, t):
        n = self.G * (t + 1)
        return n - 1 - min(self.EARLY, n // 4)

    def tensor(self, pe):
        self.tensor_stacks(pe)
        M, E, G = self.M, self.E, self.G

        def scores(t, m):
            i = M * t + m
            if i >= 2:
                pe.wait_ge(self.max_ready, i - 1)
            if t >= 1 and m < 3:
                pe.wait_ge(self.parts_copied, self.rounds * t)
            b, n = 2 * (i % 2), Q * (t + 1)
            dst = self.ps[0:Q, b:b + 2, :].rearrange("p b n -> p (b n)")
            for a in range(0, n, 512):
                z = min(n, a + 512)
                mm = pe.matmul(dst[:, a:z], self.qT[0:96, m, Q * t:Q * t + Q], self.kT[0:96, m // E, a:z],
                               start=True, stop=False, skip_group_check=True)
            cuts = [Q * t, n] if n <= 512 else [Q * t, 512, n]
            for a, z in zip(cuts, cuts[1:]):
                mm = pe.matmul(dst[:, a:z], self.ident[:, :], self.mask[:, a - Q * t:z - Q * t],
                               start=False, stop=True, skip_group_check=True)
            mm.then_inc(self.scores_ready, 1)

        def turn_max(t):
            pe.wait_ge(self.parts_ready, t + 1)
            for r in range(self.rounds):
                dst = self.bank16(2 * r, slice(96, 99), self.per_bank)
                for m in range(self.per_bank):
                    mm = pe.transpose(dst[:, m, :], self.max_parts[:, t % 2, self.per_bank * r + m, :], self.ident[:, :])
                mm.then_inc(self.parts_turned, 1)

        def turned_scores(j):
            t, g, k = self.steps[j]
            if j >= 2:
                pe.wait_ge(self.probs_ready, j - 1)
            if g == k == 0:
                pe.wait_ge(self.parts_copied, self.rounds * (t + 1))
            dst = self.ps[0:Q, 4 + j % 2, 0:E * Q].rearrange("p (e n) -> p e n", e=E)
            mm = pe.matmul(dst, self.kT[:, g, Q * k:Q * k + Q], self.qT[:, E * g:E * g + E, Q * t:Q * t + Q],
                           start=True, stop=(k < t))
            if k == t:
                mm = pe.matmul(dst, self.ident[:, :], wide(self.mask_t[:, :].unsqueeze(1), [Q, E, Q]),
                               start=False, stop=True)
            mm.then_inc(self.turned_ready, 1)

        def product(j):
            t, g, k = self.steps[j]
            pe.wait_ge(self.probs_ready, j + 1)
            if g == k == 0 and t >= 2:
                pe.wait_ge(self.out_ready, t - 1)
            pe.matmul(self.ps[32 * g:32 * g + 32, 6 + t % 2, 0:E * Q], self.v1[:, k, g, :],
                      self.probs_t[:, j % 3, :, :], start=(k == 0), stop=(k == t)).then_inc(self.product_ready, 1)

        def turn_out(t):
            pe.wait_ge(self.out_copied, t + 1)
            for e in range(E):
                mm = pe.transpose(self.ps[0:Q, 6 + t % 2, 128 * e:128 * e + 32 * G], self.out_f[:, t % 2, e, :],
                                  self.ident32[0:32 * G, 0:32 * G])
            mm.then_inc(self.out_turned, 1)

        for m in range(M):
            scores(0, m)
        turn_max(0)
        j = 0
        for t in range(T):
            n = G * (t + 1)
            turn_at = self.turn_step(t)
            m = 0
            for s in range(n):
                if t + 1 < T:
                    while m < min(M, -(-M * (s + 1) // turn_at)):
                        scores(t + 1, m)
                        m += 1
                turned_scores(j)
                if j >= self.LAG:
                    product(j - self.LAG)
                if t >= 1 and s == min(4, n - 1):
                    turn_out(t - 1)
                if t + 1 < T and s == turn_at:
                    turn_max(t + 1)
                j += 1
        for i in range(j - self.LAG, j):
            product(i)
        turn_out(T - 1)

    def scalar(self, act):
        self.copy_stacks(act, act.copy, 1, self.stack_copied_s, self.scalar_stacks)

        def copy_out(t):
            act.wait_ge(self.product_ready, self.G * (t + 1) * (t + 2) // 2)
            act.copy(self.out_f[:, t % 2, :, :],
                     self.ps[0:32 * self.G, 6 + t % 2, 0:self.E * Q].rearrange("p (e n) -> p e n", e=self.E))\
               .then_inc(self.out_copied, 1)

        def copy_parts(t):
            for r in range(self.rounds):
                act.wait_ge(self.parts_turned, self.rounds * t + r + 1)
                m = self.per_bank * r
                act.copy(self.qT[96:99, m:m + self.per_bank, Q * t:Q * t + Q],
                         self.bank16(2 * r, slice(96, 99), self.per_bank)).then_inc(self.parts_copied, 1)

        copy_parts(0)
        j = 0
        for t in range(T):
            for s in range(self.G * (t + 1)):
                act.wait_ge(self.turned_ready, j + 1)
                if j >= 3:
                    act.wait_ge(self.product_ready, j - 2)
                act.activation(self.probs_t[:, j % 3, :, :],
                               self.ps[0:Q, 4 + j % 2, 0:self.E * Q].rearrange("p (e n) -> p e n", e=self.E),
                               ACT.Exp).then_inc(self.probs_ready, 1)
                j += 1
                if t >= 1 and s == self.LAG:
                    copy_out(t - 1)
                if t + 1 < T and s == self.turn_step(t):
                    copy_parts(t + 1)
        copy_out(T - 1)

    def vector(self, dve, link):
        M = self.M
        self.copy_stacks(dve, dve.tensor_copy, 0, self.stack_copied_v)

        def finish(t):
            dve.wait_ge(self.out_turned, t + 1)
            prod = self.ps[0:Q, 6 + t % 2, 0:128 * self.E].rearrange("p (e n) -> p e n", e=self.E)[:, :, 0:32 * self.G]
            prod = prod.rearrange("p e (g n) -> p g e n", n=32)
            link(dve.reciprocal(self.inv_sum[:, :, :], prod[:, :, :, 16]))
            out = self.out_of(t).rearrange("p (g e) d -> p g e d", g=self.G)
            link(dve.tensor_tensor(out, prod[:, :, :, 0:16], wide(self.inv_sum[:, :, :].unsqueeze(3), [Q, self.G, self.E, 16]),
                                   ALU.mult))
            dve.sem_inc(self.out_ready, 1)

        for t in range(T):
            for m in range(M):
                i = M * t + m
                dve.wait_ge(self.scores_ready, i + 1)
                s = self.ps[0:Q, 2 * (i % 2):2 * (i % 2) + 2, :].rearrange("p b n -> p (b n)")[:, 0:Q * (t + 1)]
                dve.tensor_reduce(self.neg_max[:, t % 2, m:m + 1], s, AX.X, ALU.max, negate=True).then_inc(self.max_ready, 1)
            dve.wait_ge(self.max_ready, M * (t + 1))
            split3(dve, link, [self.max_parts[:, t % 2, :, j] for j in range(3)], self.neg_max[:, t % 2, :],
                   self.max_rest[:, :])
            dve.sem_inc(self.parts_ready, 1)
            if t >= 2:
                finish(t - 2)
        finish(T - 2)
        finish(T - 1)


class TurnedPasses:

    def __init__(self, sg, ps, ident, tiles):
        self.ps, self.ident = ps, ident
        self.srcT = sg.sb("srcT", [D + 1, tiles * Q])
        self.source_ready, self.turned, self.copied_v, self.copied_s, self.product = (sg.sem(n) for n in (
            "source_ready", "source_turned", "copied_by_vector", "copied_by_scalar", "product"))
        self.banks = [(k, range(5 * k, min(tiles, 5 * k + 5))) for k in range(-(-tiles // 5))]

    def ones(self, dve, link):
        link(dve.memset(self.srcT[D:D + 1, :], 1.0))

    def copy(self, eng_copy, k, done):
        n = Q * len(self.banks[k][1])
        eng_copy(self.srcT[0:D, 5 * Q * k:5 * Q * k + n], self.ps[0:D, k, 0:n]).then_inc(done, 1)

    def vector(self, dve, j, meanwhile=None):
        dve.sem_inc(self.source_ready, 1)
        for k in (0, 2, 4):
            dve.wait_ge(self.turned, 5 * j + k + 1)
            self.copy(dve.tensor_copy, k, self.copied_v)
        if meanwhile is not None:
            meanwhile()
        dve.wait_ge(self.product, j + 1)

    def scalar(self, act, j):
        for k in (1, 3):
            act.wait_ge(self.turned, 5 * j + k + 1)
            self.copy(act.copy, k, self.copied_s)

    def turn(self, pe, j, src):
        pe.wait_ge(self.source_ready, j + 1)
        for k, tiles_k in self.banks:
            for n, i in enumerate(tiles_k):
                mm = pe.transpose(self.ps[0:D, k, Q * n:Q * n + Q], src[:, i, :], self.ident[0:Q, 0:Q])
            mm.then_inc(self.turned, 1)

    def wait_bank(self, pe, j, k):
        if k % 2:
            pe.wait_ge(self.copied_s, 2 * j + k // 2 + 1)
        else:
            pe.wait_ge(self.copied_v, 3 * j + k // 2 + 1)

    def by_token(self, pe, j, weight):
        rows, width = weight.shape
        for k, tiles_k in self.banks:
            self.wait_bank(pe, j, k)
            for i in tiles_k:
                mm = pe.matmul(self.ps[0:Q, 5 + i // 8, width * (i % 8):width * (i % 8) + width],
                               self.srcT[0:rows, Q * i:Q * i + Q], weight, start=True, stop=True)
        mm.then_inc(self.product, 1)

    def result(self, width):
        return self.ps[0:Q, 5:8, 0:8 * width].rearrange("p b (t n) -> p b t n", t=8)


def in_banks(buf):
    return buf.rearrange("p (b t) n -> p b t n", b=3)


def build(nc, a, out):
    ctx = ExitStack()
    with ctx:
        def sb(name, shape, dt=F32):
            return ctx.enter_context(nc.sbuf_tensor(name, shape, dt))

        ps = ctx.enter_context(nc.psum_tensor("ps", [128, 8, 512], F32))
        h_in = nc.dram_tensor("h_tokens", (B, S, D), F32, kind="Internal").ap()

        ident16 = sb("ident16", [Q, Q], BF16)
        mask16 = sb("mask16", [Q, Q], BF16)
        mask16_t = sb("mask16_t", [Q, Q], BF16)
        ones = sb("ones", [1, Q])
        w, rows, packs = {}, {}, {}
        for pack, (p, pieces) in PACKS.items():
            if pack == "up":
                continue
            total = sum(size(s) for _, s in pieces)
            packs[pack] = sb("pack_" + pack, [Q if pack == "rows" else p, total])
            at = 0
            for n, s in pieces:
                piece = packs[pack][:, at:at + size(s)]
                at += size(s)
                if len(s) > 1:
                    names = "abc"[:len(s)]
                    piece = piece.rearrange(f"p ({' '.join(names)}) -> p {' '.join(names)}", **dict(zip(names, s)))
                (rows if pack == "rows" else w)[n] = piece
        ident, causal32, causal, keep, iota8, cos_t, sin_t, strip = (
            w[n] for n in ("ident", "causal32", "causal", "keep", "iota8", "cos", "sin", "strip"))
        att_scale = rows["att_scale"]
        up = Parts(sb, *PACKS["up"])

        x = sb("x", [Q, T, D])
        y = sb("y", [Q, T, D])
        sq = sb("sq", [Q, T, D])
        st = sb("st", [Q, 4, 24])
        xT = sb("xT", [D + 1, S])
        yT = sb("yT", [D + 1, S])
        resid = sb("resid", [Q, T, D])

        previous = []
        held_sems = []

        class Stage:

            def __init__(self, name):
                self.name, self.st, self.sems, self.sem_st = name, ExitStack(), [], ExitStack()

            def sb(self, name, shape, dt=F32):
                return self.st.enter_context(nc.sbuf_tensor(f"{self.name}_{name}", shape, dt))

            def sem(self, name, keep=False):
                s = (ctx if keep else self.sem_st).enter_context(nc.semaphore(f"{self.name}_{name}"))
                self.sems.append(s)
                return s

            def __enter__(self):
                self.st.__enter__()
                return self

            def block(self):
                return self.st.enter_context(nc.Block())

            def __exit__(self, *e):
                self.st.__exit__(*e)
                previous[:] = self.sems
                held_sems.append(self.sem_st)
                if len(held_sems) > 1:
                    held_sems.pop(0).close()

        def end_of_pass(name):
            with Stage(name) as sg:
                block = sg.block()

                @block.sync
                def _(sp):
                    clear_previous(sp, sg.sems)

        def clear_previous(sp, own):
            for s in previous:
                if s not in own:
                    sp.sem_clear(s)

        def two(b, p):
            return ps[0:p, b:b + 2, 0:HALF]

        def tiles(b, width=D):
            return ps[0:Q, b, 0:T * width].rearrange("p (t n) -> p t n", t=T)

        def turn(pe, b, src, width=D):
            for t in range(T):
                mm = pe.transpose(ps[0:width, b + t // 3, Q * (t % 3):Q * (t % 3) + Q], src[:, t, :], ident[0:Q, 0:Q])
            return mm

        def by_feature(pe, b, weight, src):
            for c in range(2):
                mm = pe.matmul(ps[0:weight.shape[1], b + c, 0:HALF], weight, src[:, HALF * c:HALF * c + HALF],
                               start=True, stop=True)
            return mm

        def by_token(pe, b, src, weight):
            n = weight.shape[1]
            for t in range(T):
                mm = pe.matmul(ps[0:Q, b, n * t:n * t + n], src[:, Q * t:Q * t + Q], weight, start=True, stop=True)
            return mm

        def turned_stack(b):
            return ps[:, b, :].bitcast(BF16)[:, 0:S]

        def turn_stacks(pe, b, stacks):
            for j in range(2):
                for t in range(T):
                    mm = pe.transpose(turned_stack(b + j)[:, Q * t:Q * t + Q], stacks[:, t, j, :], ident16[:, :])
            return mm

        def softmax_first(dve, link, logits, st):
            p, g, n = logits.shape
            top = st[0:p, 0, 0:g]
            link(dve.tensor_reduce(top, logits, AX.X, ALU.max))
            link(dve.tensor_tensor(logits, logits, wide(top.unsqueeze(2), [p, g, n]), ALU.subtract))

        def softmax_last(dve, link, e, st):
            p, g, n = e.shape
            total = st[0:p, 0, 0:g]
            link(dve.tensor_reduce(total, e, AX.X, ALU.add))
            link(dve.reciprocal(total, total))
            link(dve.tensor_tensor(e, e, wide(total.unsqueeze(2), [p, g, n]), ALU.mult))

        TT = B * T
        CH = 4
        NC = TT // CH

        def over_tiles(row, n=TT):
            return wide(row.unsqueeze(1), [Q, n, row.shape[1]])

        def heads(t):
            return t[:, :, :].rearrange("p t (n d) -> p (t n) d", n=4)

        def layer0_ffn(b, inputs, ao_all):
            with Stage("l0f") as sg:
                tensor_done, vector_done, scalar_done, vchain = (
                    sg.sem(n) for n in ("tensor_step", "vector_step", "scalar_step", "vector_chain"))
                qk = sg.sb("qk", [Q, T, 20, 16])
                v1 = sg.sb("v1", [Q, T, 4, 32])
                live = sg.sb("live", [Q, T, D])
                stacks = sg.sb("stacks", [Q, T, 2, 128], BF16)
                ab = sg.sb("ab", [128, S], BF16)
                ac = sg.sb("ac", [128, S], BF16)
                ao = sg.sb("ao", [Q, T, 16, 16])
                att = SplitAttention(nc, sg, "l0f_att", ps, 4, 4, ident16, ident, mask16, mask16_t, v1,
                                     lambda t: ao[:, t, :, :])
                block = sg.block()
                qkv_ps = ps[0:Q, 0:6, 0:384]

                @block.sync
                def _(sp):
                    clear_previous(sp, sg.sems)

                @block.vector
                def _(dve):
                    link = Chain(dve, vchain)
                    link(dve.tensor_copy(y[:, :, :], inputs[:, bass.ds(b, 1)].rearrange("p a t d -> p (a t) d")))
                    split_tokens(dve, link, stacks, y[:, :, :], sq[:, :, :])
                    dve.sem_inc(vector_done, 1)
                    link(dve.tensor_scalar(live[:, :, :], y[:, :, :], 0.0, None, ALU.not_equal))
                    dve.wait_ge(tensor_done, 1)
                    dve.tensor_copy(ab[:, :], turned_stack(6)).then_inc(vector_done, 1)
                    link(dve.memset(v1[:, :, :, :], 0.0))
                    link(dve.memset(v1[:, :, :, 16], 1.0))
                    link(dve.memset(att.kT[96:99, :, :], 1.0))
                    dve.wait_ge(tensor_done, 2)
                    link(dve.tensor_copy(qk[:, :, 16:20, :].rearrange("p t m d -> p t (m d)"), qkv_ps[:, :, 256:320]))
                    link(dve.tensor_scalar(qk[:, :, 0:16, :].rearrange("p t m d -> p t (m d)"), qkv_ps[:, :, 0:256],
                                           4.0, None, ALU.mult))
                    link(dve.tensor_copy(v1[:, :, :, 0:16], qkv_ps[:, :, 320:384].rearrange("p t (n d) -> p t n d", n=4)))
                    dve.sem_inc(vector_done, 1)
                    att.vector_stacks(dve, link, qk[:, :, 0:16, :], qk[:, :, 16:20, :])
                    att.vector(dve, link)
                    dve.wait_ge(att.out_ready, T)
                    four = ao[:, :, :, :].rearrange("p t (n e) d -> p (t n) e d", n=4)
                    kept = ao_all[:, bass.ds(b, 1)].rearrange("p a t (n e) d -> p (a t n) e d", n=4)
                    link(dve.tensor_tensor(kept, four, wide(heads(live).unsqueeze(2), [Q, 24, 4, 16]), ALU.mult))

                @block.scalar
                def _(act):
                    act.wait_ge(tensor_done, 1)
                    act.copy(ac[:, :], turned_stack(7)).then_inc(scalar_done, 1)
                    att.scalar(act)

                @block.tensor
                def _(pe):
                    pe.wait_ge(vector_done, 1)
                    turn_stacks(pe, 6, stacks).then_inc(tensor_done, 1)
                    pe.wait_ge(vector_done, 2)
                    pe.wait_ge(scalar_done, 1)
                    for t in range(T):
                        c = slice(Q * t, Q * t + Q)
                        mm = up.by_token(pe, ps[0:Q, t, 0:384], "l0f_qkv", 384, ab[:, c], ac[:, c])
                    mm.then_inc(tensor_done, 1)
                    pe.wait_ge(vector_done, 3)
                    att.tensor(pe)

        def layer0_gates(ao_all, h_all, x_all):
            with Stage("l0g") as sg:
                turned_ao, copied_ao, tensor_done, vector_done, scalar_done, vchain = (sg.sem(n) for n in (
                    "outputs_turned", "outputs_copied", "tensor_step", "vector_step", "scalar_step", "vector_chain"))
                gated = sg.sem("gated")
                passes = TurnedPasses(sg, ps, ident, TT)
                aoT = sg.sb("aoT", [128, 2, 12, Q])
                gate = sg.sb("gate", [Q, TT * 4, 4])
                fgate = sg.sb("fgate", [Q, TT, 4])
                xa = x_all[:, :, :, :].rearrange("p b t d -> p (b t) d")
                ha = h_all[:, :, :, :].rearrange("p b t d -> p (b t) d")
                ya = sg.sb("y", [Q, TT, D])
                sqa = sg.sb("sq", [Q, TT, D])
                live = sg.sb("live", [Q, TT, D])
                sta = sg.sb("st", [Q, 4, TT * 4])
                by_head = lambda buf: buf.rearrange("p t (n d) -> p (t n) d", d=16)
                rows_h = lambda row: wide(row.unsqueeze(1), [Q, TT * 4, 16])
                weights = (w["l0f_fc1"][:, :], w["l0f_fc2"][:, :], w["l0f_fgate"][:, :])
                block = sg.block()

                @block.sync
                def _(sp):
                    clear_previous(sp, sg.sems)

                @block.vector
                def _(dve):
                    link = Chain(dve, vchain)
                    passes.ones(dve, link)
                    dve.wait_ge(tensor_done, 1)
                    link(dve.tensor_tensor(gate[:, :, :].rearrange("p (t n) e -> p t (n e)", t=TT),
                                           ps[0:Q, 7, 0:16 * TT].rearrange("p (t n) -> p t n", t=TT),
                                           wide(rows["l0f_gate"].unsqueeze(1), [Q, TT, 16]), ALU.add))
                    softmax_first(dve, link, gate[:, :, :], sta)
                    dve.sem_inc(vector_done, 1)
                    dve.wait_ge(scalar_done, 1)
                    softmax_last(dve, link, gate[:, :, :], sta)
                    four = ao_all[:, :, :, :, :].rearrange("p b t (n e) d -> p (b t n) e d", n=4)
                    link(dve.tensor_tensor(four, four, wide(gate[:, :, :].unsqueeze(3), [Q, 4 * TT, 4, 16]), ALU.mult))
                    link(dve.tensor_reduce(by_head(ya[:, :, :]), four.rearrange("p g e d -> p g d e"), AX.X, ALU.add))
                    yb = ya[:, :, :].rearrange("p (b t) d -> p b (t d)", b=B)
                    rb = resid[:, :, :].rearrange("p t d -> p (t d)").unsqueeze(1)
                    link(dve.tensor_tensor(yb, yb, wide(rb, [Q, B, T * D]), ALU.add))
                    layer_norm(dve, link, by_head(xa), by_head(ya[:, :, :]), by_head(sqa[:, :, :]), sta, 1e-8)
                    affine(dve, link, by_head(xa), rows_h(rows["l0f_g"]), rows_h(rows["l0f_b"]))
                    passes.vector(dve, 0, lambda: link(dve.tensor_scalar(live[:, :, :], xa, 0.0, None, ALU.not_equal)))
                    link(dve.scalar_tensor_tensor(in_banks(ya[:, :, :]), passes.result(D), 0.0, in_banks(live[:, :, :]),
                                                  ALU.max, ALU.mult))
                    passes.vector(dve, 1)
                    link(dve.tensor_tensor(in_banks(ya[:, :, :]), passes.result(D), in_banks(live[:, :, :]), ALU.mult))
                    link(dve.tensor_tensor(xa, xa, ya[:, :, :], ALU.add))
                    layer_norm(dve, link, by_head(ya[:, :, :]), by_head(xa), by_head(sqa[:, :, :]), sta, 1e-8)
                    affine(dve, link, by_head(ya[:, :, :]), rows_h(rows["l0f_fg"]), rows_h(rows["l0f_fb"]))
                    passes.vector(dve, 2)
                    link(dve.tensor_copy(in_banks(fgate[:, :, :]), passes.result(4)))
                    softmax_first(dve, link, fgate[:, :, :], sta)
                    dve.sem_inc(vector_done, 1)
                    dve.wait_ge(scalar_done, 2)
                    softmax_last(dve, link, fgate[:, :, :], sta)
                    fg = fgate[:, :, :].rearrange("p t n -> p (t n)")
                    link(dve.tensor_tensor(by_head(ya[:, :, :]), by_head(ya[:, :, :]), wide(fg.unsqueeze(2), [Q, 4 * TT, 16]),
                                           ALU.mult))
                    link(dve.tensor_tensor(ha, ha, ya[:, :, :], ALU.add))
                    layer_norm(dve, link, xa, ha, sqa[:, :, :], sta, 1e-5)

                @block.scalar
                def _(act):
                    for b in range(B):
                        act.wait_ge(turned_ao, b + 1)
                        if b >= 2:
                            act.wait_ge(gated, b - 1)
                        src = ps[:, 3 * (b % 2):3 * (b % 2) + 3, :].rearrange("p b (k n) -> p (b k) n", n=128)[:, :, 0:Q]
                        act.copy(aoT[:, b % 2, :, :], src).then_inc(copied_ao, 1)
                    act.wait_ge(vector_done, 1)
                    act.activation(gate[:, :, :], gate[:, :, :], ACT.Exp).then_inc(scalar_done, 1)
                    for j in range(3):
                        passes.scalar(act, j)
                    act.wait_ge(vector_done, 2)
                    act.activation(fgate[:, :, :], fgate[:, :, :], ACT.Exp).then_inc(scalar_done, 1)

                @block.tensor
                def _(pe):
                    def turn_outputs(b):
                        if b >= 2:
                            pe.wait_ge(copied_ao, b - 1)
                        for i in range(12):
                            src = ao_all[:, b, i // 2, 8 * (i % 2):8 * (i % 2) + 8, :].rearrange("p m d -> p (m d)")
                            mm = pe.transpose(ps[:, 3 * (b % 2) + i // 4, 128 * (i % 4):128 * (i % 4) + Q], src,
                                              ident[0:Q, 0:Q])
                        mm.then_inc(turned_ao, 1)

                    def gates(b):
                        pe.wait_ge(copied_ao, b + 1)
                        for i in range(12):
                            at = 96 * b + 8 * i
                            mm = pe.matmul(ps[0:Q, 7, at:at + 8], aoT[:, b % 2, i, :], w["l0f_gate"][:, i % 2, :],
                                           start=True, stop=True)
                        mm.then_inc(gated, 1)
                        return mm

                    turn_outputs(0)
                    for b in range(B):
                        if b + 1 < B:
                            turn_outputs(b + 1)
                        gates(b)
                    pe.wait_ge(gated, B)
                    pe.sem_inc(tensor_done, 1)
                    for j, weight in enumerate(weights):
                        passes.turn(pe, j, xa if j == 0 else ya)
                        passes.by_token(pe, j, weight)

        def layer1_attention(b, x_all, attended):
            with Stage("l1a") as sg:
                tensor_done, vector_done, scalar_done, vchain = (
                    sg.sem(n) for n in ("tensor_step", "vector_step", "scalar_step", "vector_chain"))
                qk = sg.sb("qk", [Q, T, 2, D])
                v1 = sg.sb("v1", [Q, T, D + 1])
                qT = sg.sb("qT", [D, S])
                kT = sg.sb("kT", [D, S])
                sT = sg.sb("sT", [Q, T, S])
                den = sg.sb("den", [Q, T])
                block = sg.block()
                place = [(0, 0), (2, 0), (3, 0), (4, 0), (5, 0), (5, 192)]
                flat = qk[:, :, :, :].rearrange("p t c d -> p (t c) d")

                @block.sync
                def _(sp):
                    clear_previous(sp, sg.sems)

                @block.vector
                def _(dve):
                    link = Chain(dve, vchain)
                    dve.tensor_copy(x[:, :, :], x_all[:, bass.ds(b, 1)].rearrange("p a t d -> p (a t) d"))\
                       .then_inc(vector_done, 1)
                    link(dve.memset(v1[:, :, D:D + 1], 1.0))
                    dve.wait_ge(tensor_done, 1)
                    dve.tensor_copy(halves(xT[0:D, :]), two(0, D)).then_inc(vector_done, 1)
                    dve.wait_ge(tensor_done, 2)
                    qkv = ps[0:Q, 2:5, 0:384].rearrange("p b (a n) -> p b a n", a=2)
                    pairs = lambda t: t.rearrange("p (b a) n -> p b a n", a=2)
                    link(dve.tensor_scalar(pairs(qk[:, :, :, :].rearrange("p t c d -> p t (c d)")), qkv[:, :, :, 0:128],
                                           0.125, None, ALU.mult))
                    link(dve.tensor_copy(pairs(v1[:, :, 0:D]), qkv[:, :, :, 128:192]))
                    sum2, inv, tmp = (st[:, j, 0:12] for j in range(3))
                    s2 = sT[:, 0:3, 0:512].rearrange("p a (b d) -> p a b d", d=D)
                    sqr = sT[:, 0, 0:384].rearrange("p (g d) -> p g d", d=D)
                    for half in range(2):
                        part = flat[:, 6 * half:6 * half + 6, :]
                        link(dve.tensor_tensor(sqr, part, part, ALU.mult))
                        link(dve.tensor_reduce(sum2[:, 6 * half:6 * half + 6], sqr, AX.X, ALU.add))
                    link(dve.tensor_scalar(sum2, sum2, 1e-24, None, ALU.max))
                    rsqrt(dve, link, inv, sum2, tmp)
                    link(dve.tensor_tensor(flat, flat, wide(inv.unsqueeze(2), [Q, 12, D]), ALU.mult))
                    dve.sem_inc(vector_done, 1)
                    dve.wait_ge(scalar_done, 2)
                    dve.tensor_scalar(flat, flat, 1e-6, None, ALU.add).then_inc(vector_done, 1)
                    dve.wait_ge(tensor_done, 3)
                    dve.tensor_copy(halves(qT[:, :]), two(0, D)).then_inc(vector_done, 1)
                    dve.wait_ge(tensor_done, 4)
                    dve.tensor_copy(halves(kT[:, :]), two(5, D)).then_inc(vector_done, 1)
                    for k, (bank, col) in enumerate(place):
                        dve.wait_ge(tensor_done, 10)
                        n = S - Q * k
                        src = ps[0:Q, bank:bank + 2, :].rearrange("p b n -> p (b n)")[:, col:col + n]
                        dve.tensor_tensor(sT[:, k, Q * k:Q * k + Q], src[:, 0:Q], keep[:, :], ALU.mult).then_inc(vchain, 1)
                        link.n += 1
                        if n > Q:
                            link(dve.tensor_copy(sT[:, k, Q * k + Q:S], src[:, Q:n]))
                    dve.wait_ge(vchain, link.n)
                    dve.sem_inc(vector_done, 1)
                    dve.wait_ge(tensor_done, 11)
                    nd = tiles(6, D + 1)
                    link(dve.tensor_scalar(y[:, :, :], nd[:, :, 0:D], 1e4, -1e4, ALU.min, ALU.max))
                    link(dve.tensor_scalar(den[:, :], nd[:, :, D], 1e-6, None, ALU.max))
                    link(dve.reciprocal(den[:, :], den[:, :]))
                    link(dve.tensor_tensor(attended[:, bass.ds(b, 1)].rearrange("p a t d -> p (a t) d"), y[:, :, :],
                                           wide(den[:, :].unsqueeze(2), [Q, T, D]), ALU.mult))

                @block.scalar
                def _(act):
                    act.wait_ge(vector_done, 3)
                    act.activation(flat, flat, ACT.Exp).then_inc(scalar_done, 1)
                    act.wait_ge(scalar_done, 1)
                    act.activation(flat, flat, ACT.Ln, bias=1.0).then_inc(scalar_done, 1)

                @block.tensor
                def _(pe):
                    pe.wait_ge(vector_done, 1)
                    turn(pe, 0, x).then_inc(tensor_done, 1)
                    pe.wait_ge(vector_done, 2)
                    for t in range(T):
                        mm = pe.matmul(ps[0:Q, 2 + t // 2, 192 * (t % 2):192 * (t % 2) + 192], xT[:, Q * t:Q * t + Q],
                                       w["l1a_qkv"][:, :], start=True, stop=True)
                    mm.then_inc(tensor_done, 1)
                    pe.wait_ge(vector_done, 4)
                    turn(pe, 0, qk[:, :, 0, :]).then_inc(tensor_done, 1)
                    turn(pe, 5, qk[:, :, 1, :]).then_inc(tensor_done, 1)
                    pe.wait_ge(vector_done, 6)
                    for k, (bank, col) in enumerate(place):
                        for s in range(Q * k, S, 512):
                            e = min(S, s + 512)
                            at = bank + (s - Q * k) // 512
                            mm = pe.matmul(ps[0:Q, at, col:col + e - s], kT[:, Q * k:Q * k + Q], qT[:, s:e],
                                           start=True, stop=True)
                        mm.then_inc(tensor_done, 1)
                    pe.wait_ge(vector_done, 7)
                    for t in range(T):
                        for k in range(t + 1):
                            mm = pe.matmul(ps[0:Q, 6, 65 * t:65 * t + 65], sT[:, k, Q * t:Q * t + Q], v1[:, k, :],
                                           start=(k == 0), stop=(k == t))
                    mm.then_inc(tensor_done, 1)

        def layer1_mlp(h_all, x_all, attended):
            with Stage("l1m") as sg:
                up_ready, hidden_ready, vchain = (sg.sem(n) for n in ("up_ready", "hidden_ready", "vector_chain"))
                passes = TurnedPasses(sg, ps, ident, TT)
                xa, ha, ya = (s[:, :, :, :].rearrange("p b t d -> p (b t) d") for s in (x_all, h_all, attended))
                sqa = sg.sb("sq", [Q, TT, D])
                sta = sg.sb("st", [Q, 4, TT])
                hidden = sg.sb("hidden", [128, 2, TT * Q])
                units = [(n, c) for n in range(NC) for c in range(2)]
                block = sg.block()

                @block.sync
                def _(sp):
                    clear_previous(sp, sg.sems)

                @block.vector
                def _(dve):
                    link = Chain(dve, vchain)
                    passes.ones(dve, link)
                    passes.vector(dve, 0)
                    link(dve.tensor_tensor(in_banks(ya), passes.result(D), in_banks(xa), ALU.add))
                    layer_norm(dve, link, xa, ya, sqa[:, :, :], sta, 1e-5)
                    affine(dve, link, xa, over_tiles(rows["l1a_g1"]), over_tiles(rows["l1a_b1"]))
                    passes.vector(dve, 1, lambda: link(dve.tensor_tensor(ya, xa, over_tiles(rows["l1a_b2"]), ALU.add)))
                    link(dve.tensor_tensor(in_banks(ya), passes.result(D), in_banks(ya), ALU.add))
                    layer_norm(dve, link, xa, ya, sqa[:, :, :], sta, 1e-5)
                    affine(dve, link, xa, over_tiles(rows["l1a_g2"]), over_tiles(rows["l1a_nb2"]))
                    link(dve.tensor_tensor(ha, ha, xa, ALU.add))
                    layer_norm(dve, link, xa, ha, sqa[:, :, :], sta, 1e-5)
                    rms_norm(dve, link, ya, xa, sqa[:, :, :], sta, 1e-6, over_tiles(rows["l1f_w1"]))

                @block.scalar
                def _(act):
                    passes.scalar(act, 0)
                    passes.scalar(act, 1)
                    for u, (n, c) in enumerate(units):
                        act.wait_ge(up_ready, u + 1)
                        act.activation(hidden[:, c, CH * Q * n:CH * Q * n + CH * Q], ps[:, u % 4, 0:CH * Q], ACT.Gelu)\
                           .then_inc(hidden_ready, 1)

                @block.tensor
                def _(pe):
                    passes.turn(pe, 0, ya)
                    passes.by_token(pe, 0, w["l1a_proj"][:, :])
                    passes.turn(pe, 1, xa)
                    for k in range(5):
                        passes.wait_bank(pe, 1, k)

                    def down(n):
                        pe.wait_ge(hidden_ready, 2 * n + 2)
                        for i in range(CH * n, CH * n + CH):
                            for c in range(2):
                                mm = pe.matmul(ps[0:Q, 5 + i // 8, D * (i % 8):D * (i % 8) + D], hidden[:, c, Q * i:Q * i + Q],
                                               w["l1a_w2"][:, c, :], start=(c == 0), stop=(c == 1))
                        return mm

                    for u, (n, c) in enumerate(units):
                        if u >= 4:
                            pe.wait_ge(hidden_ready, u - 3)
                        pe.matmul(ps[:, u % 4, 0:CH * Q], w["l1a_w1"][:, 128 * c:128 * c + 128],
                                  passes.srcT[:, CH * Q * n:CH * Q * n + CH * Q], start=True, stop=True).then_inc(up_ready, 1)
                        if c == 1 and n >= 1:
                            down(n - 1)
                    down(NC - 1).then_inc(passes.product, 1)

        def top_two(dve, link, values, top, index, where, hot):
            n = values.shape[1]
            for t in range(n):
                ins = dve.max(top[:, t, :], values[:, t, :])
            link(ins)
            for t in range(n):
                ins = dve.max_index(index[:, t, :], top[:, t, :], values[:, t, :])
            link(ins)
            link(dve.tensor_copy(where[:, :, :], index[:, :, 0:2]))
            for j in range(2):
                link(dve.tensor_tensor(hot[:, j, :, :], over_tiles(iota8, n), wide(where[:, :, j:j + 1], [Q, n, 8]), ALU.is_equal))

        def experts(name, h_all, x_all, kind, norm_after=False):
            gated, soft = kind == "gated", kind == "soft"
            parts = 2 if gated else 1
            width = HP if gated else 128
            w1, w3, w2 = name + "_w1", name + "_w3", w[name + "_w2"]
            router = {"l1f": "l1f_router", "l2f": "l2f_g", "l3f": "l3f_r"}[name]
            with Stage(name + "_experts") as sg:
                tokens_ready, stacks_turned, copied_v, copied_s, router_ready, logits_ready, exps_ready, shares_ready = (
                    sg.sem(n) for n in ("tokens_ready", "stacks_turned", "ab_copied", "ac_copied", "router_ready",
                                        "logits_ready", "exps_ready", "shares_ready"))
                shares_turned, shares_copied, bias_ready, bias_used, up_ready, acted, hidden_ready, down_ready, added, vchain = (
                    sg.sem(n) for n in ("shares_turned", "shares_copied", "bias_ready", "bias_used", "up_ready", "acted",
                                        "hidden_ready", "down_ready", "added", "vector_chain"))
                ya = sg.sb("y", [Q, TT, D])
                sqa = sg.sb("sq", [Q, TT, D])
                sta = sg.sb("st", [Q, 4, TT])
                stacks = sg.sb("stacks", [Q, TT, 2, 128], BF16)
                ab = sg.sb("ab", [128, B, S], BF16)
                ac = sg.sb("ac", [128, B, S], BF16)
                logits = sg.sb("logits", [Q, TT, 8])
                top = sg.sb("top", [Q, TT, 8])
                index = sg.sb("index", [Q, TT, 8], U32)
                where = sg.sb("where", [Q, TT, 2])
                hot = sg.sb("hot", [Q, 2, TT, 8])
                share = sg.sb("share", [Q, TT, 8])
                shareT = sg.sb("shareT", [Q, 2, Q])
                second = sg.sb("second", [Q, TT])
                silu = sg.sb("silu", [HP, 2, CH * Q]) if gated else None
                hidden = sg.sb("hidden", [width, 2, parts, CH * Q])
                part_sum = sg.sb("part_sum", [Q, 2, CH, D])
                xa = x_all[:, :, :, :].rearrange("p b t d -> p (b t) d")
                ha = h_all[:, :, :, :].rearrange("p b t d -> p (b t) d")
                acc = xa if gated else sg.sb("acc", [Q, TT, D])[:, :, :]
                ab_flat, ac_flat = (s[:, :, :].rearrange("p b n -> p (b n)") for s in (ab, ac))
                units = [(e, c) for e in range(8) for c in range(NC)]
                BIAS_BANKS = (0, 3, 4, 7)
                block = sg.block()

                @block.sync
                def _(sp):
                    clear_previous(sp, sg.sems)

                @block.vector
                def _(dve):
                    link = Chain(dve, vchain)
                    if gated:
                        rms_norm(dve, link, ya[:, :, :], xa, sqa[:, :, :], sta, 1e-6, over_tiles(rows["l1f_w2"]))
                    else:
                        layer_norm(dve, link, xa, ha, sqa[:, :, :], sta, 1e-5)
                    if soft:
                        layer_norm(dve, link, ya[:, :, :], xa, sqa[:, :, :], sta, 1e-5)
                        affine(dve, link, ya[:, :, :], over_tiles(rows["l3f_g"]), over_tiles(rows["l3f_b"]))
                    split_tokens(dve, link, stacks, ya[:, :, :] if gated or soft else xa, sqa[:, :, :])
                    dve.sem_inc(tokens_ready, 1)
                    for b in range(B):
                        dve.wait_ge(stacks_turned, b + 1)
                        dve.tensor_copy(ab[:, b, :], turned_stack(2 * b)).then_inc(copied_v, 1)
                    dve.wait_ge(router_ready, 1)
                    src = ps[0:Q, 0, 0:8 * TT].rearrange("p (t n) -> p t n", t=TT)
                    if gated:
                        link(dve.tensor_copy(logits[:, :, :], src))
                        softmax_first(dve, link, logits[:, :, :], sta)
                        dve.sem_inc(logits_ready, 1)
                        dve.wait_ge(exps_ready, 1)
                        softmax_last(dve, link, logits[:, :, :], sta)
                    else:
                        link(dve.tensor_tensor(logits[:, :, :], src, over_tiles(rows[name + ("_br" if soft else "_bg")]), ALU.add))
                    top_two(dve, link, logits, top, index, where, hot)
                    first = sta[:, 0, 0:TT]
                    if gated:
                        link(dve.scalar_tensor_tensor(first, top[:, :, 0], 1e-9, top[:, :, 1], ALU.add, ALU.add))
                        link(dve.reciprocal(first, first))
                        link(dve.tensor_tensor(share[:, :, :], hot[:, 0, :, :], hot[:, 1, :, :], ALU.add))
                        link(dve.tensor_tensor(share[:, :, :], share[:, :, :], logits[:, :, :], ALU.mult))
                        link(dve.tensor_tensor(share[:, :, :], share[:, :, :], wide(first.unsqueeze(2), [Q, TT, 8]), ALU.mult))
                    else:
                        if soft:
                            link(dve.tensor_tensor(second[:, :], top[:, :, 1], top[:, :, 0], ALU.subtract))
                            dve.sem_inc(logits_ready, 1)
                            dve.wait_ge(exps_ready, 1)
                            link(dve.tensor_scalar(first, second[:, :], 1.0, None, ALU.add))
                            link(dve.reciprocal(first, first))
                            link(dve.tensor_tensor(second[:, :], second[:, :], first, ALU.mult))
                            for j, part in enumerate((first, second[:, :])):
                                link(dve.tensor_tensor(hot[:, j, :, :], hot[:, j, :, :], wide(part.unsqueeze(2), [Q, TT, 8]),
                                                       ALU.mult))
                        link(dve.tensor_tensor(share[:, :, :], hot[:, 0, :, :], hot[:, 1, :, :], ALU.add))
                        dve.sem_inc(shares_ready, 1)
                        dve.wait_ge(shares_turned, 1)
                        dve.tensor_copy(shareT[:, :, :], ps[0:Q, 0, 0:2 * Q].rearrange("p (k n) -> p k n", k=2))\
                           .then_inc(shares_copied, 1)
                        dve.wait_ge(bias_ready, 1)
                        for k, bank in enumerate(BIAS_BANKS):
                            link(dve.tensor_copy(acc[:, 6 * k:6 * k + 6, :], tiles(bank)))

                    def add(u):
                        e, c = units[u]
                        at = slice(CH * c, CH * c + CH)
                        dve.wait_ge(down_ready, u + 1)
                        src = ps[0:Q, 5 + u % 2, 0:CH * D].rearrange("p (t n) -> p t n", t=CH)
                        link(dve.tensor_tensor(part_sum[:, u % 2, :, :], src, wide(share[:, at, e:e + 1], [Q, CH, D]), ALU.mult))
                        dve.tensor_tensor(acc[:, at, :], acc[:, at, :], part_sum[:, u % 2, :, :], ALU.add).then_inc(added, 1)
                        if u % NC == NC - 1:
                            dve.wait_ge(added, u + 1)

                    for u in range(len(units)):
                        if gated:
                            for j in range(2):
                                v = 2 * u + j
                                dve.wait_ge(acted, v + 1)
                                if u >= 2:
                                    dve.wait_ge(down_ready, u - 1)
                                dve.tensor_tensor(hidden[:, u % 2, j, :], silu[:, v % 2, :], ps[0:HP, 3 + v % 2, 0:CH * Q],
                                                  ALU.mult).then_inc(hidden_ready, 1)
                        if u >= 1:
                            add(u - 1)
                    add(len(units) - 1)
                    dve.wait_ge(added, len(units))
                    link(dve.tensor_tensor(ha, ha, acc, ALU.add))
                    if norm_after:
                        layer_norm(dve, link, xa, ha, sqa[:, :, :], sta, 1e-5)

                @block.scalar
                def _(act):
                    for b in range(B):
                        act.wait_ge(stacks_turned, b + 1)
                        act.copy(ac[:, b, :], turned_stack(2 * b + 1)).then_inc(copied_s, 1)
                    if gated or soft:
                        act.wait_ge(logits_ready, 1)
                        part = logits[:, :, :] if gated else second[:, :]
                        act.activation(part, part, ACT.Exp).then_inc(exps_ready, 1)
                    for u, (e, c) in enumerate(units):
                        for j in range(parts):
                            v = parts * u + j
                            act.wait_ge(up_ready, v + 1)
                            if gated:
                                if v >= 2:
                                    act.wait_ge(hidden_ready, v - 1)
                                act.activation(silu[:, v % 2, :], ps[0:HP, 1 + v % 2, 0:CH * Q], ACT.Silu).then_inc(acted, 1)
                            else:
                                if u >= 2:
                                    act.wait_ge(down_ready, u - 1)
                                act.activation(hidden[:, u % 2, 0, :], ps[:, 1 + u % 2, 0:CH * Q], ACT.Gelu,
                                               bias=w[name + "_b1"][:, e:e + 1]).then_inc(hidden_ready, 1)

                @block.tensor
                def _(pe):
                    pe.wait_ge(tokens_ready, 1)
                    for b in range(B):
                        for j in range(2):
                            for t in range(T):
                                mm = pe.transpose(turned_stack(2 * b + j)[:, Q * t:Q * t + Q], stacks[:, T * b + t, j, :],
                                                  ident16[:, :])
                        mm.then_inc(stacks_turned, 1)
                    pe.wait_ge(copied_v, B)
                    pe.wait_ge(copied_s, B)
                    for t in range(TT):
                        c = slice(Q * t, Q * t + Q)
                        mm = up.by_token(pe, ps[0:Q, 0, 8 * t:8 * t + 8], router, 8, ab_flat[:, c], ac_flat[:, c])
                    mm.then_inc(router_ready, 1)

                    def ups(u):
                        e, c = units[u]
                        cols = slice(CH * Q * c, CH * Q * c + CH * Q)
                        for j in range(parts):
                            v = parts * u + j
                            if v >= 2:
                                pe.wait_ge(hidden_ready, v - 1)
                            if gated:
                                up.by_feature(pe, ps[0:HP, 1 + v % 2, 0:CH * Q], w1, HID * e + HP * j, HP,
                                              ab_flat[:, cols], ac_flat[:, cols])
                                mm = up.by_feature(pe, ps[0:HP, 3 + v % 2, 0:CH * Q], w3, HID * e + HP * j, HP,
                                                   ab_flat[:, cols], ac_flat[:, cols])
                            else:
                                mm = up.by_feature(pe, ps[:, 1 + u % 2, 0:CH * Q], w1, 128 * e, 128,
                                                   ab_flat[:, cols], ac_flat[:, cols])
                            mm.then_inc(up_ready, 1)

                    def down(u):
                        e, c = units[u]
                        pe.wait_ge(hidden_ready, parts * (u + 1))
                        if u >= 2:
                            pe.wait_ge(added, u - 1)
                        for t in range(CH):
                            for j in range(parts):
                                w2_part = w2[:, e, j, :] if gated else w2[:, e, :]
                                mm = pe.matmul(ps[0:Q, 5 + u % 2, D * t:D * t + D], hidden[:, u % 2, j, Q * t:Q * t + Q],
                                               w2_part, start=(j == 0), stop=(j == parts - 1))
                        mm.then_inc(down_ready, 1)

                    ups(0)
                    if not gated:
                        pe.wait_ge(shares_ready, 1)
                        flat = share[:, :, :].rearrange("p t e -> p (t e)")
                        for k in range(2):
                            mm = pe.transpose(ps[0:Q, 0, Q * k:Q * k + Q], flat[:, Q * k:Q * k + Q], ident[0:Q, 0:Q])
                        mm.then_inc(shares_turned, 1)
                        pe.wait_ge(shares_copied, 1)
                        for k, bank in enumerate(BIAS_BANKS):
                            cols = slice(6 * D * (k % 2), 6 * D * (k % 2) + 6 * D)
                            mm = pe.matmul(ps[0:Q, bank, 0:6 * D], shareT[:, k // 2, :], w[name + "_b2"][:, cols],
                                           start=True, stop=True)
                        mm.then_inc(bias_ready, 1)
                    for u in range(1, len(units)):
                        ups(u)
                        down(u - 1)
                    down(len(units) - 1)

        def layer1_ffn(b, x_all, normed):
            with Stage("l1f") as sg:
                tensor_done, vector_done, scalar_done, vchain = (
                    sg.sem(n) for n in ("tensor_step", "vector_step", "scalar_step", "vector_chain"))
                qs = sg.sb("qs", [Q, T, 128])
                ro = sg.sb("ro", [Q, T, 6, 16])
                ra = sg.sb("ra", [Q, T, 6, 8])
                rb = sg.sb("rb", [Q, T, 6, 8])
                v1 = sg.sb("v1", [Q, T, 2, 32])
                ao = sg.sb("ao", [Q, T, D])
                att = SplitAttention(nc, sg, "l1f_att", ps, 2, 2, ident16, ident, mask16, mask16_t, v1,
                                     lambda t: ao[:, t, :].rearrange("p (m d) -> p m d", m=4))
                block = sg.block()

                @block.sync
                def _(sp):
                    clear_previous(sp, sg.sems)

                @block.vector
                def _(dve):
                    link = Chain(dve, vchain)
                    dve.tensor_copy(y[:, :, :], normed[:, bass.ds(b, 1)].rearrange("p a t d -> p (a t) d"))\
                       .then_inc(vector_done, 1)
                    link(dve.memset(v1[:, :, :, :], 0.0))
                    link(dve.memset(v1[:, :, :, 16], 1.0))
                    link(dve.memset(att.kT[96:99, :, :], 1.0))
                    dve.wait_ge(tensor_done, 1)
                    dve.tensor_copy(halves(yT[0:D, :]), two(0, D)).then_inc(vector_done, 1)
                    dve.wait_ge(tensor_done, 2)
                    flat = ps[0:Q, 2:4, :].rearrange("p b n -> p (b n)")[:, 0:768]
                    link(dve.tensor_copy(qs[:, :, :].rearrange("p t n -> p (t n)"), flat))
                    v6 = qs[:, :, 0:96].rearrange("p t (n d) -> p t n d", n=6)
                    first, second = v6[:, :, :, 0:8], v6[:, :, :, 8:16]
                    c6 = wide(cos_t[:, :, :].unsqueeze(2), [Q, T, 6, 8])
                    s6 = wide(sin_t[:, :, :].unsqueeze(2), [Q, T, 6, 8])
                    link(dve.tensor_tensor(ra[:, :, :, :], first, c6, ALU.mult))
                    link(dve.tensor_tensor(rb[:, :, :, :], second, s6, ALU.mult))
                    link(dve.tensor_tensor(ro[:, :, :, 0:8], ra[:, :, :, :], rb[:, :, :, :], ALU.subtract))
                    link(dve.tensor_tensor(ra[:, :, :, :], second, c6, ALU.mult))
                    link(dve.tensor_tensor(rb[:, :, :, :], first, s6, ALU.mult))
                    link(dve.tensor_tensor(ro[:, :, :, 8:16], ra[:, :, :, :], rb[:, :, :, :], ALU.add))
                    link(dve.tensor_scalar(ro[:, :, 0:4, :], ro[:, :, 0:4, :], 0.25, None, ALU.mult))
                    link(dve.tensor_copy(v1[:, :, :, 0:16], qs[:, :, 96:128].rearrange("p t (g d) -> p t g d", g=2)))
                    att.vector_stacks(dve, link, ro[:, :, 0:4, :], ro[:, :, 4:6, :])
                    att.vector(dve, link)
                    dve.wait_ge(tensor_done, 3)
                    dve.tensor_copy(halves(yT[0:D, :]), two(0, D)).then_inc(vector_done, 1)
                    dve.wait_ge(tensor_done, 4)
                    own = x_all[:, bass.ds(b, 1)].rearrange("p a t d -> p (a t) d")
                    link(dve.tensor_tensor(own, own, tiles(2), ALU.add))

                @block.scalar
                def _(act):
                    att.scalar(act)

                @block.tensor
                def _(pe):
                    pe.wait_ge(vector_done, 1)
                    turn(pe, 0, y).then_inc(tensor_done, 1)
                    pe.wait_ge(vector_done, 2)
                    for t in range(T):
                        mm = pe.matmul(ps[0:Q, 2 + t // 4, 128 * (t % 4):128 * (t % 4) + 128], yT[0:D, Q * t:Q * t + Q],
                                       w["l1f_qkv"][:, :], start=True, stop=True)
                    mm.then_inc(tensor_done, 1)
                    att.tensor(pe)
                    pe.wait_ge(att.out_ready, T)
                    turn(pe, 0, ao).then_inc(tensor_done, 1)
                    pe.wait_ge(vector_done, 3)
                    by_token(pe, 2, yT[0:D, :], w["l1f_wo"][:, :]).then_inc(tensor_done, 1)

        def layer2_attention(b, h_all, x_all):
            H, R = 4, D // 2
            NT = S // R
            KC = (S + 127) // 128
            COLS = 6 * R
            SPREADS = 8
            with Stage("l2a") as sg:
                tensor_done, vector_done, scalar_done, vchain = (
                    sg.sem(n) for n in ("tensor_step", "vector_step", "scalar_step", "vector_chain"))
                k_parts, k_parts_copied, pick_ready, folded, started, spread, spread_copied, paired, best_ready, exp_ready, total_ready, diagonal_ready, turned, \
                    turned_copied, product_ready = (sg.sem(n) for n in (
                        "key_parts", "key_parts_copied", "pick_ready", "folded",
                        "started", "spread", "spread_copied", "paired_passes", "best_ready", "exp_ready", "total_ready",
                        "diagonal_ready", "turned", "turned_copied", "product_ready"))
                q = sg.sb("q", [128, NT, 16])
                k_ab = sg.sb("k_ab", [2 * D, S], BF16)
                k_b = sg.sb("k_b", [D, S], BF16)
                k_c = sg.sb("k_c", [D, S], BF16)
                k_rest = sg.sb("k_rest", [D, S])
                wvo = sg.sb("wvo", [D, H, D])
                vo = sg.sb("vo", [128, KC, H, D])
                pick = sg.sb("pick", [2 * D, 16, H, R], BF16)
                keys = sg.sb("keys", [128, 16, S])
                score = sg.sb("score", [128, 4, S])
                taken = sg.sb("taken", [128, 2, S])
                weight = sg.sb("weight", [128, 4, S])
                diagonal = sg.sb("diagonal", [128, 2, 128])
                weightT = sg.sb("weightT", [128, 2, KC, 128])
                best = sg.sb("best", [128, 4, 8])
                neg_max = sg.sb("neg_max", [128, 4])
                total = sg.sb("total", [128, 4])
                block = sg.block()
                order = [t for p in (2, 3, 4, 5, 6, 7, 8, 1, 0) for t in (2 * p, 2 * p + 1)]
                pairs = [((i, order[i]), (i + 1, order[i + 1])) for i in range(0, NT, 2)]
                spreads_before = lambda pair: SPREADS * (-(-R * (pair[1][1] + 1) // COLS) - 1)
                PER_PAIR = 2 * (15 + 4)
                rows_of = lambda k, t: min(128, R * (t + 1) - 128 * k)

                @block.sync
                def _(sp):
                    clear_previous(sp, sg.sems)

                @block.vector
                def _(dve):
                    link = Chain(dve, vchain)
                    dve.tensor_copy(x[:, :, :], x_all[:, bass.ds(b, 1)].rearrange("p a t d -> p (a t) d"))\
                       .then_inc(vector_done, 1)
                    dve.wait_ge(tensor_done, 1)
                    dve.tensor_copy(halves(xT[0:D, :]), two(0, D)).then_inc(vector_done, 1)
                    dve.wait_ge(scalar_done, 2)
                    link(dve.tensor_tensor(halves(k_rest[:, :]), two(2, D), halves(k_ab[0:D, :]), ALU.subtract))
                    dve.tensor_copy(k_b[:, :], k_rest[:, :]).then_inc(k_parts, 1)
                    dve.wait_ge(k_parts, 1)
                    dve.tensor_tensor(k_c[:, :], k_rest[:, :], k_b[:, :], ALU.subtract).then_inc(k_parts, 1)
                    dve.wait_ge(tensor_done, 3)
                    dve.tensor_copy(q[:, :, :].rearrange("p t d -> p (t d)"), ps[:, 6, 0:16 * NT]).then_inc(vector_done, 1)
                    dve.wait_ge(vector_done, 3)

                    issued = [0]

                    def alternate(ins):
                        ins.then_inc(paired, 1)
                        issued[0] += 1
                        if issued[0] >= 2:
                            dve.wait_ge(paired, issued[0] - 1)

                    def weigh(i, t):
                        dve.wait_ge(exp_ready, i + 1)
                        e = weight[:, i % 4, 0:R * (t + 1)]
                        link(dve.scalar_tensor_tensor(e, taken[:, i % 2, 0:R * (t + 1)], 2 * NEG, e, ALU.is_le, ALU.mult,
                                                      accum_out=total[:, i % 4:i % 4 + 1]))
                        dve.reciprocal(total[:, i % 4:i % 4 + 1], total[:, i % 4:i % 4 + 1]).then_inc(total_ready, 1)

                    for p, pair in enumerate(pairs):
                        part = lambda buf, i, t: buf[:, i % 4, 0:R * (t + 1)]
                        before = spreads_before(pair)
                        dve.wait_ge(started, 2 * p + 2)
                        dve.wait_ge(spread_copied, before + 1)
                        for d in range(1, 16):
                            if d % 2 == 0:
                                dve.wait_ge(spread_copied, before + d // 2 + 1)
                            for i, t in pair:
                                alternate(dve.scalar_tensor_tensor(part(score, i, t), keys[:, d, 0:R * (t + 1)],
                                                                   q[:, t, d:d + 1], part(score, i, t), ALU.add, ALU.max))
                        for i, t in pair:
                            diag = score[:, i % 4, R * t:R * t + R]
                            alternate(dve.tensor_tensor(diag, diag, causal32[:, :], ALU.add))
                        for i, t in pair:
                            alternate(dve.max(best[:, i % 4, :], part(score, i, t)))
                        for i, t in pair:
                            alternate(dve.tensor_scalar(neg_max[:, i % 4:i % 4 + 1], best[:, i % 4, 0:1], -1.0, None, ALU.mult))
                        dve.wait_ge(paired, issued[0])
                        dve.sem_inc(best_ready, 2)
                        if p >= 1:
                            for i, t in pairs[p - 1]:
                                weigh(i, t)
                            dve.wait_ge(total_ready, 2 * p)
                        for i, t in pair:
                            alternate(dve.match_replace(taken[:, i % 2, 0:R * (t + 1)], best[:, i % 4, :], part(score, i, t),
                                                        3 * NEG))
                    assert issued[0] == PER_PAIR * len(pairs)
                    dve.wait_ge(paired, issued[0])
                    for i, t in pairs[-1]:
                        weigh(i, t)
                    dve.wait_ge(product_ready, NT)
                    own = h_all[:, bass.ds(b, 1)].rearrange("p a t d -> p (a t) d")
                    link(dve.tensor_tensor(own, own, tiles(7), ALU.add))

                @block.scalar
                def _(act):
                    for rows_p in (slice(0, D), slice(D, 2 * D)):
                        act.copy(pick[rows_p, :, :, :], wide(ident[rows_p, rows_p].rearrange("p (n d) -> p d n", n=H)
                                                             .unsqueeze(3), [D, 16, H, R])).then_inc(pick_ready, 1)
                    act.wait_ge(folded, 1)
                    act.copy(wvo[:, :, :].rearrange("p n o -> p (n o)"), ps[0:D, 4, 0:H * D]).then_inc(scalar_done, 1)
                    act.wait_ge(tensor_done, 2)
                    act.copy(halves(k_ab[0:D, :]), two(2, D)).then_inc(scalar_done, 1)
                    act.wait_ge(k_parts, 1)
                    act.copy(k_ab[D:2 * D, :], k_b[:, :]).then_inc(k_parts_copied, 1)

                    def spread_out(s):
                        act.wait_ge(spread, s + 1)
                        c, d = s // SPREADS, 2 * (s % SPREADS)
                        act.copy(keys[:, d:d + 2, COLS * c:COLS * c + COLS],
                                 ps[:, s % 2, 0:2 * COLS].rearrange("p (d n) -> p d n", d=2)).then_inc(spread_copied, 1)

                    def diagonal_out(i):
                        act.wait_ge(total_ready, i + 1)
                        if i >= 2:
                            act.wait_ge(turned, i - 1)
                        act.activation(diagonal[:, i % 2, :], ident[:, :], ACT.Copy,
                                       scale=total[:, i % 4:i % 4 + 1]).then_inc(diagonal_ready, 1)

                    def turned_out(i, t):
                        act.wait_ge(turned, i + 1)
                        if i >= 2:
                            act.wait_ge(product_ready, i - 1)
                        full, b = R * (t + 1) // 128, 2 + 2 * (i % 2)
                        src = ps[:, b:b + 2, :].rearrange("p b (k n) -> p (b k) n", n=128)
                        if full:
                            act.copy(weightT[:, i % 2, 0:full, :], src[:, 0:full, :]).then_inc(turned_copied, 1)
                        else:
                            act.sem_inc(turned_copied, 1)
                        if R * (t + 1) % 128:
                            r = rows_of(full, t)
                            act.copy(weightT[0:r, i % 2, full, :], src[0:r, full, :]).then_inc(turned_copied, 1)
                        else:
                            act.sem_inc(turned_copied, 1)

                    def start(p):
                        if p >= 2:
                            act.wait_ge(paired, PER_PAIR * (p - 1))
                            act.wait_ge(exp_ready, 2 * p - 2)
                        act.wait_ge(spread_copied, spreads_before(pairs[p]) + 1)
                        for i, t in pairs[p]:
                            act.activation(score[:, i % 4, 0:R * (t + 1)], keys[:, 0, 0:R * (t + 1)], ACT.Identity,
                                           bias=q[:, t, 0:1]).then_inc(started, 1)

                    spread_out(0)
                    act.wait_ge(vector_done, 3)
                    start(0)
                    for s in range(1, SPREADS):
                        spread_out(s)
                    act.wait_ge(tensor_done, 4)
                    flat = vo[:, :, :, :].rearrange("p k n o -> p (k n o)")
                    act.copy(flat[:, 0:1024], ps[:, 4:6, :].rearrange("p b n -> p (b n)")).then_inc(scalar_done, 1)
                    act.copy(flat[0:S - 512, 1024:1280], ps[0:S - 512, 7, 0:256]).then_inc(scalar_done, 1)
                    for p, pair in enumerate(pairs):
                        spreads = range(SPREADS * (p + 1), SPREADS * (p + 2)) if p < 2 else ()
                        for s in spreads[:1] if p == 0 else ():
                            spread_out(s)
                        if p + 1 < len(pairs):
                            start(p + 1)
                        for s in spreads[1:] if p == 0 else spreads:
                            spread_out(s)
                        for i, t in pair:
                            act.wait_ge(best_ready, 2 * p + 2)
                            if i >= 4:
                                act.wait_ge(turned, i - 3)
                            act.activation(weight[:, i % 4, 0:R * (t + 1)], score[:, i % 4, 0:R * (t + 1)], ACT.Exp,
                                           bias=neg_max[:, i % 4:i % 4 + 1]).then_inc(exp_ready, 1)
                        if p >= 1:
                            for i, t in pairs[p - 1]:
                                diagonal_out(i)
                                turned_out(i, t)
                    for i, t in pairs[-1]:
                        diagonal_out(i)
                        turned_out(i, t)

                @block.tensor
                def _(pe):
                    for n in range(H):
                        mm = pe.matmul(ps[0:D, 4, D * n:D * n + D], w["l2a_v"][:, n, :], w["l2a_o"][:, n, :], start=True, stop=True)
                    mm.then_inc(folded, 1)
                    pe.wait_ge(vector_done, 1)
                    turn(pe, 0, x).then_inc(tensor_done, 1)
                    pe.wait_ge(vector_done, 2)
                    xf = xT[0:D, :]
                    by_feature(pe, 2, w["l2a_k"][:, :], xf).then_inc(tensor_done, 1)
                    for t in range(NT):
                        for n in range(H):
                            mm = pe.matmul(ps[R * n:R * n + R, 6, 16 * t:16 * t + 16], xf[:, R * t:R * t + R],
                                           w["l2a_q"][:, 16 * n:16 * n + 16], start=True, stop=True)
                    mm.then_inc(tensor_done, 1)
                    pe.wait_ge(k_parts, 2)
                    pe.wait_ge(k_parts_copied, 1)
                    pe.wait_ge(pick_ready, 2)

                    def spread_in(s):
                        if s >= 2:
                            pe.wait_ge(spread_copied, s - 1)
                        c = s // SPREADS
                        for j in range(2):
                            d = 2 * (s % SPREADS) + j
                            dst, cols = ps[:, s % 2, COLS * j:COLS * j + COLS], slice(COLS * c, COLS * c + COLS)
                            of = lambda rows_p: pick[rows_p, d, :, :].rearrange("p n i -> p (n i)")
                            pe.matmul(dst, of(slice(0, 2 * D)), k_ab[:, cols], start=True, stop=False)
                            mm = pe.matmul(dst, of(slice(0, D)), k_c[:, cols], start=False, stop=True)
                        mm.then_inc(spread, 1)

                    def turn_weights(i, t):
                        pe.wait_ge(diagonal_ready, i + 1)
                        if i == 0:
                            pe.wait_ge(scalar_done, 4)
                        if i >= 2:
                            pe.wait_ge(turned_copied, 2 * i - 2)
                        b = 2 + 2 * (i % 2)
                        dst = ps[:, b:b + 2, :].rearrange("p b (k n) -> p (b k) n", n=128)
                        for k in range(-(-R * (t + 1) // 128)):
                            r = rows_of(k, t)
                            mm = pe.matmul(dst[0:r, k, :], weight[:, i % 4, 128 * k:128 * k + r], diagonal[:, i % 2, :],
                                           start=True, stop=True)
                        mm.then_inc(turned, 1)

                    def products(i, t):
                        pe.wait_ge(turned_copied, 2 * i + 2)
                        chunks = range(-(-R * (t + 1) // 128))
                        out = ps[R * (t % 3):R * (t % 3) + R, 7, D * (t // 3):D * (t // 3) + D]
                        for k in chunks:
                            for n in range(H):
                                r = rows_of(k, t)
                                mm = pe.matmul(out, weightT[0:r, i % 2, k, R * n:R * n + R], vo[0:r, k, n, :],
                                               start=(k == n == 0), stop=(k == chunks[-1] and n == H - 1))
                        mm.then_inc(product_ready, 1)

                    for s in range(SPREADS):
                        spread_in(s)
                    pe.wait_ge(scalar_done, 1)
                    for k in range(KC):
                        n = min(128, S - 128 * k)
                        dst = ps[0:n, 4 + k // 2, 256 * (k % 2):256 * (k % 2) + 256] if k < 4 else ps[0:n, 7, 0:256]
                        mm = pe.matmul(dst, xf[:, 128 * k:128 * k + n], wvo[:, :, :], start=True, stop=True)
                    mm.then_inc(tensor_done, 1)
                    for p, pair in enumerate(pairs):
                        if p < 2:
                            for s in range(SPREADS * (p + 1), SPREADS * (p + 2)):
                                spread_in(s)
                        if p >= 1:
                            for i, t in pairs[p - 1]:
                                turn_weights(i, t)
                            for i, t in pairs[p - 1]:
                                products(i, t)
                    for i, t in pairs[-1]:
                        turn_weights(i, t)
                    for i, t in pairs[-1]:
                        products(i, t)

        def layer3_attention(b, h_all, x_all):
            with Stage("l3a") as sg:
                tensor_done, vector_done, scalar_done, vchain = (
                    sg.sem(n) for n in ("tensor_step", "vector_step", "scalar_step", "vector_chain"))
                qT = sg.sb("qT", [D, S])
                kT = sg.sb("kT", [D, S])
                v = sg.sb("v", [Q, T, D])
                o = sg.sb("o", [Q, T, D])
                att = Attention(nc, sg, "l3a_att", ps, 1, D, False,
                                lambda m, t: qT[:, Q * t:Q * t + Q], lambda m, s, e: kT[:, s:e],
                                lambda m, k: v[:, k, :], lambda t: o[:, t:t + 1, :])
                block = sg.block()

                @block.sync
                def _(sp):
                    clear_previous(sp, sg.sems)

                @block.vector
                def _(dve):
                    link = Chain(dve, vchain)
                    dve.tensor_copy(x[:, :, :], x_all[:, bass.ds(b, 1)].rearrange("p a t d -> p (a t) d"))\
                       .then_inc(vector_done, 1)
                    dve.wait_ge(tensor_done, 1)
                    dve.tensor_copy(halves(xT[0:D, :]), two(0, D)).then_inc(vector_done, 1)
                    dve.wait_ge(tensor_done, 3)
                    dve.tensor_copy(halves(kT[:, :]), two(4, D)).then_inc(vector_done, 1)
                    att.vector(dve, link)
                    dve.wait_ge(att.out_ready, T)
                    own = h_all[:, bass.ds(b, 1)].rearrange("p a t d -> p (a t) d")
                    link(dve.tensor_tensor(own, own, o[:, :, :], ALU.add))

                @block.scalar
                def _(act):
                    act.wait_ge(tensor_done, 2)
                    act.mul(halves(qT[:, :]), two(2, D), 0.125).then_inc(scalar_done, 1)
                    act.wait_ge(tensor_done, 4)
                    act.copy(v[:, :, :], tiles(6)).then_inc(scalar_done, 1)
                    att.scalar(act)

                @block.tensor
                def _(pe):
                    pe.wait_ge(vector_done, 1)
                    turn(pe, 0, x).then_inc(tensor_done, 1)
                    pe.wait_ge(vector_done, 2)
                    by_feature(pe, 2, w["l3a_qkv"][:, 0:64], xT).then_inc(tensor_done, 1)
                    by_feature(pe, 4, w["l3a_qkv"][:, 64:128], xT).then_inc(tensor_done, 1)
                    by_token(pe, 6, xT, w["l3a_qkv"][:, 128:192]).then_inc(tensor_done, 1)
                    pe.wait_ge(vector_done, 3)
                    pe.wait_ge(scalar_done, 2)
                    att.tensor(pe, ident)

        def row1(ap, n, p=Q):
            return wide(ap.rearrange("(a n) -> a n", a=1), [p, n])

        with Stage("load") as sg:
            loaded = sg.sem("loaded")
            tables_loaded = sg.sem("tables_loaded")
            block = sg.block()

            @block.vector
            def _(dve):
                dve.memset(ones[:, :], 1.0)
                dve.memset(xT[D:D + 1, :], 1.0)
                dve.memset(yT[D:D + 1, :], 1.0)
                dve.wait_ge(tables_loaded, 32)
                dve.tensor_copy(ident16[:, :], ident[0:Q, 0:Q])
                dve.tensor_copy(mask16[:, :], causal[:, :])
                dve.tensor_scalar(mask16_t[:, :], keep[:, :], -1.0, -NEG, ALU.add, ALU.mult)

            @block.sync
            def _(sp):
                for pack in ("w128", "w96"):
                    sp.dma_start(packs[pack][:, :], a["pack_" + pack]).then_inc(tables_loaded, 16)
                others = [pack for pack in PACKS if pack not in ("w128", "w96", "up")]
                for pack in others:
                    src = a["pack_" + pack]
                    sp.dma_start(packs[pack][:, :], wide(src, [Q, src.shape[1]]) if pack == "rows" else src)\
                      .then_inc(loaded, 16)
                sp.wait_ge(tables_loaded, 32)
                sp.wait_ge(loaded, 16 * len(others))

        ids = sb("token_ids", [128, B * TXT // 128], I32)
        base = sb("token_turns", [128, B * TXT // 128, 4])
        fourier(nc, a, ps, ident, ids, base, h_in, Stage, clear_previous, end_of_pass)
        text(nc, a, ps, ident, up, base, h_in, Stage, clear_previous)

        h_all = sb("h_all", [Q, B, T, D])
        x_all = sb("x_all", [Q, B, T, D])
        io_all = sb("io_all", [Q, B, T, D])
        xa, ha, ya = (s[:, :, :, :].rearrange("p b t d -> p (b t) d") for s in (x_all, h_all, io_all))

        def store():
            with Stage("store") as sg:
                stored = sg.sem("stored")
                block = sg.block()

                @block.sync
                def _(sp):
                    clear_previous(sp, sg.sems)
                    sp.dma_start(out.rearrange("b (t p) n -> p b t n", p=Q), h_all[:, :, :, :]).then_inc(stored, 16)
                    sp.wait_ge(stored, 16)

        with Stage("l0p") as sg:
            loaded, vchain = sg.sem("h_loaded"), sg.sem("vector_chain")
            sqa = sg.sb("sq", [Q, TT, D])
            sta = sg.sb("st", [Q, 4, TT])
            block = sg.block()

            @block.sync
            def _(sp):
                clear_previous(sp, sg.sems)
                sp.dma_start(h_all[:, :, :, :], h_in.rearrange("b (t p) n -> p b t n", p=Q)).then_inc(loaded, 16)

            @block.vector
            def _(dve):
                link = Chain(dve, vchain)
                dve.wait_ge(loaded, 16)
                layer_norm(dve, link, xa, ha, sqa[:, :, :], sta, 1e-5)
                layer_norm(dve, link, ya, xa, sqa[:, :, :], sta, 1e-5)
                affine(dve, link, ya, over_tiles(rows["l0a_g1"]), over_tiles(rows["l0a_b1"]))

        with nc.Fori(0, B) as b:
            with Stage("l0a") as sg:
                tensor_done = sg.sem("tensor_step")
                vector_done = sg.sem("vector_step")
                scalar_done = sg.sem("scalar_step")
                vchain = sg.sem("vector_chain")
                qT = sg.sb("qT", [D, S])
                kT = sg.sb("kT", [D, S])
                v = sg.sb("v", [Q, T, D])
                o = sg.sb("o", [Q, T, D])
                att = Attention(nc, sg, "l0a_att", ps, 1, D, False,
                                lambda m, t: qT[:, Q * t:Q * t + Q], lambda m, s, e: kT[:, s:e],
                                lambda m, k: v[:, k, :], lambda t: o[:, t:t + 1, :],
                                strip=lambda t: strip[:, S - Q - Q * t:S - Q - Q * t + S])
                block = sg.block()

                @block.sync
                def _(sp):
                    clear_previous(sp, sg.sems)

                @block.vector
                def _(dve):
                    link = Chain(dve, vchain)
                    own = io_all[:, bass.ds(b, 1)].rearrange("p a t d -> p (a t) d")
                    dve.tensor_copy(y[:, :, :], own).then_inc(vector_done, 1)
                    dve.wait_ge(tensor_done, 1)
                    dve.tensor_copy(halves(xT[0:D, :]), two(0, D)).then_inc(vector_done, 1)
                    dve.wait_ge(tensor_done, 3)
                    dve.tensor_copy(halves(kT[:, :]), two(4, D)).then_inc(vector_done, 1)
                    att.vector(dve, link)
                    dve.wait_ge(att.out_ready, T)
                    dve.wait_ge(vector_done, 1)
                    dve.tensor_copy(own, o[:, :, :])

                @block.scalar
                def _(act):
                    act.wait_ge(tensor_done, 2)
                    act.copy(halves(qT[:, :]), two(2, D)).then_inc(scalar_done, 1)
                    act.wait_ge(tensor_done, 4)
                    act.activation(v[:, :, :], tiles(6), ACT.Copy, scale=att_scale[:, :]).then_inc(scalar_done, 1)
                    att.scalar(act)

                @block.tensor
                def _(pe):
                    pe.wait_ge(vector_done, 1)
                    turn(pe, 0, y).then_inc(tensor_done, 1)
                    pe.wait_ge(vector_done, 2)
                    by_feature(pe, 2, w["l0a_qkv"][:, 0:64], xT).then_inc(tensor_done, 1)
                    by_feature(pe, 4, w["l0a_qkv"][:, 64:128], xT).then_inc(tensor_done, 1)
                    by_token(pe, 6, xT, w["l0a_qkv"][:, 128:192]).then_inc(tensor_done, 1)
                    pe.wait_ge(vector_done, 3)
                    pe.wait_ge(scalar_done, 2)
                    att.tensor(pe, ident)

            end_of_pass("l0a_end")

        with Stage("l0q") as sg:
            vchain = sg.sem("vector_chain")
            passes = TurnedPasses(sg, ps, ident, TT)
            sqa = sg.sb("sq", [Q, TT, D])
            sta = sg.sb("st", [Q, 4, TT])
            block = sg.block()

            @block.sync
            def _(sp):
                clear_previous(sp, sg.sems)

            @block.vector
            def _(dve):
                link = Chain(dve, vchain)
                passes.ones(dve, link)
                passes.vector(dve, 0)
                link(dve.tensor_copy(in_banks(ya), passes.result(D)))
                layer_norm(dve, link, xa, ya, sqa[:, :, :], sta, 1e-5)
                affine(dve, link, xa, over_tiles(rows["l0a_g2"]), over_tiles(rows["l0a_b2"]))
                link(dve.tensor_tensor(ha, ha, xa, ALU.add))
                layer_norm(dve, link, xa, ha, sqa[:, :, :], sta, 1e-5)
                passes.vector(dve, 1)
                link(dve.tensor_copy(in_banks(ya), passes.result(D)))
                for n in range(4):
                    dve.tensor_copy(resid[:, :, 16 * n:16 * n + 16], io_all[:, n, :, 16 * n:16 * n + 16])

            @block.scalar
            def _(act):
                passes.scalar(act, 0)
                passes.scalar(act, 1)

            @block.tensor
            def _(pe):
                passes.turn(pe, 0, ya)
                passes.by_token(pe, 0, w["l0a_proj"][:, :])
                passes.turn(pe, 1, xa)
                passes.by_token(pe, 1, w["l0f_hl"][:, :])


        with nc.sbuf_tensor("ao_all", [Q, B, T, 16, 16], F32) as ao_all:
            with nc.Fori(0, B) as b:
                layer0_ffn(b, io_all, ao_all)
                end_of_pass("l0f_end")
            layer0_gates(ao_all, h_all, x_all)
        with nc.Fori(0, B) as b:
            layer1_attention(b, x_all, io_all)
            end_of_pass("l1a_end")
        layer1_mlp(h_all, x_all, io_all)
        with nc.Fori(0, B) as b:
            layer1_ffn(b, x_all, io_all)
            end_of_pass("l1f_end")
        experts("l1f", h_all, x_all, "gated", norm_after=True)
        with nc.Fori(0, B) as b:
            layer2_attention(b, h_all, x_all)
            end_of_pass("l2a_end")
        experts("l2f", h_all, x_all, "plain", norm_after=True)
        with nc.Fori(0, B) as b:
            layer3_attention(b, h_all, x_all)
            end_of_pass("l3a_end")
        experts("l3f", h_all, x_all, "soft")
        store()


def fourier(nc, a, ps, ident, ids, base, h_in, Stage, clear_previous, end_of_pass):
    NX = G // 2
    with ExitStack() as keepers:
        def sb(name, shape, dt=F32):
            return keepers.enter_context(nc.sbuf_tensor("fno_" + name, shape, dt))

        field = sb("field", [128, NX, 128])
        y_fwd = sb("y_fwd", [128, 48])
        x_fwd = sb("x_fwd", [128, 48])
        x_inv = sb("x_inv", [48, 128])
        y_inv = sb("y_inv", [96, 256])
        feats = sb("feats", [7, G * G])
        lift = sb("lift", [7, 128])
        mixw = sb("mixw", [128, 144, C])
        w1T = sb("w1T", [C, C])
        w2bd = sb("w2bd", [128, 128])
        b1 = sb("b1", [128, 1])
        b2row = sb("b2row", [128, 128])
        by_y = sb("by_y", [128, 24, G])
        by_yT = sb("by_yT", [128, KY, 128])
        modes = sb("modes", [128, B, KY, 2, 12])
        mixed = sb("mixed", [C, B, KY, 2, KX])
        convd = sb("convd", [48, KY, 128])
        by_x = sb("by_x", [128, G, 24])
        by_xT = sb("by_xT", [96, 16, 128])
        act_g = sb("act_g", [128, G * G])
        q1 = sb("q1", [128, 16])
        q2 = sb("q2", [16, 4])
        q1b = sb("q1b", [16, 1])
        q2b = sb("q2b", [4, 1])

        with Stage("lift") as sg:
            loaded = sg.sem("loaded")
            lifted = sg.sem("lifted")
            ids_loaded, gathered = sg.sem("ids_loaded"), sg.sem("gathered", keep=True)
            block = sg.block()

            @block.sync
            def _(sp):
                clear_previous(sp, sg.sems)
                sp.dma_start(ids[:, :], a["x_txt"].rearrange("b (q n) -> (b q) n", n=ids.shape[1])).then_inc(ids_loaded, 16)
                for dst, src in ((feats[0:B, :], a["x"].rearrange("b x y a -> b (x y a)")), (feats[B:7, :], a["c_grid"]),
                                 (lift[:, :], a["lift"]), (y_fwd[:, :], a["c_y_fwd"]), (x_fwd[:, :], a["c_x_fwd"]),
                                 (x_inv[:, :], a["c_x_inv"]), (y_inv[:, :], a["c_y_inv"]), (q1[:, :], a["q1_blocks"]),
                                 (q2[:, :], a["q2_blocks"]), (q1b[:, :], a["q1_bias"]), (q2b[:, :], a["q2_bias"])):
                    sp.dma_start(dst, src).then_inc(loaded, 16)
                sp.wait_ge(loaded, 16 * 11)

            @block.gpsimd
            def _(pool):
                pool.wait_ge(ids_loaded, 16)
                for n in range(ids.shape[1]):
                    pool.indirect_dma_start(base[:, n, :], None, a["L0_txt_turns"],
                                            bass.IndirectOffsetOnAxis(ap=ids[:, n:n + 1], axis=0)).then_inc(gathered, 16)
                pool.wait_ge(gathered, 16 * ids.shape[1])

            @block.tensor
            def _(pe):
                pe.wait_ge(loaded, 16 * 11)
                for i in range(NX):
                    mm = pe.matmul(ps[:, i // 4, 128 * (i % 4):128 * (i % 4) + 128], feats[:, 128 * i:128 * i + 128],
                                   lift[:, :], start=True, stop=True)
                    if i % 4 == 3:
                        mm.then_inc(lifted, 1)

            @block.vector
            def _(dve):
                for k in range(8):
                    dve.wait_ge(lifted, k + 1)
                    dve.tensor_copy(field[:, 4 * k:4 * k + 4, :].rearrange("p a n -> p (a n)"), ps[:, k, :])

        with nc.Fori(0, 4) as layer:
            with Stage("fno") as sg:
                loaded = sg.sem("weights_loaded")
                names = ("y_step", "y_turned", "x_step", "mix", "conv", "x_back", "x_turned", "y_back", "conv2")
                did = {n: sg.sem("tensor_" + n) for n in names}
                got_v = {n: sg.sem("vector_" + n) for n in names}
                got_s = {n: sg.sem("scalar_" + n) for n in names}
                vchain = sg.sem("vector_chain")
                block = sg.block()

                @block.sync
                def _(sp):
                    clear_previous(sp, sg.sems)
                    fw = a["fw_mix"][bass.ds(layer, 1)].rearrange("l p m o -> (l p) m o")
                    sp.dma_start(mixw[:, :, :], fw).then_inc(loaded, 16)
                    w1 = a["w1_T"][bass.ds(layer, 1)].rearrange("l i o -> (l i) o")
                    sp.dma_start(w1T[:, :], w1).then_inc(loaded, 16)
                    sp.dma_start(w2bd[:, :], a["w2_blocks"][bass.ds(layer, 1)].rearrange("l i o -> (l i) o")).then_inc(loaded, 16)
                    sp.dma_start(b1[:, :], a["b1_tiled"][bass.ds(layer, 1)].rearrange("l n a -> (l n) a")).then_inc(loaded, 16)
                    b2 = a["b2_tiled"][bass.ds(layer, 1)].rearrange("l a n -> (l a) n")
                    sp.dma_start(b2row[:, :], wide(b2, [128, 128])).then_inc(loaded, 16)
                    sp.wait_ge(loaded, 16 * 5)

                @block.tensor
                def _(pe):
                    for i in range(NX):
                        mm = pe.matmul(ps[:, i // 8, 48 * (i % 8):48 * (i % 8) + 48], field[:, i, :], y_fwd[:, :],
                                       start=True, stop=True)
                        if i % 8 == 7:
                            mm.then_inc(did["y_step"], 1)
                    pe.wait_ge(got_v["y_step"], 2)
                    pe.wait_ge(got_s["y_step"], 2)
                    for k in range(KY):
                        mm = pe.transpose(ps[:, 4 + k // 4, 128 * (k % 4):128 * (k % 4) + 128],
                                          by_y[:, 2 * k:2 * k + 2, :].rearrange("p c x -> p (c x)"), ident[:, :])
                        if k % 4 == 3:
                            mm.then_inc(did["y_turned"], 1)
                    pe.wait_ge(got_v["y_turned"], 2)
                    pe.wait_ge(got_s["y_turned"], 1)
                    for k in range(KY):
                        mm = pe.matmul(ps[:, k // 6, 48 * (k % 6):48 * (k % 6) + 48], by_yT[:, k, :], x_fwd[:, :],
                                       start=True, stop=True)
                    mm.then_inc(did["x_step"], 1)
                    pe.wait_ge(got_v["x_step"], 1)
                    pe.wait_ge(got_s["x_step"], 1)
                    pe.wait_ge(loaded, 16 * 5)
                    for m in range(72):
                        for g in range(4):
                            j, ky = m // KY, m % KY
                            hh, kh = g // 2, g % 2
                            rows = slice(2 * C * hh, 2 * C * hh + 2 * C)
                            col = 8 * ((j % 3) * KY + ky)
                            dst = ps[C * g:C * g + C, 2 * g + j // 3, col:col + 8]
                            mm = pe.matmul(dst, mixw[rows, 72 * kh + m, :],
                                           modes[rows, :, ky, :, 6 * kh + j].rearrange("p b c -> p c b"),
                                           start=True, stop=True, tile_position=(2 * C * hh, C * g))
                        if m % 36 == 35:
                            mm.then_inc(did["mix"], 1)
                    pe.wait_ge(got_v["mix"], 8)
                    for ky in range(KY):
                        for b in range(B):
                            mm = pe.matmul(ps[0:48, ky // 4, 128 * (ky % 4) + C * b:128 * (ky % 4) + C * b + C],
                                           mixed[:, b, ky, :, :].rearrange("p c k -> p (c k)"), w1T[:, :],
                                           start=True, stop=True)
                    mm.then_inc(did["conv"], 1)
                    pe.wait_ge(got_v["conv"], 1)
                    pe.wait_ge(got_s["conv"], 2)
                    for ky in range(KY):
                        mm = pe.matmul(ps[:, 3 + ky // 4, 128 * (ky % 4):128 * (ky % 4) + 128], convd[:, ky, :],
                                       x_inv[:, :], start=True, stop=True)
                        if ky % 4 == 3:
                            mm.then_inc(did["x_back"], 1)
                    pe.wait_ge(got_v["x_back"], 2)
                    pe.wait_ge(got_s["x_back"], 1)
                    for i in range(16):
                        mm = pe.transpose(ps[0:96, i // 4, 128 * (i % 4):128 * (i % 4) + 128],
                                          by_x[:, 4 * i:4 * i + 4, :].rearrange("p x k -> p (x k)"), ident[:, :])
                        if i % 4 == 3:
                            mm.then_inc(did["x_turned"], 1)
                    pe.wait_ge(got_v["x_turned"], 2)
                    pe.wait_ge(got_s["x_turned"], 2)
                    for i in range(16):
                        mm = pe.matmul(ps[:, i // 2, 256 * (i % 2):256 * (i % 2) + 256], by_xT[:, i, :], y_inv[:, :],
                                       start=True, stop=True)
                        if i % 2:
                            mm.then_inc(did["y_back"], 1)
                    for i in range(NX):
                        if i % 4 == 0:
                            pe.wait_ge(got_s["y_back"], i // 4 + 1)
                        mm = pe.matmul(ps[:, i // 4, 128 * (i % 4):128 * (i % 4) + 128], act_g[:, 128 * i:128 * i + 128],
                                       w2bd[:, :], start=True, stop=True)
                        if i % 4 == 3:
                            mm.then_inc(did["conv2"], 1)

                def y_out(k):
                    return (by_y[:, :, 16 * k:16 * k + 16].rearrange("p k x -> p x k"),
                            ps[:, k, 0:384].rearrange("p (x k) -> p x k", k=24))

                def x_out(k):
                    return (by_x[:, :, 8 * k:8 * k + 8].rearrange("p x (k c) -> p k c x", c=2),
                            ps[:, 3 + k, :].rearrange("p (k c x) -> p k c x", k=4, c=2))

                def regroup(k):
                    for b in range(B):
                        src = ps[C * b:C * b + C, k, 0:288].rearrange("p (y c k) -> p y c k", y=6, c=2)
                        for hh in range(2):
                            part = src[:, :, :, 12 * hh:12 * hh + 12]
                            at = 2 * C * hh
                            ky = slice(6 * k, 6 * k + 6)
                            yield modes[at:at + C, b, ky, :, :], part, 1
                            yield modes[at + C:at + 2 * C, b, ky, 0, :], part[:, :, 1, :], -1
                            yield modes[at + C:at + 2 * C, b, ky, 1, :], part[:, :, 0, :], 1

                @block.scalar
                def _(act):
                    for k in (1, 3):
                        act.wait_ge(did["y_step"], k + 1)
                        act.copy(*y_out(k)).then_inc(got_s["y_step"], 1)
                    act.wait_ge(did["y_turned"], 2)
                    act.copy(by_yT[:, 4:8, :].rearrange("p a n -> p (a n)"), ps[:, 5, :]).then_inc(got_s["y_turned"], 1)
                    act.wait_ge(did["x_step"], 1)
                    for dst, src, sign in regroup(1):
                        if sign < 0:
                            ins = act.mul(dst, src, -1.0)
                        else:
                            ins = act.copy(dst, src)
                    ins.then_inc(got_s["x_step"], 1)
                    act.wait_ge(did["conv"], 1)
                    for k in (0, 1):
                        act.copy(convd[:, 4 * k:4 * k + 4, :].rearrange("p a n -> p (a n)"), ps[0:48, k, :])\
                           .then_inc(got_s["conv"], 1)
                    act.wait_ge(did["x_back"], 2)
                    act.copy(*x_out(1)).then_inc(got_s["x_back"], 1)
                    for k in (1, 3):
                        act.wait_ge(did["x_turned"], k + 1)
                        act.copy(by_xT[:, 4 * k:4 * k + 4, :].rearrange("p a n -> p (a n)"), ps[0:96, k, :])\
                           .then_inc(got_s["x_turned"], 1)
                    for k in range(8):
                        act.wait_ge(did["y_back"], k + 1)
                        act.activation(act_g[:, 512 * k:512 * k + 512], ps[:, k, :], ACT.Relu, bias=b1[:, :])\
                           .then_inc(got_s["y_back"], 1)

                @block.vector
                def _(dve):
                    link = Chain(dve, vchain)
                    for k in (0, 2):
                        dve.wait_ge(did["y_step"], k + 1)
                        dve.tensor_copy(*y_out(k)).then_inc(got_v["y_step"], 1)
                    for k in (0, 2):
                        dve.wait_ge(did["y_turned"], k + 1)
                        dve.tensor_copy(by_yT[:, 4 * k:4 * k + 4, :].rearrange("p a n -> p (a n)"), ps[:, 4 + k, :])\
                           .then_inc(got_v["y_turned"], 1)
                    dve.wait_ge(did["x_step"], 1)
                    for dst, src, sign in regroup(0):
                        if sign < 0:
                            ins = dve.tensor_scalar(dst, src, -1.0, None, ALU.mult)
                        else:
                            ins = dve.tensor_copy(dst, src)
                    ins.then_inc(got_v["x_step"], 1)
                    for j3 in range(2):
                        dve.wait_ge(did["mix"], j3 + 1)
                        for g in range(4):
                            k0 = 6 * g + 3 * j3
                            for b in range(B):
                                src = ps[C * g:C * g + C, 2 * g + j3, 0:288].rearrange("p (j y c b) -> p j (y c) b", j=3, y=KY, c=2)
                                dst = mixed[:, b, :, :, k0:k0 + 3].rearrange("p y c j -> p j (y c)")
                                ins = dve.tensor_copy(dst, src[:, :, :, b])
                            ins.then_inc(got_v["mix"], 1)
                    dve.wait_ge(did["conv"], 1)
                    dve.tensor_copy(convd[:, 8:12, :].rearrange("p a n -> p (a n)"), ps[0:48, 2, :]).then_inc(got_v["conv"], 1)
                    for k in (0, 2):
                        dve.wait_ge(did["x_back"], k + 1)
                        dve.tensor_copy(*x_out(k)).then_inc(got_v["x_back"], 1)
                    for k in (0, 2):
                        dve.wait_ge(did["x_turned"], k + 1)
                        dve.tensor_copy(by_xT[:, 4 * k:4 * k + 4, :].rearrange("p a n -> p (a n)"), ps[0:96, k, :])\
                           .then_inc(got_v["x_turned"], 1)
                    for k in range(8):
                        dve.wait_ge(did["conv2"], k + 1)
                        part = field[:, 4 * k:4 * k + 4, :]
                        link(dve.tensor_tensor(part, part, ps[:, k, :].rearrange("p (a n) -> p a n", a=4), ALU.add))
                        dve.tensor_tensor(part, part, wide(b2row[:, :].unsqueeze(1), [128, 4, 128]), ALU.add)

            end_of_pass("fno_end")

        with Stage("img") as sg:
            turned, copied, read, acted, done, fin = (sg.sem(n) for n in
                                                      ("turned", "copied", "read_out", "acted", "second", "final"))
            stored = sg.sem("stored")
            hidden = mixw[0:16, :, :].rearrange("p m o -> p (m o)")[:, 0:G * G]
            res = field[0:B, :, :].rearrange("p i n -> p (i n)")
            block = sg.block()

            @block.sync
            def _(sp):
                clear_previous(sp, sg.sems)
                sp.wait_ge(fin, 8)
                sp.dma_start(h_in[:, 0:IMG, :].rearrange("b x y -> b (x y)"), res[:, :]).then_inc(stored, 16)
                sp.wait_ge(stored, 16)

            @block.tensor
            def _(pe):
                for i in range(NX):
                    mm = pe.transpose(ps[:, i // 4, 128 * (i % 4):128 * (i % 4) + 128], field[:, i, :], ident[:, :])
                    if i % 4 == 3:
                        mm.then_inc(turned, 1)
                for k in range(8):
                    pe.wait_ge(copied, k + 1)
                    pe.matmul(ps[0:16, k, :], q1[:, :], act_g[:, 512 * k:512 * k + 512], start=True, stop=True)\
                      .then_inc(read, 1)
                for k in range(8):
                    pe.wait_ge(acted, k + 1)
                    pe.matmul(ps[0:4, k, :], q2[:, :], hidden[:, 512 * k:512 * k + 512], start=True, stop=True)\
                      .then_inc(done, 1)

            @block.vector
            def _(dve):
                for k in range(8):
                    dve.wait_ge(turned, k + 1)
                    dve.tensor_copy(act_g[:, 512 * k:512 * k + 512], ps[:, k, :]).then_inc(copied, 1)
                for k in range(8):
                    dve.wait_ge(done, k + 1)
                    dve.tensor_scalar(res[:, 512 * k:512 * k + 512], ps[0:4, k, :], q2b[:, :], None, ALU.add)\
                       .then_inc(fin, 1)

            @block.scalar
            def _(act):
                for k in range(8):
                    act.wait_ge(read, k + 1)
                    act.activation(hidden[:, 512 * k:512 * k + 512], ps[0:16, k, :], ACT.Relu, bias=q1b[:, :])\
                       .then_inc(acted, 1)


def text(nc, a, ps, ident, up, base, h_in, Stage, clear_previous):
    N = 16
    with Stage("txt") as sg:
        mag = sg.sb("mag", [128, N, 4])
        whole_i = sg.sb("whole_i", [128, N, 4], I32)
        whole = sg.sb("whole", [128, N, 4])
        over = sg.sb("over", [128, N, 4])
        powers = sg.sb("powers", [128, N, 4, 5])
        powT = sg.sb("powT", [20, N, 128])
        coef = sg.sb("coef", [20, D])
        emb = sg.sb("emb", [128, N, D])
        whole_w = sg.sb("weights", [128, up.n])
        rest_w = sg.sb("weights_rest", [128, up.n])
        weights_loaded, first_part, rest_ready, second_part, third_part = (sg.sem(n) for n in (
            "weights_loaded", "first_part", "rest_ready", "second_part", "third_part"))
        quarter = [slice(up.n * k // 4, up.n * (k + 1) // 4) for k in range(4)]
        loaded, ready, turned, copied, made, stored, vchain, emb_done = (sg.sem(n) for n in (
            "loaded", "powers_ready", "turned", "copied", "made", "stored", "vector_chain", "emb_done"))
        block = sg.block()

        @block.sync
        def _(sp):
            clear_previous(sp, sg.sems)
            sp.dma_start(coef[:, :], a["L0_txt_poly_coeffs"].rearrange("t d o -> (t d) o")).then_inc(loaded, 16)
            for r in (slice(0, D), slice(D, 2 * D)):
                sp.dma_start(whole_w[r, :], a["pack_up"]).then_inc(weights_loaded, 16)
            sp.wait_ge(emb_done, 2)
            for b in range(B):
                sp.dma_start(h_in[b, IMG:S, :].rearrange("(q n) d -> q n d", n=N), emb[32 * b:32 * b + 32, :, :])\
                  .then_inc(stored, 16)
            sp.wait_ge(stored, 16 * B)

        @block.vector
        def _(dve):
            link = Chain(dve, vchain)
            flat = lambda t: t[:, :, :].rearrange("p n t -> p (n t)")
            link(dve.tensor_scalar(flat(mag), flat(base), -1.0, None, ALU.mult))
            link(dve.tensor_tensor(flat(mag), flat(mag), flat(base), ALU.max))
            link(dve.tensor_copy(flat(whole_i), flat(mag)))
            link(dve.tensor_copy(flat(whole), flat(whole_i)))
            link(dve.tensor_tensor(flat(over), flat(whole), flat(mag), ALU.is_gt))
            link(dve.tensor_tensor(flat(whole), flat(whole), flat(over), ALU.subtract))
            link(dve.tensor_scalar(flat(over), flat(base), 0.0, 2.0, ALU.is_ge, ALU.mult))
            link(dve.scalar_tensor_tensor(flat(whole), flat(over), -1.0, flat(whole), ALU.add, ALU.mult))
            pw = powers[:, :, :, :].rearrange("p n t d -> p (n t) d")
            link(dve.memset(pw[:, :, 0], 1.0))
            link(dve.tensor_copy(pw[:, :, 1], flat(whole)))
            for d in range(2, 5):
                ins = dve.tensor_tensor(pw[:, :, d], pw[:, :, d - 1], flat(whole), ALU.mult)
                link(ins)
            dve.sem_inc(ready, 1)
            for k in range(4):
                dve.wait_ge(turned, k + 1)
                dve.tensor_copy(powT[:, 4 * k:4 * k + 4, :].rearrange("p a n -> p (a n)"), ps[0:20, k, :]).then_inc(copied, 1)
            for k in range(2):
                dve.wait_ge(made, k + 1)
                dve.tensor_copy(emb[:, 8 * k:8 * k + 8, :].rearrange("p a n -> p (a n)"), ps[:, 4 + k, :]).then_inc(emb_done, 1)
            for k, c in enumerate(quarter):
                dve.wait_ge(first_part, k + 1)
                dve.tensor_tensor(rest_w[:, c], whole_w[:, c], up.pp[:, c], ALU.subtract).then_inc(rest_ready, 1)
            for k, c in enumerate(quarter):
                dve.wait_ge(second_part, k + 1)
                dve.tensor_tensor(up.rp[0:D, c], rest_w[0:D, c], up.qq[0:D, c], ALU.subtract).then_inc(third_part, 1)

        @block.scalar
        def _(act):
            act.wait_ge(weights_loaded, 32)
            for c in quarter:
                act.copy(up.pp[:, c], whole_w[:, c]).then_inc(first_part, 1)
            for k, c in enumerate(quarter):
                act.wait_ge(rest_ready, k + 1)
                act.copy(up.qq[:, c], rest_w[:, c]).then_inc(second_part, 1)
            act.copy(up.rp[D:2 * D, :], up.pp[D:2 * D, :]).then_inc(third_part, 1)

        @block.tensor
        def _(pe):
            pe.wait_ge(ready, 1)
            for n in range(N):
                mm = pe.transpose(ps[0:20, n // 4, 128 * (n % 4):128 * (n % 4) + 128],
                                  powers[:, n, :, :].rearrange("p t d -> p (t d)"), ident[:, :])
                if n % 4 == 3:
                    mm.then_inc(turned, 1)
            pe.wait_ge(loaded, 16)
            for n in range(N):
                pe.wait_ge(copied, n // 4 + 1)
                mm = pe.matmul(ps[:, 4 + n // 8, D * (n % 8):D * (n % 8) + D], powT[:, n, :], coef[:, :],
                               start=True, stop=True)
                if n % 8 == 7:
                    mm.then_inc(made, 1)


def tables():
    f = np.float32
    t = {"c_ident": np.eye(128, dtype=f)}
    r = np.arange(Q)
    t["c_causal"] = np.where(r[None, :] > r[:, None], f(NEG), f(0)).astype(f)
    t["c_causal32"] = np.tile(t["c_causal"][0:32, 0:32], (4, 1))
    t["c_keep"] = (r[None, :] >= r[:, None]).astype(f)
    t["c_iota8"] = np.tile(np.arange(8, dtype=f), (Q, 1))
    inv = 1.0 / 10000.0 ** (np.arange(0, 16, 2, dtype=f) / 16)
    fr = np.outer(np.arange(S, dtype=f), inv)
    t["c_cos"] = np.ascontiguousarray(np.cos(fr).astype(f).reshape(T, Q, 8).transpose(1, 0, 2))
    t["c_sin"] = np.ascontiguousarray(np.sin(fr).astype(f).reshape(T, Q, 8).transpose(1, 0, 2))
    xs = np.arange(G)
    ky = np.arange(KY)
    kx = np.concatenate([np.arange(12), np.arange(G - 12, G)])
    ty = 2 * np.pi * ((xs[:, None] * ky[None, :]) % G) / G
    tx = 2 * np.pi * ((xs[:, None] * kx[None, :]) % G) / G
    yf = np.zeros((2, G, 2, KY, 2))
    for p in range(2):
        yf[p, :, p, :, 0], yf[p, :, p, :, 1] = np.cos(ty), -np.sin(ty)
    t["c_y_fwd"] = yf.reshape(128, 48).astype(f)
    xf = np.zeros((2, G, 2, KX))
    xf[0, :, 0], xf[0, :, 1], xf[1, :, 0], xf[1, :, 1] = np.cos(tx), -np.sin(tx), np.sin(tx), np.cos(tx)
    t["c_x_fwd"] = (xf.reshape(128, 48) / G).astype(f)
    xi = np.zeros((2, KX, 2, G))
    xi[0, :, 0], xi[0, :, 1], xi[1, :, 0], xi[1, :, 1] = np.cos(tx).T, np.sin(tx).T, -np.sin(tx).T, np.cos(tx).T
    t["c_x_inv"] = xi.reshape(48, 128).astype(f)
    c = np.where(ky == 0, 1.0, 2.0)[:, None] / G
    yi = np.zeros((4, KY, 2, 4, G))
    for p in range(4):
        yi[p, :, 0, p], yi[p, :, 1, p] = c * np.cos(ty).T, -c * np.sin(ty).T
    t["c_y_inv"] = yi.reshape(96, 256).astype(f)
    lin = np.linspace(0.0, 1.0, G).astype(f)
    t["c_grid"] = np.stack([np.repeat(lin, G), np.tile(lin, G), np.ones(G * G, f)])
    return t


def layouts(v, k):
    o = dict(v)
    c = np.ascontiguousarray
    idx = np.clip(np.arange(Q)[:, None] * 0 + (np.arange(S + S - Q)[None, :] - np.arange(Q)[:, None]) - (S - Q) + S - 1,
                  0, v["L0_attn_bias_table"].shape[0] - 1)
    f = np.float32
    given = {"ident": k["c_ident"], "causal32": k["c_causal32"], "causal": k["c_causal"], "keep": k["c_keep"],
             "iota8": k["c_iota8"], "cos": k["c_cos"], "sin": k["c_sin"], "strip": v["L0_attn_bias_table"][idx]}
    qkv = np.zeros((64, 384), f)
    gate = np.zeros((128, 2, 8), f)
    fc = np.zeros((2, 65, 64), f)
    for n in range(4):
        r = slice(16 * n, 16 * n + 16)
        qkv[r, 64 * n:64 * n + 64] = v["L0_ffn_wq"][n].transpose(2, 0, 1).reshape(16, 64)
        qkv[r, 256 + 16 * n:272 + 16 * n] = v["L0_ffn_wk"][n].T
        qkv[r, 320 + 16 * n:336 + 16 * n] = v["L0_ffn_wv"][n].T
        gate[64 * (n % 2):64 * (n % 2) + 64, n // 2, 4 * (n % 2):4 * (n % 2) + 4] = v["L0_ffn_gate_w"][n].T
        for j in range(2):
            fc[j, r, r] = v[f"L0_ffn_fc{j + 1}_w"].T
            fc[j, 64, r] = v[f"L0_ffn_fc{j + 1}_b"]
    bias = lambda weight, b: np.concatenate([weight, b.reshape(1, -1)])
    given.update({
        "l0f_gate": gate, "l0f_qkv": qkv, "l0f_fc1": fc[0], "l0f_fc2": fc[1],
        "l1a_w2": v["L1_attn_w2"].reshape(2, 128, 64).transpose(1, 0, 2),
        "l0a_qkv": bias(v["L0_attn_qkv_w"], v["L0_attn_qkv_b"]), "l0a_proj": bias(v["L0_attn_proj_w"], v["L0_attn_proj_b"]),
        "l0f_hl": bias(v["L0_ffn_hl_w"].reshape(64, 64).T, v["L0_ffn_hl_b"]),
        "l1a_qkv": bias(v["L1_attn_qkv_w"], v["L1_attn_qkv_b"]), "l1a_proj": bias(v["L1_attn_proj_w"], v["L1_attn_proj_b"]),
        "l1a_w1": bias(v["L1_attn_w1"], v["L1_attn_b1"]),
        "l3a_qkv": np.concatenate([bias(v["L3_attn_W" + n], v["L3_attn_b" + n]) for n in "qkv"], 1),
        "l0f_fgate": v["L0_ffn_fgate_w"].T,
        "l1f_qkv": np.concatenate([v["L1_ffn_w" + n].T for n in "qkv"], 1), "l1f_wo": v["L1_ffn_wo"].T,
        "l2a_q": v["L2_attn_Wq"].T, "l2a_k": v["L2_attn_Wk"].T,
        "l1f_w2": v["L1_ffn_w2"].reshape(8, 64, 2, HP).transpose(3, 0, 2, 1),
        "l2a_v": v["L2_attn_Wv"].reshape(4, 16, D).transpose(1, 0, 2),
        "l2a_o": v["L2_attn_Wo"].T.reshape(4, 16, D).transpose(1, 0, 2),
        "att_scale": v["L0_attn_scale"],
        "l1f_router": v["L1_ffn_router_w"].T, "l2f_g": v["L2_ffn_Wg"], "l3f_r": v["L3_ffn_Wr"]})
    for n in "23":
        given[f"l{n}f_w2"] = v[f"L{n}_ffn_W2"].transpose(1, 0, 2)
        given[f"l{n}f_b1"] = v[f"L{n}_ffn_b1"].T
        blocks = np.zeros((12, 8, 12, D), f)
        for j in range(12):
            blocks[j, :, j, :] = v[f"L{n}_ffn_b2"]
        given[f"l{n}f_b2"] = blocks
        given[f"l{n}f_w1"] = v[f"L{n}_ffn_W1"].transpose(1, 0, 2)
    rows = {"l0a_g1": "L0_attn_ln1_g", "l0a_b1": "L0_attn_ln1_b", "l0a_g2": "L0_attn_ln2_g", "l0a_b2": "L0_attn_ln2_b",
            "l1a_g1": "L1_attn_ln1_g", "l1a_b1": "L1_attn_ln1_b", "l1a_g2": "L1_attn_ln2_g", "l1a_nb2": "L1_attn_ln2_b",
            "l1f_w1": "L1_ffn_ln1_w", "l1f_w2": "L1_ffn_ln2_w", "l1a_b2": "L1_attn_b2", "l3f_g": "L3_ffn_gamma", "l3f_b": "L3_ffn_beta",
            "l0f_g": "L0_ffn_ln_g", "l0f_b": "L0_ffn_ln_b", "l0f_fg": "L0_ffn_fnorm_g", "l0f_fb": "L0_ffn_fnorm_b",
            "l0f_gate": "L0_ffn_gate_b", "l2f_bg": "L2_ffn_bg", "l3f_br": "L3_ffn_br", "att_scale": "L0_attn_scale"}
    up = {"l1f_w1": v["L1_ffn_w1"].transpose(2, 0, 1), "l1f_w3": v["L1_ffn_w3"].transpose(2, 0, 1)}
    for pack, (p, pieces) in PACKS.items():
        of = lambda n: v[rows[n]] if pack == "rows" else up.get(n, given.get(n)) if pack == "up" else given[n]
        o["pack_" + pack] = c(np.concatenate([np.asarray(of(n)).reshape(p, -1) for n, _ in pieces], 1))
    lift = np.zeros((7, 128), f)
    w2 = np.zeros((4, 128, 128), f)
    q1, q2 = np.zeros((128, 16), f), np.zeros((16, 4), f)
    for b in range(B):
        cs = slice(C * b, C * b + C)
        lift[b, cs], lift[4:6, cs], lift[6, cs] = v["L0_tok_p_w"].T[0], v["L0_tok_p_w"].T[1:3], v["L0_tok_p_b"]
        w2[:, cs, cs] = v["L0_tok_w2_w"].transpose(0, 2, 1)
        q1[cs, 4 * b:4 * b + 4] = v["L0_tok_q1_w"].T
        q2[4 * b:4 * b + 4, b:b + 1] = v["L0_tok_q2_w"].T
    o["lift"], o["w2_blocks"], o["q1_blocks"], o["q2_blocks"] = lift, w2, q1, q2
    o["q1_bias"] = c(np.tile(v["L0_tok_q1_b"], B).reshape(16, 1))
    o["q2_bias"] = c(np.tile(v["L0_tok_q2_b"], B).reshape(4, 1))
    o["b1_tiled"] = c(np.tile(v["L0_tok_w1_b"], (1, B)).reshape(4, 128, 1))
    o["b2_tiled"] = c(np.tile(v["L0_tok_w2_b"], (1, B)).reshape(4, 1, 128))
    o["fw_mix"] = c(v["L0_tok_fw"].transpose(0, 1, 6, 2, 4, 5, 3).reshape(4, 128, 144, C))
    o["w1_T"] = c(v["L0_tok_w1_w"].transpose(0, 2, 1))
    used = ("x", "x_txt", "L0_txt_turns", "L0_txt_poly_coeffs")
    return {n: x for n, x in o.items() if n in used or n not in v}


def prepare(nc, inputs):
    arrays = {}
    args = {}
    k = tables()
    fno = {n: k[n] for n in ("c_y_fwd", "c_x_fwd", "c_x_inv", "c_y_inv", "c_grid")}
    for name, x in {**layouts({n: np.asarray(x) for n, x in inputs.items()}, k), **fno}.items():
        if x.ndim == 0:
            x = x.reshape(1)
        arrays["in_" + name] = np.ascontiguousarray(x)
        args[name] = nc.dram_tensor("in_" + name, x.shape, mybir.dt.from_np(x.dtype), kind="ExternalInput").ap()
    out = nc.dram_tensor("out_0", (B, S, D), F32, kind="ExternalOutput").ap()
    build(nc, args, out)
    return arrays


def kernel(**inputs):
    from concourse import bacc
    from concourse.bass_utils import run_bass_kernel_spmd

    nc = bacc.Bacc("TRN2", target_bir_lowering=False, num_devices=1)
    arrays = prepare(nc, inputs)
    r = run_bass_kernel_spmd(nc, [arrays], core_ids=[0])
    return r.results[0]["out_0"]
```
